# Optimizing a Trainium2 kernel written in Bass

```python
import numpy as np
import jax
import jax.numpy as jnp

def _softmax(x, axis=-1):
    return jax.nn.softmax(x, axis=axis)

def _gelu(x):
    return jax.nn.gelu(x, approximate=True)

def _silu(x):
    return jax.nn.silu(x)

def _sigmoid(x):
    return jax.nn.sigmoid(x)

def _layernorm(x, axis=-1, eps=1e-05):
    m = jnp.mean(x, axis=axis, keepdims=True)
    v = jnp.var(x, axis=axis, keepdims=True)
    return (x - m) / jnp.sqrt(v + eps)

def _scatter_add(tgt, idx, src, axis=0):
    return tgt.at[idx].add(src)

def _segment_sum(src, seg, n):
    return jax.ops.segment_sum(src, seg, n)
kernel_name = 'mk_gnn_ffn_d4_gnn_r32_7aec33'

def setup_inputs(seed: int=0):
    np.random.seed(seed)
    _w = jnp.asarray

    def _rec_inputs():
        import jax
        import jax.numpy as jnp
        _gk = jax.random.key(seed)
        x = -0.0002117 + 1 * jax.random.normal(jax.random.fold_in(_gk, 1), (3125, 256), jnp.float32)
        _s = jax.random.randint(jax.random.fold_in(_gk, 2), (25000,), 0, 3125, jnp.int32)
        _d = jax.random.randint(jax.random.fold_in(_gk, 3), (25000,), 0, 3125, jnp.int32)
        _loop = jnp.arange(3125, dtype=jnp.int32)
        src = jnp.concatenate([_s, _d, _loop])
        dst = jnp.concatenate([_d, _s, _loop])
        _o = jnp.argsort(dst, stable=True)
        src = src[_o]
        dst = dst[_o]
        edge_attr_3 = -1.09012e-05 + 0.99985 * jax.random.normal(jax.random.fold_in(_gk, 12), (53125, 3), jnp.float32)
        edge_weight = jax.random.uniform(jax.random.fold_in(_gk, 14), (53125,), jnp.float32, 0.0, 1)
        return (x, src, dst, edge_attr_3, edge_weight)
    x, src, dst, edge_attr_3, edge_weight = _rec_inputs()

    def _L0_gnn_setup():
        import jax, jax.numpy as jnp
        import numpy as np
        N_NODES = 3125
        N_EDGES = 50000
        D_IN = 256
        D_OUT = 256
        key = jax.random.key(seed)
        k1, k2, k3, k4, k5 = jax.random.split(key, 5)
        feat = jax.random.normal(k1, (N_NODES, D_IN), dtype=jnp.float32)
        lim = float(np.sqrt(6.0 / (D_IN + D_OUT)))
        W_neigh = jax.random.uniform(k2, (D_OUT, D_IN), minval=-lim, maxval=lim, dtype=jnp.float32)
        W_self = jax.random.uniform(k3, (D_OUT, D_IN), minval=-lim, maxval=lim, dtype=jnp.float32)
        b_self = jnp.zeros((D_OUT,), dtype=jnp.float32)
        src = jax.random.randint(k4, (N_EDGES,), 0, N_NODES, dtype=jnp.int32)
        dst = jax.random.randint(k5, (N_EDGES,), 0, N_NODES, dtype=jnp.int32)
        return {'feat': feat, 'W_neigh': W_neigh, 'W_self': W_self, 'b_self': b_self, 'src': src, 'dst': dst}
    _L0_gnn_all = _L0_gnn_setup()
    _L0_gnn_in = {k: v for k, v in _L0_gnn_all.items() if k in ('W_neigh', 'W_self', 'b_self')}
    del _L0_gnn_all

    def _L0_ffn_setup():
        import jax, jax.numpy as jnp
        import numpy as np
        B, S, D = (8, 128, 256)
        H = 4 * D
        CAPACITY = 0.5
        key = jax.random.key(seed)
        ks = jax.random.split(key, 6)
        x = jax.random.normal(ks[0], (B, S, D), dtype=jnp.float32)
        attention_mask = jnp.zeros((B, 1, 1, S), dtype=jnp.float32)
        wr = jax.random.normal(ks[1], (D, 1), dtype=jnp.float32) * 0.02
        br = jnp.zeros((1,), dtype=jnp.float32)
        w1 = jax.random.normal(ks[2], (D, H), dtype=jnp.float32) * 0.02
        b1 = jnp.zeros((H,), dtype=jnp.float32)
        w2 = jax.random.normal(ks[3], (H, D), dtype=jnp.float32) * 0.02
        b2 = jnp.zeros((D,), dtype=jnp.float32)
        return {'x': x, 'attention_mask': attention_mask, 'wr': wr, 'br': br, 'w1': w1, 'b1': b1, 'w2': w2, 'b2': b2}
    _L0_ffn_all = _L0_ffn_setup()
    _L0_ffn_in = {k: v for k, v in _L0_ffn_all.items() if k in ('attention_mask', 'wr', 'br', 'w1', 'b1', 'w2', 'b2')}
    del _L0_ffn_all

    def _L1_gnn_setup():
        import jax, jax.numpy as jnp
        import numpy as np
        N = 50000
        E = 12500
        IN = 256
        H = 8
        D = 32
        EF = 3
        key = jax.random.key(seed)
        ks = jax.random.split(key, 8)
        x = jax.random.normal(ks[0], (N, IN), dtype=jnp.float32)
        edge_index = jax.random.randint(ks[1], (2, E), 0, N, dtype=jnp.int64)
        edge_attr = jax.random.normal(ks[2], (E, EF), dtype=jnp.float32)
        W = jax.random.normal(ks[3], (H * D, IN), dtype=jnp.float32) * np.float32(np.sqrt(2.0 / (IN + H * D)))
        a_src = jax.random.normal(ks[4], (H, D), dtype=jnp.float32) * np.float32(np.sqrt(2.0 / (H + D)))
        a_dst = jax.random.normal(ks[5], (H, D), dtype=jnp.float32) * np.float32(np.sqrt(2.0 / (H + D)))
        edge_W = jax.random.normal(ks[6], (H * D, EF), dtype=jnp.float32) * np.float32(np.sqrt(2.0 / (EF + H * D)))
        edge_b = jnp.zeros((H * D,), dtype=jnp.float32)
        bias = jnp.zeros((H * D,), dtype=jnp.float32)
        return {'x': x, 'W': W, 'a_src': a_src, 'a_dst': a_dst, 'edge_W': edge_W, 'edge_b': edge_b, 'bias': bias, 'edge_attr': edge_attr, 'edge_index': edge_index}
    _L1_gnn_all = _L1_gnn_setup()
    _L1_gnn_in = {k: v for k, v in _L1_gnn_all.items() if k in ('W', 'a_src', 'a_dst', 'edge_W', 'edge_b', 'bias')}
    del _L1_gnn_all

    def _L1_ffn_setup():
        import math
        import jax, jax.numpy as jnp
        import numpy as np
        CAPACITY_FACTOR = 1.25
        key = jax.random.key(seed)
        ks = jax.random.split(key, 5)
        B, L, D, F, E = (8, 256, 256, 1024, 8)
        h = jax.random.normal(ks[0], (B, L, D), dtype=jnp.float32)
        gate_w = jax.random.normal(ks[1], (D, E), dtype=jnp.float32) * 0.02
        gate_b = jnp.zeros((E,), dtype=jnp.float32)
        w1 = jax.random.normal(ks[2], (E, D, F), dtype=jnp.float32) * (1.0 / math.sqrt(D))
        b1 = jnp.zeros((E, F), dtype=jnp.float32)
        w2 = jax.random.normal(ks[3], (E, F, D), dtype=jnp.float32) * (1.0 / math.sqrt(F))
        b2 = jnp.zeros((E, D), dtype=jnp.float32)
        return {'h': h, 'gate_w': gate_w, 'gate_b': gate_b, 'w1': w1, 'b1': b1, 'w2': w2, 'b2': b2}
    _L1_ffn_all = _L1_ffn_setup()
    _L1_ffn_in = {k: v for k, v in _L1_ffn_all.items() if k in ('gate_w', 'gate_b', 'w1', 'b1', 'w2', 'b2')}
    del _L1_ffn_all

    def _L2_gnn_setup():
        import jax, jax.numpy as jnp
        import numpy as np
        N = 3125
        E = 100000
        D_IN = 256
        D_OUT = 256
        key = jax.random.key(seed)
        k = jax.random.split(key, 8)
        stdv = 1.0 / np.sqrt(D_OUT)
        x = jax.random.normal(k[0], (N, D_IN), dtype=jnp.float32)
        edge_row = jax.random.randint(k[1], (E,), 0, N, dtype=jnp.int32)
        edge_col = jax.random.randint(k[2], (E,), 0, N, dtype=jnp.int32)
        edge_val = jax.random.uniform(k[3], (E,), dtype=jnp.float32)
        weight_l = jax.random.uniform(k[4], (D_IN, D_OUT), minval=-stdv, maxval=stdv, dtype=jnp.float32)
        bias_l = jax.random.uniform(k[5], (D_OUT,), minval=-stdv, maxval=stdv, dtype=jnp.float32)
        weight_r = jax.random.uniform(k[6], (D_IN, D_OUT), minval=-stdv, maxval=stdv, dtype=jnp.float32)
        bias_r = jax.random.uniform(k[7], (D_OUT,), minval=-stdv, maxval=stdv, dtype=jnp.float32)
        return {'x': x, 'edge_row': edge_row, 'edge_col': edge_col, 'edge_val': edge_val, 'weight_l': weight_l, 'bias_l': bias_l, 'weight_r': weight_r, 'bias_r': bias_r}
    _L2_gnn_all = _L2_gnn_setup()
    _L2_gnn_in = {k: v for k, v in _L2_gnn_all.items() if k in ('weight_l', 'bias_l', 'weight_r', 'bias_r')}
    del _L2_gnn_all

    def _L2_ffn_setup():
        import jax, jax.numpy as jnp
        import numpy as np
        E = 8
        K = 2
        D = 256
        H = 512
        DOUT = 256
        EPS = 1e-05
        key = jax.random.key(seed)
        ks = jax.random.split(key, 9)
        s = 0.02
        return {'x': jax.random.normal(ks[0], (4, 256, D), jnp.float32), 'gamma': 1.0 + 0.05 * jax.random.normal(ks[1], (D,), jnp.float32), 'beta': 0.05 * jax.random.normal(ks[2], (D,), jnp.float32), 'Wr': 0.01 * jax.random.normal(ks[3], (D, E), jnp.float32), 'br': jnp.zeros((E,), jnp.float32), 'W1': s * jax.random.normal(ks[4], (E, D, H), jnp.float32), 'b1': s * jax.random.normal(ks[5], (E, H), jnp.float32), 'W2': s * jax.random.normal(ks[6], (E, H, DOUT), jnp.float32), 'b2': s * jax.random.normal(ks[7], (E, DOUT), jnp.float32)}
    _L2_ffn_all = _L2_ffn_setup()
    _L2_ffn_in = {k: v for k, v in _L2_ffn_all.items() if k in ('gamma', 'beta', 'Wr', 'br', 'W1', 'b1', 'W2', 'b2')}
    del _L2_ffn_all

    def _L3_gnn_setup():
        import jax, jax.numpy as jnp
        import numpy as np
        NUM_NODES = 3125
        IN_CH = 256
        HIDDEN = 128
        OUT_CH = 256
        NUM_EDGES = 100000

        def gcn_conv(x, W, b, src, dst, num_nodes):
            h = x @ W
            loop = jnp.arange(num_nodes, dtype=src.dtype)
            s = jnp.concatenate([src, loop])
            d = jnp.concatenate([dst, loop])
            deg = jax.ops.segment_sum(jnp.ones_like(d, dtype=h.dtype), d, num_segments=num_nodes)
            dinv = jnp.where(deg > 0, jax.lax.rsqrt(deg), 0.0)
            norm = dinv[s] * dinv[d]
            msg = h[s] * norm[:, None]
            out = jax.ops.segment_sum(msg, d, num_segments=num_nodes)
            return out + b
        key = jax.random.key(seed)
        k1, k2, k3, k4 = jax.random.split(key, 4)
        edge_index = jax.random.randint(k1, (2, NUM_EDGES), 0, NUM_NODES, dtype=jnp.int64)
        node_features = jax.random.normal(k2, (NUM_NODES, IN_CH), dtype=jnp.float32)
        W1 = jax.random.normal(k3, (IN_CH, HIDDEN), dtype=jnp.float32) * (1.0 / np.sqrt(IN_CH))
        b1 = jnp.zeros((HIDDEN,), dtype=jnp.float32)
        W2 = jax.random.normal(k4, (HIDDEN, OUT_CH), dtype=jnp.float32) * (1.0 / np.sqrt(HIDDEN))
        b2 = jnp.zeros((OUT_CH,), dtype=jnp.float32)
        return {'node_features': node_features, 'W1': W1, 'b1': b1, 'W2': W2, 'b2': b2, 'edge_index': edge_index}
    _L3_gnn_all = _L3_gnn_setup()
    _L3_gnn_in = {k: v for k, v in _L3_gnn_all.items() if k in ('W1', 'b1', 'W2', 'b2')}
    del _L3_gnn_all

    def _L3_ffn_setup():
        import jax, jax.numpy as jnp
        import numpy as np
        C = 256
        HID = 1024
        E = 8
        TEMP = 1.0
        key = jax.random.key(seed)
        ks = jax.random.split(key, 7)
        x = jax.random.normal(ks[0], (8, 512, C), dtype=jnp.float32)
        W1 = jax.random.normal(ks[1], (C, HID), dtype=jnp.float32) * 0.02
        b1 = jnp.zeros((HID,), dtype=jnp.float32)
        Wg = jax.random.normal(ks[2], (HID, E), dtype=jnp.float32) * 0.02
        bg = jnp.zeros((E,), dtype=jnp.float32)
        Wd = jax.random.normal(ks[3], (E, HID, C), dtype=jnp.float32) * 0.02
        bd = jnp.zeros((E, C), dtype=jnp.float32)
        return {'x': x, 'W1': W1, 'b1': b1, 'Wg': Wg, 'bg': bg, 'Wd': Wd, 'bd': bd}
    _L3_ffn_all = _L3_ffn_setup()
    _L3_ffn_in = {k: v for k, v in _L3_ffn_all.items() if k in ('W1', 'b1', 'Wg', 'bg', 'Wd', 'bd')}
    del _L3_ffn_all
    return {'x': x, 'src': src, 'dst': dst, 'edge_attr_3': edge_attr_3, 'edge_weight': edge_weight, 'L0_gnn_W_neigh': _L0_gnn_in['W_neigh'], 'L0_gnn_W_self': _L0_gnn_in['W_self'], 'L0_gnn_b_self': _L0_gnn_in['b_self'], 'L0_ffn_attention_mask': _L0_ffn_in['attention_mask'], 'L0_ffn_wr': _L0_ffn_in['wr'], 'L0_ffn_br': _L0_ffn_in['br'], 'L0_ffn_w1': _L0_ffn_in['w1'], 'L0_ffn_b1': _L0_ffn_in['b1'], 'L0_ffn_w2': _L0_ffn_in['w2'], 'L0_ffn_b2': _L0_ffn_in['b2'], 'L1_gnn_W': _L1_gnn_in['W'], 'L1_gnn_a_src': _L1_gnn_in['a_src'], 'L1_gnn_a_dst': _L1_gnn_in['a_dst'], 'L1_gnn_edge_W': _L1_gnn_in['edge_W'], 'L1_gnn_edge_b': _L1_gnn_in['edge_b'], 'L1_gnn_bias': _L1_gnn_in['bias'], 'L1_ffn_gate_w': _L1_ffn_in['gate_w'], 'L1_ffn_gate_b': _L1_ffn_in['gate_b'], 'L1_ffn_w1': _L1_ffn_in['w1'], 'L1_ffn_b1': _L1_ffn_in['b1'], 'L1_ffn_w2': _L1_ffn_in['w2'], 'L1_ffn_b2': _L1_ffn_in['b2'], 'L2_gnn_weight_l': _L2_gnn_in['weight_l'], 'L2_gnn_bias_l': _L2_gnn_in['bias_l'], 'L2_gnn_weight_r': _L2_gnn_in['weight_r'], 'L2_gnn_bias_r': _L2_gnn_in['bias_r'], 'L2_ffn_gamma': _L2_ffn_in['gamma'], 'L2_ffn_beta': _L2_ffn_in['beta'], 'L2_ffn_Wr': _L2_ffn_in['Wr'], 'L2_ffn_br': _L2_ffn_in['br'], 'L2_ffn_W1': _L2_ffn_in['W1'], 'L2_ffn_b1': _L2_ffn_in['b1'], 'L2_ffn_W2': _L2_ffn_in['W2'], 'L2_ffn_b2': _L2_ffn_in['b2'], 'L3_gnn_W1': _L3_gnn_in['W1'], 'L3_gnn_b1': _L3_gnn_in['b1'], 'L3_gnn_W2': _L3_gnn_in['W2'], 'L3_gnn_b2': _L3_gnn_in['b2'], 'L3_ffn_W1': _L3_ffn_in['W1'], 'L3_ffn_b1': _L3_ffn_in['b1'], 'L3_ffn_Wg': _L3_ffn_in['Wg'], 'L3_ffn_bg': _L3_ffn_in['bg'], 'L3_ffn_Wd': _L3_ffn_in['Wd'], 'L3_ffn_bd': _L3_ffn_in['bd']}

def reference(x, src, dst, edge_attr_3, edge_weight, L0_gnn_W_neigh, L0_gnn_W_self, L0_gnn_b_self, L0_ffn_attention_mask, L0_ffn_wr, L0_ffn_br, L0_ffn_w1, L0_ffn_b1, L0_ffn_w2, L0_ffn_b2, L1_gnn_W, L1_gnn_a_src, L1_gnn_a_dst, L1_gnn_edge_W, L1_gnn_edge_b, L1_gnn_bias, L1_ffn_gate_w, L1_ffn_gate_b, L1_ffn_w1, L1_ffn_b1, L1_ffn_w2, L1_ffn_b2, L2_gnn_weight_l, L2_gnn_bias_l, L2_gnn_weight_r, L2_gnn_bias_r, L2_ffn_gamma, L2_ffn_beta, L2_ffn_Wr, L2_ffn_br, L2_ffn_W1, L2_ffn_b1, L2_ffn_W2, L2_ffn_b2, L3_gnn_W1, L3_gnn_b1, L3_gnn_W2, L3_gnn_b2, L3_ffn_W1, L3_ffn_b1, L3_ffn_Wg, L3_ffn_bg, L3_ffn_Wd, L3_ffn_bd):
    import jax
    import jax.numpy as jnp

    def _L0_gnn_ref(feat, W_neigh, W_self, b_self, src, dst):
        import jax, jax.numpy as jnp
        import numpy as np
        N_NODES = 3125
        N_EDGES = 50000
        D_IN = 256
        D_OUT = 256
        msgs = feat[src]
        neigh_sum = jax.ops.segment_sum(msgs, dst, num_segments=N_NODES)
        deg = jax.ops.segment_sum(jnp.ones((src.shape[0],), dtype=feat.dtype), dst, num_segments=N_NODES)
        h_neigh = neigh_sum / jnp.maximum(deg, 1.0)[:, None]
        h_neigh = h_neigh @ W_neigh.T
        h_self = feat @ W_self.T + b_self
        return h_self + h_neigh

    def _L0_ffn_ref(x, attention_mask, wr, br, w1, b1, w2, b2):
        import jax, jax.numpy as jnp
        import numpy as np
        B, S, D = (8, 128, 256)
        H = 4 * D
        CAPACITY = 0.5
        b, s, d = x.shape
        weights = (jnp.einsum('bsd,do->bso', x, wr) + br)[..., 0]
        k = max(1, int(CAPACITY * s))
        kk = k - 1 if k > 1 else 1
        _, idx = jax.lax.top_k(weights, k)
        sel_idx = idx[:, :kk]
        sel = jnp.take_along_axis(x, sel_idx[:, :, None], axis=1)
        h = jax.nn.gelu(jnp.einsum('bkd,dh->bkh', sel, w1) + b1)
        y = jnp.einsum('bkh,hd->bkd', h, w2) + b2
        w_sel = jnp.take_along_axis(weights, sel_idx, axis=1)
        y = y * w_sel[..., None]
        batch_idx = jnp.arange(b)[:, None]
        processed = jnp.zeros_like(x).at[batch_idx, sel_idx].set(y)
        return processed + x

    def _L1_gnn_ref(x, W, a_src, a_dst, edge_W, edge_b, bias, edge_attr, edge_index):
        import jax, jax.numpy as jnp
        import numpy as np
        N = 50000
        E = 12500
        IN = 256
        H = 8
        D = 32
        EF = 3
        n = x.shape[0]
        h = (x @ W.T).reshape(n, H, D)
        src, dst = (edge_index[0], edge_index[1])
        h_src = h[src]
        h_dst = h[dst]
        alpha = jnp.einsum('ehd,hd->eh', h_src, a_src) + jnp.einsum('ehd,hd->eh', h_dst, a_dst)
        enc = jax.nn.relu(edge_attr @ edge_W.T + edge_b).reshape(-1, H, D)
        alpha = alpha + jnp.sum(enc * h_dst, axis=-1)
        alpha = jnp.where(alpha >= 0, alpha, 0.2 * alpha)
        amax = jax.ops.segment_max(alpha, dst, num_segments=n)
        ex = jnp.exp(alpha - amax[dst])
        denom = jax.ops.segment_sum(ex, dst, num_segments=n)
        attn = ex / jnp.maximum(denom[dst], 1e-10)
        out = jax.ops.segment_sum(h_src * attn[..., None], dst, num_segments=n)
        return out.reshape(n, H * D) + bias

    def _L1_ffn_ref(h, gate_w, gate_b, w1, b1, w2, b2):
        import math
        import jax, jax.numpy as jnp
        import numpy as np
        CAPACITY_FACTOR = 1.25
        B, L, D = h.shape
        E = gate_w.shape[1]
        T = B * L
        C = max(1, math.ceil(CAPACITY_FACTOR * T / E))
        x = h.reshape(T, D)
        logits = x @ gate_w + gate_b
        probs = jax.nn.softmax(logits, axis=-1)
        idx = jnp.argmax(probs, axis=-1)
        prb = jnp.take_along_axis(probs, idx[:, None], axis=1)[:, 0]
        one_hot = jax.nn.one_hot(idx, E, dtype=jnp.float32)
        pos = (jnp.cumsum(one_hot, axis=0) * one_hot).sum(-1).astype(jnp.int32) - 1
        kept = pos < C
        pos_safe = jnp.where(kept, pos, C)
        buf = jnp.zeros((E, C, D), dtype=h.dtype).at[idx, pos_safe].set(x, mode='drop')
        hmid = jax.nn.relu(jnp.einsum('ecd,edf->ecf', buf, w1) + b1[:, None, :])
        ybuf = jnp.einsum('ecf,efd->ecd', hmid, w2) + b2[:, None, :]
        pos_g = jnp.minimum(pos, C - 1)
        y_tok = ybuf[idx, pos_g] * (prb * kept)[:, None]
        y = y_tok.reshape(B, L, D)
        y = jnp.nan_to_num(y, nan=0.0, posinf=10000.0, neginf=-10000.0)
        return y

    def _L2_gnn_ref(x, edge_row, edge_col, edge_val, weight_l, bias_l, weight_r, bias_r):
        import jax, jax.numpy as jnp
        import numpy as np
        N = 3125
        E = 100000
        D_IN = 256
        D_OUT = 256
        h = x @ weight_l
        msgs = edge_val[:, None] * h[edge_col]
        agg = jax.ops.segment_sum(msgs, edge_row, num_segments=N)
        out = agg + bias_l
        out = out + x @ weight_r + bias_r
        return out

    def _L2_ffn_ref(x, gamma, beta, Wr, br, W1, b1, W2, b2):
        import jax, jax.numpy as jnp
        import numpy as np
        E = 8
        K = 2
        D = 256
        H = 512
        DOUT = 256
        EPS = 1e-05
        mu = jnp.mean(x, axis=-1, keepdims=True)
        var = jnp.mean(jnp.square(x - mu), axis=-1, keepdims=True)
        xn = (x - mu) * jax.lax.rsqrt(var + EPS) * gamma + beta
        logits = jnp.einsum('bsd,de->bse', xn, Wr) + br
        top_vals, top_idx = jax.lax.top_k(logits, K)
        w = jax.nn.softmax(top_vals, axis=-1)
        w_full = jnp.einsum('bsk,bske->bse', w, jax.nn.one_hot(top_idx, E, dtype=w.dtype))
        y = jnp.zeros(x.shape[:-1] + (DOUT,), x.dtype)
        for e in range(E):
            h = jax.nn.gelu(jnp.einsum('bsd,dh->bsh', xn, W1[e]) + b1[e], approximate=False)
            y_e = jnp.einsum('bsh,hd->bsd', h, W2[e]) + b2[e]
            y = y + y_e * w_full[..., e, None]
        return y

    def _L3_gnn_ref(node_features, W1, b1, W2, b2, edge_index):
        import jax, jax.numpy as jnp
        import numpy as np
        NUM_NODES = 3125
        IN_CH = 256
        HIDDEN = 128
        OUT_CH = 256
        NUM_EDGES = 100000

        def gcn_conv(x, W, b, src, dst, num_nodes):
            h = x @ W
            loop = jnp.arange(num_nodes, dtype=src.dtype)
            s = jnp.concatenate([src, loop])
            d = jnp.concatenate([dst, loop])
            deg = jax.ops.segment_sum(jnp.ones_like(d, dtype=h.dtype), d, num_segments=num_nodes)
            dinv = jnp.where(deg > 0, jax.lax.rsqrt(deg), 0.0)
            norm = dinv[s] * dinv[d]
            msg = h[s] * norm[:, None]
            out = jax.ops.segment_sum(msg, d, num_segments=num_nodes)
            return out + b
        src, dst = (edge_index[0], edge_index[1])
        x = gcn_conv(node_features, W1, b1, src, dst, NUM_NODES)
        x = jax.nn.relu(x)
        x = gcn_conv(x, W2, b2, src, dst, NUM_NODES)
        return x

    def _L3_ffn_ref(x, W1, b1, Wg, bg, Wd, bd):
        import jax, jax.numpy as jnp
        import numpy as np
        C = 256
        HID = 1024
        E = 8
        TEMP = 1.0
        orig_shape = x.shape
        xf = x.reshape(-1, orig_shape[-1])
        H = jax.nn.gelu(xf @ W1 + b1, approximate=False)
        probs = jax.nn.softmax((H @ Wg + bg) / TEMP, axis=-1)
        assign = jnp.argmax(probs, axis=-1)
        out = jnp.zeros_like(xf)
        for e in range(Wd.shape[0]):
            y = H @ Wd[e] + bd[e]
            sel = (assign == e)[:, None]
            out = out + jnp.where(sel, probs[:, e:e + 1] * y, 0.0)
        return out.reshape(orig_shape)
    edge_index = jnp.stack([src, dst])
    x = x + _L0_gnn_ref(_layernorm(x, axis=-1), L0_gnn_W_neigh, L0_gnn_W_self, L0_gnn_b_self, src, dst)
    x = x + _L0_ffn_ref(_layernorm(x, axis=-1)[None], L0_ffn_attention_mask, L0_ffn_wr, L0_ffn_br, L0_ffn_w1, L0_ffn_b1, L0_ffn_w2, L0_ffn_b2)[0]
    x = x + _L1_gnn_ref(_layernorm(x, axis=-1), L1_gnn_W, L1_gnn_a_src, L1_gnn_a_dst, L1_gnn_edge_W, L1_gnn_edge_b, L1_gnn_bias, edge_attr_3, edge_index)
    x = x + _L1_ffn_ref(_layernorm(x, axis=-1)[None], L1_ffn_gate_w, L1_ffn_gate_b, L1_ffn_w1, L1_ffn_b1, L1_ffn_w2, L1_ffn_b2)[0]
    x = x + _L2_gnn_ref(_layernorm(x, axis=-1), src, dst, edge_weight, L2_gnn_weight_l, L2_gnn_bias_l, L2_gnn_weight_r, L2_gnn_bias_r)
    x = x + _L2_ffn_ref(_layernorm(x, axis=-1)[None], L2_ffn_gamma, L2_ffn_beta, L2_ffn_Wr, L2_ffn_br, L2_ffn_W1, L2_ffn_b1, L2_ffn_W2, L2_ffn_b2)[0]
    x = x + _L3_gnn_ref(_layernorm(x, axis=-1), L3_gnn_W1, L3_gnn_b1, L3_gnn_W2, L3_gnn_b2, edge_index)
    x = x + _L3_ffn_ref(_layernorm(x, axis=-1)[None], L3_ffn_W1, L3_ffn_b1, L3_ffn_Wg, L3_ffn_bg, L3_ffn_Wd, L3_ffn_bd)[0]
    return x

_drawn_inputs = setup_inputs


def setup_inputs(seed=0):
    import zlib

    import numpy as np

    out = dict(_drawn_inputs(seed))
    spreads = {'L0_gnn_b_self': (0.0, 0.1),
     'L0_ffn_b1': (0.0, 0.8),
     'L0_ffn_b2': (0.0, 0.655),
     'L1_gnn_edge_b': (0.0, 0.309),
     'L1_gnn_bias': (0.0, 0.1),
     'L1_ffn_gate_b': (0.0, 0.279),
     'L1_ffn_b1': (0.0, 0.8),
     'L1_ffn_b2': (0.0, 0.8),
     'L2_ffn_br': (0.0, 0.534),
     'L3_gnn_b1': (0.0, 0.464),
     'L3_gnn_b2': (0.0, 0.1),
     'L3_ffn_b1': (0.0, 0.8),
     'L3_ffn_bg': (0.0, 0.8),
     'L3_ffn_bd': (0.0, 0.8)}
    factors = {'L0_ffn_wr': 4.437,
     'L0_ffn_w1': 5.383,
     'L0_ffn_w2': 4.75,
     'L2_gnn_bias_l': 4.45,
     'L2_gnn_bias_r': 4.536,
     'L2_ffn_gamma': 8.0,
     'L2_ffn_beta': 8.0,
     'L2_ffn_Wr': 3.719,
     'L2_ffn_W1': 3.122,
     'L2_ffn_b1': 8.0,
     'L2_ffn_W2': 3.053,
     'L2_ffn_b2': 8.0,
     'L3_ffn_W1': 7.753,
     'L3_ffn_Wg': 8.0,
     'L3_ffn_Wd': 8.0}
    for name, (base, spread) in spreads.items():
        noise = np.random.default_rng([zlib.crc32(name.encode()), seed]).standard_normal(out[name].shape)
        drawn = base * np.exp(spread * noise) if base else spread * noise
        out[name] = jnp.asarray(drawn.astype(out[name].dtype))
    for name, factor in factors.items():
        out[name] = (out[name] * factor).astype(out[name].dtype)
    return out
```

```python
import concourse.bass as bass
from concourse import mybir
from concourse.bass import ds
from contextlib import ExitStack

F32, I32, U32 = mybir.dt.float32, mybir.dt.int32, mybir.dt.uint32
ALU, ACT, AX = mybir.AluOpType, mybir.ActivationFunctionType, mybir.AxisListType
P = 128
NODES, D = 3125, 256
EDGES = 53125
NT = 26
ROWS = NT * P
FULL = NODES // P
REST = NODES - FULL * P
ET = 416
EPS = 1e-5


class Core:
    pass


def tensors(nc, g, stack):
    def sb(name, shape, dt=F32):
        return stack.enter_context(nc.sbuf_tensor(g.tag + name, shape, dt))
    g.x = sb("x_nodes", [P, NT, D])
    g.xn = sb("xn_nodes", [P, NT, D])
    g.acc = sb("edge_sums", [P, NT, D])
    g.deg = sb("in_degree", [P, NT])
    g.srcc = sb("src_cols", [P, ET], I32)
    g.dstc = sb("dst_cols", [P, ET], I32)
    g.local = sb("dst_local", [P, ET + 8])
    g.window = sb("dst_window", [1, ET], I32)
    g.ident = sb("identity", [P, P])
    g.iota = sb("iota_row", [P, 2 * P])
    g.ones = sb("ones", [P, P])
    g.eps = sb("eps", [P, 1])
    g.stats = sb("ln_stats", [P, NT, 6])
    g.mv = sb("ln_mean_var", [P, NT, 2])
    g.rstd = sb("ln_rstd", [P, NT])
    g.ps = [stack.enter_context(nc.psum_tensor(f"bank{b}", [P, 512], F32)) for b in range(8)]


def load_graph(nc, g, a):
    with ExitStack() as stack:
        sem = lambda n: nc.alloc_semaphore(g.tag + n)
        x_cleared, x_loaded, idx_loaded = sem("x_cleared"), sem("x_loaded"), sem("idx_loaded")
        consts, ident0, win = sem("consts"), sem("ident_cleared"), sem("win_ready")
        win_sum, step = sem("win_sum"), sem("window_step")
        wf = stack.enter_context(nc.sbuf_tensor(g.tag + "window_f", [1, ET], F32))
        wi = stack.enter_context(nc.sbuf_tensor(g.tag + "window_tile", [1, ET], I32))
        df = stack.enter_context(nc.sbuf_tensor(g.tag + "dst_f", [P, ET], F32))
        block = stack.enter_context(nc.Block(g.tag + "load_graph"))

        @block.sync
        def _(sp):
            sp.dma_start(g.dstc[:, :], a.dst_cols).then_inc(idx_loaded, 16)
            sp.dma_start(g.srcc[:, :], a.src_cols).then_inc(idx_loaded, 16)
            sp.wait_ge(x_cleared, 1)
            sp.dma_start(g.x[:, 0:FULL, :], a.x[0:FULL * P, :].rearrange("(t p) d -> p t d", p=P)).then_inc(x_loaded, 16)
            sp.dma_start(g.x[0:REST, FULL, :], a.x[FULL * P:NODES, :]).then_inc(x_loaded, 16)
            sp.wait_ge(x_loaded, 32)

        @block.gpsimd
        def _(pool):
            nc.gpsimd.memset(g.ident[:, :], 0.0).then_inc(ident0, 1)
            nc.gpsimd.iota(g.iota[:, :], [[1, 2 * P]], base=0, channel_multiplier=0,
                           allow_small_or_imprecise_dtypes=True).then_inc(consts, 1)
            pool.wait_ge(ident0, 1)
            nc.gpsimd.affine_select(out=g.ident[:, :], in_=g.ident[:, :], compare_op=ALU.not_equal, fill=1.0,
                                    base=0, pattern=[[-1, P]], channel_multiplier=1).then_inc(consts, 1)

        @block.vector
        def _(dve):
            nc.vector.memset(g.x[:, FULL:NT, :], 0.0).then_inc(x_cleared, 1)
            nc.vector.memset(g.ones[:, :], 1.0).then_inc(consts, 1)
            nc.vector.memset(g.eps[:, :], EPS).then_inc(consts, 1)
            nc.vector.memset(g.local[:, ET:ET + 8], 0.0).then_inc(consts, 1)
            dve.wait_ge(idx_loaded, 32)
            nc.vector.tensor_scalar(wi[:, :], g.dstc[0:1, :], 7, None, ALU.logical_shift_right).then_inc(step, 1)
            nc.vector.tensor_copy(df[:, :], g.dstc[:, :]).then_inc(step, 1)
            dve.wait_ge(step, 2)
            nc.vector.tensor_copy(wf[:, :], wi[:, :]).then_inc(win, 1)
            nc.vector.tensor_copy(g.window[:, :], wi[:, :]).then_inc(step, 1)
            dve.wait_ge(win_sum, 1)
            nc.vector.scalar_tensor_tensor(out=g.local[:, 0:ET], in0=g.ps[0][:, 0:ET], scalar=-float(P), in1=df[:, :],
                                           op0=ALU.mult, op1=ALU.add).then_inc(step, 1)
            dve.wait_ge(step, 4)

        @block.tensor
        def _(pe):
            pe.wait_ge(win, 1)
            pe.wait_ge(consts, 5)
            nc.tensor.matmul(g.ps[0][:, 0:ET], g.ones[0:1, :], wf[0:1, :], start=True, stop=True).then_inc(win_sum, 1)


def layer_norm(nc, g, table):
    with ExitStack() as stack:
        sem = lambda n: nc.alloc_semaphore(g.tag + n)
        stat, aggr, root, inv, normed, stored = (sem("ln_" + n) for n in ("stat", "aggr", "root", "inv", "normed", "stored"))
        block = stack.enter_context(nc.Block(g.tag + "layer_norm"))

        @block.vector
        def _(dve):
            with nc.vector.Fori(0, NT) as t:
                nc.vector.bn_stats(g.stats[:, ds(t, 1), :], g.x[:, ds(t, 1), :]).then_inc(stat, 1)
            dve.wait_ge(stat, NT)
            for t in range(NT):
                nc.vector.bn_aggr(g.mv[:, t, :], g.stats[:, t, :]).then_inc(aggr, 1)
            dve.wait_ge(root, 1)
            nc.vector.reciprocal(g.rstd[:, :], g.rstd[:, :]).then_inc(inv, 1)
            dve.wait_ge(inv, 1)
            with nc.vector.Fori(0, NT) as t:
                nc.vector.tensor_scalar(g.xn[:, ds(t, 1), :], g.x[:, ds(t, 1), :], g.mv[:, ds(t, 1), 0],
                                        g.rstd[:, ds(t, 1)], ALU.subtract, ALU.mult).then_inc(normed, 1)

        @block.scalar
        def _(act):
            act.wait_ge(aggr, NT)
            nc.scalar.activation(g.rstd[:, :], g.mv[:, :, 1], ACT.Sqrt, bias=g.eps[:, 0:1]).then_inc(root, 1)

        @block.sync
        def _(sp):
            sp.wait_ge(normed, NT)
            if table is None:
                return
            sp.dma_start(table.rearrange("(t p) d -> p t d", p=P), g.xn[:, :, :]).then_inc(stored, 16)
            sp.wait_ge(stored, 16)


def sum_edges(nc, g, table, width, count_degree=False, name="sum"):
    U = 8
    with ExitStack() as stack:
        sem = lambda n: nc.alloc_semaphore(g.tag + name + n)
        gathered = [sem(f"gathered{u}") for u in range(U)]
        copied, hot, summed, added, cleared, claimed = sem("idx_copied"), sem("hot_ready"), sem("tile_summed"), sem("tile_added"), sem("acc_cleared"), sem("slot_claimed")
        idx = stack.enter_context(nc.sbuf_tensor(g.tag + name + "gather_idx", [P, 2, U // 2], I32))
        rows = stack.enter_context(nc.sbuf_tensor(g.tag + name + "gathered_rows", [P, U, width], F32))
        onehot = stack.enter_context(nc.sbuf_tensor(g.tag + name + "onehot", [P, 4, 2 * P], F32))
        block = stack.enter_context(nc.Block(g.tag + name + "sum_edges"))
        acc = g.acc[:, :, :].rearrange("p t d -> p (t d)")

        @block.gpsimd
        def _(pool):
            with nc.gpsimd.Fori(0, ET // U) as i:
                for h in range(2):
                    pool.wait_ge(summed, U * i + (h + 1) * U // 2)
                    nc.gpsimd.tensor_copy(idx[:, h, :], g.srcc[:, ds(U * i + h * U // 2, U // 2)]).then_inc(copied, 1)
                    pool.wait_ge(copied, 2 * i + h + 1)
                    for u in range(h * U // 2, (h + 1) * U // 2):
                        pool.wait_ge(summed, U * i + u + 1)
                        pool.sem_inc(claimed, 1)
                        nc.gpsimd.indirect_dma_start(
                            rows[:, u, :], None, table,
                            bass.IndirectOffsetOnAxis(ap=idx[:, h, u % 4:u % 4 + 1].bitcast(U32), axis=0)).then_inc(gathered[u], 16)

        @block.tensor
        def _(pe):
            pe.sem_inc(summed, U)
            with nc.tensor.Fori(0, ET // U) as i:
                for u in range(U):
                    pe.wait_ge(hot, U * i + u + 1)
                    pe.wait_ge(added, U * i + u + 1)
                    pe.wait_ge(gathered[u], 16 * (i + 1))
                    bank = g.ps[u % 4]
                    if count_degree:
                        nc.tensor.matmul(g.ps[4 + u % 4][:, 0:1], onehot[:, u % 4, 0:P], g.ones[:, 0:1], start=True, stop=True)
                        nc.tensor.matmul(g.ps[4 + u % 4][:, 1:2], onehot[:, u % 4, P:2 * P], g.ones[:, 0:1], start=True, stop=True)
                    nc.tensor.matmul(bank[:, 0:width], onehot[:, u % 4, 0:P], rows[:, u, :], start=True, stop=True)
                    nc.tensor.matmul(bank[:, width:2 * width], onehot[:, u % 4, P:2 * P], rows[:, u, :],
                                     start=True, stop=True).then_inc(summed, 1)

        @block.vector
        def _(dve):
            base = [nc.vector.alloc_register(g.tag + name + f"window{u}") for u in range(U)]
            nc.vector.memset(g.acc[:, :, :], 0.0).then_inc(cleared, 1)
            nc.vector.memset(g.deg[:, :], 0.0).then_inc(cleared, 1)
            dve.wait_ge(cleared, 2)

            def build(n, slot):
                nc.vector.tensor_scalar(onehot[:, slot, :], g.iota[:, :], g.local[:, ds(n, 1)] if not isinstance(n, int) else g.local[:, n:n + 1], None,
                                        ALU.is_equal).then_inc(hot, 1)
            build(0, 0)
            build(1, 1)
            nc.vector.sem_inc(added, 4)
            with nc.vector.Fori(0, ET // U) as i:
                nc.vector.reg_load(base, g.window[0:1, ds(U * i, U)])
                for u in range(U):
                    build(U * i + u + 2, (u + 2) % 4)
                    w = nc.vector.snap(base[u], min_val=0, max_val=NT - 2)
                    dve.wait_ge(summed, U * i + u + 1 + U)
                    dve.wait_ge(added, U * i + u + 4)
                    if count_degree:
                        nc.vector.tensor_tensor(g.deg[:, ds(w, 2)], g.deg[:, ds(w, 2)], g.ps[4 + u % 4][:, 0:2], ALU.add)
                    nc.vector.tensor_tensor(acc[:, ds(w * width, 2 * width)], acc[:, ds(w * width, 2 * width)],
                                            g.ps[u % 4][:, 0:2 * width], ALU.add).then_inc(added, 1)


def project(nc, g, name, weights, bias, width, stage, finish, chunks=2):
    K = len(weights)
    with ExitStack() as stack:
        sem = lambda n: nc.alloc_semaphore(g.tag + name + n)
        staged = [sem(f"_staged{k}") for k in range(K)]
        turned, lhs_ready, product, used = sem("_turned"), sem("_lhs_ready"), sem("_product"), sem("_used")
        rows = stack.enter_context(nc.sbuf_tensor(g.tag + name + "_rows", [P, 2, K, chunks * P], F32))
        lhs = stack.enter_context(nc.sbuf_tensor(g.tag + name + "_lhs", [P, 2, K * chunks * P], F32))
        block = stack.enter_context(nc.Block(g.tag + name))

        def staging(eng, who, t, s):
            for k in range(K):
                if stage[k][0] == who:
                    eng.wait_ge(turned, t + 1)
                    stage[k][1](rows[:, s, k, :], t).then_inc(staged[k], 1)

        @block.gpsimd
        def _(pool):
            if any(w == "pool" for w, _ in stage):
                with nc.gpsimd.Fori(0, NT // 2) as i:
                    for s in range(2):
                        staging(pool, "pool", 2 * i + s, s)

        @block.tensor
        def _(pe):
            pe.sem_inc(turned, 2)
            pe.sem_inc(product, 2)
            with nc.tensor.Fori(0, NT // 2) as i:
                for s in range(2):
                    t = 2 * i + s
                    pe.wait_ge(lhs_ready, t + 1)
                    for k in range(K):
                        pe.wait_ge(staged[k], t + 1)
                        for c in range(chunks):
                            last = nc.tensor.transpose(g.ps[s][:, (chunks * k + c) * P:(chunks * k + c + 1) * P],
                                                       rows[:, s, k, c * P:(c + 1) * P], g.ident[:, :])
                    last.then_inc(turned, 1)
                for s in range(2):
                    t = 2 * i + s
                    pe.wait_ge(lhs_ready, t + 3)
                    pe.wait_ge(used, t + 1)
                    if bias is not None:
                        nc.tensor.matmul(g.ps[2 + s][:, 0:width], g.ones[0:1, :], bias, start=True, stop=False)
                    for k in range(K):
                        for c in range(chunks):
                            last = nc.tensor.matmul(g.ps[2 + s][:, 0:width], lhs[:, s, (chunks * k + c) * P:(chunks * k + c + 1) * P],
                                                    weights[k][:, c, 0:width], start=(bias is None and k == 0 and c == 0),
                                                    stop=(k == K - 1 and c == chunks - 1))
                    last.then_inc(product, 1)

        @block.scalar
        def _(act):
            act.sem_inc(lhs_ready, 2)
            with nc.scalar.Fori(0, NT // 2) as i:
                for s in range(2):
                    t = 2 * i + s
                    staging(act, "act", t, s)
                    act.wait_ge(turned, t + 3)
                    act.wait_ge(product, t + 1)
                    nc.scalar.activation(lhs[:, s, :], g.ps[s][:, 0:K * chunks * P], ACT.Copy).then_inc(lhs_ready, 1)

        @block.vector
        def _(dve):
            dve.sem_inc(used, 2)
            with nc.vector.Fori(0, NT // 2) as i:
                for s in range(2):
                    staging(dve, "dve", 2 * i + s, s)
                for s in range(2):
                    t = 2 * i + s
                    dve.wait_ge(product, t + 3)
                    finish(dve, g.ps[2 + s][:, 0:width], t, s).then_inc(used, 1)


def load_weights(nc, g, name, pairs):
    with ExitStack() as stack:
        loaded = nc.alloc_semaphore(g.tag + name + "_loaded")
        block = stack.enter_context(nc.Block(g.tag + name + "_load"))

        @block.sync
        def _(sp):
            for dst, src in pairs:
                sp.dma_start(dst, src).then_inc(loaded, 16)
            sp.wait_ge(loaded, 16 * len(pairs))


def rows_in(w, c=P):
    return w.rearrange("(c p) n -> p c n", p=c)


def across(v):
    return v.rearrange("(o n) -> o n", o=1).to_broadcast([P, v.shape[0]])


def layer0_gnn(nc, g, a, table):
    layer_norm(nc, g, table)
    sum_edges(nc, g, table, D, count_degree=True)
    with ExitStack() as stack:
        sb = lambda n, s: stack.enter_context(nc.sbuf_tensor(g.tag + n, s, F32))
        w_self, w_neigh, b_self, inv = sb("w_self", [P, 2, D]), sb("w_neigh", [P, 2, D]), sb("b_self", [1, D]), sb("inv_deg", [P, NT])
        load_weights(nc, g, "l0g", [(w_self[:, :, :], rows_in(a.l0g_w_self_t)), (w_neigh[:, :, :], rows_in(a.l0g_w_neigh_t)),
                                 (b_self[:, :], a.l0g_b_self)])
        with ExitStack() as s2:
            step = nc.alloc_semaphore(g.tag + "inv_step")
            block = s2.enter_context(nc.Block(g.tag + "inv_degree"))

            @block.vector
            def _(dve):
                nc.vector.tensor_scalar(inv[:, :], g.deg[:, :], 1.0, None, ALU.max).then_inc(step, 1)
                dve.wait_ge(step, 1)
                nc.vector.reciprocal(inv[:, :], inv[:, :]).then_inc(step, 1)
                dve.wait_ge(step, 2)

        project(nc, g, "l0g", [w_self, w_neigh], b_self[0:1, :], D,
                [("pool", lambda out, t: nc.gpsimd.tensor_copy(out, g.xn[:, ds(t, 1), :])),
                 ("dve", lambda out, t: nc.vector.tensor_scalar(out, g.acc[:, ds(t, 1), :], inv[:, ds(t, 1)], None, ALU.mult))],
                lambda dve, bank, t, s: nc.vector.tensor_tensor(g.x[:, ds(t, 1), :], g.x[:, ds(t, 1), :], bank, ALU.add))


def turn_nodes(nc, g, xnt):
    with ExitStack() as stack:
        sem = lambda n: nc.alloc_semaphore(g.tag + "turn_" + n)
        staged, turned, placed = sem("staged"), sem("turned"), sem("placed")
        rows = stack.enter_context(nc.sbuf_tensor(g.tag + "turn_rows", [P, 2, D], F32))
        block = stack.enter_context(nc.Block(g.tag + "turn_nodes"))

        @block.gpsimd
        def _(pool):
            with nc.gpsimd.Fori(0, NT // 2) as i:
                for s in range(2):
                    pool.wait_ge(turned, 2 * i + s + 1)
                    nc.gpsimd.tensor_copy(rows[:, s, :], g.xn[:, ds(2 * i + s, 1), :]).then_inc(staged, 1)

        @block.tensor
        def _(pe):
            pe.sem_inc(turned, 2)
            with nc.tensor.Fori(0, NT // 2) as i:
                for s in range(2):
                    pe.wait_ge(staged, 2 * i + s + 1)
                    pe.wait_ge(placed, 2 * i + s + 1)
                    nc.tensor.transpose(g.ps[s][:, 0:P], rows[:, s, 0:P], g.ident[:, :])
                    nc.tensor.transpose(g.ps[s][:, P:2 * P], rows[:, s, P:2 * P], g.ident[:, :]).then_inc(turned, 1)

        @block.scalar
        def _(act):
            act.sem_inc(placed, 2)
            with nc.scalar.Fori(0, NT // 2) as i:
                for s in range(2):
                    act.wait_ge(turned, 2 * i + s + 3)
                    nc.scalar.activation(xnt[:, :, ds((2 * i + s) * P, P)],
                                         g.ps[s][:, 0:2 * P].rearrange("p (c n) -> p c n", c=2), ACT.Copy).then_inc(placed, 1)


KEEP = max(1, int(0.5 * NODES)) - 1
H0 = 1024
NEG = -3.0e38


def router_scores(nc, g, wr, br, scores):
    with ExitStack() as stack:
        done, added = (nc.alloc_semaphore(g.tag + "router_" + n) for n in ("dot", "bias"))
        prod = stack.enter_context(nc.sbuf_tensor(g.tag + "router_prod", [P, 4, D], F32))
        block = stack.enter_context(nc.Block(g.tag + "router_scores"))

        @block.vector
        def _(dve):
            for t in range(NT):
                if t >= 4:
                    dve.wait_ge(done, t - 3)
                nc.vector.scalar_tensor_tensor(out=prod[:, t % 4, :], in0=g.xn[:, t, :], scalar=1.0, in1=wr[:, :],
                                               op0=ALU.mult, op1=ALU.mult, accum_out=scores[:, t:t + 1]).then_inc(done, 1)
            dve.wait_ge(done, NT)
            nc.vector.tensor_scalar(scores[:, :], scores[:, :], br[:, 0:1], None, ALU.add).then_inc(added, 1)
            dve.wait_ge(added, 1)


def scores_across(nc, g, scores, scratch, srow):
    with ExitStack() as stack:
        sem = lambda n: nc.alloc_semaphore(g.tag + "across_" + n)
        turned, copied, stored, loaded = sem("turned"), sem("copied"), sem("stored"), sem("loaded")
        rows = stack.enter_context(nc.sbuf_tensor(g.tag + "score_rows", [NT, P], F32))
        block = stack.enter_context(nc.Block(g.tag + "scores_across"))

        @block.tensor
        def _(pe):
            nc.tensor.transpose(g.ps[0][0:NT, 0:P], scores[:, 0:NT], g.ident[:, :]).then_inc(turned, 1)

        @block.vector
        def _(dve):
            dve.wait_ge(turned, 1)
            nc.vector.tensor_copy(rows[:, :], g.ps[0][0:NT, 0:P]).then_inc(copied, 1)

        @block.sync
        def _(sp):
            sp.wait_ge(copied, 1)
            sp.dma_start(scratch.rearrange("(t p) -> t p", p=P), rows[:, :]).then_inc(stored, 16)
            sp.wait_ge(stored, 16)
            sp.dma_start(srow[:, :], across(scratch)).then_inc(loaded, 16)
            sp.wait_ge(loaded, 16)


def layer0_ffn(nc, g, a, table):
    layer_norm(nc, g, None)
    scratch = nc.dram_tensor("score_scratch", (ROWS,), F32).ap()
    with ExitStack() as stack:
        sb = lambda n, s: stack.enter_context(nc.sbuf_tensor(g.tag + n, s, F32))
        wr, br = sb("wr_rows", [P, D]), sb("br", [P, 1])
        w1, b1, w2, b2 = sb("l0_w1", [P, 2, H0]), sb("l0_b1", [P, H0 // P]), sb("l0_w2", [P, H0 // P, D]), sb("l0_b2", [1, D])
        scores, gate, srow, xnt = sb("scores", [P, NT]), sb("gate", [P, NT]), sb("score_row", [P, ROWS]), sb("xnt", [P, 2, ROWS])
        load_weights(nc, g, "l0f", [(wr[:, :], across(a.l0f_wr)), (br[:, :], across(a.l0f_br)), (w1[:, :, :], rows_in(a.l0f_w1)),
                                 (b1[:, :], a.l0f_b1_cols), (w2[:, :, :], rows_in(a.l0f_w2)), (b2[:, :], a.l0f_b2)])
        router_scores(nc, g, wr, br, scores)
        scores_across(nc, g, scores, scratch, srow)
        turn_nodes(nc, g, xnt)
        G = 2 * P
        NF = H0 // P
        with ExitStack() as s2:
            sem = lambda n: nc.alloc_semaphore(g.tag + "mod_" + n)
            ranked, selected, hidden, active, summed, used, skip = (sem(n) for n in
                ("ranked", "selected", "hidden", "active", "summed", "used", "skip"))
            above, ahead, same = (s2.enter_context(nc.sbuf_tensor(g.tag + n, [P, NT], F32)) for n in ("above", "ahead", "same"))
            junk = s2.enter_context(nc.sbuf_tensor(g.tag + "rank_junk", [P, 3, ROWS], F32))
            before = s2.enter_context(nc.sbuf_tensor(g.tag + "before", [P, P], F32))
            ht = s2.enter_context(nc.sbuf_tensor(g.tag + "hidden_t", [P, NF, G], F32))
            block = s2.enter_context(nc.Block(g.tag + "mod_ffn"))

            @block.gpsimd
            def _(pool):
                nc.gpsimd.affine_select(out=before[:, :], in_=g.ones[:, :], compare_op=ALU.is_gt, fill=0.0, base=0,
                                        pattern=[[-1, P]], channel_multiplier=1).then_inc(skip, 1)
                with nc.gpsimd.Fori(0, NT) as t:
                    nc.gpsimd.tensor_tensor(g.x[:, ds(t, 1), :], g.x[:, ds(t, 1), :], g.xn[:, ds(t, 1), :], ALU.add).then_inc(skip, 1)

            @block.tensor
            def _(pe):
                pe.sem_inc(hidden, 4)
                with nc.tensor.Fori(0, ROWS // G) as i:
                    for f in range(NF):
                        pe.wait_ge(active, NF * i + f + 1)
                        for c in range(2):
                            last = nc.tensor.matmul(g.ps[f % 4][:, 0:G], w1[:, c, f * P:(f + 1) * P],
                                                    xnt[:, c, ds(i * G, G)], start=(c == 0), stop=(c == 1))
                        last.then_inc(hidden, 1)
                    for s in range(2):
                        pe.wait_ge(used, 2 * i + s + 1)
                        nc.tensor.matmul(g.ps[4 + s][:, 0:D], g.ones[0:1, :], b2[0:1, :], start=True, stop=False)
                        for f in range(NF):
                            if s == 0:
                                pe.wait_ge(active, NF * i + f + 5)
                            last = nc.tensor.matmul(g.ps[4 + s][:, 0:D], ht[:, f, s * P:(s + 1) * P], w2[:, f, :],
                                                    start=False, stop=(f == NF - 1))
                        last.then_inc(summed, 1)

            @block.scalar
            def _(act):
                act.sem_inc(active, 4)
                act.sem_inc(summed, 2)
                with nc.scalar.Fori(0, ROWS // G) as i:
                    for f in range(NF):
                        act.wait_ge(hidden, NF * i + f + 5)
                        if f == 0:
                            act.wait_ge(summed, 2 * i + 2)
                        nc.scalar.activation(ht[:, f, :], g.ps[f % 4][:, 0:G], ACT.Gelu_apprx_tanh,
                                             bias=b1[:, f:f + 1]).then_inc(active, 1)

            @block.vector
            def _(dve):
                dve.sem_inc(used, 2)
                dve.wait_ge(skip, 1)
                n = 0
                for t in range(FULL + 1):
                    for k, (lo, hi, op, to) in enumerate(((0, t * P, ALU.is_ge, ahead), (t * P, NODES, ALU.is_gt, above))):
                        if n >= 3:
                            dve.wait_ge(ranked, n - 2)
                        if hi > lo:
                            nc.vector.tensor_scalar(junk[:, k, lo:hi], srow[:, lo:hi], scores[:, t:t + 1], 0.0, op, ALU.add,
                                                    accum_out=to[:, t:t + 1]).then_inc(ranked, 1)
                        else:
                            nc.vector.memset(to[:, t:t + 1], 0.0).then_inc(ranked, 1)
                        n += 1
                    w = min(P, NODES - t * P)
                    if n >= 3:
                        dve.wait_ge(ranked, n - 2)
                    nc.vector.scalar_tensor_tensor(out=junk[:, 2, 0:w], in0=srow[:, t * P:t * P + w], scalar=scores[:, t:t + 1],
                                                   in1=before[:, 0:w], op0=ALU.is_equal, op1=ALU.mult,
                                                   accum_out=same[:, t:t + 1]).then_inc(ranked, 1)
                    n += 1
                for to in (above, ahead, same):
                    nc.vector.memset(to[:, FULL + 1:NT], 0.0).then_inc(ranked, 1)
                    n += 1
                dve.wait_ge(ranked, n)
                nc.vector.tensor_tensor(above[:, :], above[:, :], ahead[:, :], ALU.add).then_inc(selected, 1)
                dve.wait_ge(selected, 1)
                nc.vector.tensor_tensor(above[:, :], above[:, :], same[:, :], ALU.add).then_inc(selected, 1)
                dve.wait_ge(selected, 2)
                nc.vector.scalar_tensor_tensor(out=gate[:, :], in0=above[:, :], scalar=float(KEEP), in1=scores[:, :],
                                               op0=ALU.is_lt, op1=ALU.mult).then_inc(selected, 1)
                dve.wait_ge(selected, 3)
                dve.wait_ge(skip, NT + 1)
                with nc.vector.Fori(0, ROWS // G) as i:
                    for s in range(2):
                        t = 2 * i + s
                        dve.wait_ge(summed, t + 3)
                        nc.vector.scalar_tensor_tensor(out=g.x[:, ds(t, 1), :], in0=g.ps[4 + s][:, 0:D], scalar=gate[:, ds(t, 1)],
                                                       in1=g.x[:, ds(t, 1), :], op0=ALU.mult, op1=ALU.add).then_inc(used, 1)


HEADS, HD = 8, 32
SLOPE = 0.2
CH = 16
CT = ET // CH
CE = CT * P
AW = HEADS + D + HEADS


def layer1_gnn(nc, g, a, table):
    layer_norm(nc, g, None)
    htable = nc.dram_tensor("gat_rows", (ROWS, HEADS + D), F32).ap()
    with ExitStack() as stack:
        sb = lambda n, s, d=F32: stack.enter_context(nc.sbuf_tensor(g.tag + n, s, d))
        alpha = sb("alpha", [P, ET, HEADS])
        den = sb("denominator", [P, NT, HEADS])
        gat_features(nc, g, a, stack_outer=stack, htable=htable, alpha=alpha)
        edge_softmax(nc, g, a, alpha)
        weighted_sum(nc, g, htable, alpha, den)
        with ExitStack() as s2:
            bias = s2.enter_context(nc.sbuf_tensor(g.tag + "bias", [P, D], F32))
            load_weights(nc, g, "gat_bias", [(bias[:, :], across(a.l1g_bias))])
            step = nc.alloc_semaphore(g.tag + "out_step")
            block = s2.enter_context(nc.Block(g.tag + "gat_out"))
            heads = lambda v: v.rearrange("p t (h d) -> p (t h) d", d=HD)

            @block.vector
            def _(dve):
                nc.vector.tensor_scalar(den[:, :, :], den[:, :, :], 1e-10, None, ALU.max).then_inc(step, 1)
                dve.wait_ge(step, 1)
                nc.vector.reciprocal(den[:, :, :], den[:, :, :]).then_inc(step, 1)
                dve.wait_ge(step, 2)
                nc.vector.tensor_tensor(heads(g.acc[:, :, :]), heads(g.acc[:, :, :]),
                                        den[:, :, :].rearrange("p t h -> p (t h)").unsqueeze(2).to_broadcast([P, NT * HEADS, HD]),
                                        ALU.mult).then_inc(step, 1)
                dve.wait_ge(step, 3)
                nc.vector.tensor_tensor(g.x[:, :, :], g.x[:, :, :], g.acc[:, :, :], ALU.add).then_inc(step, 1)
                dve.wait_ge(step, 4)
                nc.vector.tensor_tensor(g.x[:, :, :], g.x[:, :, :], bias[:, :].unsqueeze(1).to_broadcast([P, NT, D]),
                                        ALU.add).then_inc(step, 1)
                dve.wait_ge(step, 5)


def gat_features(nc, g, a, stack_outer, htable, alpha):
    with ExitStack() as stack:
        sb = lambda n, s, d=F32: stack.enter_context(nc.sbuf_tensor(g.tag + n, s, d))
        wt, w, acol, blockd = sb("w_t", [P, 2, AW]), sb("w", [P, 2, D]), sb("a_cols", [P, 4]), sb("a_blocks", [P, 2, 2 * HEADS])
        hs = sb("h_nodes", [P, NT, AW])
        edge_w = sb("edge_w", [4, D])
        load_weights(nc, g, "gat", [(wt[:, :, HEADS:HEADS + D], rows_in(a.l1g_w_t)), (w[:, :, :], rows_in(a.l1g_w)),
                                    (acol[:, 0:2], a.l1g_a_src_cols), (acol[:, 2:4], a.l1g_a_dst_cols),
                                    (edge_w[0:3, :], a.l1g_edge_w_t), (edge_w[3:4, :], a.l1g_edge_b)])
        with ExitStack() as s2:
            sem = lambda n: nc.alloc_semaphore(g.tag + n)
            spread, masked, folded, placed = sem("a_spread"), sem("a_masked"), sem("a_folded"), sem("a_placed")
            block = s2.enter_context(nc.Block(g.tag + "fold_scores"))

            @block.vector
            def _(dve):
                for c in range(2):
                    for k in range(2):
                        nc.vector.tensor_scalar(blockd[:, c, k * HEADS:(k + 1) * HEADS], g.ones[:, 0:HEADS],
                                                acol[:, 2 * k + c:2 * k + c + 1], None, ALU.mult).then_inc(spread, 1)
                dve.wait_ge(folded, 1)
                for c in range(2):
                    nc.vector.tensor_copy(wt[:, c, 0:HEADS], g.ps[c][:, 0:HEADS]).then_inc(placed, 1)
                    nc.vector.tensor_copy(wt[:, c, HEADS + D:AW], g.ps[c][:, HEADS:2 * HEADS]).then_inc(placed, 1)
                dve.wait_ge(placed, 4)

            @block.gpsimd
            def _(pool):
                pool.wait_ge(spread, 4)
                for c in range(2):
                    v = blockd[:, c, :].rearrange("p (k h) -> p k h", k=2)
                    nc.gpsimd.affine_select(out=v, in_=v, compare_op=ALU.is_ge, fill=0.0, base=c * P,
                                            pattern=[[0, 2], [-HD, HEADS]], channel_multiplier=1).then_inc(masked, 1)
                pool.wait_ge(masked, 2)
                for c in range(2):
                    v = blockd[:, c, :].rearrange("p (k h) -> p k h", k=2)
                    nc.gpsimd.affine_select(out=v, in_=v, compare_op=ALU.is_ge, fill=0.0, base=HD - 1 - c * P,
                                            pattern=[[0, 2], [HD, HEADS]], channel_multiplier=-1).then_inc(masked, 1)

            @block.tensor
            def _(pe):
                pe.wait_ge(masked, 4)
                for m in range(2):
                    for c in range(2):
                        last = nc.tensor.matmul(g.ps[m][:, 0:2 * HEADS], w[:, c, m * P:(m + 1) * P], blockd[:, c, :],
                                                start=(c == 0), stop=(c == 1))
                last.then_inc(folded, 1)

        project(nc, g, "gat_h", [wt], None, AW,
                [("pool", lambda out, t: nc.gpsimd.tensor_copy(out, g.xn[:, ds(t, 1), :]))],
                lambda dve, bank, t, s: nc.vector.tensor_copy(hs[:, ds(t, 1), :], bank))
        with ExitStack() as s2:
            stored = nc.alloc_semaphore(g.tag + "h_stored")
            block = s2.enter_context(nc.Block(g.tag + "store_h"))

            @block.sync
            def _(sp):
                sp.dma_start(htable.rearrange("(t p) d -> p t d", p=P), hs[:, :, 0:HEADS + D]).then_inc(stored, 16)
                sp.wait_ge(stored, 16)

        U = 8
        with ExitStack() as s2:
            sem = lambda n: nc.alloc_semaphore(g.tag + "s_" + n)
            gathered = [sem(f"gathered{u}") for u in range(U)]
            attrs = [sem(f"attrs{h}") for h in range(2)]
            copied, claimed, hot, turned, hot_t, looked, encoded, relued, based, mixed, reduced = (sem(n) for n in (
                "idx_copied", "claimed", "hot", "turned", "hot_t", "looked_up", "encoded", "relued", "based", "mixed", "reduced"))
            sb2 = lambda n, s, d=F32: s2.enter_context(nc.sbuf_tensor(g.tag + n, s, d))
            idx, rows = sb2("s_idx", [P, 2, U // 2], I32), sb2("s_rows", [P, U, HEADS + D])
            onehot, onehot_t = sb2("s_onehot", [P, 2, 2 * P]), sb2("s_onehot_t", [P, 2, 2 * P])
            enc, mix, edge_attr = sb2("s_enc", [P, 2, D]), sb2("s_mix", [P, 2, D]), sb2("edge_attr", [4, 2, U // 2 * P])
            base_score = sb2("base_score", [P, ET, HEADS])
            block = s2.enter_context(nc.Block(g.tag + "edge_scores"))
            hflat = hs[:, :, :].rearrange("p t d -> p (t d)")

            @block.gpsimd
            def _(pool):
                with nc.gpsimd.Fori(0, ET // U) as i:
                    for h in range(2):
                        pool.wait_ge(based, U * i + (h + 1) * U // 2)
                        nc.gpsimd.tensor_copy(idx[:, h, :], g.srcc[:, ds(U * i + h * U // 2, U // 2)]).then_inc(copied, 1)
                        pool.wait_ge(copied, 2 * i + h + 1)
                        for u in range(h * U // 2, (h + 1) * U // 2):
                            pool.wait_ge(based, U * i + u + 1)
                            pool.sem_inc(claimed, 1)
                            nc.gpsimd.indirect_dma_start(
                                rows[:, u, :], None, htable,
                                bass.IndirectOffsetOnAxis(ap=idx[:, h, u % 4:u % 4 + 1].bitcast(U32), axis=0)).then_inc(gathered[u], 16)

            @block.sync
            def _(sp):
                with nc.sync.Fori(0, ET // U) as i:
                    for h in range(2):
                        sp.wait_ge(encoded, U * i + (h + 1) * U // 2)
                        sp.dma_start(edge_attr[:, h, :], a.edge_attr_t[:, ds((2 * i + h) * (U // 2 * P), U // 2 * P)]).then_inc(attrs[h], 16)

            @block.tensor
            def _(pe):
                window = [nc.tensor.alloc_register(g.tag + f"pe_window{u}") for u in range(U)]
                pe.sem_inc(turned, 2)
                pe.sem_inc(looked, 2)
                pe.sem_inc(encoded, U)
                with nc.tensor.Fori(0, ET // U) as i:
                    nc.tensor.reg_load(window, g.window[0:1, ds(U * i, U)])
                    for v in range(0, U, 2):
                        if v % 4 == 0:
                            pe.wait_ge(attrs[v // 4], 16 * (i + 1))
                        for u in (v, v + 1):
                            n = U * i + u
                            pe.wait_ge(hot, n + 1)
                            pe.wait_ge(hot_t, n + 1)
                            nc.tensor.transpose(g.ps[u % 2][:, 0:P], onehot[:, u % 2, 0:P], g.ident[:, :])
                            nc.tensor.transpose(g.ps[u % 2][:, P:2 * P], onehot[:, u % 2, P:2 * P], g.ident[:, :]).then_inc(turned, 1)
                            pe.wait_ge(relued, n + 1)
                            nc.tensor.matmul(g.ps[2 + u % 2][:, 0:D], edge_attr[:, u // 4, u % 4 * P:(u % 4 + 1) * P], edge_w[:, :],
                                             start=True, stop=True).then_inc(encoded, 1)
                        for u in (v, v + 1):
                            n = U * i + u
                            w = nc.tensor.snap(window[u], min_val=0, max_val=NT - 2)
                            pe.wait_ge(hot_t, n + 3)
                            pe.wait_ge(based, n + U - 1)
                            for k in range(2):
                                last = nc.tensor.matmul(g.ps[4 + u % 2][:, 0:D + HEADS], onehot_t[:, u % 2, k * P:(k + 1) * P],
                                                        hflat[:, ds(w * AW + (k * AW + HEADS), D + HEADS)],
                                                        start=(k == 0), stop=(k == 1))
                            last.then_inc(looked, 1)

            @block.scalar
            def _(act):
                act.sem_inc(hot_t, 2)
                act.sem_inc(relued, 2)
                with nc.scalar.Fori(0, ET // U) as i:
                    for u in range(U):
                        n = U * i + u
                        act.wait_ge(turned, n + 3)
                        act.wait_ge(looked, n + 1)
                        nc.scalar.activation(onehot_t[:, u % 2, :], g.ps[u % 2][:, 0:2 * P], ACT.Copy).then_inc(hot_t, 1)
                        act.wait_ge(encoded, n + U + 1)
                        act.wait_ge(mixed, n + 1)
                        nc.scalar.activation(enc[:, u % 2, :], g.ps[2 + u % 2][:, 0:D], ACT.Relu).then_inc(relued, 1)

            @block.vector
            def _(dve):
                dve.sem_inc(based, U)
                dve.sem_inc(mixed, 2)
                dve.sem_inc(reduced, 2)

                def build(n, slot):
                    nc.vector.tensor_scalar(onehot[:, slot, :], g.iota[:, :], g.local[:, ds(n, 1)], None, ALU.is_equal).then_inc(hot, 1)
                build(0, 0)
                build(1, 1)
                with nc.vector.Fori(0, ET // U) as i:
                    for u in range(U):
                        n = U * i + u
                        dve.wait_ge(turned, n + 3)
                        build(n + 2, u % 2)
                        dve.wait_ge(looked, n + 3)
                        dve.wait_ge(relued, n + 3)
                        dve.wait_ge(reduced, n + 1)
                        nc.vector.tensor_tensor(mix[:, u % 2, :], g.ps[4 + u % 2][:, 0:D], enc[:, u % 2, :], ALU.mult).then_inc(mixed, 1)
                        dve.wait_ge(gathered[u], 16 * (i + 1))
                        nc.vector.tensor_tensor(base_score[:, ds(n, 1), :], g.ps[4 + u % 2][:, D:D + HEADS].unsqueeze(1),
                                                rows[:, u, 0:HEADS].unsqueeze(1), ALU.add).then_inc(based, 1)
                        dve.wait_ge(mixed, n + 3)
                        nc.vector.tensor_reduce(alpha[:, ds(n, 1), :], mix[:, u % 2, :].rearrange("p (o h d) -> p o h d", o=1, d=HD),
                                                AX.X, ALU.add).then_inc(reduced, 1)
                dve.wait_ge(reduced, ET + 2)
                dve.wait_ge(based, ET + U)
                nc.vector.tensor_tensor(alpha[:, :, :], alpha[:, :, :], base_score[:, :, :], ALU.add).then_inc(reduced, 1)
                dve.wait_ge(reduced, ET + 3)


def edge_softmax(nc, g, a, alpha):
    BIG = 1e30
    by_chunk = alpha[:, :, :].rearrange("p (c i) h -> p i c h", c=CH)
    by_chunk4 = alpha[:, :, :].rearrange("p (c i) h -> p c i h", c=CH)
    with ExitStack() as stack:
        sem = lambda n: nc.alloc_semaphore(g.tag + "m_" + n)
        sb = lambda n, s, d=F32: stack.enter_context(nc.sbuf_tensor(g.tag + n, s, d))
        dst_loaded, turned, placed, step, diff, ends, wide, cols, expd, back, home = (sem(n) for n in (
            "dst", "turned", "placed", "step", "diff", "ends", "wide", "cols", "exp", "back", "home"))
        ordered = sb("ordered", [P, CT, CH * HEADS])
        dst = sb("dst_chunks", [P, CE + 2], I32)
        score, fwd, bwd, fresh, fresh_b = sb("score_t", [P, CE]), sb("fwd", [P, CE]), sb("bwd", [P, CE]), sb("fresh", [P, CE]), sb("fresh_b", [P, CE])
        edge, row = sb("chunk_edge", [P, 4]), sb("chunk_edge_row", [1, 4 * P])
        dist, same, before = sb("dist", [P, P], I32), sb("same_head", [P, P], I32), sb("chunk_mask", [P, 2, P])
        cand, cand2, carry, same_f, dist_f = sb("cand", [P, 2, P]), sb("cand2", [P, 2, P]), sb("carry", [P, 2]), sb("same_f", [P, P]), sb("dist_f", [P, P])
        block = stack.enter_context(nc.Block(g.tag + "edge_softmax"))
        groups = [(q, min(4, CT - q)) for q in range(0, CT, 4)]

        @block.sync
        def _(sp):
            for c in range(CH):
                sp.dma_start(dst[c * HEADS:(c + 1) * HEADS, :],
                             a.dst_row[c * CE:c * CE + CE + 2].rearrange("(o n) -> o n", o=1).to_broadcast([HEADS, CE + 2])).then_inc(dst_loaded, 16)

        @block.gpsimd
        def _(pool):
            nc.gpsimd.iota(dist[:, :], [[-1, P]], base=0, channel_multiplier=1).then_inc(diff, 1)

        @block.tensor
        def _(pe):
            pe.wait_ge(ends, 1)
            for k, (q, m) in enumerate(groups):
                if k >= 4:
                    pe.wait_ge(placed, k - 3)
                for i in range(m):
                    last = nc.tensor.transpose(g.ps[k % 4][:, i * P:(i + 1) * P], ordered[:, q + i, :], g.ident[:, :])
                last.then_inc(turned, 1)
            pe.wait_ge(ends, 2)
            for r in range(4):
                last = nc.tensor.transpose(g.ps[4][0:1, r * P:(r + 1) * P], edge[:, r:r + 1], g.ident[:, :])
            last.then_inc(wide, 1)
            pe.wait_ge(ends, 3)
            nc.tensor.matmul(g.ps[5][:, :], g.ones[0:1, :], row[0:1, :], start=True, stop=True).then_inc(wide, 1)
            for k, (q, m) in enumerate(groups):
                pe.wait_ge(expd, k + 1)
                if k >= 4:
                    pe.wait_ge(home, k - 3)
                for i in range(m):
                    last = nc.tensor.transpose(g.ps[k % 4][:, i * P:(i + 1) * P], score[:, (q + i) * P:(q + i + 1) * P], g.ident[:, :])
                last.then_inc(back, 1)

        @block.scalar
        def _(act):
            for k, (q, m) in enumerate(groups):
                act.wait_ge(turned, k + 1)
                nc.scalar.activation(score[:, q * P:(q + m) * P], g.ps[k % 4][:, 0:m * P], ACT.Copy).then_inc(placed, 1)
            for k, (q, m) in enumerate(groups):
                if k == 0:
                    act.wait_ge(step, 18)
                nc.scalar.activation(score[:, q * P:(q + m) * P], score[:, q * P:(q + m) * P], ACT.Exp).then_inc(expd, 1)

        @block.vector
        def _(dve):
            count = [0]

            def done(ins):
                count[0] += 1
                ins.then_inc(step, 1)
                dve.wait_ge(step, count[0])

            prev, cur, nxt = dst[:, 0:CE], dst[:, 1:CE + 1], dst[:, 2:CE + 2]
            flat = fwd[:, :].rearrange("p (t h) -> p t h", h=HEADS)
            done(nc.vector.tensor_scalar(flat, alpha[:, :, :], SLOPE, None, ALU.mult))
            nc.vector.tensor_tensor(ordered[:, :, :].rearrange("p i (c h) -> p c i h", c=CH), by_chunk4,
                                    fwd[:, :].rearrange("p (c i h) -> p c i h", c=CH, h=HEADS), ALU.max).then_inc(ends, 1)
            dve.wait_ge(diff, 1)
            done(nc.vector.tensor_scalar(same[:, :], dist[:, :], 7, None, ALU.bitwise_and))
            done(nc.vector.tensor_scalar(same_f[:, :], same[:, :], 0.0, None, ALU.is_equal))
            done(nc.vector.tensor_copy(dist_f[:, :], dist[:, :]))
            done(nc.vector.scalar_tensor_tensor(out=before[:, 0, :], in0=dist_f[:, :], scalar=0.0, in1=same_f[:, :], op0=ALU.is_gt, op1=ALU.mult))
            done(nc.vector.scalar_tensor_tensor(out=before[:, 1, :], in0=dist_f[:, :], scalar=0.0, in1=same_f[:, :], op0=ALU.is_lt, op1=ALU.mult))
            dve.wait_ge(dst_loaded, 16 * CH)
            done(nc.vector.tensor_tensor(fresh[:, :], cur, prev, ALU.not_equal))
            done(nc.vector.tensor_scalar(fresh[:, :], fresh[:, :], -BIG, None, ALU.mult))
            done(nc.vector.tensor_tensor(fresh_b[:, :], cur, nxt, ALU.not_equal))
            done(nc.vector.tensor_scalar(fresh_b[:, :], fresh_b[:, :], -BIG, None, ALU.mult))
            dve.wait_ge(placed, len(groups))

            def runs(first, last):
                nc.vector.tensor_tensor_scan(fwd[:, :], fresh[:, :], score[:, :], first, ALU.add, ALU.max)
                done(nc.vector.tensor_tensor_scan(bwd[:, ::-1], fresh_b[:, ::-1], score[:, ::-1], last, ALU.add, ALU.max))
            runs(-BIG, -BIG)
            nc.vector.tensor_copy(edge[:, 0:1], fwd[:, CE - 1:CE])
            nc.vector.tensor_copy(edge[:, 1:2], bwd[:, 0:1])
            nc.vector.tensor_copy(edge[:, 2:3], cur[:, CE - 1:CE])
            nc.vector.tensor_copy(edge[:, 3:4], cur[:, 0:1]).then_inc(ends, 1)
            dve.wait_ge(wide, 1)
            nc.vector.tensor_copy(row[:, :], g.ps[4][0:1, :]).then_inc(ends, 1)
            dve.wait_ge(wide, 2)
            at = lambda r: g.ps[5][:, r * P:(r + 1) * P]
            nc.vector.scalar_tensor_tensor(out=cand[:, 0, :], in0=at(2), scalar=edge[:, 3:4], in1=before[:, 0, :], op0=ALU.is_equal, op1=ALU.mult)
            done(nc.vector.scalar_tensor_tensor(out=cand[:, 1, :], in0=at(3), scalar=edge[:, 2:3], in1=before[:, 1, :], op0=ALU.is_equal, op1=ALU.mult))
            done(nc.vector.tensor_tensor(cand2[:, :, :], cand[:, :, :], g.ps[5][:, 0:2 * P].rearrange("p (k n) -> p k n", k=2), ALU.mult))
            done(nc.vector.tensor_scalar(cand[:, :, :], cand[:, :, :], 1.0, BIG, ALU.subtract, ALU.mult))
            done(nc.vector.tensor_tensor(cand[:, :, :], cand[:, :, :], cand2[:, :, :], ALU.add))
            done(nc.vector.tensor_reduce(carry[:, :], cand[:, :, :], AX.X, ALU.max))
            nc.vector.tensor_tensor_scan(fwd[:, :], fresh[:, :], score[:, :], carry[:, 0:1], ALU.add, ALU.max)
            nc.vector.tensor_tensor_scan(bwd[:, ::-1], fresh_b[:, ::-1], score[:, ::-1], carry[:, 1:2], ALU.add, ALU.max).then_inc(step, 1)
            count[0] += 1
            dve.wait_ge(step, count[0])
            nc.vector.tensor_tensor(fwd[:, :], fwd[:, :], bwd[:, :], ALU.max).then_inc(diff, 1)
            dve.wait_ge(diff, 2)
            nc.vector.tensor_tensor(score[:, :], score[:, :], fwd[:, :], ALU.subtract).then_inc(step, 1)
            assert count[0] == 17
            for k, (q, m) in enumerate(groups):
                dve.wait_ge(back, k + 1)
                nc.vector.tensor_copy(by_chunk[:, q:q + m], g.ps[k % 4][:, 0:m * P].rearrange("p (i c h) -> p i c h", i=m, c=CH)).then_inc(home, 1)
            dve.wait_ge(home, len(groups))


def weighted_sum(nc, g, htable, weight, den):
    U = 8
    with ExitStack() as stack:
        sem = lambda n: nc.alloc_semaphore(g.tag + "w_" + n)
        gathered = [sem(f"gathered{u}") for u in range(U)]
        copied, claimed, hot, weighed, summed, added, cleared = (sem(n) for n in (
            "idx_copied", "claimed", "hot", "weighed", "summed", "added", "cleared"))
        sb = lambda n, s, d=F32: stack.enter_context(nc.sbuf_tensor(g.tag + "w_" + n, s, d))
        idx, rows = sb("idx", [P, 2, U // 2], I32), sb("rows", [P, U, HEADS + D])
        onehot, part = sb("onehot", [P, 4, 2 * P]), sb("part", [P, 4, D])
        block = stack.enter_context(nc.Block(g.tag + "weighted_sum"))
        acc = g.acc[:, :, :].rearrange("p t d -> p (t d)")
        denf = den[:, :, :].rearrange("p t h -> p (t h)")

        @block.gpsimd
        def _(pool):
            with nc.gpsimd.Fori(0, ET // U) as i:
                for h in range(2):
                    pool.wait_ge(weighed, U * i + (h + 1) * U // 2)
                    nc.gpsimd.tensor_copy(idx[:, h, :], g.srcc[:, ds(U * i + h * U // 2, U // 2)]).then_inc(copied, 1)
                    pool.wait_ge(copied, 2 * i + h + 1)
                    for u in range(h * U // 2, (h + 1) * U // 2):
                        pool.wait_ge(weighed, U * i + u + 1)
                        pool.sem_inc(claimed, 1)
                        nc.gpsimd.indirect_dma_start(
                            rows[:, u, :], None, htable,
                            bass.IndirectOffsetOnAxis(ap=idx[:, h, u % 4:u % 4 + 1].bitcast(U32), axis=0)).then_inc(gathered[u], 16)

        @block.tensor
        def _(pe):
            pe.sem_inc(summed, 4)
            with nc.tensor.Fori(0, ET // U) as i:
                for u in range(U):
                    n = U * i + u
                    pe.wait_ge(weighed, n + U + 1)
                    pe.wait_ge(added, n + 1)
                    for k in range(2):
                        hotk = onehot[:, u % 4, k * P:(k + 1) * P]
                        nc.tensor.matmul(g.ps[4 + u % 4][:, k * HEADS:(k + 1) * HEADS], hotk, weight[:, ds(n, 1), :], start=True, stop=True)
                        last = nc.tensor.matmul(g.ps[u % 4][:, k * D:(k + 1) * D], hotk, part[:, u % 4, :], start=True, stop=True)
                    last.then_inc(summed, 1)

        @block.vector
        def _(dve):
            base = [nc.vector.alloc_register(g.tag + f"window{u}") for u in range(U)]
            nc.vector.memset(g.acc[:, :, :], 0.0).then_inc(cleared, 1)
            nc.vector.memset(den[:, :, :], 0.0).then_inc(cleared, 1)
            dve.wait_ge(cleared, 2)

            def weigh(i, n, u):
                nc.vector.tensor_scalar(onehot[:, u % 4, :], g.iota[:, :], g.local[:, ds(n, 1)], None, ALU.is_equal)
                dve.wait_ge(gathered[u], 16 * (i + 1))
                nc.vector.tensor_tensor(part[:, u % 4, :].rearrange("p (h d) -> p h d", d=HD),
                                        rows[:, u, HEADS:].rearrange("p (h d) -> p h d", d=HD),
                                        weight[:, ds(n, 1), :].rearrange("p o h -> p (o h)").unsqueeze(2).to_broadcast([P, HEADS, HD]),
                                        ALU.mult).then_inc(weighed, 1)

            def collect(n, u, w):
                dve.wait_ge(summed, n + 5)
                dve.wait_ge(added, n + 4)
                nc.vector.tensor_tensor(denf[:, ds(w * HEADS, 2 * HEADS)], denf[:, ds(w * HEADS, 2 * HEADS)],
                                        g.ps[4 + u % 4][:, 0:2 * HEADS], ALU.add)
                nc.vector.tensor_tensor(acc[:, ds(w * D, 2 * D)], acc[:, ds(w * D, 2 * D)],
                                        g.ps[u % 4][:, 0:2 * D], ALU.add).then_inc(added, 1)
            dve.sem_inc(weighed, U)
            dve.sem_inc(added, 4)
            with nc.vector.Fori(0, ET // U) as i:
                nc.vector.reg_load(base, g.window[0:1, ds(U * i, U)])
                for u in range(U):
                    n = U * i + u
                    dve.wait_ge(summed, n + 1)
                    weigh(i, n, u)
                    if u >= 1:
                        collect(n - 1, u - 1, nc.vector.snap(base[u - 1], min_val=0, max_val=NT - 2))
                collect(U * i + U - 1, U - 1, nc.vector.snap(base[U - 1], min_val=0, max_val=NT - 2))


E = 8


class Route:
    pass


def route(nc, g, name, logits, picks, capacity, slots, r, clear):
    with ExitStack() as stack:
        sem = lambda n: nc.alloc_semaphore(g.tag + name + n)
        sb = lambda n, s, d=F32: stack.enter_context(nc.sbuf_tensor(g.tag + name + n, s, d))
        step, masks, counted, shifted, expd, zeroed, zero = (sem(n) for n in (
            "_step", "_masks", "_counted", "_shifted", "_exp", "_zeroed", "_zero"))
        wide = [P, NT, E]
        rev, valid, number, upto = sb("_rev", [P, E]), sb("_valid", [P, NT]), sb("_number", [P, NT]), sb("_upto", [P, P])
        best, first = [sb(f"_best{k}", [P, NT]) for k in range(2)], sb("_first", [P, NT])
        pick = [sb(f"_pick{k}", wide) for k in range(picks)]
        tmp, rest, every, cum, totals, incl = sb("_tmp", wide), sb("_rest", wide), sb("_every", wide), sb("_cum", wide), sb("_totals", wide), sb("_incl", wide)
        zeros, ni, nf, ends = sb("_zeros", [P, NT]), sb("_ni", [P, E], I32), sb("_nf", [P, E]), sb("_ends", [P, E])
        start, rowf, flag, place, tile_no, owner = sb("_start", [P, E]), sb("_rowf", [P, NT]), sb("_flag", [P, NT]), sb("_place", [P, NT]), sb("_tile_no", [1, 64]), sb("_owner", [1, 64])
        expt, z = sb("_expt", wide), sb("_z", [P, NT])
        block = stack.enter_context(nc.Block(g.tag + name))
        per_node = lambda v: v[:, :].unsqueeze(2).to_broadcast(wide)
        per_expert = lambda v: v[:, :].unsqueeze(1).to_broadcast(wide)

        @block.sync
        def _(sp):
            dram, zero_rows, n = clear
            sp.wait_ge(zero, 1)
            for k in range(n):
                sp.dma_start(dram[k], zero_rows).then_inc(zeroed, 16)
            sp.wait_ge(zeroed, 16 * n)

        @block.gpsimd
        def _(pool):
            nc.gpsimd.memset(clear[1], 0.0).then_inc(zero, 1)
            nc.gpsimd.iota(rev[:, :], [[-1, E]], base=E, channel_multiplier=0, allow_small_or_imprecise_dtypes=True).then_inc(masks, 1)
            nc.gpsimd.iota(number[:, :], [[P, NT]], base=0, channel_multiplier=1, allow_small_or_imprecise_dtypes=True).then_inc(masks, 1)
            nc.gpsimd.iota(tile_no[:, :], [[1, 64]], base=0, channel_multiplier=0, allow_small_or_imprecise_dtypes=True).then_inc(masks, 1)
            nc.gpsimd.affine_select(out=upto[:, :], in_=g.ones[:, :], compare_op=ALU.is_ge, fill=0.0, base=0,
                                    pattern=[[1, P]], channel_multiplier=-1).then_inc(masks, 1)
            nc.gpsimd.affine_select(out=valid[:, :], in_=g.ones[:, 0:NT], compare_op=ALU.is_ge, fill=0.0, base=NODES - 1,
                                    pattern=[[-P, NT]], channel_multiplier=-1).then_inc(masks, 1)

        @block.tensor
        def _(pe):
            pe.wait_ge(counted, 1)
            nc.tensor.matmul(g.ps[0][:, 0:NT * E], upto[:, :], every[:, :, :].rearrange("p t e -> p (t e)"), start=True, stop=True)
            nc.tensor.matmul(g.ps[1][:, 0:NT * E], g.ones[:, :], every[:, :, :].rearrange("p t e -> p (t e)"), start=True, stop=True).then_inc(counted, 1)

        @block.scalar
        def _(act):
            act.wait_ge(shifted, 1)
            if picks == 1:
                nc.scalar.activation(expt[:, :, :], tmp[:, :, :], ACT.Exp).then_inc(expd, 1)
            else:
                nc.scalar.activation(z[:, :], z[:, :], ACT.Exp).then_inc(expd, 1)

        @block.vector
        def _(dve):
            count = [0]

            def done(ins):
                count[0] += 1
                ins.then_inc(step, 1)
                dve.wait_ge(step, count[0])

            dve.wait_ge(masks, 5)
            done(nc.vector.memset(zeros[:, :], 0.0))
            left = logits
            for k in range(picks):
                done(nc.vector.tensor_reduce(best[k][:, :], left[:, :, :], AX.X, ALU.max))
                done(nc.vector.tensor_tensor(tmp[:, :, :], left[:, :, :], per_node(best[k]), ALU.is_equal))
                done(nc.vector.tensor_tensor(tmp[:, :, :], tmp[:, :, :], per_expert(rev), ALU.mult))
                done(nc.vector.tensor_reduce(first[:, :], tmp[:, :, :], AX.X, ALU.max))
                done(nc.vector.tensor_tensor(pick[k][:, :, :], per_expert(rev), per_node(first), ALU.is_equal))
                if k + 1 < picks:
                    done(nc.vector.scalar_tensor_tensor(out=rest[:, :, :], in0=pick[k][:, :, :], scalar=-1e30, in1=left[:, :, :],
                                                        op0=ALU.mult, op1=ALU.add))
                    left = rest
                done(nc.vector.tensor_tensor(pick[k][:, :, :], pick[k][:, :, :], per_node(valid), ALU.mult))
            if picks == 2:
                done(nc.vector.tensor_tensor(every[:, :, :], pick[0][:, :, :], pick[1][:, :, :], ALU.add))
                nc.vector.tensor_tensor(z[:, :], best[1][:, :], best[0][:, :], ALU.subtract).then_inc(shifted, 1)
            else:
                done(nc.vector.tensor_copy(every[:, :, :], pick[0][:, :, :]))
                nc.vector.tensor_tensor(tmp[:, :, :], logits[:, :, :], per_node(best[0]), ALU.subtract).then_inc(shifted, 1)
            dve.sem_inc(counted, 1)
            dve.wait_ge(expd, 1)
            if picks == 1:
                done(nc.vector.tensor_reduce(z[:, :], expt[:, :, :], AX.X, ALU.add))
                done(nc.vector.reciprocal(r.weight[:, 0, :], z[:, :]))
            else:
                done(nc.vector.tensor_scalar(flag[:, :], z[:, :], 1.0, None, ALU.add))
                done(nc.vector.reciprocal(r.weight[:, 0, :], flag[:, :]))
                done(nc.vector.tensor_tensor(r.weight[:, 1, :], r.weight[:, 0, :], z[:, :], ALU.mult))
            dve.wait_ge(counted, 2)
            done(nc.vector.tensor_copy(totals[:, :, :], g.ps[1][:, 0:NT * E].rearrange("p (t e) -> p t e", e=E)))
            for e in range(E):
                last = nc.vector.tensor_tensor_scan(incl[:, :, e], totals[:, :, e], zeros[:, :], 0.0, ALU.add, ALU.add)
            done(last)
            done(nc.vector.tensor_tensor(cum[:, :, :], incl[:, :, :], totals[:, :, :], ALU.subtract))
            done(nc.vector.tensor_tensor(cum[:, :, :], cum[:, :, :], g.ps[0][:, 0:NT * E].rearrange("p (t e) -> p t e", e=E), ALU.add))
            if capacity:
                done(nc.vector.tensor_scalar(start[:, :], rev[:, :], -float(slots), float(E * slots), ALU.mult, ALU.add))
            else:
                done(nc.vector.tensor_scalar(ni[:, :], incl[:, NT - 1, :], float(P - 1), None, ALU.add))
                done(nc.vector.tensor_scalar(ni[:, :], ni[:, :], 7, None, ALU.logical_shift_right))
                done(nc.vector.tensor_copy(nf[:, :], ni[:, :]))
                done(nc.vector.tensor_tensor_scan(ends[:, :], nf[:, :], zeros[:, 0:E], 0.0, ALU.add, ALU.add))
                done(nc.vector.tensor_tensor(start[:, :], ends[:, :], nf[:, :], ALU.subtract))
                done(nc.vector.tensor_scalar(start[:, :], start[:, :], float(P), None, ALU.mult))
                done(nc.vector.memset(owner[:, :], 0.0))
                for e in range(E - 1):
                    done(nc.vector.scalar_tensor_tensor(out=owner[:, :], in0=tile_no[:, :], scalar=ends[0:1, e:e + 1], in1=owner[:, :],
                                                        op0=ALU.is_ge, op1=ALU.add))
                done(nc.vector.tensor_copy(r.expert[:, :], owner[:, 0:r.expert.shape[1]]))
            for k in range(picks):
                done(nc.vector.tensor_tensor(tmp[:, :, :], pick[k][:, :, :], cum[:, :, :], ALU.mult))
                done(nc.vector.tensor_reduce(rowf[:, :], tmp[:, :, :], AX.X, ALU.add))
                done(nc.vector.tensor_tensor(tmp[:, :, :], pick[k][:, :, :], per_expert(start), ALU.mult))
                done(nc.vector.tensor_reduce(place[:, :], tmp[:, :, :], AX.X, ALU.add))
                if capacity:
                    done(nc.vector.tensor_scalar(flag[:, :], rowf[:, :], float(capacity), None, ALU.is_le))
                    done(nc.vector.tensor_tensor(r.weight[:, k, :], r.weight[:, k, :], flag[:, :], ALU.mult))
                    done(nc.vector.tensor_tensor(flag[:, :], flag[:, :], valid[:, :], ALU.mult))
                else:
                    done(nc.vector.tensor_copy(flag[:, :], valid[:, :]))
                done(nc.vector.tensor_scalar(z[:, :], rowf[:, :], float(capacity or ROWS * 2), -1.0, ALU.min, ALU.add))
                done(nc.vector.tensor_tensor(z[:, :], z[:, :], place[:, :], ALU.add))
                done(nc.vector.tensor_scalar(r.read[:, k, :], z[:, :], 0.0, None, ALU.max))
                done(nc.vector.tensor_scalar(rowf[:, :], rowf[:, :], -1.0, None, ALU.add))
                done(nc.vector.tensor_tensor(rowf[:, :], rowf[:, :], place[:, :], ALU.add))
                done(nc.vector.tensor_tensor(rowf[:, :], rowf[:, :], flag[:, :], ALU.mult))
                done(nc.vector.tensor_scalar(flag[:, :], flag[:, :], -1.0, 1.0, ALU.mult, ALU.add))
                done(nc.vector.tensor_scalar(place[:, :], number[:, :], float(r.spare + k * ROWS), None, ALU.add))
                done(nc.vector.tensor_tensor(place[:, :], place[:, :], flag[:, :], ALU.mult))
                done(nc.vector.tensor_tensor(r.write[:, k, :], rowf[:, :], place[:, :], ALU.add))


def new_route(nc, g, stack, name, picks, rows):
    r = Route()
    sb = lambda n, s, d=F32: stack.enter_context(nc.sbuf_tensor(g.tag + name + n, s, d))
    r.weight, r.read, r.write = sb("_weight", [P, picks, NT]), sb("_read", [P, picks, NT], I32), sb("_write", [P, picks, NT], I32)
    r.expert, r.spare, r.rows = sb("_expert", [1, rows // P], I32), rows, rows
    r.sorted = nc.dram_tensor(g.tag + name + "_sorted", (rows + picks * ROWS, D), F32).ap()
    r.result = nc.dram_tensor(g.tag + name + "_result", (rows, D), F32).ap()
    return r


def clear_rows(r, zeros):
    n = zeros.shape[1] // D
    v = r.sorted[0:r.rows, :].rearrange("(k p j) d -> k p (j d)", p=P, j=n)
    return v, zeros, r.rows // (P * n)


def send_rows(nc, g, name, r, picks, src):
    with ExitStack() as stack:
        sent = nc.alloc_semaphore(g.tag + name + "_sent")
        block = stack.enter_context(nc.Block(g.tag + name + "_send"))

        @block.gpsimd
        def _(pool):
            for k in range(picks):
                for t in range(NT):
                    nc.gpsimd.indirect_dma_start(
                        r.sorted, bass.IndirectOffsetOnAxis(ap=r.write[:, k, t:t + 1].bitcast(U32), axis=0),
                        src[:, t, :], None).then_inc(sent, 16)
            pool.wait_ge(sent, 16 * NT * picks)


def collect_rows(nc, g, name, r, picks, out):
    S = 8
    with ExitStack() as stack:
        sem = lambda n: nc.alloc_semaphore(g.tag + name + n)
        back = [sem(f"_back{s}") for s in range(S)]
        used = sem("_used")
        rows = stack.enter_context(nc.sbuf_tensor(g.tag + name + "_back_rows", [P, S, D], F32))
        block = stack.enter_context(nc.Block(g.tag + name + "_collect"))
        order = [(t, k) for t in range(NT) for k in range(picks)]

        @block.gpsimd
        def _(pool):
            for n, (t, k) in enumerate(order):
                if n >= S:
                    pool.wait_ge(used, n - S + 1)
                nc.gpsimd.indirect_dma_start(
                    rows[:, n % S, :], None, r.result,
                    bass.IndirectOffsetOnAxis(ap=r.read[:, k, t:t + 1].bitcast(U32), axis=0)).then_inc(back[n % S], 16)

        @block.vector
        def _(dve):
            for n, (t, k) in enumerate(order):
                dve.wait_ge(back[n % S], 16 * (n // S + 1))
                if k:
                    dve.wait_ge(used, n)
                if out is None:
                    nc.vector.tensor_scalar(g.acc[:, t, :], rows[:, n % S, :], r.weight[:, k, t:t + 1], None, ALU.mult).then_inc(used, 1)
                else:
                    nc.vector.scalar_tensor_tensor(out=out[:, t, :], in0=rows[:, n % S, :], scalar=r.weight[:, k, t:t + 1],
                                                   in1=out[:, t, :], op0=ALU.mult, op1=ALU.add).then_inc(used, 1)
            dve.wait_ge(used, len(order))


def gate_logits(nc, g, name, src, wg, bg, logits):
    project(nc, g, name, [wg], bg, E,
            [("pool", lambda out, t: nc.gpsimd.tensor_copy(out, src[:, ds(t, 1), :]))],
            lambda dve, bank, t, s: nc.vector.tensor_copy(logits[:, ds(t, 1), :], bank))


CAP, SLOTS, H1 = -(-5 * NODES // (4 * E)), 512, 1024


def layer1_ffn(nc, g, a, table):
    layer_norm(nc, g, None)
    with ExitStack() as stack:
        sb = lambda n, s, d=F32: stack.enter_context(nc.sbuf_tensor(g.tag + n, s, d))
        wg, bg, logits = sb("gate_w", [P, 2, E]), sb("gate_b", [1, E]), sb("logits", [P, NT, E])
        r = new_route(nc, g, stack, "sw", 1, E * SLOTS)
        load_weights(nc, g, "sw", [(wg[:, :, :], rows_in(a.l1f_gate_w)), (bg[:, :], a.l1f_gate_b)])
        gate_logits(nc, g, "sw_gate", g.xn, wg, bg[0:1, :], logits)
        with ExitStack() as s2:
            zeros = s2.enter_context(nc.sbuf_tensor(g.tag + "zero_rows", [P, 8 * D], F32))
            route(nc, g, "sw_route", logits, 1, CAP, SLOTS, r, clear_rows(r, zeros[:, :]))
        send_rows(nc, g, "sw", r, 1, g.xn)
        NF, NR = H1 // P, SLOTS // P
        with ExitStack() as s2:
            sem = lambda n: nc.alloc_semaphore(g.tag + "e_" + n)
            sb2 = lambda n, s: s2.enter_context(nc.sbuf_tensor(g.tag + "e_" + n, s, F32))
            loaded = [sem(f"loaded{s}") for s in range(2)]
            stored = [sem(f"stored{s}") for s in range(2)]
            turned, xt_ready, hidden, active, product, copied, freed = (
                sem(n) for n in ("turned", "xt_ready", "hidden", "active", "product", "copied", "freed"))
            w1, w2, b1, b2 = sb2("w1", [P, 2, 2, H1]), sb2("w2", [P, 2, NF, D]), sb2("b1", [P, 2, NF]), sb2("b2", [1, 2, D])
            rows, xt, ht, y = sb2("rows", [P, 2, NR, D]), sb2("xt", [P, 2, SLOTS]), sb2("ht", [P, NF, SLOTS]), sb2("y", [P, 2, NR, D])
            block = s2.enter_context(nc.Block(g.tag + "experts"))

            @block.sync
            def _(sp):
                with nc.sync.Fori(0, E // 2) as i:
                    for s in range(2):
                        e = 2 * i + s
                        sp.wait_ge(product, NR * e + NR)
                        for dst, src in ((rows[:, s, :, :], r.sorted[ds(e * SLOTS, SLOTS), :].rearrange("(r p) d -> p r d", p=P)),
                                         (w1[:, s, :, :], a.l1f_w1[ds(e, 1), :, :].rearrange("e (c p) h -> p (e c) h", p=P)),
                                         (b1[:, s, :], a.l1f_b1_cols[:, ds(e * NF, NF)]),
                                         (w2[:, s, :, :], a.l1f_w2[ds(e, 1), :, :].rearrange("e (c p) h -> p (e c) h", p=P)),
                                         (b2[:, s, :], a.l1f_b2[ds(e, 1), :])):
                            sp.dma_start(dst, src).then_inc(loaded[s], 16)

            @block.tensor
            def _(pe):
                pe.sem_inc(product, 2 * NR)
                pe.sem_inc(hidden, 4)
                with nc.tensor.Fori(0, E // 2) as i:
                    for s in range(2):
                        e = 2 * i + s
                        pe.wait_ge(loaded[s], 80 * (i + 1))
                        for c in range(2):
                            pe.wait_ge(xt_ready, 2 * e + c + 1)
                            for n in range(NR):
                                last = nc.tensor.transpose(g.ps[c][:, n * P:(n + 1) * P], rows[:, s, n, c * P:(c + 1) * P], g.ident[:, :])
                            last.then_inc(turned, 1)
                        pe.wait_ge(xt_ready, 2 * e + 4)
                        for f in range(NF):
                            pe.wait_ge(active, NF * e + f + 1)
                            for c in range(2):
                                last = nc.tensor.matmul(g.ps[2 + f % 4][:, :], w1[:, s, c, f * P:(f + 1) * P], xt[:, c, :],
                                                        start=(c == 0), stop=(c == 1))
                            last.then_inc(hidden, 1)
                        for n in range(NR):
                            pe.wait_ge(copied, NR * e + n + 1)
                            nc.tensor.matmul(g.ps[6 + n % 2][:, 0:D], g.ones[0:1, :], b2[0:1, s, :], start=True, stop=False)
                            for f in range(NF):
                                if n == 0:
                                    pe.wait_ge(active, NF * e + f + 5)
                                last = nc.tensor.matmul(g.ps[6 + n % 2][:, 0:D], ht[:, f, n * P:(n + 1) * P], w2[:, s, f, :],
                                                        start=False, stop=(f == NF - 1))
                            last.then_inc(product, 1)

            @block.scalar
            def _(act):
                act.sem_inc(xt_ready, 2)
                act.sem_inc(active, 4)
                with nc.scalar.Fori(0, E // 2) as i:
                    for s in range(2):
                        e = 2 * i + s
                        act.wait_ge(hidden, NF * e + 4)
                        for c in range(2):
                            act.wait_ge(turned, 2 * e + c + 1)
                            nc.scalar.activation(xt[:, c, :], g.ps[c][:, :], ACT.Copy).then_inc(xt_ready, 1)
                        act.wait_ge(product, NR * (e + 2))
                        for f in range(NF):
                            act.wait_ge(hidden, NF * e + f + 5)
                            nc.scalar.activation(ht[:, f, :], g.ps[2 + f % 4][:, :], ACT.Relu, bias=b1[:, s, f:f + 1]).then_inc(active, 1)

            @block.vector
            def _(dve):
                dve.sem_inc(copied, 2)
                dve.sem_inc(freed, 2)
                with nc.vector.Fori(0, E // 2) as i:
                    for s in range(2):
                        dve.wait_ge(freed, 2 * i + s + 1)
                        for n in range(NR):
                            dve.wait_ge(product, NR * (2 * i + s) + n + 2 * NR + 1)
                            nc.vector.tensor_copy(y[:, s, n, :], g.ps[6 + n % 2][:, 0:D]).then_inc(copied, 1)

            @block.gpsimd
            def _(pool):
                with nc.gpsimd.Fori(0, E // 2) as i:
                    for s in range(2):
                        e = 2 * i + s
                        pool.wait_ge(copied, NR * (e + 1) + 2)
                        pool.dma_start(r.result[ds(e * SLOTS, SLOTS), :].rearrange("(r p) d -> p r d", p=P), y[:, s, :, :]).then_inc(stored[s], 16)
                        pool.wait_ge(stored[s], 16 * (i + 1))
                        pool.sem_inc(freed, 1)

        collect_rows(nc, g, "sw", r, 1, None)
        with ExitStack() as s2:
            step = nc.alloc_semaphore(g.tag + "guard_step")
            mask = s2.enter_context(nc.sbuf_tensor(g.tag + "mask", [P, NT * D], mybir.dt.uint8))
            caps = s2.enter_context(nc.sbuf_tensor(g.tag + "caps", [P, 3], F32))
            block = s2.enter_context(nc.Block(g.tag + "guard"))
            y = g.acc[:, :, :].rearrange("p t d -> p (t d)")

            @block.vector
            def _(dve):
                count = [0]

                def done(ins):
                    count[0] += 1
                    ins.then_inc(step, 1)
                    dve.wait_ge(step, count[0])
                BIGGEST = 3.4028234663852886e38
                for k, v in enumerate((1e4, -1e4, 0.0)):
                    done(nc.vector.memset(caps[:, k:k + 1], v))
                for k, (op, v) in enumerate(((ALU.is_gt, BIGGEST), (ALU.is_lt, -BIGGEST))):
                    done(nc.vector.tensor_scalar(mask[:, :], y, v, None, op))
                    done(nc.vector.copy_predicated(y, mask[:, :], caps[:, k:k + 1].to_broadcast([P, NT * D])))
                done(nc.vector.tensor_tensor(mask[:, :], y, y, ALU.not_equal))
                done(nc.vector.copy_predicated(y, mask[:, :], caps[:, 2:3].to_broadcast([P, NT * D])))
                done(nc.vector.tensor_tensor(g.x[:, :, :], g.x[:, :, :], g.acc[:, :, :], ALU.add))


H2 = 512
T2 = (2 * NODES + E * (P - 1)) // P
T2 += T2 % 2


def norm_again(nc, g, gamma, beta, out):
    with ExitStack() as stack:
        sem = lambda n: nc.alloc_semaphore(g.tag + "again_" + n)
        stat, aggr, root, inv, normed, scaled = (sem(n) for n in ("stat", "aggr", "root", "inv", "normed", "scaled"))
        block = stack.enter_context(nc.Block(g.tag + "norm_again"))

        @block.vector
        def _(dve):
            with nc.vector.Fori(0, NT) as t:
                nc.vector.bn_stats(g.stats[:, ds(t, 1), :], g.xn[:, ds(t, 1), :]).then_inc(stat, 1)
            dve.wait_ge(stat, NT)
            for t in range(NT):
                nc.vector.bn_aggr(g.mv[:, t, :], g.stats[:, t, :]).then_inc(aggr, 1)
            dve.wait_ge(root, 1)
            nc.vector.reciprocal(g.rstd[:, :], g.rstd[:, :]).then_inc(inv, 1)
            dve.wait_ge(inv, 1)
            with nc.vector.Fori(0, NT) as t:
                nc.vector.tensor_scalar(out[:, ds(t, 1), :], g.xn[:, ds(t, 1), :], g.mv[:, ds(t, 1), 0],
                                        g.rstd[:, ds(t, 1)], ALU.subtract, ALU.mult).then_inc(normed, 1)
            dve.wait_ge(normed, NT)
            wide = [P, NT, D]
            nc.vector.tensor_tensor(out[:, :, :], out[:, :, :], gamma[:, :].unsqueeze(1).to_broadcast(wide), ALU.mult).then_inc(scaled, 1)
            dve.wait_ge(scaled, 1)
            nc.vector.tensor_tensor(out[:, :, :], out[:, :, :], beta[:, :].unsqueeze(1).to_broadcast(wide), ALU.add).then_inc(scaled, 1)
            dve.wait_ge(scaled, 2)

        @block.scalar
        def _(act):
            act.wait_ge(aggr, NT)
            nc.scalar.activation(g.rstd[:, :], g.mv[:, :, 1], ACT.Sqrt, bias=g.eps[:, 0:1]).then_inc(root, 1)


def layer2_ffn(nc, g, a, table):
    layer_norm(nc, g, None)
    with ExitStack() as stack:
        sb = lambda n, s, d=F32: stack.enter_context(nc.sbuf_tensor(g.tag + n, s, d))
        r = new_route(nc, g, stack, "mo", 2, T2 * P)
        with ExitStack() as s2:
            sb2 = lambda n, s: s2.enter_context(nc.sbuf_tensor(g.tag + n, s, F32))
            gamma, beta, wr, br, logits = sb2("gamma", [P, D]), sb2("beta", [P, D]), sb2("wr", [P, 2, E]), sb2("br", [1, E]), sb2("logits", [P, NT, E])
            zeros = sb2("zero_rows", [P, 4 * D])
            load_weights(nc, g, "mo", [(gamma[:, :], across(a.l2f_gamma)), (beta[:, :], across(a.l2f_beta)),
                                       (wr[:, :, :], rows_in(a.l2f_wr)), (br[:, :], a.l2f_br)])
            norm_again(nc, g, gamma, beta, g.acc)
            gate_logits(nc, g, "mo_gate", g.acc, wr, br[0:1, :], logits)
            route(nc, g, "mo_route", logits, 2, None, None, r, clear_rows(r, zeros[:, :]))
        send_rows(nc, g, "mo", r, 2, g.acc)
        NC = H2 // P
        with ExitStack() as s2:
            sem = lambda n: nc.alloc_semaphore(g.tag + "e_" + n)
            sb2 = lambda n, s: s2.enter_context(nc.sbuf_tensor(g.tag + "e_" + n, s, F32))
            w1, w2, b1, b2 = sb2("w1", [P, 2, E * H2]), sb2("w2", [P, NC, E * D]), sb2("b1", [P, E * H2]), sb2("b2", [P, E * D])
            load_weights(nc, g, "mo_experts", [(w1[:, c, :].rearrange("p (e h) -> p e h", e=E), a.l2f_w1[:, c * P:(c + 1) * P, :].rearrange("e p h -> p e h")) for c in range(2)]
                         + [(w2[:, c, :].rearrange("p (e h) -> p e h", e=E), a.l2f_w2[:, c * P:(c + 1) * P, :].rearrange("e p h -> p e h")) for c in range(NC)]
                         + [(b1[:, :], across(a.l2f_b1)), (b2[:, :], across(a.l2f_b2))])
            loaded = [sem(f"loaded{s}") for s in range(2)]
            stored = [sem(f"stored{s}") for s in range(2)]
            turned, xt_ready, hidden, biased, active, turned_h, ht_ready, product, copied, freed = (sem(n) for n in (
                "turned", "xt_ready", "hidden", "biased", "active", "turned_h", "ht_ready", "product", "copied", "freed"))
            rows, xt, h, ht, y = sb2("rows", [P, 2, D]), sb2("xt", [P, 2, D]), sb2("h", [P, 2, H2]), sb2("ht", [P, 2, H2]), sb2("y", [P, 2, D])
            block = s2.enter_context(nc.Block(g.tag + "experts"))

            @block.sync
            def _(sp):
                with nc.sync.Fori(0, T2 // 2) as i:
                    for s in range(2):
                        sp.wait_ge(turned, 2 * i + s + 1)
                        sp.dma_start(rows[:, s, :], r.sorted[ds((2 * i + s) * P, P), :]).then_inc(loaded[s], 16)

            @block.tensor
            def _(pe):
                own = [nc.tensor.alloc_register(g.tag + f"owner{s}") for s in range(2)]
                pe.sem_inc(turned, 2)
                pe.sem_inc(hidden, 2)
                pe.sem_inc(turned_h, 2)
                pe.sem_inc(product, 2)
                with nc.tensor.Fori(0, T2 // 2) as i:
                    nc.tensor.reg_load(own, r.expert[0:1, ds(2 * i, 2)])
                    for s in range(2):
                        t = 2 * i + s
                        pe.wait_ge(loaded[s], 16 * (i + 1))
                        pe.wait_ge(xt_ready, t + 1)
                        nc.tensor.transpose(g.ps[s][:, 0:P], rows[:, s, 0:P], g.ident[:, :])
                        nc.tensor.transpose(g.ps[s][:, P:D], rows[:, s, P:D], g.ident[:, :]).then_inc(turned, 1)
                    for s in range(2):
                        t = 2 * i + s
                        e = nc.tensor.snap(own[s], min_val=0, max_val=E - 1)
                        pe.wait_ge(xt_ready, t + 3)
                        pe.wait_ge(biased, t + 1)
                        for c in range(2):
                            last = nc.tensor.matmul(g.ps[2 + s][:, :], xt[:, s, c * P:(c + 1) * P], w1[:, c, ds(e * H2, H2)],
                                                    start=(c == 0), stop=(c == 1))
                        last.then_inc(hidden, 1)
                    for s in range(2):
                        t = 2 * i + s
                        pe.wait_ge(active, t + 1)
                        pe.wait_ge(ht_ready, t + 1)
                        for c in range(NC):
                            last = nc.tensor.transpose(g.ps[4 + s][:, c * P:(c + 1) * P], h[:, s, c * P:(c + 1) * P], g.ident[:, :])
                        last.then_inc(turned_h, 1)
                    for s in range(2):
                        t = 2 * i + s
                        e = nc.tensor.snap(own[s], min_val=0, max_val=E - 1)
                        pe.wait_ge(ht_ready, t + 3)
                        pe.wait_ge(copied, t + 1)
                        for c in range(NC):
                            last = nc.tensor.matmul(g.ps[6 + s][:, 0:D], ht[:, s, c * P:(c + 1) * P], w2[:, c, ds(e * D, D)],
                                                    start=(c == 0), stop=(c == NC - 1))
                        last.then_inc(product, 1)

            @block.scalar
            def _(act):
                act.sem_inc(xt_ready, 2)
                with nc.scalar.Fori(0, T2 // 2) as i:
                    for s in range(2):
                        t = 2 * i + s
                        act.wait_ge(turned, t + 3)
                        act.wait_ge(hidden, t + 1)
                        nc.scalar.activation(xt[:, s, :], g.ps[s][:, 0:D], ACT.Copy).then_inc(xt_ready, 1)
                    for s in range(2):
                        t = 2 * i + s
                        act.wait_ge(biased, t + 3)
                        nc.scalar.activation(h[:, s, :], h[:, s, :], ACT.Gelu).then_inc(active, 1)

            @block.vector
            def _(dve):
                own = [nc.vector.alloc_register(g.tag + f"dve_owner{s}") for s in range(2)]
                dve.sem_inc(biased, 2)
                dve.sem_inc(ht_ready, 2)
                dve.sem_inc(copied, 2)
                dve.sem_inc(freed, 2)
                with nc.vector.Fori(0, T2 // 2) as i:
                    nc.vector.reg_load(own, r.expert[0:1, ds(2 * i, 2)])
                    for s in range(2):
                        t = 2 * i + s
                        e = nc.vector.snap(own[s], min_val=0, max_val=E - 1)
                        dve.wait_ge(hidden, t + 3)
                        dve.wait_ge(turned_h, t + 1)
                        nc.vector.tensor_tensor(h[:, s, :], g.ps[2 + s][:, :], b1[:, ds(e * H2, H2)], ALU.add).then_inc(biased, 1)
                    for s in range(2):
                        t = 2 * i + s
                        dve.wait_ge(turned_h, t + 3)
                        dve.wait_ge(product, t + 1)
                        nc.vector.tensor_copy(ht[:, s, :], g.ps[4 + s][:, :]).then_inc(ht_ready, 1)
                    for s in range(2):
                        t = 2 * i + s
                        e = nc.vector.snap(own[s], min_val=0, max_val=E - 1)
                        dve.wait_ge(product, t + 3)
                        dve.wait_ge(freed, t + 1)
                        nc.vector.tensor_tensor(y[:, s, :], g.ps[6 + s][:, 0:D], b2[:, ds(e * D, D)], ALU.add).then_inc(copied, 1)

            @block.gpsimd
            def _(pool):
                with nc.gpsimd.Fori(0, T2 // 2) as i:
                    for s in range(2):
                        pool.wait_ge(copied, 2 * i + s + 3)
                        pool.dma_start(r.result[ds((2 * i + s) * P, P), :], y[:, s, :]).then_inc(stored[s], 16)
                        pool.wait_ge(stored[s], 16 * (i + 1))
                        pool.sem_inc(freed, 1)

        collect_rows(nc, g, "mo", r, 2, g.x)


H3 = 1024
T3 = (NODES + E * (P - 1)) // P
T3 += T3 % 2


def layer3_ffn(nc, g, a, table):
    layer_norm(nc, g, None)
    NF = H3 // P
    with ExitStack() as stack:
        sb = lambda n, s, d=F32: stack.enter_context(nc.sbuf_tensor(g.tag + n, s, d))
        r = new_route(nc, g, stack, "top", 1, T3 * P)
        w1, b1 = sb("w1", [P, 2, H3]), sb("b1", [P, NF])
        with ExitStack() as s1:
            sb1 = lambda n, s: s1.enter_context(nc.sbuf_tensor(g.tag + n, s, F32))
            wg, bg, logits, zeros = sb1("wg", [P, NF, E]), sb1("bg", [1, E]), sb1("logits", [P, NT, E]), sb1("zero_rows", [P, 4 * D])
            load_weights(nc, g, "top", [(w1[:, :, :], rows_in(a.l3f_w1)), (b1[:, :], a.l3f_b1_cols),
                                        (wg[:, :, :], rows_in(a.l3f_wg)), (bg[:, :], a.l3f_bg)])
            with ExitStack() as s2:
                sem = lambda n: nc.alloc_semaphore(g.tag + "g_" + n)
                xnt = s2.enter_context(nc.sbuf_tensor(g.tag + "xnt", [P, 2, ROWS], F32))
                ht = s2.enter_context(nc.sbuf_tensor(g.tag + "g_ht", [P, NF, 2 * P], F32))
                turn_nodes(nc, g, xnt)
                hidden, active, product, used = sem("hidden"), sem("active"), sem("product"), sem("used")
                block = s2.enter_context(nc.Block(g.tag + "gate"))
                G = 2 * P

                @block.tensor
                def _(pe):
                    pe.sem_inc(hidden, 4)
                    pe.sem_inc(product, 2)
                    with nc.tensor.Fori(0, ROWS // G) as i:
                        for f in range(NF):
                            pe.wait_ge(active, NF * i + f + 1)
                            for c in range(2):
                                last = nc.tensor.matmul(g.ps[f % 4][:, 0:G], w1[:, c, f * P:(f + 1) * P], xnt[:, c, ds(i * G, G)],
                                                        start=(c == 0), stop=(c == 1))
                            last.then_inc(hidden, 1)
                        for s in range(2):
                            pe.wait_ge(used, 2 * i + s + 1)
                            nc.tensor.matmul(g.ps[4 + s][:, 0:E], g.ones[0:1, :], bg[0:1, :], start=True, stop=False)
                            for f in range(NF):
                                if s == 0:
                                    pe.wait_ge(active, NF * i + f + 5)
                                last = nc.tensor.matmul(g.ps[4 + s][:, 0:E], ht[:, f, s * P:(s + 1) * P], wg[:, f, :],
                                                        start=False, stop=(f == NF - 1))
                            last.then_inc(product, 1)

                @block.scalar
                def _(act):
                    act.sem_inc(active, 4)
                    with nc.scalar.Fori(0, ROWS // G) as i:
                        act.wait_ge(product, 2 * i + 2)
                        for f in range(NF):
                            act.wait_ge(hidden, NF * i + f + 5)
                            nc.scalar.activation(ht[:, f, :], g.ps[f % 4][:, 0:G], ACT.Gelu, bias=b1[:, f:f + 1]).then_inc(active, 1)

                @block.vector
                def _(dve):
                    dve.sem_inc(used, 2)
                    with nc.vector.Fori(0, ROWS // G) as i:
                        for s in range(2):
                            dve.wait_ge(product, 2 * i + s + 3)
                            nc.vector.tensor_copy(logits[:, ds(2 * i + s, 1), :], g.ps[4 + s][:, 0:E]).then_inc(used, 1)

            route(nc, g, "top_route", logits, 1, None, None, r, clear_rows(r, zeros[:, :]))
        send_rows(nc, g, "top", r, 1, g.xn)
        with ExitStack() as s2:
            sem = lambda n: nc.alloc_semaphore(g.tag + "e_" + n)
            sb2 = lambda n, s: s2.enter_context(nc.sbuf_tensor(g.tag + "e_" + n, s, F32))
            wd, bd = sb2("wd", [P, NF, E * D]), sb2("bd", [P, E * D])
            load_weights(nc, g, "top_experts", [(wd[:, f, :].rearrange("p (e h) -> p e h", e=E),
                                                 a.l3f_wd[:, f * P:(f + 1) * P, :].rearrange("e p h -> p e h")) for f in range(NF)]
                         + [(bd[:, :], across(a.l3f_bd))])
            loaded, stored, turned, xt_ready, hidden, active, product, copied, freed = (sem(n) for n in (
                "loaded", "stored", "turned", "xt_ready", "hidden", "active", "product", "copied", "freed"))
            rows, xt, ht, y = sb2("rows", [P, 2, D]), sb2("xt", [P, 2, 2 * P]), sb2("ht", [P, NF, 2 * P]), sb2("y", [P, 2, D])
            block = s2.enter_context(nc.Block(g.tag + "experts"))

            @block.sync
            def _(sp):
                with nc.sync.Fori(0, T3 // 2) as i:
                    sp.wait_ge(turned, i + 1)
                    sp.dma_start(rows[:, :, :], r.sorted[ds(2 * i * P, 2 * P), :].rearrange("(r p) d -> p r d", p=P)).then_inc(loaded, 16)

            @block.tensor
            def _(pe):
                own = [nc.tensor.alloc_register(g.tag + f"owner{s}") for s in range(2)]
                pe.sem_inc(turned, 1)
                pe.sem_inc(hidden, 3)
                pe.sem_inc(product, 2)
                with nc.tensor.Fori(0, T3 // 2) as i:
                    nc.tensor.reg_load(own, r.expert[0:1, ds(2 * i, 2)])
                    pe.wait_ge(loaded, 16 * (i + 1))
                    pe.wait_ge(xt_ready, i + 1)
                    for c in range(2):
                        for s in range(2):
                            last = nc.tensor.transpose(g.ps[0][:, (2 * c + s) * P:(2 * c + s + 1) * P], rows[:, s, c * P:(c + 1) * P], g.ident[:, :])
                    last.then_inc(turned, 1)
                    pe.wait_ge(xt_ready, i + 2)
                    for f in range(NF):
                        pe.wait_ge(active, NF * i + f + 1)
                        for c in range(2):
                            last = nc.tensor.matmul(g.ps[1 + f % 4][:, 0:2 * P], w1[:, c, f * P:(f + 1) * P], xt[:, c, :],
                                                    start=(c == 0), stop=(c == 1))
                        last.then_inc(hidden, 1)
                    for s in range(2):
                        t = 2 * i + s
                        e = nc.tensor.snap(own[s], min_val=0, max_val=E - 1)
                        pe.wait_ge(copied, t + 1)
                        for f in range(NF):
                            if s == 0:
                                pe.wait_ge(active, NF * i + f + 5)
                            last = nc.tensor.matmul(g.ps[5 + s][:, 0:D], ht[:, f, s * P:(s + 1) * P], wd[:, f, ds(e * D, D)],
                                                    start=(f == 0), stop=(f == NF - 1))
                        last.then_inc(product, 1)

            @block.scalar
            def _(act):
                act.sem_inc(xt_ready, 1)
                act.sem_inc(active, 4)
                with nc.scalar.Fori(0, T3 // 2) as i:
                    act.wait_ge(turned, i + 2)
                    act.wait_ge(hidden, NF * i + 3)
                    nc.scalar.activation(xt[:, :, :], g.ps[0][:, :].rearrange("p (c n) -> p c n", c=2), ACT.Copy).then_inc(xt_ready, 1)
                    act.wait_ge(product, 2 * i + 2)
                    for f in range(NF):
                        act.wait_ge(hidden, NF * i + f + 4)
                        nc.scalar.activation(ht[:, f, :], g.ps[1 + f % 4][:, 0:2 * P], ACT.Gelu, bias=b1[:, f:f + 1]).then_inc(active, 1)

            @block.vector
            def _(dve):
                own = [nc.vector.alloc_register(g.tag + f"dve_owner{s}") for s in range(2)]
                dve.sem_inc(copied, 2)
                dve.sem_inc(freed, 2)
                with nc.vector.Fori(0, T3 // 2) as i:
                    nc.vector.reg_load(own, r.expert[0:1, ds(2 * i, 2)])
                    for s in range(2):
                        t = 2 * i + s
                        e = nc.vector.snap(own[s], min_val=0, max_val=E - 1)
                        dve.wait_ge(product, t + 3)
                        dve.wait_ge(freed, t + 1)
                        nc.vector.tensor_tensor(y[:, s, :], g.ps[5 + s][:, 0:D], bd[:, ds(e * D, D)], ALU.add).then_inc(copied, 1)

            @block.gpsimd
            def _(pool):
                with nc.gpsimd.Fori(0, T3 // 2) as i:
                    for s in range(2):
                        pool.wait_ge(copied, 2 * i + s + 3)
                        pool.dma_start(r.result[ds((2 * i + s) * P, P), :], y[:, s, :]).then_inc(stored, 16)
                        pool.wait_ge(stored, 16 * (2 * i + s + 1))
                        pool.sem_inc(freed, 1)

        collect_rows(nc, g, "top", r, 1, g.x)


TABLES = 4
U8 = 8


def mark_repeats(nc, g, a, to_row):
    with ExitStack() as stack:
        sem = lambda n: nc.alloc_semaphore(g.tag + "r_" + n)
        sb = lambda n, s, d=F32: stack.enter_context(nc.sbuf_tensor(g.tag + "r_" + n, s, d))
        loaded = [sem(f"loaded{h}") for h in range(2)]
        before, counted, step, srcf_done = sem("before"), sem("counted"), sem("step"), sem("srcf")
        across_src, lower, junk = sb("src_across", [P, 2, U8 * P], I32), sb("lower", [P, P]), sb("junk", [P, 2, P])
        srcf, count, spare = sb("srcf", [P, ET]), sb("count", [P, ET]), sb("spare", [P, ET])
        block = stack.enter_context(nc.Block(g.tag + "mark_repeats"))

        @block.gpsimd
        def _(pool):
            nc.gpsimd.affine_select(out=lower[:, :], in_=g.ones[:, :], compare_op=ALU.is_gt, fill=0.0, base=0,
                                    pattern=[[-1, P]], channel_multiplier=1).then_inc(before, 1)
            nc.gpsimd.iota(spare[:, :], [[0, ET]], base=ROWS, channel_multiplier=1, allow_small_or_imprecise_dtypes=True).then_inc(before, 1)

        @block.sync
        def _(sp):
            sp.sem_inc(step, 1)
            with nc.sync.Fori(0, ET // U8 // 2) as i:
                for h in range(2):
                    sp.wait_ge(counted, (2 * i + h) * U8 + U8)
                    sp.dma_start(across_src[:, h, :], a.src_row[ds((2 * i + h) * U8 * P, U8 * P)]
                                 .rearrange("(o n) -> o n", o=1).to_broadcast([P, U8 * P])).then_inc(loaded[h], 16)

        @block.vector
        def _(dve):
            dve.sem_inc(counted, 2 * U8)
            nc.vector.tensor_copy(srcf[:, :], g.srcc[:, :]).then_inc(srcf_done, 1)
            dve.wait_ge(srcf_done, 1)
            dve.wait_ge(before, 2)
            with nc.vector.Fori(0, ET // U8 // 2) as i:
                for h in range(2):
                    dve.wait_ge(loaded[h], 16 * (i + 1))
                    for u in range(U8):
                        n = (2 * i + h) * U8 + u
                        dve.wait_ge(counted, n + 2 * U8 - 1)
                        nc.vector.scalar_tensor_tensor(out=junk[:, u % 2, :], in0=across_src[:, h, u * P:(u + 1) * P], scalar=srcf[:, ds(n, 1)],
                                                       in1=lower[:, :], op0=ALU.is_equal, op1=ALU.mult,
                                                       accum_out=count[:, ds(n, 1)]).then_inc(counted, 1)
            dve.wait_ge(counted, ET + 2 * U8)
            nc.vector.tensor_scalar(count[:, :], count[:, :], 0.0, None, ALU.is_gt).then_inc(step, 1)
            nc.vector.tensor_tensor(spare[:, :], spare[:, :], srcf[:, :], ALU.subtract).then_inc(step, 1)
            dve.wait_ge(step, 3)
            nc.vector.tensor_tensor(count[:, :], count[:, :], spare[:, :], ALU.mult).then_inc(step, 1)
            dve.wait_ge(step, 4)
            nc.vector.tensor_tensor(to_row[:, :], count[:, :], srcf[:, :], ALU.add).then_inc(step, 1)
            dve.wait_ge(step, 5)


def scatter_edges(nc, g, a, to_row, tables):
    with ExitStack() as stack:
        sem = lambda n: nc.alloc_semaphore(g.tag + "s_" + n)
        sb = lambda n, s, d=F32: stack.enter_context(nc.sbuf_tensor(g.tag + "s_" + n, s, d))
        weights, srcf = sb("weights", [P, ET + U8]), sb("srcf", [P, ET + U8])
        zeros = sb("zeros", [P, 8 * D])
        load_weights(nc, g, "edge_weights", [(weights[:, 0:ET], a.edge_weight_cols)])
        loaded = [sem(f"loaded{h}") for h in range(2)]
        scattered = [sem(f"scattered{k}") for k in range(TABLES)]
        hot, turned, hot_t, looked, placed, mixed, summed, ready, sent, copied, claimed, zeroed, zero, shared, retired = (sem(n) for n in (
            "hot", "turned", "hot_t", "looked", "placed", "mixed", "summed", "ready", "sent", "idx", "claimed", "zeroed", "zero", "shared", "retired"))
        across_src = sb("src_across", [P, 2, U8 * P], I32)
        idx = sb("idx", [P, 2, 4], I32)
        onehot, onehot_t, mix = sb("onehot", [P, 2, 2 * P]), sb("onehot_t", [P, 2, 2 * P]), sb("mix", [P, 2, P])
        found, rows = sb("found", [P, 2, D]), sb("rows", [P, U8, D])
        with ExitStack() as s2:
            prep = nc.alloc_semaphore(g.tag + "s_prep")
            block = s2.enter_context(nc.Block(g.tag + "clear_tables"))

            @block.vector
            def _(dve):
                nc.vector.memset(zeros[:, :], 0.0).then_inc(zero, 1)
                nc.vector.tensor_copy(srcf[:, 0:ET], g.srcc[:, :]).then_inc(prep, 1)
                nc.vector.memset(srcf[:, ET:], 0.0).then_inc(prep, 1)
                nc.vector.memset(weights[:, ET:], 0.0).then_inc(prep, 1)
                dve.wait_ge(prep, 3)

            @block.sync
            def _(sp):
                sp.wait_ge(zero, 1)
                for k in range(TABLES):
                    for r0 in range(0, ROWS, 8 * P):
                        m = min(8, (ROWS - r0) // P)
                        sp.dma_start(tables[k][r0:r0 + m * P, :].rearrange("(p j) d -> p (j d)", p=P), zeros[:, 0:m * D]).then_inc(zeroed, 16)
                    sp.dma_start(tables[k][ROWS:ROWS + P, :], zeros[:, 0:D]).then_inc(zeroed, 16)
                sp.wait_ge(zeroed, 16 * TABLES * (-(-ROWS // (8 * P)) + 1))

        block = stack.enter_context(nc.Block(g.tag + "scatter_edges"))
        xflat = g.xn[:, :, :].rearrange("p t d -> p (t d)")

        @block.sync
        def _(sp):
            with nc.sync.Fori(0, ET // U8 // 2) as i:
                for h in range(2):
                    sp.wait_ge(mixed, (2 * i + h) * U8 + U8)
                    sp.dma_start(across_src[:, h, :], a.src_row[ds((2 * i + h) * U8 * P, U8 * P)]
                                 .rearrange("(o n) -> o n", o=1).to_broadcast([P, U8 * P])).then_inc(loaded[h], 16)

        @block.gpsimd
        def _(pool):
            def eight(i):
                first = isinstance(i, int)
                for h in range(2):
                    nc.gpsimd.tensor_copy(idx[:, h, :], to_row[:, ds(U8 * i + 4 * h, 4)]).then_inc(copied, 1)
                    pool.wait_ge(copied, 2 * i + h + 1)
                    for k in range(TABLES):
                        u = 4 * h + k
                        pool.wait_ge(ready, U8 * i + u + 5)
                        pool.sem_inc(claimed, 1)
                        nc.gpsimd.indirect_dma_start(
                            tables[k], bass.IndirectOffsetOnAxis(ap=idx[:, h, k:k + 1].bitcast(U32), axis=0),
                            rows[:, u, :], None, bounds_check=ROWS + P - 1, compute_op=ALU.add).then_inc(scattered[k], 16)
                        n = (k + 1) % TABLES
                        if first and h == 0 and k < TABLES - 1:
                            continue
                        pool.wait_ge(scattered[n], 16 * (2 * i + h + (1 if k == TABLES - 1 else 0)))
                        pool.sem_inc(retired, 1)
            eight(0)
            with nc.gpsimd.Fori(1, ET // U8) as i:
                eight(i)
            for k in range(TABLES):
                pool.wait_ge(scattered[k], 16 * ET // TABLES)

        @block.tensor
        def _(pe):
            window = [nc.tensor.alloc_register(g.tag + f"sw{u}") for u in range(U8)]
            pe.sem_inc(turned, 2)
            pe.sem_inc(looked, 2)
            pe.sem_inc(summed, 2)
            with nc.tensor.Fori(0, ET // U8) as i:
                nc.tensor.reg_load(window, g.window[0:1, ds(U8 * i, U8)])
                for v in range(0, U8, 2):
                    for u in (v, v + 1):
                        n = U8 * i + u
                        pe.wait_ge(hot, n + 1)
                        pe.wait_ge(hot_t, n + 1)
                        nc.tensor.transpose(g.ps[u % 2][:, 0:P], onehot[:, u % 2, 0:P], g.ident[:, :])
                        nc.tensor.transpose(g.ps[u % 2][:, P:2 * P], onehot[:, u % 2, P:2 * P], g.ident[:, :]).then_inc(turned, 1)
                    for u in (v, v + 1):
                        n = U8 * i + u
                        w = nc.tensor.snap(window[u], min_val=0, max_val=NT - 2)
                        pe.wait_ge(hot_t, n + 3)
                        pe.wait_ge(placed, n + 1)
                        for k in range(2):
                            last = nc.tensor.matmul(g.ps[2 + u % 2][:, 0:D], onehot_t[:, u % 2, k * P:(k + 1) * P],
                                                    xflat[:, ds(w * D + k * D, D)], start=(k == 0), stop=(k == 1))
                        last.then_inc(looked, 1)
                    for u in (v, v + 1):
                        n = U8 * i + u
                        pe.wait_ge(placed, n + 3)
                        pe.wait_ge(mixed, n + 2 * U8 + 1)
                        pe.wait_ge(ready, n + 1)
                        nc.tensor.matmul(g.ps[4 + u % 4][:, 0:D], mix[:, u % 2, :], found[:, u % 2, :], start=True, stop=True).then_inc(summed, 1)

        @block.scalar
        def _(act):
            act.sem_inc(hot_t, 2)
            act.sem_inc(placed, 2)
            with nc.scalar.Fori(0, ET // U8) as i:
                for v in range(0, U8, 2):
                    for u in (v, v + 1):
                        n = U8 * i + u
                        act.wait_ge(turned, n + 3)
                        act.wait_ge(looked, n + 1)
                        nc.scalar.activation(onehot_t[:, u % 2, :], g.ps[u % 2][:, 0:2 * P], ACT.Copy).then_inc(hot_t, 1)
                    for u in (v, v + 1):
                        n = U8 * i + u
                        act.wait_ge(looked, n + 3)
                        act.wait_ge(summed, n + 1)
                        nc.scalar.activation(found[:, u % 2, :], g.ps[2 + u % 2][:, 0:D], ACT.Copy).then_inc(placed, 1)

        @block.vector
        def _(dve):
            dve.sem_inc(mixed, 2 * U8)
            dve.sem_inc(retired, U8)
            dve.sem_inc(ready, 4)

            def build(n, slot):
                nc.vector.tensor_scalar(onehot[:, slot, :], g.iota[:, :], g.local[:, ds(n, 1)], None, ALU.is_equal).then_inc(hot, 1)
            build(0, 0)
            build(1, 1)
            with nc.vector.Fori(0, ET // U8 // 2) as i:
                for h in range(2):
                    dve.wait_ge(loaded[h], 16 * (i + 1))
                    for u in range(U8):
                        n = (2 * i + h) * U8 + u
                        dve.wait_ge(turned, n + 3)
                        build(n + 2, u % 2)
                        dve.wait_ge(summed, n + 1)
                        nc.vector.tensor_scalar(mix[:, u % 2, :], across_src[:, h, u * P:(u + 1) * P], srcf[:, ds(n, 1)],
                                                weights[:, ds(n, 1)], ALU.is_equal, ALU.mult).then_inc(mixed, 1)
                        dve.wait_ge(summed, n + 3)
                        dve.wait_ge(retired, n + 1)
                        nc.vector.tensor_copy(rows[:, u, :], g.ps[4 + u % 4][:, 0:D]).then_inc(ready, 1)


def sum_tables(nc, g, tables):
    with ExitStack() as stack:
        sem = lambda n: nc.alloc_semaphore(g.tag + "t_" + n)
        part = [stack.enter_context(nc.sbuf_tensor(g.tag + f"t_part{k}", [P, NT, D], F32)) for k in range(2)]
        loaded = [sem(f"loaded{k}") for k in range(TABLES)]
        added = sem("added")
        block = stack.enter_context(nc.Block(g.tag + "sum_tables"))
        dst = [g.acc, part[0], part[1], part[0]]

        @block.sync
        def _(sp):
            for k in range(TABLES):
                if k == 3:
                    sp.wait_ge(added, 1)
                sp.dma_start(dst[k][:, :, :], tables[k][0:ROWS, :].rearrange("(t p) d -> p t d", p=P)).then_inc(loaded[k], 16)

        @block.vector
        def _(dve):
            dve.wait_ge(loaded[0], 16)
            for k in range(1, TABLES):
                dve.wait_ge(loaded[k], 16)
                if k > 1:
                    dve.wait_ge(added, k - 1)
                nc.vector.tensor_tensor(g.acc[:, :, :], g.acc[:, :, :], dst[k][:, :, :], ALU.add).then_inc(added, 1)
            dve.wait_ge(added, TABLES - 1)


def layer2_gnn(nc, g, a, table):
    layer_norm(nc, g, None)
    tables = [nc.dram_tensor(f"source_sums{k}", (ROWS + P, D), F32).ap() for k in range(TABLES)]
    with ExitStack() as stack:
        to_row = stack.enter_context(nc.sbuf_tensor(g.tag + "to_row", [P, ET], I32))
        mark_repeats(nc, g, a, to_row)
        scatter_edges(nc, g, a, to_row, tables)
    sum_tables(nc, g, tables)
    with ExitStack() as stack:
        sb = lambda n, s: stack.enter_context(nc.sbuf_tensor(g.tag + n, s, F32))
        wl, wr, bias = sb("wl", [P, 2, D]), sb("wr", [P, 2, D]), sb("bias", [1, 3, D])
        load_weights(nc, g, "l2g", [(wl[:, :, :], rows_in(a.l2g_w_l)), (wr[:, :, :], rows_in(a.l2g_w_r)),
                                    (bias[:, 0, :], a.l2g_b_l), (bias[:, 1, :], a.l2g_b_r)])
        with ExitStack() as s2:
            step = nc.alloc_semaphore(g.tag + "bias_step")
            block = s2.enter_context(nc.Block(g.tag + "bias"))

            @block.vector
            def _(dve):
                nc.vector.tensor_tensor(bias[:, 2, :], bias[:, 0, :], bias[:, 1, :], ALU.add).then_inc(step, 1)
                dve.wait_ge(step, 1)
        project(nc, g, "l2g", [wl, wr], bias[0:1, 2, :], D,
                [("pool", lambda out, t: nc.gpsimd.tensor_copy(out, g.acc[:, ds(t, 1), :])),
                 ("dve", lambda out, t: nc.vector.tensor_copy(out, g.xn[:, ds(t, 1), :]))],
                lambda dve, bank, t, s: nc.vector.tensor_tensor(g.x[:, ds(t, 1), :], g.x[:, ds(t, 1), :], bank, ALU.add))


C3 = 128


def node_steps(nc, g, name, steps, table=None, rows=None):
    with ExitStack() as stack:
        step, stored = nc.alloc_semaphore(g.tag + name + "_step"), nc.alloc_semaphore(g.tag + name + "_stored")
        block = stack.enter_context(nc.Block(g.tag + name))

        @block.vector
        def _(dve):
            for n, s in enumerate(steps):
                s().then_inc(step, 1)
                dve.wait_ge(step, n + 1)

        @block.sync
        def _(sp):
            if table is not None:
                sp.wait_ge(step, len(steps))
                sp.dma_start(table.rearrange("(t p) d -> p t d", p=P), rows).then_inc(stored, 16)
                sp.wait_ge(stored, 16)


def layer3_gnn(nc, g, a, table):
    layer_norm(nc, g, None)
    htable = nc.dram_tensor("gcn_rows", (ROWS, C3), F32).ap()
    htable2 = nc.dram_tensor("gcn_rows2", (ROWS, C3), F32).ap()
    with ExitStack() as stack:
        sb = lambda n, s: stack.enter_context(nc.sbuf_tensor(g.tag + n, s, F32))
        w1, w2, b1, b2 = sb("w1", [P, 2, C3]), sb("w2", [P, 1, D]), sb("b1", [P, C3]), sb("b2", [1, D])
        dinv, hs = sb("dinv", [P, NT]), sb("hs", [P, NT, C3])
        load_weights(nc, g, "l3g", [(w1[:, :, :], rows_in(a.l3g_w1)), (w2[:, 0, :], a.l3g_w2), (b1[:, :], across(a.l3g_b1)), (b2[:, :], a.l3g_b2)])
        with ExitStack() as s2:
            step = nc.alloc_semaphore(g.tag + "dinv_step")
            block = s2.enter_context(nc.Block(g.tag + "dinv"))

            @block.scalar
            def _(act):
                nc.scalar.activation(dinv[:, :], g.deg[:, :], ACT.Sqrt, bias=g.ones[:, 0:1]).then_inc(step, 1)

            @block.vector
            def _(dve):
                dve.wait_ge(step, 1)
                nc.vector.reciprocal(dinv[:, :], dinv[:, :]).then_inc(step, 1)
                dve.wait_ge(step, 2)
        wide = [P, NT, C3]
        acc = g.acc[:, :, :].rearrange("p t d -> p (t d)")[:, 0:NT * C3].rearrange("p (t d) -> p t d", d=C3)
        dw = dinv[:, :].unsqueeze(2).to_broadcast(wide)
        tt = lambda out, x, y, op: (lambda: nc.vector.tensor_tensor(out, x, y, op))
        project(nc, g, "gcn1", [w1], None, C3,
                [("pool", lambda out, t: nc.gpsimd.tensor_copy(out, g.xn[:, ds(t, 1), :]))],
                lambda dve, bank, t, s: nc.vector.tensor_scalar(hs[:, ds(t, 1), :], bank, dinv[:, ds(t, 1)], None, ALU.mult))
        node_steps(nc, g, "gcn_rows", [], htable, hs[:, :, :])
        sum_edges(nc, g, htable, C3, name="gcn_sum1")
        node_steps(nc, g, "gcn_mid", [
            tt(acc, acc, hs[:, :, :], ALU.add), tt(acc, acc, dw, ALU.mult),
            tt(acc, acc, b1[:, :].unsqueeze(1).to_broadcast(wide), ALU.add),
            lambda: nc.vector.tensor_scalar(acc, acc, 0.0, None, ALU.max),
            tt(hs[:, :, :], acc, dw, ALU.mult)], htable2, hs[:, :, :])
        sum_edges(nc, g, htable2, C3, name="gcn_sum2")
        node_steps(nc, g, "gcn_end", [tt(acc, acc, hs[:, :, :], ALU.add), tt(hs[:, :, :], acc, dw, ALU.mult)])
        project(nc, g, "gcn2", [w2], b2[0:1, :], D,
                [("pool", lambda out, t: nc.gpsimd.tensor_copy(out, hs[:, ds(t, 1), :]))],
                lambda dve, bank, t, s: nc.vector.tensor_tensor(g.x[:, ds(t, 1), :], g.x[:, ds(t, 1), :], bank, ALU.add), chunks=1)


def store_out(nc, g, src, out):
    with ExitStack() as stack:
        stored = nc.alloc_semaphore("out_stored")
        block = stack.enter_context(nc.Block("store_out"))

        @block.sync
        def _(sp):
            sp.dma_start(out[0:FULL * P, :].rearrange("(t p) d -> p t d", p=P), src[:, 0:FULL, :]).then_inc(stored, 16)
            sp.dma_start(out[FULL * P:NODES, :], src[0:REST, FULL, :]).then_inc(stored, 16)
            sp.wait_ge(stored, 32)


def build(nc, a, out, stages):
    g = Core()
    g.tag = ""
    with ExitStack() as stack:
        tensors(nc, g, stack)
        table = nc.dram_tensor("xn_rows", (ROWS, D), F32).ap()
        load_graph(nc, g, a)
        for s in stages:
            g.tag = s.__name__ + "_"
            held = nc.snapshot_sems()
            s(nc, g, a, table)
            nc.clear_and_free_semaphores(nc.allocated_since(held))
            nc.all_engine_barrier()
        store_out(nc, g, g.x, out)


def _layout(inputs):
    import numpy as _np
    n = lambda v: _np.ascontiguousarray(_np.asarray(v))
    v = {k: _np.asarray(x) for k, x in inputs.items()}
    pad = _np.full(ET * P - EDGES, 3199, _np.int32)
    row = lambda u: _np.concatenate([u, pad])
    cols = lambda u: n(row(u).reshape(ET, P).T)
    flat = lambda u: n(u.reshape(-1))
    one = lambda u: n(u.reshape(1, -1))
    laid = {"x": n(v["x"]), "src_cols": cols(v["src"]), "dst_cols": cols(v["dst"]),
            "l0g_w_self_t": n(v["L0_gnn_W_self"].T), "l0g_w_neigh_t": n(v["L0_gnn_W_neigh"].T), "l0g_b_self": one(v["L0_gnn_b_self"]),
            "l0f_wr": flat(v["L0_ffn_wr"]), "l0f_br": n(v["L0_ffn_br"]), "l0f_w1": n(v["L0_ffn_w1"]), "l0f_w2": n(v["L0_ffn_w2"]),
            "l0f_b1_cols": n(v["L0_ffn_b1"].reshape(-1, P).T), "l0f_b2": one(v["L0_ffn_b2"]),
            "l1g_w_t": n(v["L1_gnn_W"].T), "l1g_w": n(v["L1_gnn_W"]), "l1g_a_src_cols": n(v["L1_gnn_a_src"].reshape(2, P).T),
            "l1g_a_dst_cols": n(v["L1_gnn_a_dst"].reshape(2, P).T), "l1g_edge_w_t": n(v["L1_gnn_edge_W"].T),
            "l1g_edge_b": one(v["L1_gnn_edge_b"]), "l1g_bias": n(v["L1_gnn_bias"]),
            "edge_attr_t": n(_np.concatenate([_np.concatenate([v["edge_attr_3"], _np.zeros((ET * P - EDGES, 3), _np.float32)]).T,
                                              _np.ones((1, ET * P), _np.float32)])),
            "l1f_gate_w": n(v["L1_ffn_gate_w"]), "l1f_gate_b": one(v["L1_ffn_gate_b"]), "l1f_w1": n(v["L1_ffn_w1"]), "l1f_w2": n(v["L1_ffn_w2"]),
            "l1f_b1_cols": n(v["L1_ffn_b1"].reshape(-1, P).T), "l1f_b2": n(v["L1_ffn_b2"]),
            "l2f_gamma": n(v["L2_ffn_gamma"]), "l2f_beta": n(v["L2_ffn_beta"]), "l2f_wr": n(v["L2_ffn_Wr"]), "l2f_br": one(v["L2_ffn_br"]),
            "l2f_w1": n(v["L2_ffn_W1"]), "l2f_b1": flat(v["L2_ffn_b1"]), "l2f_w2": n(v["L2_ffn_W2"]), "l2f_b2": flat(v["L2_ffn_b2"]),
            "l3f_w1": n(v["L3_ffn_W1"]), "l3f_b1_cols": n(v["L3_ffn_b1"].reshape(-1, P).T), "l3f_wg": n(v["L3_ffn_Wg"]),
            "l3f_bg": one(v["L3_ffn_bg"]), "l3f_wd": n(v["L3_ffn_Wd"]), "l3f_bd": flat(v["L3_ffn_bd"]),
            "l2g_w_l": n(v["L2_gnn_weight_l"]), "l2g_w_r": n(v["L2_gnn_weight_r"]), "l2g_b_l": one(v["L2_gnn_bias_l"]), "l2g_b_r": one(v["L2_gnn_bias_r"]),
            "edge_weight_cols": n(_np.concatenate([v["edge_weight"], _np.zeros(ET * P - EDGES, _np.float32)]).reshape(ET, P).T),
            "src_row": n(row(v["src"])),
            "l3g_w1": n(v["L3_gnn_W1"]), "l3g_w2": n(v["L3_gnn_W2"]), "l3g_b1": n(v["L3_gnn_b1"]), "l3g_b2": one(v["L3_gnn_b2"]),
            "dst_row": n(_np.concatenate([_np.full(1, -1, _np.int32), row(v["dst"]), _np.full(1, -1, _np.int32)]))}
    return laid


def kernel(**inputs):
    import numpy as _np
    import concourse.bacc as _bacc
    from concourse import mybir as _mybir
    from concourse.bass_utils import run_bass_kernel_spmd as _run

    nc = _bacc.Bacc("TRN2", target_bir_lowering=False, num_devices=1)
    laid = _layout(inputs)
    a = Core()
    arrays = {}
    for name, v in laid.items():
        arrays[f"in_{name}"] = v
        a.__dict__[name] = nc.dram_tensor(f"in_{name}", v.shape, _mybir.dt.from_np(v.dtype), kind="ExternalInput").ap()
    out = nc.dram_tensor("out_0", (NODES, D), F32, kind="ExternalOutput").ap()
    build(nc, a, out, STAGES)
    r = _run(nc, [arrays], core_ids=[0])
    return r.results[0]["out_0"]
STAGES = [layer0_gnn, layer0_ffn, layer1_gnn, layer1_ffn, layer2_gnn, layer2_ffn, layer3_gnn, layer3_ffn]
```

```python
import concourse.bass as bass
from concourse import mybir
from concourse.bass import ds
from contextlib import ExitStack

F32, I32, U32 = mybir.dt.float32, mybir.dt.int32, mybir.dt.uint32
ALU, ACT, AX = mybir.AluOpType, mybir.ActivationFunctionType, mybir.AxisListType
P = 128
NODES, D = 3125, 256
EDGES = 53125
NT = 26
ROWS = NT * P
FULL = NODES // P
REST = NODES - FULL * P
ET = 416
U = 16
H = U // 2
EPS = 1e-5


class Core:
    pass


def tensors(nc, g, stack):
    def sb(name, shape, dt=F32):
        return stack.enter_context(nc.sbuf_tensor(g.tag + name, shape, dt))
    g.x = sb("x_nodes", [P, NT, D])
    g.xn = sb("xn_nodes", [P, NT, D])
    g.acc = sb("edge_sums", [P, NT, D])
    g.acct = sb("edge_sums_turned", [P, 2, ROWS])
    g.deg = sb("in_degree", [P, NT])
    g.srcc = sb("src_cols", [P, ET], I32)
    g.dstc = sb("dst_cols", [P, ET], I32)
    g.local = sb("dst_local", [P, ET + 8])
    g.window = sb("dst_window", [1, ET], I32)
    g.ident = sb("identity", [P, P])
    g.iota = sb("iota_row", [P, 2 * P])
    g.ones = sb("ones", [P, P])
    g.node_id = sb("node_id", [P, NT])
    g.eps = sb("eps", [P, 1])
    g.stats = sb("ln_stats", [P, NT, 6])
    g.mv = sb("ln_mean_var", [P, NT, 2])
    g.rstd = sb("ln_rstd", [P, NT])
    g.ps = [stack.enter_context(nc.psum_tensor(f"bank{b}", [P, 512], F32)) for b in range(8)]


def load_graph(nc, g, a):
    with ExitStack() as stack:
        sem = lambda n: nc.alloc_semaphore(g.tag + n)
        x_cleared, x_loaded, idx_loaded = sem("x_cleared"), sem("x_loaded"), sem("idx_loaded")
        consts, ident0, win = sem("consts"), sem("ident_cleared"), sem("win_ready")
        win_sum, step = sem("win_sum"), sem("window_step")
        wi = stack.enter_context(nc.sbuf_tensor(g.tag + "window_tile", [1, ET], I32))
        df = stack.enter_context(nc.sbuf_tensor(g.tag + "dst_f", [P, ET], F32))
        block = stack.enter_context(nc.Block(g.tag + "load_graph"))

        @block.sync
        def _(sp):
            sp.dma_start(g.dstc[:, :], a.dst_cols).then_inc(idx_loaded, 16)
            sp.dma_start(g.srcc[:, :], a.src_cols).then_inc(idx_loaded, 16)
            sp.wait_ge(x_cleared, 1)
            sp.dma_start(g.x[:, 0:FULL, :], a.x[0:FULL * P, :].rearrange("(t p) d -> p t d", p=P)).then_inc(x_loaded, 16)
            sp.dma_start(g.x[0:REST, FULL, :], a.x[FULL * P:NODES, :]).then_inc(x_loaded, 16)
            sp.wait_ge(x_loaded, 32)

        @block.gpsimd
        def _(pool):
            nc.gpsimd.memset(g.ident[:, :], 0.0).then_inc(ident0, 1)
            nc.gpsimd.iota(g.iota[:, :], [[1, 2 * P]], base=0, channel_multiplier=0,
                           allow_small_or_imprecise_dtypes=True).then_inc(consts, 1)
            nc.gpsimd.iota(g.node_id[:, :], [[P, NT]], base=0, channel_multiplier=1,
                           allow_small_or_imprecise_dtypes=True).then_inc(consts, 1)
            pool.wait_ge(ident0, 1)
            nc.gpsimd.affine_select(out=g.ident[:, :], in_=g.ident[:, :], compare_op=ALU.not_equal, fill=1.0,
                                    base=0, pattern=[[-1, P]], channel_multiplier=1).then_inc(consts, 1)

        @block.vector
        def _(dve):
            nc.vector.memset(g.x[:, FULL:NT, :], 0.0).then_inc(x_cleared, 1)
            nc.vector.memset(g.ones[:, :], 1.0).then_inc(consts, 1)
            nc.vector.memset(g.eps[:, :], EPS).then_inc(consts, 1)
            nc.vector.memset(g.local[:, ET:ET + 8], 0.0).then_inc(consts, 1)
            dve.wait_ge(idx_loaded, 32)
            nc.vector.tensor_scalar(wi[:, :], g.dstc[0:1, :], 7, None, ALU.logical_shift_right).then_inc(step, 1)
            nc.vector.tensor_copy(df[:, :], g.dstc[:, :]).then_inc(win, 1)
            dve.wait_ge(step, 1)
            nc.vector.tensor_copy(g.window[:, :], wi[:, :]).then_inc(step, 1)
            dve.wait_ge(win_sum, 1)
            nc.vector.tensor_tensor(g.local[:, 0:ET], df[:, :], g.ps[0][:, 0:ET], ALU.subtract).then_inc(step, 1)
            dve.wait_ge(step, 3)

        @block.tensor
        def _(pe):
            pe.wait_ge(win, 1)
            pe.wait_ge(consts, 6)
            nc.tensor.matmul(g.ps[0][:, 0:ET], g.ones[0:1, :], df[0:1, :], start=True, stop=True).then_inc(win_sum, 1)


def layer_norm(nc, g, table):
    with ExitStack() as stack:
        sem = lambda n: nc.alloc_semaphore(g.tag + n)
        stat, aggr, root, inv, normed, stored = (sem("ln_" + n) for n in ("stat", "aggr", "root", "inv", "normed", "stored"))
        block = stack.enter_context(nc.Block(g.tag + "layer_norm"))

        @block.vector
        def _(dve):
            with nc.vector.Fori(0, NT) as t:
                nc.vector.bn_stats(g.stats[:, ds(t, 1), :], g.x[:, ds(t, 1), :]).then_inc(stat, 1)
            dve.wait_ge(stat, NT)
            for t in range(NT):
                nc.vector.bn_aggr(g.mv[:, t, :], g.stats[:, t, :]).then_inc(aggr, 1)
            dve.wait_ge(root, 1)
            nc.vector.reciprocal(g.rstd[:, :], g.rstd[:, :]).then_inc(inv, 1)
            dve.wait_ge(inv, 1)
            with nc.vector.Fori(0, NT) as t:
                nc.vector.tensor_scalar(g.xn[:, ds(t, 1), :], g.x[:, ds(t, 1), :], g.mv[:, ds(t, 1), 0],
                                        g.rstd[:, ds(t, 1)], ALU.subtract, ALU.mult).then_inc(normed, 1)

        @block.scalar
        def _(act):
            act.wait_ge(aggr, NT)
            nc.scalar.activation(g.rstd[:, :], g.mv[:, :, 1], ACT.Sqrt, bias=g.eps[:, 0:1]).then_inc(root, 1)

        @block.sync
        def _(sp):
            sp.wait_ge(normed, NT)
            if table is None:
                return
            sp.dma_start(table.rearrange("(t p) d -> p t d", p=P), g.xn[:, :, :]).then_inc(stored, 16)
            sp.wait_ge(stored, 16)


def copy_indices(nc, g, act, i, idx, copied, used):
    for h in range(2):
        act.wait_ge(used, U * i + (h + 1) * H)
        nc.scalar.activation(idx[:, h * H:(h + 1) * H], g.srcc[:, ds(U * i + h * H, H)], ACT.Copy).then_inc(copied, 1)


def gather_sources(nc, g, pool, table, rows, idx, copied, used, claimed, gathered):
    with nc.gpsimd.Fori(0, ET // U) as i:
        for u in range(U):
            if u % H == 0:
                pool.wait_ge(copied, 2 * i + u // H + 1)
            pool.wait_ge(used, U * i + u + 1)
            pool.sem_inc(claimed, 1)
            nc.gpsimd.indirect_dma_start(rows[:, u, :], None, table,
                                         bass.IndirectOffsetOnAxis(ap=idx[:, u:u + 1].bitcast(U32), axis=0)).then_inc(gathered[u], 16)


def turn_sums(nc, g, name, chunks, den_t=None, den=None):
    with ExitStack() as stack:
        turned, back = nc.alloc_semaphore(g.tag + name + "_turned"), [nc.alloc_semaphore(g.tag + name + f"_back{k}") for k in range(2)]
        block = stack.enter_context(nc.Block(g.tag + name + "_turn_sums"))
        W, acc = chunks * P, g.acc[:, :, :].rearrange("p t d -> p (t d)")

        @block.tensor
        def _(pe):
            for t in range(NT):
                if t >= 4:
                    pe.wait_ge(back[t % 2], (t - 4) // 2 + 1)
                for c in range(chunks):
                    last = nc.tensor.transpose(g.ps[t % 4][:, c * P:(c + 1) * P], g.acct[:, c, t * P:(t + 1) * P], g.ident[:, :])
                if den is not None:
                    last = nc.tensor.transpose(g.ps[t % 4][:, W:W + HEADS], den_t[:, t * P:(t + 1) * P], g.ident[0:HEADS, 0:HEADS])
                last.then_inc(turned, 1)

        @block.vector
        def _(dve):
            for t in range(0, NT, 2):
                dve.wait_ge(turned, t + 1)
                last = nc.vector.tensor_copy(acc[:, t * W:(t + 1) * W], g.ps[t % 4][:, 0:W])
                if den is not None:
                    last = nc.vector.tensor_copy(den[:, t, :], g.ps[t % 4][:, W:W + HEADS])
                last.then_inc(back[0], 1)
            dve.wait_ge(back[0], NT // 2)

        @block.scalar
        def _(act):
            for t in range(1, NT, 2):
                act.wait_ge(turned, t + 1)
                last = nc.scalar.activation(acc[:, t * W:(t + 1) * W], g.ps[t % 4][:, 0:W], ACT.Copy)
                if den is not None:
                    last = nc.scalar.activation(den[:, t, :], g.ps[t % 4][:, W:W + HEADS], ACT.Copy)
                last.then_inc(back[1], 1)
            act.wait_ge(back[1], NT // 2)


def sum_edges(nc, g, table, width, count_degree=False, name="sum", meanwhile=None):
    chunks = width // P
    with ExitStack() as stack:
        sem = lambda n: nc.alloc_semaphore(g.tag + name + n)
        sb = lambda n, s, d=F32: stack.enter_context(nc.sbuf_tensor(g.tag + name + n, s, d))
        gathered = [sem(f"gathered{u}") for u in range(U)]
        copied, hot, summed, added, cleared, claimed = sem("idx_copied"), sem("hot_ready"), sem("tile_summed"), sem("tile_added"), sem("acc_cleared"), sem("slot_claimed")
        idx, rows, onehot = sb("gather_idx", [P, U], I32), sb("gathered_rows", [P, U, width]), sb("onehot", [P, 4, P])
        deg_row = sb("deg_row", [1, ROWS]) if count_degree else None
        with ExitStack() as s2:
            block = s2.enter_context(nc.Block(g.tag + name + "sum_edges"))

            @block.gpsimd
            def _(pool):
                gather_sources(nc, g, pool, table, rows, idx, copied, summed, claimed, gathered)

            @block.scalar
            def _(act):
                with nc.scalar.Fori(0, ET // U) as i:
                    copy_indices(nc, g, act, i, idx, copied, summed)

            @block.sync
            def _(sp):
                if meanwhile is not None:
                    meanwhile(sp)

            @block.tensor
            def _(pe):
                pe.sem_inc(summed, U)
                with nc.tensor.Fori(0, ET // U) as i:
                    for u in range(U):
                        pe.wait_ge(hot, U * i + u + 1)
                        pe.wait_ge(added, U * i + u + 1)
                        pe.wait_ge(gathered[u], 16 * (i + 1))
                        if count_degree:
                            nc.tensor.matmul(g.ps[4 + u % 4][0:1, 0:P], g.ones[:, 0:1], onehot[:, u % 4, :], start=True, stop=True)
                        for c in range(chunks):
                            last = nc.tensor.matmul(g.ps[u % 4][:, c * P:(c + 1) * P], rows[:, u, c * P:(c + 1) * P],
                                                    onehot[:, u % 4, :], start=True, stop=True)
                        last.then_inc(summed, 1)

            @block.vector
            def _(dve):
                base = [nc.vector.alloc_register(g.tag + name + f"base{u}") for u in range(8)]
                nc.vector.memset(g.acct[:, 0:chunks, :], 0.0).then_inc(cleared, 1)
                if count_degree:
                    nc.vector.memset(deg_row[:, :], 0.0).then_inc(cleared, 1)
                dve.wait_ge(cleared, 1 + count_degree)

                def build(n, slot):
                    nc.vector.tensor_scalar(onehot[:, slot, :], g.iota[:, 0:P], g.local[:, ds(n, 1)], None, ALU.is_equal).then_inc(hot, 1)
                build(0, 0)
                build(1, 1)
                nc.vector.sem_inc(added, 4)
                with nc.vector.Fori(0, ET // U) as i:
                    for u in range(U):
                        if u % 8 == 0:
                            nc.vector.reg_load(base, g.dstc[0:1, ds(U * i + u, 8)])
                        build(U * i + u + 2, (u + 2) % 4)
                        b = nc.vector.snap(base[u % 8], min_val=0, max_val=ROWS - P)
                        dve.wait_ge(summed, U * i + u + 1 + U)
                        dve.wait_ge(added, U * i + u + 4)
                        if count_degree:
                            nc.vector.tensor_tensor(deg_row[:, ds(b, P)], deg_row[:, ds(b, P)], g.ps[4 + u % 4][0:1, 0:P], ALU.add)
                        nc.vector.tensor_tensor(g.acct[:, 0:chunks, ds(b, P)], g.acct[:, 0:chunks, ds(b, P)],
                                                g.ps[u % 4][:, 0:width].rearrange("p (c n) -> p c n", c=chunks), ALU.add).then_inc(added, 1)
        if count_degree:
            with ExitStack() as s2:
                turned, placed = sem("deg_turned"), sem("deg_placed")
                block = s2.enter_context(nc.Block(g.tag + name + "turn_degree"))

                @block.tensor
                def _(pe):
                    for t in range(NT):
                        last = nc.tensor.matmul(g.ps[0][:, t:t + 1], deg_row[0:1, t * P:(t + 1) * P], g.ones[0:1, 0:1], start=True, stop=True)
                    last.then_inc(turned, 1)

                @block.vector
                def _(dve):
                    dve.wait_ge(turned, 1)
                    nc.vector.tensor_copy(g.deg[:, :], g.ps[0][:, 0:NT]).then_inc(placed, 1)
                    dve.wait_ge(placed, 1)
    turn_sums(nc, g, name, chunks)


def project(nc, g, name, weights, bias, width, stage, finish, chunks=2, meanwhile=None):
    K = len(weights)
    with ExitStack() as stack:
        sem = lambda n: nc.alloc_semaphore(g.tag + name + n)
        staged = [sem(f"_staged{k}") for k in range(K)]
        turned, lhs_ready, product, used = sem("_turned"), sem("_lhs_ready"), sem("_product"), sem("_used")
        rows = stack.enter_context(nc.sbuf_tensor(g.tag + name + "_rows", [P, 2, K, chunks * P], F32))
        lhs = stack.enter_context(nc.sbuf_tensor(g.tag + name + "_lhs", [P, 2, K * chunks * P], F32))
        block = stack.enter_context(nc.Block(g.tag + name))

        def staging(eng, who, t, s):
            for k in range(K):
                if stage[k][0] == who:
                    eng.wait_ge(turned, t + 1)
                    stage[k][1](rows[:, s, k, :], t).then_inc(staged[k], 1)

        @block.sync
        def _(sp):
            if meanwhile is not None:
                meanwhile(sp)

        @block.gpsimd
        def _(pool):
            if any(w == "pool" for w, _ in stage):
                with nc.gpsimd.Fori(0, NT // 2) as i:
                    for s in range(2):
                        staging(pool, "pool", 2 * i + s, s)

        @block.tensor
        def _(pe):
            pe.sem_inc(turned, 2)
            pe.sem_inc(product, 2)
            with nc.tensor.Fori(0, NT // 2) as i:
                for s in range(2):
                    t = 2 * i + s
                    pe.wait_ge(lhs_ready, t + 1)
                    for k in range(K):
                        pe.wait_ge(staged[k], t + 1)
                        for c in range(chunks):
                            last = nc.tensor.transpose(g.ps[s][:, (chunks * k + c) * P:(chunks * k + c + 1) * P],
                                                       rows[:, s, k, c * P:(c + 1) * P], g.ident[:, :])
                    last.then_inc(turned, 1)
                for s in range(2):
                    t = 2 * i + s
                    pe.wait_ge(lhs_ready, t + 3)
                    pe.wait_ge(used, t + 1)
                    if bias is not None:
                        nc.tensor.matmul(g.ps[2 + s][:, 0:width], g.ones[0:1, :], bias, start=True, stop=False)
                    for k in range(K):
                        for c in range(chunks):
                            last = nc.tensor.matmul(g.ps[2 + s][:, 0:width], lhs[:, s, (chunks * k + c) * P:(chunks * k + c + 1) * P],
                                                    weights[k][:, c, 0:width], start=(bias is None and k == 0 and c == 0),
                                                    stop=(k == K - 1 and c == chunks - 1))
                    last.then_inc(product, 1)

        @block.scalar
        def _(act):
            act.sem_inc(lhs_ready, 2)
            with nc.scalar.Fori(0, NT // 2) as i:
                for s in range(2):
                    t = 2 * i + s
                    staging(act, "act", t, s)
                    act.wait_ge(turned, t + 3)
                    act.wait_ge(product, t + 1)
                    nc.scalar.activation(lhs[:, s, :], g.ps[s][:, 0:K * chunks * P], ACT.Copy).then_inc(lhs_ready, 1)

        @block.vector
        def _(dve):
            dve.sem_inc(used, 2)
            with nc.vector.Fori(0, NT // 2) as i:
                for s in range(2):
                    staging(dve, "dve", 2 * i + s, s)
                for s in range(2):
                    t = 2 * i + s
                    dve.wait_ge(product, t + 3)
                    finish(dve, g.ps[2 + s][:, 0:width], t, s).then_inc(used, 1)


def load_weights(nc, g, name, pairs):
    with ExitStack() as stack:
        loaded = nc.alloc_semaphore(g.tag + name + "_loaded")
        block = stack.enter_context(nc.Block(g.tag + name + "_load"))

        @block.sync
        def _(sp):
            for dst, src in pairs:
                sp.dma_start(dst, src).then_inc(loaded, 16)
            sp.wait_ge(loaded, 16 * len(pairs))


def loads(nc, g, name, pairs):
    loaded = nc.alloc_semaphore(g.tag + name + "_loaded")

    def run(sp):
        for dst, src in pairs:
            sp.dma_start(dst, src).then_inc(loaded, 16)
        sp.wait_ge(loaded, 16 * len(pairs))
    return run


def rows_in(w, c=P):
    return w.rearrange("(c p) n -> p c n", p=c)


def across(v):
    return v.rearrange("(o n) -> o n", o=1).to_broadcast([P, v.shape[0]])


def layer0_gnn(nc, g, a, table):
    layer_norm(nc, g, table)
    g.tables = source_tables(nc)
    with ExitStack() as stack:
        zeros = stack.enter_context(nc.sbuf_tensor(g.tag + "zeros", [P, 4 * D], F32))
        zero, zeroed = nc.alloc_semaphore(g.tag + "zero"), nc.alloc_semaphore(g.tag + "zeroed")

        def meanwhile(sp):
            sp.wait_ge(zero, 1)
            clear_tables(nc, g, sp, zeros, g.tables, zeroed)
        with ExitStack() as s2:
            block = s2.enter_context(nc.Block(g.tag + "zeros"))

            @block.vector
            def _(dve):
                nc.vector.memset(zeros[:, :], 0.0).then_inc(zero, 1)
        sum_edges(nc, g, table, D, count_degree=True, meanwhile=meanwhile)
    with ExitStack() as stack:
        sb = lambda n, s: stack.enter_context(nc.sbuf_tensor(g.tag + n, s, F32))
        w_self, w_neigh, b_self, inv = sb("w_self", [P, 2, D]), sb("w_neigh", [P, 2, D]), sb("b_self", [1, D]), sb("inv_deg", [P, NT])
        load_weights(nc, g, "l0g", [(w_self[:, :, :], rows_in(a.l0g_w_self_t)), (w_neigh[:, :, :], rows_in(a.l0g_w_neigh_t)),
                                 (b_self[:, :], a.l0g_b_self)])
        with ExitStack() as s2:
            step = nc.alloc_semaphore(g.tag + "inv_step")
            block = s2.enter_context(nc.Block(g.tag + "inv_degree"))

            @block.vector
            def _(dve):
                nc.vector.tensor_scalar(inv[:, :], g.deg[:, :], 1.0, None, ALU.max).then_inc(step, 1)
                dve.wait_ge(step, 1)
                nc.vector.reciprocal(inv[:, :], inv[:, :]).then_inc(step, 1)
                dve.wait_ge(step, 2)

        project(nc, g, "l0g", [w_self, w_neigh], b_self[0:1, :], D,
                [("pool", lambda out, t: nc.gpsimd.tensor_copy(out, g.xn[:, ds(t, 1), :])),
                 ("dve", lambda out, t: nc.vector.tensor_scalar(out, g.acc[:, ds(t, 1), :], inv[:, ds(t, 1)], None, ALU.mult))],
                lambda dve, bank, t, s: nc.vector.tensor_tensor(g.x[:, ds(t, 1), :], g.x[:, ds(t, 1), :], bank, ALU.add))


def turn_nodes(nc, g, xnt):
    with ExitStack() as stack:
        sem = lambda n: nc.alloc_semaphore(g.tag + "turn_" + n)
        staged, turned, placed = sem("staged"), sem("turned"), sem("placed")
        rows = stack.enter_context(nc.sbuf_tensor(g.tag + "turn_rows", [P, 2, D], F32))
        block = stack.enter_context(nc.Block(g.tag + "turn_nodes"))

        @block.gpsimd
        def _(pool):
            with nc.gpsimd.Fori(0, NT // 2) as i:
                for s in range(2):
                    pool.wait_ge(turned, 2 * i + s + 1)
                    nc.gpsimd.tensor_copy(rows[:, s, :], g.xn[:, ds(2 * i + s, 1), :]).then_inc(staged, 1)

        @block.tensor
        def _(pe):
            pe.sem_inc(turned, 2)
            with nc.tensor.Fori(0, NT // 2) as i:
                for s in range(2):
                    pe.wait_ge(staged, 2 * i + s + 1)
                    pe.wait_ge(placed, 2 * i + s + 1)
                    nc.tensor.transpose(g.ps[s][:, 0:P], rows[:, s, 0:P], g.ident[:, :])
                    nc.tensor.transpose(g.ps[s][:, P:2 * P], rows[:, s, P:2 * P], g.ident[:, :]).then_inc(turned, 1)

        @block.scalar
        def _(act):
            act.sem_inc(placed, 2)
            with nc.scalar.Fori(0, NT // 2) as i:
                for s in range(2):
                    act.wait_ge(turned, 2 * i + s + 3)
                    nc.scalar.activation(xnt[:, :, ds((2 * i + s) * P, P)],
                                         g.ps[s][:, 0:2 * P].rearrange("p (c n) -> p c n", c=2), ACT.Copy).then_inc(placed, 1)


KEEP = max(1, int(0.5 * NODES)) - 1
H0 = 1024
NEG = -3.0e38


def router_scores(nc, g, wr, br, scores):
    with ExitStack() as stack:
        done, added = (nc.alloc_semaphore(g.tag + "router_" + n) for n in ("dot", "bias"))
        prod = stack.enter_context(nc.sbuf_tensor(g.tag + "router_prod", [P, 4, D], F32))
        block = stack.enter_context(nc.Block(g.tag + "router_scores"))

        @block.vector
        def _(dve):
            for t in range(NT):
                if t >= 4:
                    dve.wait_ge(done, t - 3)
                nc.vector.scalar_tensor_tensor(out=prod[:, t % 4, :], in0=g.xn[:, t, :], scalar=1.0, in1=wr[:, :],
                                               op0=ALU.mult, op1=ALU.mult, accum_out=scores[:, t:t + 1]).then_inc(done, 1)
            dve.wait_ge(done, NT)
            nc.vector.tensor_scalar(scores[:, :], scores[:, :], br[:, 0:1], None, ALU.add).then_inc(added, 1)
            dve.wait_ge(added, 1)


def scores_across(nc, g, scores, scratch, srow):
    with ExitStack() as stack:
        sem = lambda n: nc.alloc_semaphore(g.tag + "across_" + n)
        turned, copied, stored, loaded = sem("turned"), sem("copied"), sem("stored"), sem("loaded")
        rows = stack.enter_context(nc.sbuf_tensor(g.tag + "score_rows", [NT, P], F32))
        block = stack.enter_context(nc.Block(g.tag + "scores_across"))

        @block.tensor
        def _(pe):
            nc.tensor.transpose(g.ps[0][0:NT, 0:P], scores[:, 0:NT], g.ident[:, :]).then_inc(turned, 1)

        @block.vector
        def _(dve):
            dve.wait_ge(turned, 1)
            nc.vector.tensor_copy(rows[:, :], g.ps[0][0:NT, 0:P]).then_inc(copied, 1)

        @block.sync
        def _(sp):
            sp.wait_ge(copied, 1)
            sp.dma_start(scratch.rearrange("(t p) -> t p", p=P), rows[:, :]).then_inc(stored, 16)
            sp.wait_ge(stored, 16)
            sp.dma_start(srow[:, :], across(scratch)).then_inc(loaded, 16)
            sp.wait_ge(loaded, 16)


def layer0_ffn(nc, g, a, table):
    layer_norm(nc, g, None)
    scratch = nc.dram_tensor("score_scratch", (ROWS,), F32).ap()
    with ExitStack() as stack:
        sb = lambda n, s: stack.enter_context(nc.sbuf_tensor(g.tag + n, s, F32))
        wr, br = sb("wr_rows", [P, D]), sb("br", [P, 1])
        w1, b1, w2, b2 = sb("l0_w1", [P, 2, H0]), sb("l0_b1", [P, H0 // P]), sb("l0_w2", [P, H0 // P, D]), sb("l0_b2", [1, D])
        scores, gate, srow, xnt = sb("scores", [P, NT]), sb("gate", [P, NT]), sb("score_row", [P, ROWS]), g.acct
        load_weights(nc, g, "l0f", [(wr[:, :], across(a.l0f_wr)), (br[:, :], across(a.l0f_br)), (w1[:, :, :], rows_in(a.l0f_w1)),
                                 (b1[:, :], a.l0f_b1_cols), (w2[:, :, :], rows_in(a.l0f_w2)), (b2[:, :], a.l0f_b2)])
        router_scores(nc, g, wr, br, scores)
        scores_across(nc, g, scores, scratch, srow)
        turn_nodes(nc, g, xnt)
        G = 2 * P
        NF = H0 // P
        with ExitStack() as s2:
            sem = lambda n: nc.alloc_semaphore(g.tag + "mod_" + n)
            ranked, selected, hidden, active, summed, used, skip = (sem(n) for n in
                ("ranked", "selected", "hidden", "active", "summed", "used", "skip"))
            above, ahead, same = (s2.enter_context(nc.sbuf_tensor(g.tag + n, [P, NT], F32)) for n in ("above", "ahead", "same"))
            junk = s2.enter_context(nc.sbuf_tensor(g.tag + "rank_junk", [P, 3, ROWS], F32))
            before = s2.enter_context(nc.sbuf_tensor(g.tag + "before", [P, P], F32))
            ht = s2.enter_context(nc.sbuf_tensor(g.tag + "hidden_t", [P, NF, G], F32))
            block = s2.enter_context(nc.Block(g.tag + "mod_ffn"))

            @block.gpsimd
            def _(pool):
                nc.gpsimd.affine_select(out=before[:, :], in_=g.ones[:, :], compare_op=ALU.is_gt, fill=0.0, base=0,
                                        pattern=[[-1, P]], channel_multiplier=1).then_inc(skip, 1)
                with nc.gpsimd.Fori(0, NT) as t:
                    nc.gpsimd.tensor_tensor(g.x[:, ds(t, 1), :], g.x[:, ds(t, 1), :], g.xn[:, ds(t, 1), :], ALU.add).then_inc(skip, 1)

            @block.tensor
            def _(pe):
                pe.sem_inc(hidden, 4)
                with nc.tensor.Fori(0, ROWS // G) as i:
                    for f in range(NF):
                        pe.wait_ge(active, NF * i + f + 1)
                        for c in range(2):
                            last = nc.tensor.matmul(g.ps[f % 4][:, 0:G], w1[:, c, f * P:(f + 1) * P],
                                                    xnt[:, c, ds(i * G, G)], start=(c == 0), stop=(c == 1))
                        last.then_inc(hidden, 1)
                    for s in range(2):
                        pe.wait_ge(used, 2 * i + s + 1)
                        nc.tensor.matmul(g.ps[4 + s][:, 0:D], g.ones[0:1, :], b2[0:1, :], start=True, stop=False)
                        for f in range(NF):
                            if s == 0:
                                pe.wait_ge(active, NF * i + f + 5)
                            last = nc.tensor.matmul(g.ps[4 + s][:, 0:D], ht[:, f, s * P:(s + 1) * P], w2[:, f, :],
                                                    start=False, stop=(f == NF - 1))
                        last.then_inc(summed, 1)

            @block.scalar
            def _(act):
                act.sem_inc(active, 4)
                act.sem_inc(summed, 2)
                act.sem_inc(used, 2)
                with nc.scalar.Fori(0, ROWS // G) as i:
                    for f in range(NF):
                        act.wait_ge(hidden, NF * i + f + 5)
                        if f == 0:
                            act.wait_ge(summed, 2 * i + 2)
                        nc.scalar.activation(ht[:, f, :], g.ps[f % 4][:, 0:G], ACT.Gelu_apprx_tanh,
                                             bias=b1[:, f:f + 1]).then_inc(active, 1)
                    for s in range(2):
                        act.wait_ge(summed, 2 * i + s + 3)
                        nc.scalar.activation(g.acc[:, ds(2 * i + s, 1), :], g.ps[4 + s][:, 0:D], ACT.Copy).then_inc(used, 1)

            @block.vector
            def _(dve):
                dve.wait_ge(skip, 1)
                n = 0
                for t in range(FULL + 1):
                    for k, (lo, hi, op, to) in enumerate(((0, t * P, ALU.is_ge, ahead), (t * P, NODES, ALU.is_gt, above))):
                        if n >= 3:
                            dve.wait_ge(ranked, n - 2)
                        if hi > lo:
                            nc.vector.tensor_scalar(junk[:, k, lo:hi], srow[:, lo:hi], scores[:, t:t + 1], 0.0, op, ALU.add,
                                                    accum_out=to[:, t:t + 1]).then_inc(ranked, 1)
                        else:
                            nc.vector.memset(to[:, t:t + 1], 0.0).then_inc(ranked, 1)
                        n += 1
                    w = min(P, NODES - t * P)
                    if n >= 3:
                        dve.wait_ge(ranked, n - 2)
                    nc.vector.scalar_tensor_tensor(out=junk[:, 2, 0:w], in0=srow[:, t * P:t * P + w], scalar=scores[:, t:t + 1],
                                                   in1=before[:, 0:w], op0=ALU.is_equal, op1=ALU.mult,
                                                   accum_out=same[:, t:t + 1]).then_inc(ranked, 1)
                    n += 1
                for to in (above, ahead, same):
                    nc.vector.memset(to[:, FULL + 1:NT], 0.0).then_inc(ranked, 1)
                    n += 1
                dve.wait_ge(ranked, n)
                nc.vector.tensor_tensor(above[:, :], above[:, :], ahead[:, :], ALU.add).then_inc(selected, 1)
                dve.wait_ge(selected, 1)
                nc.vector.tensor_tensor(above[:, :], above[:, :], same[:, :], ALU.add).then_inc(selected, 1)
                dve.wait_ge(selected, 2)
                nc.vector.scalar_tensor_tensor(out=gate[:, :], in0=above[:, :], scalar=float(KEEP), in1=scores[:, :],
                                               op0=ALU.is_lt, op1=ALU.mult).then_inc(selected, 1)
                dve.wait_ge(selected, 3)
                dve.wait_ge(skip, NT + 1)
                dve.wait_ge(used, NT + 2)
                with nc.vector.Fori(0, NT) as t:
                    nc.vector.scalar_tensor_tensor(out=g.x[:, ds(t, 1), :], in0=g.acc[:, ds(t, 1), :], scalar=gate[:, ds(t, 1)],
                                                   in1=g.x[:, ds(t, 1), :], op0=ALU.mult, op1=ALU.add)


HEADS, HD = 8, 32
SLOPE = 0.2
CH = 16
CT = ET // CH
CE = CT * P
AW = HEADS + D + HEADS


def layer1_gnn(nc, g, a, table):
    layer_norm(nc, g, None)
    htable = nc.dram_tensor("gat_rows", (ROWS, D), F32).ap()
    stable = nc.dram_tensor("gat_source_scores", (ROWS, HEADS), F32).ap()
    with ExitStack() as stack:
        sb = lambda n, s, d=F32: stack.enter_context(nc.sbuf_tensor(g.tag + n, s, d))
        alpha = sb("alpha", [P, ET, HEADS])
        den = sb("denominator", [P, NT, HEADS])
        gat_features(nc, g, a, htable, stable, alpha)
        edge_softmax(nc, g, a, alpha)
        weighted_sum(nc, g, htable, alpha, den)
        with ExitStack() as s2:
            bias = s2.enter_context(nc.sbuf_tensor(g.tag + "bias", [P, D], F32))
            load_weights(nc, g, "gat_bias", [(bias[:, :], across(a.l1g_bias))])
            step = nc.alloc_semaphore(g.tag + "out_step")
            block = s2.enter_context(nc.Block(g.tag + "gat_out"))
            heads = lambda v: v.rearrange("p t (h d) -> p (t h) d", d=HD)

            @block.vector
            def _(dve):
                nc.vector.tensor_scalar(den[:, :, :], den[:, :, :], 1e-10, None, ALU.max).then_inc(step, 1)
                dve.wait_ge(step, 1)
                nc.vector.reciprocal(den[:, :, :], den[:, :, :]).then_inc(step, 1)
                dve.wait_ge(step, 2)
                nc.vector.tensor_tensor(heads(g.acc[:, :, :]), heads(g.acc[:, :, :]),
                                        den[:, :, :].rearrange("p t h -> p (t h)").unsqueeze(2).to_broadcast([P, NT * HEADS, HD]),
                                        ALU.mult).then_inc(step, 1)
                dve.wait_ge(step, 3)
                nc.vector.tensor_tensor(g.x[:, :, :], g.x[:, :, :], g.acc[:, :, :], ALU.add).then_inc(step, 1)
                dve.wait_ge(step, 4)
                nc.vector.tensor_tensor(g.x[:, :, :], g.x[:, :, :], bias[:, :].unsqueeze(1).to_broadcast([P, NT, D]),
                                        ALU.add).then_inc(step, 1)
                dve.wait_ge(step, 5)


def gat_features(nc, g, a, htable, stable, alpha):
    with ExitStack() as stack:
        sb = lambda n, s, d=F32: stack.enter_context(nc.sbuf_tensor(g.tag + n, s, d))
        wt, w, acol, blockd = sb("w_t", [P, 2, AW]), sb("w", [P, 2, D]), sb("a_cols", [P, 4]), sb("a_blocks", [P, 2, 2 * HEADS])
        hs = sb("h_nodes", [P, NT, AW])
        edge_w = sb("edge_w", [4, D])
        load_weights(nc, g, "gat", [(wt[:, :, HEADS:HEADS + D], rows_in(a.l1g_w_t)), (w[:, :, :], rows_in(a.l1g_w)),
                                    (acol[:, 0:2], a.l1g_a_src_cols), (acol[:, 2:4], a.l1g_a_dst_cols),
                                    (edge_w[0:3, :], a.l1g_edge_w_t), (edge_w[3:4, :], a.l1g_edge_b)])
        with ExitStack() as s2:
            sem = lambda n: nc.alloc_semaphore(g.tag + n)
            spread, masked, folded, placed = sem("a_spread"), sem("a_masked"), sem("a_folded"), sem("a_placed")
            block = s2.enter_context(nc.Block(g.tag + "fold_scores"))

            @block.vector
            def _(dve):
                for c in range(2):
                    for k in range(2):
                        nc.vector.tensor_scalar(blockd[:, c, k * HEADS:(k + 1) * HEADS], g.ones[:, 0:HEADS],
                                                acol[:, 2 * k + c:2 * k + c + 1], None, ALU.mult).then_inc(spread, 1)
                dve.wait_ge(folded, 1)
                for c in range(2):
                    nc.vector.tensor_copy(wt[:, c, 0:HEADS], g.ps[c][:, 0:HEADS]).then_inc(placed, 1)
                    nc.vector.tensor_copy(wt[:, c, HEADS + D:AW], g.ps[c][:, HEADS:2 * HEADS]).then_inc(placed, 1)
                dve.wait_ge(placed, 4)

            @block.gpsimd
            def _(pool):
                pool.wait_ge(spread, 4)
                for c in range(2):
                    v = blockd[:, c, :].rearrange("p (k h) -> p k h", k=2)
                    nc.gpsimd.affine_select(out=v, in_=v, compare_op=ALU.is_ge, fill=0.0, base=c * P,
                                            pattern=[[0, 2], [-HD, HEADS]], channel_multiplier=1).then_inc(masked, 1)
                pool.wait_ge(masked, 2)
                for c in range(2):
                    v = blockd[:, c, :].rearrange("p (k h) -> p k h", k=2)
                    nc.gpsimd.affine_select(out=v, in_=v, compare_op=ALU.is_ge, fill=0.0, base=HD - 1 - c * P,
                                            pattern=[[0, 2], [HD, HEADS]], channel_multiplier=-1).then_inc(masked, 1)

            @block.tensor
            def _(pe):
                pe.wait_ge(masked, 4)
                for m in range(2):
                    for c in range(2):
                        last = nc.tensor.matmul(g.ps[m][:, 0:2 * HEADS], w[:, c, m * P:(m + 1) * P], blockd[:, c, :],
                                                start=(c == 0), stop=(c == 1))
                last.then_inc(folded, 1)

        project(nc, g, "gat_h", [wt], None, AW,
                [("pool", lambda out, t: nc.gpsimd.tensor_copy(out, g.xn[:, ds(t, 1), :]))],
                lambda dve, bank, t, s: nc.vector.tensor_copy(hs[:, ds(t, 1), :], bank))
        with ExitStack() as s2:
            stored = nc.alloc_semaphore(g.tag + "h_stored")
            block = s2.enter_context(nc.Block(g.tag + "store_h"))

            @block.sync
            def _(sp):
                sp.dma_start(htable.rearrange("(t p) d -> p t d", p=P), hs[:, :, HEADS:HEADS + D]).then_inc(stored, 16)
                sp.dma_start(stable.rearrange("(t p) d -> p t d", p=P), hs[:, :, 0:HEADS]).then_inc(stored, 16)
                sp.wait_ge(stored, 32)
        edge_scores(nc, g, a, hs, edge_w, stable, alpha)


def edge_scores(nc, g, a, hs, edge_w, stable, alpha):
    with ExitStack() as stack:
        sem = lambda n: nc.alloc_semaphore(g.tag + "s_" + n)
        gathered = [sem(f"gathered{u}") for u in range(U)]
        attrs = [sem(f"attrs{h}") for h in range(2)]
        copied, claimed, hot, looked, encoded, relued, based, mixed, reduced = (sem(n) for n in (
            "idx_copied", "claimed", "hot", "looked_up", "encoded", "relued", "based", "mixed", "reduced"))
        sb = lambda n, s, d=F32: stack.enter_context(nc.sbuf_tensor(g.tag + "s_" + n, s, d))
        idx, rows = sb("idx", [P, U], I32), sb("rows", [P, U, HEADS])
        dst, onehot_t = sb("dst_across", [P, 2, H * P], I32), sb("onehot_t", [P, 4, 2, P])
        enc, mix, edge_attr = sb("enc", [P, 4, D]), sb("mix", [P, 2, D]), sb("edge_attr", [4, 2, H * P])
        base_score = sb("base_score", [P, ET, HEADS])
        block = stack.enter_context(nc.Block(g.tag + "edge_scores"))
        hflat = hs[:, :, :].rearrange("p t d -> p (t d)")

        @block.gpsimd
        def _(pool):
            gather_sources(nc, g, pool, stable, rows, idx, copied, based, claimed, gathered)

        @block.sync
        def _(sp):
            with nc.sync.Fori(0, ET // U) as i:
                for h in range(2):
                    sp.wait_ge(mixed, U * i + (h + 1) * H)
                    sp.dma_start(edge_attr[:, h, :], a.edge_attr_t[:, ds((2 * i + h) * (H * P), H * P)]).then_inc(attrs[h], 16)
                    sp.dma_start(dst[:, h, :], a.dst_row[ds((2 * i + h) * (H * P) + 1, H * P)]
                                 .rearrange("(o n) -> o n", o=1).to_broadcast([P, H * P])).then_inc(attrs[h], 16)

        @block.tensor
        def _(pe):
            window = [nc.tensor.alloc_register(g.tag + f"pe_window{u}") for u in range(8)]
            pe.sem_inc(looked, 4)
            pe.sem_inc(encoded, 2)
            with nc.tensor.Fori(0, ET // U) as i:
                for u in range(U):
                    n = U * i + u
                    if u % 8 == 0:
                        nc.tensor.reg_load(window, g.window[0:1, ds(U * i + u, 8)])
                    if u % H == 0:
                        pe.wait_ge(attrs[u // H], 32 * (i + 1))
                    pe.wait_ge(relued, n + 1)
                    nc.tensor.matmul(g.ps[u % 4][:, 0:D], edge_attr[:, u // H, u % H * P:(u % H + 1) * P], edge_w[:, :],
                                     start=True, stop=True).then_inc(encoded, 1)
                    w = nc.tensor.snap(window[u % 8], min_val=0, max_val=NT - 2)
                    pe.wait_ge(hot, n + 1)
                    pe.wait_ge(based, n + U - 3)
                    for k in range(2):
                        last = nc.tensor.matmul(g.ps[4 + u % 4][:, 0:D + HEADS], onehot_t[:, u % 4, k, :],
                                                hflat[:, ds(w * AW + (k * AW + HEADS), D + HEADS)], start=(k == 0), stop=(k == 1))
                    last.then_inc(looked, 1)

        @block.scalar
        def _(act):
            act.sem_inc(relued, 4)
            with nc.scalar.Fori(0, ET // U) as i:
                for u in range(U):
                    if u % H == 0:
                        h = u // H
                        act.wait_ge(based, U * i + (h + 1) * H)
                        nc.scalar.activation(idx[:, h * H:(h + 1) * H], g.srcc[:, ds(U * i + h * H, H)], ACT.Copy).then_inc(copied, 1)
                    n = U * i + u
                    act.wait_ge(encoded, n + 3)
                    act.wait_ge(mixed, n + U - 3)
                    nc.scalar.activation(enc[:, u % 4, :], g.ps[u % 4][:, 0:D], ACT.Relu).then_inc(relued, 1)

        @block.vector
        def _(dve):
            window = [nc.vector.alloc_register(g.tag + f"dve_window{u}") for u in range(8)]
            dve.sem_inc(based, U)
            dve.sem_inc(mixed, U)
            dve.sem_inc(reduced, 2)

            def use(i, n, u):
                dve.wait_ge(looked, n + 5)
                dve.wait_ge(relued, n + 5)
                dve.wait_ge(reduced, n + 1)
                nc.vector.tensor_tensor(mix[:, u % 2, :], g.ps[4 + u % 4][:, 0:D], enc[:, u % 4, :], ALU.mult).then_inc(mixed, 1)
                dve.wait_ge(gathered[u], 16 * (i + 1))
                nc.vector.tensor_tensor(base_score[:, ds(n, 1), :], g.ps[4 + u % 4][:, D:D + HEADS].unsqueeze(1),
                                        rows[:, u, 0:HEADS].unsqueeze(1), ALU.add).then_inc(based, 1)
                dve.wait_ge(mixed, n + U + 1)
                nc.vector.tensor_reduce(alpha[:, ds(n, 1), :], mix[:, u % 2, :].rearrange("p (o h d) -> p o h d", o=1, d=HD),
                                        AX.X, ALU.add).then_inc(reduced, 1)

            def build(i, n, u, w):
                if u % H == 0:
                    dve.wait_ge(attrs[u // H], 32 * (i + 1))
                if isinstance(n, int):
                    if n >= 4:
                        dve.wait_ge(looked, n + 1)
                else:
                    dve.wait_ge(looked, n + 1)
                nc.vector.tensor_tensor(onehot_t[:, u % 4, :, :], dst[:, u // H, u % H * P:(u % H + 1) * P].unsqueeze(1).to_broadcast([P, 2, P]),
                                        g.node_id[:, ds(w, 2)].unsqueeze(2).to_broadcast([P, 2, P]), ALU.is_equal).then_inc(hot, 1)

            LAG = 2
            def windows(i, h):
                nc.vector.reg_load(window, g.window[0:1, ds(U * i + h * H + LAG, 8)])
            nc.vector.reg_load(window, g.window[0:1, 0:8])
            for u in range(LAG):
                build(0, u, u, nc.vector.snap(window[u], min_val=0, max_val=NT - 2))

            def round(i, last=False):
                for u in range(U):
                    if u % 8 == 0 and not (last and u == 8):
                        windows(i, u // 8)
                    if last and u == 8:
                        nc.vector.reg_load(window[0:6], g.window[0:1, ET - 6:ET])
                    m = u + LAG
                    if not (last and m >= U):
                        build(i + m // U, U * i + m, m % U, nc.vector.snap(window[u % 8], min_val=0, max_val=NT - 2))
                    use(i, U * i + u, u)
            with nc.vector.Fori(0, ET // U - 1) as i:
                round(i)
            round(ET // U - 1, last=True)
            dve.wait_ge(reduced, ET + 2)
            dve.wait_ge(based, ET + U)
            nc.vector.tensor_tensor(alpha[:, :, :], alpha[:, :, :], base_score[:, :, :], ALU.add).then_inc(reduced, 1)
            dve.wait_ge(reduced, ET + 3)


def edge_softmax(nc, g, a, alpha):
    BIG = 1e30
    by_chunk = alpha[:, :, :].rearrange("p (c i) h -> p i c h", c=CH)
    by_chunk4 = alpha[:, :, :].rearrange("p (c i) h -> p c i h", c=CH)
    with ExitStack() as stack:
        sem = lambda n: nc.alloc_semaphore(g.tag + "m_" + n)
        sb = lambda n, s, d=F32: stack.enter_context(nc.sbuf_tensor(g.tag + n, s, d))
        dst_loaded, turned, placed, step, diff, ends, wide, cols, expd, back, home = (sem(n) for n in (
            "dst", "turned", "placed", "step", "diff", "ends", "wide", "cols", "exp", "back", "home"))
        ordered = sb("ordered", [P, CT, CH * HEADS])
        dst = sb("dst_chunks", [P, CE + 2], I32)
        score, fwd, bwd = sb("score_t", [P, CE]), sb("fwd", [P, CE]), sb("bwd", [P, CE])
        fresh, fresh_b = g.acct[:, 0, :], g.acct[:, 1, :]
        edge, row = sb("chunk_edge", [P, 4]), sb("chunk_edge_row", [1, 4 * P])
        dist, same, before = sb("dist", [P, P], I32), sb("same_head", [P, P], I32), sb("chunk_mask", [P, 2, P])
        cand, cand2, carry, same_f, dist_f = sb("cand", [P, 2, P]), sb("cand2", [P, 2, P]), sb("carry", [P, 2]), sb("same_f", [P, P]), sb("dist_f", [P, P])
        block = stack.enter_context(nc.Block(g.tag + "edge_softmax"))
        groups = [(q, min(4, CT - q)) for q in range(0, CT, 4)]

        @block.sync
        def _(sp):
            for c in range(CH):
                sp.dma_start(dst[c * HEADS:(c + 1) * HEADS, :],
                             a.dst_row[c * CE:c * CE + CE + 2].rearrange("(o n) -> o n", o=1).to_broadcast([HEADS, CE + 2])).then_inc(dst_loaded, 16)

        @block.gpsimd
        def _(pool):
            nc.gpsimd.iota(dist[:, :], [[-1, P]], base=0, channel_multiplier=1).then_inc(diff, 1)

        @block.tensor
        def _(pe):
            pe.wait_ge(ends, 1)
            for k, (q, m) in enumerate(groups):
                if k >= 4:
                    pe.wait_ge(placed, k - 3)
                for i in range(m):
                    last = nc.tensor.transpose(g.ps[k % 4][:, i * P:(i + 1) * P], ordered[:, q + i, :], g.ident[:, :])
                last.then_inc(turned, 1)
            pe.wait_ge(ends, 2)
            for r in range(4):
                last = nc.tensor.transpose(g.ps[4][0:1, r * P:(r + 1) * P], edge[:, r:r + 1], g.ident[:, :])
            last.then_inc(wide, 1)
            pe.wait_ge(ends, 3)
            nc.tensor.matmul(g.ps[5][:, :], g.ones[0:1, :], row[0:1, :], start=True, stop=True).then_inc(wide, 1)
            for k, (q, m) in enumerate(groups):
                pe.wait_ge(expd, k + 1)
                if k >= 4:
                    pe.wait_ge(home, k - 3)
                for i in range(m):
                    last = nc.tensor.transpose(g.ps[k % 4][:, i * P:(i + 1) * P], score[:, (q + i) * P:(q + i + 1) * P], g.ident[:, :])
                last.then_inc(back, 1)

        @block.scalar
        def _(act):
            for k, (q, m) in enumerate(groups):
                act.wait_ge(turned, k + 1)
                nc.scalar.activation(score[:, q * P:(q + m) * P], g.ps[k % 4][:, 0:m * P], ACT.Copy).then_inc(placed, 1)
            for k, (q, m) in enumerate(groups):
                if k == 0:
                    act.wait_ge(step, 18)
                nc.scalar.activation(score[:, q * P:(q + m) * P], score[:, q * P:(q + m) * P], ACT.Exp).then_inc(expd, 1)

        @block.vector
        def _(dve):
            count = [0]

            def done(ins):
                count[0] += 1
                ins.then_inc(step, 1)
                dve.wait_ge(step, count[0])

            prev, cur, nxt = dst[:, 0:CE], dst[:, 1:CE + 1], dst[:, 2:CE + 2]
            flat = fwd[:, :].rearrange("p (t h) -> p t h", h=HEADS)
            done(nc.vector.tensor_scalar(flat, alpha[:, :, :], SLOPE, None, ALU.mult))
            nc.vector.tensor_tensor(ordered[:, :, :].rearrange("p i (c h) -> p c i h", c=CH), by_chunk4,
                                    fwd[:, :].rearrange("p (c i h) -> p c i h", c=CH, h=HEADS), ALU.max).then_inc(ends, 1)
            dve.wait_ge(diff, 1)
            done(nc.vector.tensor_scalar(same[:, :], dist[:, :], 7, None, ALU.bitwise_and))
            done(nc.vector.tensor_scalar(same_f[:, :], same[:, :], 0.0, None, ALU.is_equal))
            done(nc.vector.tensor_copy(dist_f[:, :], dist[:, :]))
            done(nc.vector.scalar_tensor_tensor(out=before[:, 0, :], in0=dist_f[:, :], scalar=0.0, in1=same_f[:, :], op0=ALU.is_gt, op1=ALU.mult))
            done(nc.vector.scalar_tensor_tensor(out=before[:, 1, :], in0=dist_f[:, :], scalar=0.0, in1=same_f[:, :], op0=ALU.is_lt, op1=ALU.mult))
            dve.wait_ge(dst_loaded, 16 * CH)
            done(nc.vector.tensor_tensor(fresh[:, :], cur, prev, ALU.not_equal))
            done(nc.vector.tensor_scalar(fresh[:, :], fresh[:, :], -BIG, None, ALU.mult))
            done(nc.vector.tensor_tensor(fresh_b[:, :], cur, nxt, ALU.not_equal))
            done(nc.vector.tensor_scalar(fresh_b[:, :], fresh_b[:, :], -BIG, None, ALU.mult))
            dve.wait_ge(placed, len(groups))

            def runs(first, last):
                nc.vector.tensor_tensor_scan(fwd[:, :], fresh[:, :], score[:, :], first, ALU.add, ALU.max)
                done(nc.vector.tensor_tensor_scan(bwd[:, ::-1], fresh_b[:, ::-1], score[:, ::-1], last, ALU.add, ALU.max))
            runs(-BIG, -BIG)
            nc.vector.tensor_copy(edge[:, 0:1], fwd[:, CE - 1:CE])
            nc.vector.tensor_copy(edge[:, 1:2], bwd[:, 0:1])
            nc.vector.tensor_copy(edge[:, 2:3], cur[:, CE - 1:CE])
            nc.vector.tensor_copy(edge[:, 3:4], cur[:, 0:1]).then_inc(ends, 1)
            dve.wait_ge(wide, 1)
            nc.vector.tensor_copy(row[:, :], g.ps[4][0:1, :]).then_inc(ends, 1)
            dve.wait_ge(wide, 2)
            at = lambda r: g.ps[5][:, r * P:(r + 1) * P]
            nc.vector.scalar_tensor_tensor(out=cand[:, 0, :], in0=at(2), scalar=edge[:, 3:4], in1=before[:, 0, :], op0=ALU.is_equal, op1=ALU.mult)
            done(nc.vector.scalar_tensor_tensor(out=cand[:, 1, :], in0=at(3), scalar=edge[:, 2:3], in1=before[:, 1, :], op0=ALU.is_equal, op1=ALU.mult))
            done(nc.vector.tensor_tensor(cand2[:, :, :], cand[:, :, :], g.ps[5][:, 0:2 * P].rearrange("p (k n) -> p k n", k=2), ALU.mult))
            done(nc.vector.tensor_scalar(cand[:, :, :], cand[:, :, :], 1.0, BIG, ALU.subtract, ALU.mult))
            done(nc.vector.tensor_tensor(cand[:, :, :], cand[:, :, :], cand2[:, :, :], ALU.add))
            done(nc.vector.tensor_reduce(carry[:, :], cand[:, :, :], AX.X, ALU.max))
            nc.vector.tensor_tensor_scan(fwd[:, :], fresh[:, :], score[:, :], carry[:, 0:1], ALU.add, ALU.max)
            nc.vector.tensor_tensor_scan(bwd[:, ::-1], fresh_b[:, ::-1], score[:, ::-1], carry[:, 1:2], ALU.add, ALU.max).then_inc(step, 1)
            count[0] += 1
            dve.wait_ge(step, count[0])
            nc.vector.tensor_tensor(fwd[:, :], fwd[:, :], bwd[:, :], ALU.max).then_inc(diff, 1)
            dve.wait_ge(diff, 2)
            nc.vector.tensor_tensor(score[:, :], score[:, :], fwd[:, :], ALU.subtract).then_inc(step, 1)
            assert count[0] == 17
            for k, (q, m) in enumerate(groups):
                dve.wait_ge(back, k + 1)
                nc.vector.tensor_copy(by_chunk[:, q:q + m], g.ps[k % 4][:, 0:m * P].rearrange("p (i c h) -> p i c h", i=m, c=CH)).then_inc(home, 1)
            dve.wait_ge(home, len(groups))


def weighted_sum(nc, g, htable, weight, den):
    with ExitStack() as stack:
        sem = lambda n: nc.alloc_semaphore(g.tag + "w_" + n)
        gathered = [sem(f"gathered{u}") for u in range(U)]
        copied, claimed, weighed, weights, summed, added, cleared = (sem(n) for n in (
            "idx_copied", "claimed", "weighed", "weights", "summed", "added", "cleared"))
        sb = lambda n, s, d=F32: stack.enter_context(nc.sbuf_tensor(g.tag + "w_" + n, s, d))
        idx, rows = sb("idx", [P, U], I32), sb("rows", [P, U, D])
        onehot, part = sb("onehot", [P, 4, P]), sb("part", [P, 4, D + HEADS])
        den_t = sb("den_turned", [HEADS, ROWS])
        with ExitStack() as s2:
            block = s2.enter_context(nc.Block(g.tag + "weighted_sum"))

            @block.gpsimd
            def _(pool):
                gather_sources(nc, g, pool, htable, rows, idx, copied, weighed, claimed, gathered)

            @block.tensor
            def _(pe):
                pe.sem_inc(summed, 4)
                with nc.tensor.Fori(0, ET // U) as i:
                    for u in range(U):
                        n = U * i + u
                        pe.wait_ge(weights, n + 1)
                        pe.wait_ge(weighed, n + U + 1)
                        pe.wait_ge(added, n + 1)
                        nc.tensor.matmul(g.ps[4 + u % 4][0:HEADS, 0:P], part[:, u % 4, D:D + HEADS], onehot[:, u % 4, :], start=True, stop=True)
                        for c in range(2):
                            last = nc.tensor.matmul(g.ps[u % 4][:, c * P:(c + 1) * P], part[:, u % 4, c * P:(c + 1) * P],
                                                    onehot[:, u % 4, :], start=True, stop=True)
                        last.then_inc(summed, 1)

            @block.scalar
            def _(act):
                with nc.scalar.Fori(0, ET // U) as i:
                    for u in range(U):
                        if u % H == 0:
                            h = u // H
                            act.wait_ge(weighed, U * i + (h + 1) * H)
                            nc.scalar.activation(idx[:, h * H:(h + 1) * H], g.srcc[:, ds(U * i + h * H, H)], ACT.Copy).then_inc(copied, 1)
                        act.wait_ge(summed, U * i + u + 1)
                        nc.scalar.activation(part[:, u % 4, D:D + HEADS].unsqueeze(1), weight[:, ds(U * i + u, 1), :], ACT.Copy).then_inc(weights, 1)

            @block.vector
            def _(dve):
                base = [nc.vector.alloc_register(g.tag + f"base{u}") for u in range(8)]
                nc.vector.memset(g.acct[:, :, :], 0.0).then_inc(cleared, 1)
                nc.vector.memset(den_t[:, :], 0.0).then_inc(cleared, 1)
                dve.wait_ge(cleared, 2)
                dve.sem_inc(weighed, U)
                dve.sem_inc(added, 4)

                def weigh(i, n, u):
                    if not (isinstance(n, int) and n < 4):
                        dve.wait_ge(summed, n + 1)
                    nc.vector.tensor_scalar(onehot[:, u % 4, :], g.iota[:, 0:P], g.local[:, ds(n, 1)], None, ALU.is_equal)
                    dve.wait_ge(gathered[u], 16 * (i + 1))
                    nc.vector.tensor_tensor(part[:, u % 4, 0:D].rearrange("p (h d) -> p h d", d=HD),
                                            rows[:, u, :].rearrange("p (h d) -> p h d", d=HD),
                                            weight[:, ds(n, 1), :].rearrange("p o h -> p (o h)").unsqueeze(2).to_broadcast([P, HEADS, HD]),
                                            ALU.mult).then_inc(weighed, 1)

                def collect(n, u, b):
                    dve.wait_ge(summed, n + 5)
                    dve.wait_ge(added, n + 4)
                    nc.vector.tensor_tensor(den_t[:, ds(b, P)], den_t[:, ds(b, P)], g.ps[4 + u % 4][0:HEADS, 0:P], ALU.add)
                    nc.vector.tensor_tensor(g.acct[:, :, ds(b, P)], g.acct[:, :, ds(b, P)],
                                            g.ps[u % 4][:, 0:D].rearrange("p (c n) -> p c n", c=2), ALU.add).then_inc(added, 1)

                LAG = 2
                for u in range(LAG):
                    weigh(0, u, u)

                def round(i, last=False):
                    for u in range(U):
                        if u % 8 == 0:
                            nc.vector.reg_load(base, g.dstc[0:1, ds(U * i + u, 8)])
                        m = u + LAG
                        if not (last and m >= U):
                            weigh(i + m // U, U * i + m, m % U)
                        collect(U * i + u, u, nc.vector.snap(base[u % 8], min_val=0, max_val=ROWS - P))
                with nc.vector.Fori(0, ET // U - 1) as i:
                    round(i)
                round(ET // U - 1, last=True)
        turn_sums(nc, g, "w", 2, den_t, den)


E = 8


class Route:
    pass


def route(nc, g, name, logits, picks, capacity, slots, r, clear, meanwhile=None):
    with ExitStack() as stack:
        sem = lambda n: nc.alloc_semaphore(g.tag + name + n)
        sb = lambda n, s, d=F32: stack.enter_context(nc.sbuf_tensor(g.tag + name + n, s, d))
        step, masks, counted, shifted, expd, zeroed, zero = (sem(n) for n in (
            "_step", "_masks", "_counted", "_shifted", "_exp", "_zeroed", "_zero"))
        wide = [P, NT, E]
        rev, valid, number, upto = sb("_rev", [P, E]), sb("_valid", [P, NT]), sb("_number", [P, NT]), sb("_upto", [P, P])
        best, first = [sb(f"_best{k}", [P, NT]) for k in range(2)], sb("_first", [P, NT])
        pick = [sb(f"_pick{k}", wide) for k in range(picks)]
        tmp, rest, every, cum, totals, incl = sb("_tmp", wide), sb("_rest", wide), sb("_every", wide), sb("_cum", wide), sb("_totals", wide), sb("_incl", wide)
        zeros, ni, nf, ends = sb("_zeros", [P, NT]), sb("_ni", [P, E], I32), sb("_nf", [P, E]), sb("_ends", [P, E])
        start, rowf, flag, place, tile_no, owner = sb("_start", [P, E]), sb("_rowf", [P, NT]), sb("_flag", [P, NT]), sb("_place", [P, NT]), sb("_tile_no", [1, 64]), sb("_owner", [1, 64])
        expt, z = sb("_expt", wide), sb("_z", [P, NT])
        block = stack.enter_context(nc.Block(g.tag + name))
        per_node = lambda v: v[:, :].unsqueeze(2).to_broadcast(wide)
        per_expert = lambda v: v[:, :].unsqueeze(1).to_broadcast(wide)

        @block.sync
        def _(sp):
            dram, zero_rows, n = clear
            sp.wait_ge(zero, 1)
            for k in range(n):
                sp.dma_start(dram[k], zero_rows).then_inc(zeroed, 16)
            if meanwhile is not None:
                meanwhile(sp)
            sp.wait_ge(zeroed, 16 * n)

        @block.gpsimd
        def _(pool):
            nc.gpsimd.memset(clear[1], 0.0).then_inc(zero, 1)
            nc.gpsimd.iota(rev[:, :], [[-1, E]], base=E, channel_multiplier=0, allow_small_or_imprecise_dtypes=True).then_inc(masks, 1)
            nc.gpsimd.iota(number[:, :], [[P, NT]], base=0, channel_multiplier=1, allow_small_or_imprecise_dtypes=True).then_inc(masks, 1)
            nc.gpsimd.iota(tile_no[:, :], [[1, 64]], base=0, channel_multiplier=0, allow_small_or_imprecise_dtypes=True).then_inc(masks, 1)
            nc.gpsimd.affine_select(out=upto[:, :], in_=g.ones[:, :], compare_op=ALU.is_ge, fill=0.0, base=0,
                                    pattern=[[1, P]], channel_multiplier=-1).then_inc(masks, 1)
            nc.gpsimd.affine_select(out=valid[:, :], in_=g.ones[:, 0:NT], compare_op=ALU.is_ge, fill=0.0, base=NODES - 1,
                                    pattern=[[-P, NT]], channel_multiplier=-1).then_inc(masks, 1)

        @block.tensor
        def _(pe):
            pe.wait_ge(counted, 1)
            nc.tensor.matmul(g.ps[0][:, 0:NT * E], upto[:, :], every[:, :, :].rearrange("p t e -> p (t e)"), start=True, stop=True)
            nc.tensor.matmul(g.ps[1][:, 0:NT * E], g.ones[:, :], every[:, :, :].rearrange("p t e -> p (t e)"), start=True, stop=True).then_inc(counted, 1)

        @block.scalar
        def _(act):
            act.wait_ge(shifted, 1)
            if picks == 1:
                nc.scalar.activation(expt[:, :, :], tmp[:, :, :], ACT.Exp).then_inc(expd, 1)
            else:
                nc.scalar.activation(z[:, :], z[:, :], ACT.Exp).then_inc(expd, 1)

        @block.vector
        def _(dve):
            count = [0]

            def done(ins):
                count[0] += 1
                ins.then_inc(step, 1)
                dve.wait_ge(step, count[0])

            dve.wait_ge(masks, 5)
            done(nc.vector.memset(zeros[:, :], 0.0))
            left = logits
            for k in range(picks):
                done(nc.vector.tensor_reduce(best[k][:, :], left[:, :, :], AX.X, ALU.max))
                done(nc.vector.tensor_tensor(tmp[:, :, :], left[:, :, :], per_node(best[k]), ALU.is_equal))
                done(nc.vector.tensor_tensor(tmp[:, :, :], tmp[:, :, :], per_expert(rev), ALU.mult))
                done(nc.vector.tensor_reduce(first[:, :], tmp[:, :, :], AX.X, ALU.max))
                done(nc.vector.tensor_tensor(pick[k][:, :, :], per_expert(rev), per_node(first), ALU.is_equal))
                if k + 1 < picks:
                    done(nc.vector.scalar_tensor_tensor(out=rest[:, :, :], in0=pick[k][:, :, :], scalar=-1e30, in1=left[:, :, :],
                                                        op0=ALU.mult, op1=ALU.add))
                    left = rest
                done(nc.vector.tensor_tensor(pick[k][:, :, :], pick[k][:, :, :], per_node(valid), ALU.mult))
            if picks == 2:
                done(nc.vector.tensor_tensor(every[:, :, :], pick[0][:, :, :], pick[1][:, :, :], ALU.add))
                nc.vector.tensor_tensor(z[:, :], best[1][:, :], best[0][:, :], ALU.subtract).then_inc(shifted, 1)
            else:
                done(nc.vector.tensor_copy(every[:, :, :], pick[0][:, :, :]))
                nc.vector.tensor_tensor(tmp[:, :, :], logits[:, :, :], per_node(best[0]), ALU.subtract).then_inc(shifted, 1)
            dve.sem_inc(counted, 1)
            dve.wait_ge(expd, 1)
            if picks == 1:
                done(nc.vector.tensor_reduce(z[:, :], expt[:, :, :], AX.X, ALU.add))
                done(nc.vector.reciprocal(r.weight[:, 0, :], z[:, :]))
            else:
                done(nc.vector.tensor_scalar(flag[:, :], z[:, :], 1.0, None, ALU.add))
                done(nc.vector.reciprocal(r.weight[:, 0, :], flag[:, :]))
                done(nc.vector.tensor_tensor(r.weight[:, 1, :], r.weight[:, 0, :], z[:, :], ALU.mult))
            dve.wait_ge(counted, 2)
            done(nc.vector.tensor_copy(totals[:, :, :], g.ps[1][:, 0:NT * E].rearrange("p (t e) -> p t e", e=E)))
            for e in range(E):
                last = nc.vector.tensor_tensor_scan(incl[:, :, e], totals[:, :, e], zeros[:, :], 0.0, ALU.add, ALU.add)
            done(last)
            done(nc.vector.tensor_tensor(cum[:, :, :], incl[:, :, :], totals[:, :, :], ALU.subtract))
            done(nc.vector.tensor_tensor(cum[:, :, :], cum[:, :, :], g.ps[0][:, 0:NT * E].rearrange("p (t e) -> p t e", e=E), ALU.add))
            if capacity:
                done(nc.vector.tensor_scalar(start[:, :], rev[:, :], -float(slots), float(E * slots), ALU.mult, ALU.add))
            else:
                done(nc.vector.tensor_scalar(ni[:, :], incl[:, NT - 1, :], float(P - 1), None, ALU.add))
                done(nc.vector.tensor_scalar(ni[:, :], ni[:, :], 7, None, ALU.logical_shift_right))
                done(nc.vector.tensor_copy(nf[:, :], ni[:, :]))
                done(nc.vector.tensor_tensor_scan(ends[:, :], nf[:, :], zeros[:, 0:E], 0.0, ALU.add, ALU.add))
                done(nc.vector.tensor_tensor(start[:, :], ends[:, :], nf[:, :], ALU.subtract))
                done(nc.vector.tensor_scalar(start[:, :], start[:, :], float(P), None, ALU.mult))
                done(nc.vector.memset(owner[:, :], 0.0))
                for e in range(E - 1):
                    done(nc.vector.scalar_tensor_tensor(out=owner[:, :], in0=tile_no[:, :], scalar=ends[0:1, e:e + 1], in1=owner[:, :],
                                                        op0=ALU.is_ge, op1=ALU.add))
                done(nc.vector.tensor_copy(r.expert[:, :], owner[:, 0:r.expert.shape[1]]))
            for k in range(picks):
                done(nc.vector.tensor_tensor(tmp[:, :, :], pick[k][:, :, :], cum[:, :, :], ALU.mult))
                done(nc.vector.tensor_reduce(rowf[:, :], tmp[:, :, :], AX.X, ALU.add))
                done(nc.vector.tensor_tensor(tmp[:, :, :], pick[k][:, :, :], per_expert(start), ALU.mult))
                done(nc.vector.tensor_reduce(place[:, :], tmp[:, :, :], AX.X, ALU.add))
                if capacity:
                    done(nc.vector.tensor_scalar(flag[:, :], rowf[:, :], float(capacity), None, ALU.is_le))
                    done(nc.vector.tensor_tensor(r.weight[:, k, :], r.weight[:, k, :], flag[:, :], ALU.mult))
                    done(nc.vector.tensor_tensor(flag[:, :], flag[:, :], valid[:, :], ALU.mult))
                else:
                    done(nc.vector.tensor_copy(flag[:, :], valid[:, :]))
                done(nc.vector.tensor_scalar(z[:, :], rowf[:, :], float(capacity or ROWS * 2), -1.0, ALU.min, ALU.add))
                done(nc.vector.tensor_tensor(z[:, :], z[:, :], place[:, :], ALU.add))
                done(nc.vector.tensor_scalar(r.read[:, k, :], z[:, :], 0.0, None, ALU.max))
                done(nc.vector.tensor_scalar(rowf[:, :], rowf[:, :], -1.0, None, ALU.add))
                done(nc.vector.tensor_tensor(rowf[:, :], rowf[:, :], place[:, :], ALU.add))
                done(nc.vector.tensor_tensor(rowf[:, :], rowf[:, :], flag[:, :], ALU.mult))
                done(nc.vector.tensor_scalar(flag[:, :], flag[:, :], -1.0, 1.0, ALU.mult, ALU.add))
                done(nc.vector.tensor_scalar(place[:, :], number[:, :], float(r.spare + k * ROWS), None, ALU.add))
                done(nc.vector.tensor_tensor(place[:, :], place[:, :], flag[:, :], ALU.mult))
                done(nc.vector.tensor_tensor(r.write[:, k, :], rowf[:, :], place[:, :], ALU.add))


def new_route(nc, g, stack, name, picks, rows):
    r = Route()
    sb = lambda n, s, d=F32: stack.enter_context(nc.sbuf_tensor(g.tag + name + n, s, d))
    r.weight, r.read, r.write = sb("_weight", [P, picks, NT]), sb("_read", [P, picks, NT], I32), sb("_write", [P, picks, NT], I32)
    r.expert, r.spare, r.rows = sb("_expert", [1, rows // P], I32), rows, rows
    r.sorted = nc.dram_tensor(g.tag + name + "_sorted", (rows + picks * ROWS, D), F32).ap()
    r.result = nc.dram_tensor(g.tag + name + "_result", (rows, D), F32).ap()
    return r


def clear_rows(r, zeros):
    n = zeros.shape[1] // D
    v = r.sorted[0:r.rows, :].rearrange("(k p j) d -> k p (j d)", p=P, j=n)
    return v, zeros, r.rows // (P * n)


def send_rows(nc, g, name, r, picks, src):
    with ExitStack() as stack:
        sent = nc.alloc_semaphore(g.tag + name + "_sent")
        block = stack.enter_context(nc.Block(g.tag + name + "_send"))

        @block.gpsimd
        def _(pool):
            for k in range(picks):
                for t in range(NT):
                    nc.gpsimd.indirect_dma_start(
                        r.sorted, bass.IndirectOffsetOnAxis(ap=r.write[:, k, t:t + 1].bitcast(U32), axis=0),
                        src[:, t, :], None).then_inc(sent, 16)
            pool.wait_ge(sent, 16 * NT * picks)


def collect_rows(nc, g, name, r, picks, out):
    S = 8
    with ExitStack() as stack:
        sem = lambda n: nc.alloc_semaphore(g.tag + name + n)
        back = [sem(f"_back{s}") for s in range(S)]
        used = sem("_used")
        rows = stack.enter_context(nc.sbuf_tensor(g.tag + name + "_back_rows", [P, S, D], F32))
        block = stack.enter_context(nc.Block(g.tag + name + "_collect"))
        order = [(t, k) for t in range(NT) for k in range(picks)]

        @block.gpsimd
        def _(pool):
            for n, (t, k) in enumerate(order):
                if n >= S:
                    pool.wait_ge(used, n - S + 1)
                nc.gpsimd.indirect_dma_start(
                    rows[:, n % S, :], None, r.result,
                    bass.IndirectOffsetOnAxis(ap=r.read[:, k, t:t + 1].bitcast(U32), axis=0)).then_inc(back[n % S], 16)

        @block.vector
        def _(dve):
            for n, (t, k) in enumerate(order):
                dve.wait_ge(back[n % S], 16 * (n // S + 1))
                if k:
                    dve.wait_ge(used, n)
                if out is None:
                    nc.vector.tensor_scalar(g.acc[:, t, :], rows[:, n % S, :], r.weight[:, k, t:t + 1], None, ALU.mult).then_inc(used, 1)
                else:
                    nc.vector.scalar_tensor_tensor(out=out[:, t, :], in0=rows[:, n % S, :], scalar=r.weight[:, k, t:t + 1],
                                                   in1=out[:, t, :], op0=ALU.mult, op1=ALU.add).then_inc(used, 1)
            dve.wait_ge(used, len(order))


def gate_logits(nc, g, name, src, wg, bg, logits, meanwhile=None):
    project(nc, g, name, [wg], bg, E,
            [("pool", lambda out, t: nc.gpsimd.tensor_copy(out, src[:, ds(t, 1), :]))],
            lambda dve, bank, t, s: nc.vector.tensor_copy(logits[:, ds(t, 1), :], bank), meanwhile=meanwhile)


CAP, SLOTS, H1 = -(-5 * NODES // (4 * E)), 512, 1024


def layer1_ffn(nc, g, a, table):
    layer_norm(nc, g, None)
    with ExitStack() as stack:
        sb = lambda n, s, d=F32: stack.enter_context(nc.sbuf_tensor(g.tag + n, s, d))
        wg, bg, logits = sb("gate_w", [P, 2, E]), sb("gate_b", [1, E]), sb("logits", [P, NT, E])
        r = new_route(nc, g, stack, "sw", 1, E * SLOTS)
        load_weights(nc, g, "sw", [(wg[:, :, :], rows_in(a.l1f_gate_w)), (bg[:, :], a.l1f_gate_b)])
        gate_logits(nc, g, "sw_gate", g.xn, wg, bg[0:1, :], logits)
        with ExitStack() as s2:
            zeros = s2.enter_context(nc.sbuf_tensor(g.tag + "zero_rows", [P, 8 * D], F32))
            route(nc, g, "sw_route", logits, 1, CAP, SLOTS, r, clear_rows(r, zeros[:, :]))
        send_rows(nc, g, "sw", r, 1, g.xn)
        NF, NR = H1 // P, SLOTS // P
        with ExitStack() as s2:
            sem = lambda n: nc.alloc_semaphore(g.tag + "e_" + n)
            sb2 = lambda n, s: s2.enter_context(nc.sbuf_tensor(g.tag + "e_" + n, s, F32))
            loaded = [sem(f"loaded{s}") for s in range(2)]
            stored = [sem(f"stored{s}") for s in range(2)]
            turned, xt_ready, hidden, active, product, copied, freed = (
                sem(n) for n in ("turned", "xt_ready", "hidden", "active", "product", "copied", "freed"))
            w1, w2, b1, b2 = sb2("w1", [P, 2, 2, H1]), sb2("w2", [P, 2, NF, D]), sb2("b1", [P, 2, NF]), sb2("b2", [1, 2, D])
            rows, xt, ht, y = sb2("rows", [P, 2, NR, D]), sb2("xt", [P, 2, SLOTS]), sb2("ht", [P, NF, SLOTS]), sb2("y", [P, 2, NR, D])
            block = s2.enter_context(nc.Block(g.tag + "experts"))

            @block.sync
            def _(sp):
                with nc.sync.Fori(0, E // 2) as i:
                    for s in range(2):
                        e = 2 * i + s
                        sp.wait_ge(product, NR * e + NR)
                        for dst, src in ((rows[:, s, :, :], r.sorted[ds(e * SLOTS, SLOTS), :].rearrange("(r p) d -> p r d", p=P)),
                                         (w1[:, s, :, :], a.l1f_w1[ds(e, 1), :, :].rearrange("e (c p) h -> p (e c) h", p=P)),
                                         (b1[:, s, :], a.l1f_b1_cols[:, ds(e * NF, NF)]),
                                         (w2[:, s, :, :], a.l1f_w2[ds(e, 1), :, :].rearrange("e (c p) h -> p (e c) h", p=P)),
                                         (b2[:, s, :], a.l1f_b2[ds(e, 1), :])):
                            sp.dma_start(dst, src).then_inc(loaded[s], 16)

            @block.tensor
            def _(pe):
                pe.sem_inc(product, 2 * NR)
                pe.sem_inc(hidden, 4)
                with nc.tensor.Fori(0, E // 2) as i:
                    for s in range(2):
                        e = 2 * i + s
                        pe.wait_ge(loaded[s], 80 * (i + 1))
                        for c in range(2):
                            pe.wait_ge(xt_ready, 2 * e + c + 1)
                            for n in range(NR):
                                last = nc.tensor.transpose(g.ps[c][:, n * P:(n + 1) * P], rows[:, s, n, c * P:(c + 1) * P], g.ident[:, :])
                            last.then_inc(turned, 1)
                        pe.wait_ge(xt_ready, 2 * e + 4)
                        for f in range(NF):
                            pe.wait_ge(active, NF * e + f + 1)
                            for c in range(2):
                                last = nc.tensor.matmul(g.ps[2 + f % 4][:, :], w1[:, s, c, f * P:(f + 1) * P], xt[:, c, :],
                                                        start=(c == 0), stop=(c == 1))
                            last.then_inc(hidden, 1)
                        for n in range(NR):
                            pe.wait_ge(copied, NR * e + n + 1)
                            nc.tensor.matmul(g.ps[6 + n % 2][:, 0:D], g.ones[0:1, :], b2[0:1, s, :], start=True, stop=False)
                            for f in range(NF):
                                if n == 0:
                                    pe.wait_ge(active, NF * e + f + 5)
                                last = nc.tensor.matmul(g.ps[6 + n % 2][:, 0:D], ht[:, f, n * P:(n + 1) * P], w2[:, s, f, :],
                                                        start=False, stop=(f == NF - 1))
                            last.then_inc(product, 1)

            @block.scalar
            def _(act):
                act.sem_inc(xt_ready, 2)
                act.sem_inc(active, 4)
                with nc.scalar.Fori(0, E // 2) as i:
                    for s in range(2):
                        e = 2 * i + s
                        act.wait_ge(hidden, NF * e + 4)
                        for c in range(2):
                            act.wait_ge(turned, 2 * e + c + 1)
                            nc.scalar.activation(xt[:, c, :], g.ps[c][:, :], ACT.Copy).then_inc(xt_ready, 1)
                        act.wait_ge(product, NR * (e + 2))
                        for f in range(NF):
                            act.wait_ge(hidden, NF * e + f + 5)
                            nc.scalar.activation(ht[:, f, :], g.ps[2 + f % 4][:, :], ACT.Relu, bias=b1[:, s, f:f + 1]).then_inc(active, 1)

            @block.vector
            def _(dve):
                dve.sem_inc(copied, 2)
                dve.sem_inc(freed, 2)
                with nc.vector.Fori(0, E // 2) as i:
                    for s in range(2):
                        dve.wait_ge(freed, 2 * i + s + 1)
                        for n in range(NR):
                            dve.wait_ge(product, NR * (2 * i + s) + n + 2 * NR + 1)
                            nc.vector.tensor_copy(y[:, s, n, :], g.ps[6 + n % 2][:, 0:D]).then_inc(copied, 1)

            @block.gpsimd
            def _(pool):
                with nc.gpsimd.Fori(0, E // 2) as i:
                    for s in range(2):
                        e = 2 * i + s
                        pool.wait_ge(copied, NR * (e + 1) + 2)
                        pool.dma_start(r.result[ds(e * SLOTS, SLOTS), :].rearrange("(r p) d -> p r d", p=P), y[:, s, :, :]).then_inc(stored[s], 16)
                        pool.wait_ge(stored[s], 16 * (i + 1))
                        pool.sem_inc(freed, 1)

        collect_rows(nc, g, "sw", r, 1, None)
        with ExitStack() as s2:
            step = nc.alloc_semaphore(g.tag + "guard_step")
            mask = s2.enter_context(nc.sbuf_tensor(g.tag + "mask", [P, NT * D], mybir.dt.uint8))
            caps = s2.enter_context(nc.sbuf_tensor(g.tag + "caps", [P, 3], F32))
            block = s2.enter_context(nc.Block(g.tag + "guard"))
            y = g.acc[:, :, :].rearrange("p t d -> p (t d)")

            @block.vector
            def _(dve):
                count = [0]

                def done(ins):
                    count[0] += 1
                    ins.then_inc(step, 1)
                    dve.wait_ge(step, count[0])
                BIGGEST = 3.4028234663852886e38
                for k, v in enumerate((1e4, -1e4, 0.0)):
                    done(nc.vector.memset(caps[:, k:k + 1], v))
                for k, (op, v) in enumerate(((ALU.is_gt, BIGGEST), (ALU.is_lt, -BIGGEST))):
                    done(nc.vector.tensor_scalar(mask[:, :], y, v, None, op))
                    done(nc.vector.copy_predicated(y, mask[:, :], caps[:, k:k + 1].to_broadcast([P, NT * D])))
                done(nc.vector.tensor_tensor(mask[:, :], y, y, ALU.not_equal))
                done(nc.vector.copy_predicated(y, mask[:, :], caps[:, 2:3].to_broadcast([P, NT * D])))
                done(nc.vector.tensor_tensor(g.x[:, :, :], g.x[:, :, :], g.acc[:, :, :], ALU.add))


H2 = 512
T2 = (2 * NODES + E * (P - 1)) // P
T2 += T2 % 2


def norm_again(nc, g, gamma, beta, out):
    with ExitStack() as stack:
        sem = lambda n: nc.alloc_semaphore(g.tag + "again_" + n)
        stat, aggr, root, inv, normed, scaled = (sem(n) for n in ("stat", "aggr", "root", "inv", "normed", "scaled"))
        block = stack.enter_context(nc.Block(g.tag + "norm_again"))

        @block.vector
        def _(dve):
            with nc.vector.Fori(0, NT) as t:
                nc.vector.bn_stats(g.stats[:, ds(t, 1), :], g.xn[:, ds(t, 1), :]).then_inc(stat, 1)
            dve.wait_ge(stat, NT)
            for t in range(NT):
                nc.vector.bn_aggr(g.mv[:, t, :], g.stats[:, t, :]).then_inc(aggr, 1)
            dve.wait_ge(root, 1)
            nc.vector.reciprocal(g.rstd[:, :], g.rstd[:, :]).then_inc(inv, 1)
            dve.wait_ge(inv, 1)
            with nc.vector.Fori(0, NT) as t:
                nc.vector.tensor_scalar(out[:, ds(t, 1), :], g.xn[:, ds(t, 1), :], g.mv[:, ds(t, 1), 0],
                                        g.rstd[:, ds(t, 1)], ALU.subtract, ALU.mult).then_inc(normed, 1)
            dve.wait_ge(normed, NT)
            wide = [P, NT, D]
            nc.vector.tensor_tensor(out[:, :, :], out[:, :, :], gamma[:, :].unsqueeze(1).to_broadcast(wide), ALU.mult).then_inc(scaled, 1)
            dve.wait_ge(scaled, 1)
            nc.vector.tensor_tensor(out[:, :, :], out[:, :, :], beta[:, :].unsqueeze(1).to_broadcast(wide), ALU.add).then_inc(scaled, 1)
            dve.wait_ge(scaled, 2)

        @block.scalar
        def _(act):
            act.wait_ge(aggr, NT)
            nc.scalar.activation(g.rstd[:, :], g.mv[:, :, 1], ACT.Sqrt, bias=g.eps[:, 0:1]).then_inc(root, 1)


def layer2_ffn(nc, g, a, table):
    layer_norm(nc, g, None)
    with ExitStack() as stack:
        sb = lambda n, s, d=F32: stack.enter_context(nc.sbuf_tensor(g.tag + n, s, d))
        r = new_route(nc, g, stack, "mo", 2, T2 * P)
        NC = H2 // P
        w1, w2 = sb("w1", [P, 2, E * H2]), sb("w2", [P, NC, E * D])
        flat = g.xn[:, :, :].rearrange("p t d -> p (t d)")
        b1, b2 = flat[:, 0:E * H2], flat[:, E * H2:E * (H2 + D)]
        by_expert = lambda w, c: w[:, c * P:(c + 1) * P, :].rearrange("e p h -> p e h")
        weights = ([(w1[:, c, :].rearrange("p (e h) -> p e h", e=E), by_expert(a.l2f_w1, c)) for c in range(2)]
                   + [(w2[:, c, :].rearrange("p (e h) -> p e h", e=E), by_expert(a.l2f_w2, c)) for c in range(NC)])
        with ExitStack() as s2:
            sb2 = lambda n, s: s2.enter_context(nc.sbuf_tensor(g.tag + n, s, F32))
            gamma, beta, wr, br, logits = sb2("gamma", [P, D]), sb2("beta", [P, D]), sb2("wr", [P, 2, E]), sb2("br", [1, E]), sb2("logits", [P, NT, E])
            load_weights(nc, g, "mo", [(gamma[:, :], across(a.l2f_gamma)), (beta[:, :], across(a.l2f_beta)),
                                       (wr[:, :, :], rows_in(a.l2f_wr)), (br[:, :], a.l2f_br)])
            norm_again(nc, g, gamma, beta, g.acc)
            gate_logits(nc, g, "mo_gate", g.acc, wr, br[0:1, :], logits, loads(nc, g, "mo_experts", weights))
            route(nc, g, "mo_route", logits, 2, None, None, r, clear_rows(r, g.acct[:, 0, 0:4 * D]),
                  loads(nc, g, "mo_biases", [(b1, across(a.l2f_b1)), (b2, across(a.l2f_b2))]))
        send_rows(nc, g, "mo", r, 2, g.acc)
        with ExitStack() as s2:
            sem = lambda n: nc.alloc_semaphore(g.tag + "e_" + n)
            loaded = [sem(f"loaded{s}") for s in range(2)]
            stored = [sem(f"stored{s}") for s in range(2)]
            turned, xt_ready, hidden, biased, active, turned_h, ht_ready, product, copied, freed = (sem(n) for n in (
                "turned", "xt_ready", "hidden", "biased", "active", "turned_h", "ht_ready", "product", "copied", "freed"))
            two = lambda k, lo, n: g.acct[:, k, lo:lo + 2 * n].rearrange("p (s n) -> p s n", s=2)
            rows, xt, h, ht, y = two(0, 0, D), two(0, 2 * D, D), two(0, 4 * D, H2), two(1, 0, H2), two(1, 2 * H2, D)
            block = s2.enter_context(nc.Block(g.tag + "experts"))

            @block.sync
            def _(sp):
                with nc.sync.Fori(0, T2 // 2) as i:
                    for s in range(2):
                        sp.wait_ge(turned, 2 * i + s + 1)
                        sp.dma_start(rows[:, s, :], r.sorted[ds((2 * i + s) * P, P), :]).then_inc(loaded[s], 16)

            @block.tensor
            def _(pe):
                own = [nc.tensor.alloc_register(g.tag + f"owner{s}") for s in range(2)]
                pe.sem_inc(turned, 2)
                pe.sem_inc(hidden, 2)
                pe.sem_inc(turned_h, 2)
                pe.sem_inc(product, 2)
                with nc.tensor.Fori(0, T2 // 2) as i:
                    nc.tensor.reg_load(own, r.expert[0:1, ds(2 * i, 2)])
                    for s in range(2):
                        t = 2 * i + s
                        pe.wait_ge(loaded[s], 16 * (i + 1))
                        pe.wait_ge(xt_ready, t + 1)
                        nc.tensor.transpose(g.ps[s][:, 0:P], rows[:, s, 0:P], g.ident[:, :])
                        nc.tensor.transpose(g.ps[s][:, P:D], rows[:, s, P:D], g.ident[:, :]).then_inc(turned, 1)
                    for s in range(2):
                        t = 2 * i + s
                        e = nc.tensor.snap(own[s], min_val=0, max_val=E - 1)
                        pe.wait_ge(xt_ready, t + 3)
                        pe.wait_ge(biased, t + 1)
                        for c in range(2):
                            last = nc.tensor.matmul(g.ps[2 + s][:, :], xt[:, s, c * P:(c + 1) * P], w1[:, c, ds(e * H2, H2)],
                                                    start=(c == 0), stop=(c == 1))
                        last.then_inc(hidden, 1)
                    for s in range(2):
                        t = 2 * i + s
                        pe.wait_ge(active, t + 1)
                        pe.wait_ge(ht_ready, t + 1)
                        for c in range(NC):
                            last = nc.tensor.transpose(g.ps[4 + s][:, c * P:(c + 1) * P], h[:, s, c * P:(c + 1) * P], g.ident[:, :])
                        last.then_inc(turned_h, 1)
                    for s in range(2):
                        t = 2 * i + s
                        e = nc.tensor.snap(own[s], min_val=0, max_val=E - 1)
                        pe.wait_ge(ht_ready, t + 3)
                        pe.wait_ge(copied, t + 1)
                        for c in range(NC):
                            last = nc.tensor.matmul(g.ps[6 + s][:, 0:D], ht[:, s, c * P:(c + 1) * P], w2[:, c, ds(e * D, D)],
                                                    start=(c == 0), stop=(c == NC - 1))
                        last.then_inc(product, 1)

            @block.scalar
            def _(act):
                act.sem_inc(xt_ready, 2)
                with nc.scalar.Fori(0, T2 // 2) as i:
                    for s in range(2):
                        t = 2 * i + s
                        act.wait_ge(turned, t + 3)
                        act.wait_ge(hidden, t + 1)
                        nc.scalar.activation(xt[:, s, :], g.ps[s][:, 0:D], ACT.Copy).then_inc(xt_ready, 1)
                    for s in range(2):
                        t = 2 * i + s
                        act.wait_ge(biased, t + 3)
                        nc.scalar.activation(h[:, s, :], h[:, s, :], ACT.Gelu).then_inc(active, 1)

            @block.vector
            def _(dve):
                own = [nc.vector.alloc_register(g.tag + f"dve_owner{s}") for s in range(2)]
                dve.sem_inc(biased, 2)
                dve.sem_inc(ht_ready, 2)
                dve.sem_inc(copied, 2)
                dve.sem_inc(freed, 2)
                with nc.vector.Fori(0, T2 // 2) as i:
                    nc.vector.reg_load(own, r.expert[0:1, ds(2 * i, 2)])
                    for s in range(2):
                        t = 2 * i + s
                        e = nc.vector.snap(own[s], min_val=0, max_val=E - 1)
                        dve.wait_ge(hidden, t + 3)
                        dve.wait_ge(turned_h, t + 1)
                        nc.vector.tensor_tensor(h[:, s, :], g.ps[2 + s][:, :], b1[:, ds(e * H2, H2)], ALU.add).then_inc(biased, 1)
                    for s in range(2):
                        t = 2 * i + s
                        dve.wait_ge(turned_h, t + 3)
                        dve.wait_ge(product, t + 1)
                        nc.vector.tensor_copy(ht[:, s, :], g.ps[4 + s][:, :]).then_inc(ht_ready, 1)
                    for s in range(2):
                        t = 2 * i + s
                        e = nc.vector.snap(own[s], min_val=0, max_val=E - 1)
                        dve.wait_ge(product, t + 3)
                        dve.wait_ge(freed, t + 1)
                        nc.vector.tensor_tensor(y[:, s, :], g.ps[6 + s][:, 0:D], b2[:, ds(e * D, D)], ALU.add).then_inc(copied, 1)

            @block.gpsimd
            def _(pool):
                with nc.gpsimd.Fori(0, T2 // 2) as i:
                    for s in range(2):
                        pool.wait_ge(copied, 2 * i + s + 3)
                        pool.dma_start(r.result[ds((2 * i + s) * P, P), :], y[:, s, :]).then_inc(stored[s], 16)
                        pool.wait_ge(stored[s], 16 * (i + 1))
                        pool.sem_inc(freed, 1)

        collect_rows(nc, g, "mo", r, 2, g.x)


H3 = 1024
T3 = (NODES + E * (P - 1)) // P
T3 += T3 % 2


def layer3_ffn(nc, g, a, table):
    layer_norm(nc, g, None)
    NF = H3 // P
    with ExitStack() as stack:
        sb = lambda n, s, d=F32: stack.enter_context(nc.sbuf_tensor(g.tag + n, s, d))
        r = new_route(nc, g, stack, "top", 1, T3 * P)
        w1, b1, wd, bd = sb("w1", [P, 2, H3]), sb("b1", [P, NF]), sb("wd", [P, NF, E * D]), g.acc[:, :, :].rearrange("p t d -> p (t d)")[:, 0:E * D]
        with ExitStack() as s1:
            sb1 = lambda n, s: s1.enter_context(nc.sbuf_tensor(g.tag + n, s, F32))
            wg, bg, logits = sb1("wg", [P, NF, E]), sb1("bg", [1, E]), sb1("logits", [P, NT, E])
            load_weights(nc, g, "top", [(w1[:, :, :], rows_in(a.l3f_w1)), (b1[:, :], a.l3f_b1_cols),
                                        (wg[:, :, :], rows_in(a.l3f_wg)), (bg[:, :], a.l3f_bg)])
            with ExitStack() as s2:
                sem = lambda n: nc.alloc_semaphore(g.tag + "g_" + n)
                xnt = g.acct
                ht = s2.enter_context(nc.sbuf_tensor(g.tag + "g_ht", [P, NF, 2 * P], F32))
                turn_nodes(nc, g, xnt)
                hidden, active, product, used = sem("hidden"), sem("active"), sem("product"), sem("used")
                block = s2.enter_context(nc.Block(g.tag + "gate"))
                G = 2 * P
                experts_in = loads(nc, g, "top_experts", [
                    (wd[:, f, :].rearrange("p (e h) -> p e h", e=E), a.l3f_wd[:, f * P:(f + 1) * P, :].rearrange("e p h -> p e h")) for f in range(NF)]
                    + [(bd, across(a.l3f_bd))])

                @block.sync
                def _(sp):
                    experts_in(sp)

                @block.tensor
                def _(pe):
                    pe.sem_inc(hidden, 4)
                    pe.sem_inc(product, 2)
                    with nc.tensor.Fori(0, ROWS // G) as i:
                        for f in range(NF):
                            pe.wait_ge(active, NF * i + f + 1)
                            for c in range(2):
                                last = nc.tensor.matmul(g.ps[f % 4][:, 0:G], w1[:, c, f * P:(f + 1) * P], xnt[:, c, ds(i * G, G)],
                                                        start=(c == 0), stop=(c == 1))
                            last.then_inc(hidden, 1)
                        for s in range(2):
                            pe.wait_ge(used, 2 * i + s + 1)
                            nc.tensor.matmul(g.ps[4 + s][:, 0:E], g.ones[0:1, :], bg[0:1, :], start=True, stop=False)
                            for f in range(NF):
                                if s == 0:
                                    pe.wait_ge(active, NF * i + f + 5)
                                last = nc.tensor.matmul(g.ps[4 + s][:, 0:E], ht[:, f, s * P:(s + 1) * P], wg[:, f, :],
                                                        start=False, stop=(f == NF - 1))
                            last.then_inc(product, 1)

                @block.scalar
                def _(act):
                    act.sem_inc(active, 4)
                    with nc.scalar.Fori(0, ROWS // G) as i:
                        act.wait_ge(product, 2 * i + 2)
                        for f in range(NF):
                            act.wait_ge(hidden, NF * i + f + 5)
                            nc.scalar.activation(ht[:, f, :], g.ps[f % 4][:, 0:G], ACT.Gelu, bias=b1[:, f:f + 1]).then_inc(active, 1)

                @block.vector
                def _(dve):
                    dve.sem_inc(used, 2)
                    with nc.vector.Fori(0, ROWS // G) as i:
                        for s in range(2):
                            dve.wait_ge(product, 2 * i + s + 3)
                            nc.vector.tensor_copy(logits[:, ds(2 * i + s, 1), :], g.ps[4 + s][:, 0:E]).then_inc(used, 1)

            route(nc, g, "top_route", logits, 1, None, None, r, clear_rows(r, g.acct[:, 0, 0:4 * D]))
        send_rows(nc, g, "top", r, 1, g.xn)
        with ExitStack() as s2:
            sem = lambda n: nc.alloc_semaphore(g.tag + "e_" + n)
            sb2 = lambda n, s: s2.enter_context(nc.sbuf_tensor(g.tag + "e_" + n, s, F32))
            loaded, stored, turned, xt_ready, hidden, active, product, copied, freed = (sem(n) for n in (
                "loaded", "stored", "turned", "xt_ready", "hidden", "active", "product", "copied", "freed"))
            rows, xt, ht, y = sb2("rows", [P, 2, D]), sb2("xt", [P, 2, 2 * P]), sb2("ht", [P, NF, 2 * P]), sb2("y", [P, 2, D])
            block = s2.enter_context(nc.Block(g.tag + "experts"))

            @block.sync
            def _(sp):
                with nc.sync.Fori(0, T3 // 2) as i:
                    sp.wait_ge(turned, i + 1)
                    sp.dma_start(rows[:, :, :], r.sorted[ds(2 * i * P, 2 * P), :].rearrange("(r p) d -> p r d", p=P)).then_inc(loaded, 16)

            @block.tensor
            def _(pe):
                own = [nc.tensor.alloc_register(g.tag + f"owner{s}") for s in range(2)]
                pe.sem_inc(turned, 1)
                pe.sem_inc(hidden, 3)
                pe.sem_inc(product, 2)
                with nc.tensor.Fori(0, T3 // 2) as i:
                    nc.tensor.reg_load(own, r.expert[0:1, ds(2 * i, 2)])
                    pe.wait_ge(loaded, 16 * (i + 1))
                    pe.wait_ge(xt_ready, i + 1)
                    for c in range(2):
                        for s in range(2):
                            last = nc.tensor.transpose(g.ps[0][:, (2 * c + s) * P:(2 * c + s + 1) * P], rows[:, s, c * P:(c + 1) * P], g.ident[:, :])
                    last.then_inc(turned, 1)
                    pe.wait_ge(xt_ready, i + 2)
                    for f in range(NF):
                        pe.wait_ge(active, NF * i + f + 1)
                        for c in range(2):
                            last = nc.tensor.matmul(g.ps[1 + f % 4][:, 0:2 * P], w1[:, c, f * P:(f + 1) * P], xt[:, c, :],
                                                    start=(c == 0), stop=(c == 1))
                        last.then_inc(hidden, 1)
                    for s in range(2):
                        t = 2 * i + s
                        e = nc.tensor.snap(own[s], min_val=0, max_val=E - 1)
                        pe.wait_ge(copied, t + 1)
                        for f in range(NF):
                            if s == 0:
                                pe.wait_ge(active, NF * i + f + 5)
                            last = nc.tensor.matmul(g.ps[5 + s][:, 0:D], ht[:, f, s * P:(s + 1) * P], wd[:, f, ds(e * D, D)],
                                                    start=(f == 0), stop=(f == NF - 1))
                        last.then_inc(product, 1)

            @block.scalar
            def _(act):
                act.sem_inc(xt_ready, 1)
                act.sem_inc(active, 4)
                with nc.scalar.Fori(0, T3 // 2) as i:
                    act.wait_ge(turned, i + 2)
                    act.wait_ge(hidden, NF * i + 3)
                    nc.scalar.activation(xt[:, :, :], g.ps[0][:, :].rearrange("p (c n) -> p c n", c=2), ACT.Copy).then_inc(xt_ready, 1)
                    act.wait_ge(product, 2 * i + 2)
                    for f in range(NF):
                        act.wait_ge(hidden, NF * i + f + 4)
                        nc.scalar.activation(ht[:, f, :], g.ps[1 + f % 4][:, 0:2 * P], ACT.Gelu, bias=b1[:, f:f + 1]).then_inc(active, 1)

            @block.vector
            def _(dve):
                own = [nc.vector.alloc_register(g.tag + f"dve_owner{s}") for s in range(2)]
                dve.sem_inc(copied, 2)
                dve.sem_inc(freed, 2)
                with nc.vector.Fori(0, T3 // 2) as i:
                    nc.vector.reg_load(own, r.expert[0:1, ds(2 * i, 2)])
                    for s in range(2):
                        t = 2 * i + s
                        e = nc.vector.snap(own[s], min_val=0, max_val=E - 1)
                        dve.wait_ge(product, t + 3)
                        dve.wait_ge(freed, t + 1)
                        nc.vector.tensor_tensor(y[:, s, :], g.ps[5 + s][:, 0:D], bd[:, ds(e * D, D)], ALU.add).then_inc(copied, 1)

            @block.gpsimd
            def _(pool):
                with nc.gpsimd.Fori(0, T3 // 2) as i:
                    for s in range(2):
                        pool.wait_ge(copied, 2 * i + s + 3)
                        pool.dma_start(r.result[ds((2 * i + s) * P, P), :], y[:, s, :]).then_inc(stored, 16)
                        pool.wait_ge(stored, 16 * (2 * i + s + 1))
                        pool.sem_inc(freed, 1)

        collect_rows(nc, g, "top", r, 1, g.x)


TABLES = 4


def source_tables(nc):
    return [nc.dram_tensor(f"source_sums{k}", (ROWS + P, D), F32).ap() for k in range(TABLES)]


def clear_tables(nc, g, sp, zeros, tables, zeroed):
    n = 0
    for k in range(TABLES):
        for r0 in range(0, ROWS + P, 4 * P):
            m = min(4, (ROWS + P - r0) // P)
            sp.dma_start(tables[k][r0:r0 + m * P, :].rearrange("(p j) d -> p (j d)", p=P), zeros[:, 0:m * D]).then_inc(zeroed, 16)
            n += 16
    sp.wait_ge(zeroed, n)


def scatter_edges(nc, g, a, tables):
    with ExitStack() as stack:
        sem = lambda n: nc.alloc_semaphore(g.tag + "s_" + n)
        sb = lambda n, s, d=F32: stack.enter_context(nc.sbuf_tensor(g.tag + "s_" + n, s, d))
        weights, srcf = sb("weights", [P, ET + 8]), sb("srcf", [P, ET + 8])
        loaded = [sem(f"loaded{h}") for h in range(2)]
        scattered = [sem(f"scattered{k}") for k in range(TABLES)]
        prep, weights_in, hot, looked, placed, mixed, summed, ready, claimed, counted, step, chosen, retired = (sem(n) for n in (
            "prep", "weights_in", "hot", "looked", "placed", "mixed", "summed", "ready", "claimed", "counted", "step", "chosen", "retired"))
        src, dst = sb("src_across", [P, 2, H * P], I32), sb("dst_across", [P, 2, H * P], I32)
        idx, count, spare, away, lower, junk = sb("idx", [P, U], I32), sb("count", [P, H]), sb("spare", [P, 1]), sb("away", [P, H]), sb("lower", [P, P]), sb("junk", [P, 2, P])
        onehot_t, mix = sb("onehot_t", [P, 4, 2, P]), sb("mix", [P, 4, P])
        found, rows = sb("found", [P, 4, D]), sb("rows", [P, U, D])
        block = stack.enter_context(nc.Block(g.tag + "scatter_edges"))
        xflat = g.xn[:, :, :].rearrange("p t d -> p (t d)")

        @block.sync
        def _(sp):
            sp.dma_start(weights[:, 0:ET], a.edge_weight_cols).then_inc(weights_in, 16)
            with nc.sync.Fori(0, ET // U) as i:
                for h in range(2):
                    sp.wait_ge(mixed, U * i + (h + 1) * H)
                    for t, v, first in ((src, a.src_row, 0), (dst, a.dst_row, 1)):
                        sp.dma_start(t[:, h, :], v[ds((2 * i + h) * H * P + first, H * P)]
                                     .rearrange("(o n) -> o n", o=1).to_broadcast([P, H * P])).then_inc(loaded[h], 16)

        @block.gpsimd
        def _(pool):
            nc.gpsimd.affine_select(out=lower[:, :], in_=g.ones[:, :], compare_op=ALU.is_gt, fill=0.0, base=0,
                                    pattern=[[-1, P]], channel_multiplier=1).then_inc(prep, 1)
            nc.gpsimd.iota(spare[:, :], [[0, 1]], base=ROWS, channel_multiplier=1, allow_small_or_imprecise_dtypes=True).then_inc(prep, 1)

            def round(i):
                first = isinstance(i, int)
                for u in range(U):
                    k = u % TABLES
                    if u % H == 0:
                        pool.wait_ge(chosen, 2 * i + u // H + 1)
                    pool.wait_ge(ready, U * i + u + 5)
                    pool.sem_inc(claimed, 1)
                    nc.gpsimd.indirect_dma_start(
                        tables[k], bass.IndirectOffsetOnAxis(ap=idx[:, u:u + 1].bitcast(U32), axis=0),
                        rows[:, u, :], None, bounds_check=ROWS + P - 1, compute_op=ALU.add).then_inc(scattered[k], 16)
                    n = (k + 1) % TABLES
                    if first and u < TABLES - 1:
                        continue
                    pool.wait_ge(scattered[n], 16 * (U // TABLES * i + u // TABLES + (1 if k == TABLES - 1 else 0)))
                    pool.sem_inc(retired, 1)
            round(0)
            with nc.gpsimd.Fori(1, ET // U) as i:
                round(i)
            for k in range(TABLES):
                pool.wait_ge(scattered[k], 16 * ET // TABLES)

        @block.tensor
        def _(pe):
            window = [nc.tensor.alloc_register(g.tag + f"sw{u}") for u in range(8)]
            pe.sem_inc(looked, 4)
            pe.sem_inc(summed, 4)
            with nc.tensor.Fori(0, ET // U) as i:
                for v in range(0, U, 2):
                    if v % 8 == 0:
                        nc.tensor.reg_load(window, g.window[0:1, ds(U * i + v, 8)])
                    for u in (v, v + 1):
                        n = U * i + u
                        w = nc.tensor.snap(window[u % 8], min_val=0, max_val=NT - 2)
                        pe.wait_ge(hot, n + 1)
                        pe.wait_ge(placed, n + 1)
                        for k in range(2):
                            last = nc.tensor.matmul(g.ps[u % 4][:, 0:D], onehot_t[:, u % 4, k, :],
                                                    xflat[:, ds(w * D + k * D, D)], start=(k == 0), stop=(k == 1))
                        last.then_inc(looked, 1)
                    for u in (v, v + 1):
                        n = U * i + u
                        pe.wait_ge(placed, n + 5)
                        pe.wait_ge(mixed, n + U + 1)
                        pe.wait_ge(ready, n + 1)
                        nc.tensor.matmul(g.ps[4 + u % 4][:, 0:D], mix[:, u % 4, :], found[:, u % 4, :], start=True, stop=True).then_inc(summed, 1)

        @block.scalar
        def _(act):
            act.sem_inc(placed, 4)
            with nc.scalar.Fori(0, ET // U) as i:
                for u in range(U):
                    n = U * i + u
                    act.wait_ge(looked, n + 5)
                    act.wait_ge(summed, n + 1)
                    nc.scalar.activation(found[:, u % 4, :], g.ps[u % 4][:, 0:D], ACT.Copy).then_inc(placed, 1)

        @block.vector
        def _(dve):
            window = [nc.vector.alloc_register(g.tag + f"dve_window{u}") for u in range(8)]
            dve.sem_inc(mixed, U)
            dve.sem_inc(retired, U)
            dve.sem_inc(ready, 4)
            dve.sem_inc(counted, 2)
            nc.vector.tensor_copy(srcf[:, 0:ET], g.srcc[:, :]).then_inc(prep, 1)
            dve.wait_ge(prep, 3)
            dve.wait_ge(weights_in, 16)
            HOT, MIX = 3, 2

            def windows(i, h, count=8):
                nc.vector.reg_load(window[0:count], g.window[0:1, ds(U * i + h * H + HOT, count)])

            def build(i, u, w, n):
                if not (isinstance(n, int) and n < 4):
                    dve.wait_ge(looked, n + 1)
                nc.vector.tensor_tensor(onehot_t[:, u % 4, :, :], dst[:, u // H, u % H * P:(u % H + 1) * P].unsqueeze(1).to_broadcast([P, 2, P]),
                                        g.node_id[:, ds(w, 2)].unsqueeze(2).to_broadcast([P, 2, P]), ALU.is_equal).then_inc(hot, 1)

            def share(i, u, n):
                if not (isinstance(n, int) and n < 4):
                    dve.wait_ge(summed, n + 1)
                nc.vector.tensor_scalar(mix[:, u % 4, :], src[:, u // H, u % H * P:(u % H + 1) * P], srcf[:, ds(n, 1)],
                                        weights[:, ds(n, 1)], ALU.is_equal, ALU.mult).then_inc(mixed, 1)

            def count_before(u, n):
                if not (isinstance(n, int) and n < 2):
                    dve.wait_ge(counted, n + 1)
                nc.vector.scalar_tensor_tensor(out=junk[:, u % 2, :], in0=src[:, u // H, u % H * P:(u % H + 1) * P], scalar=srcf[:, ds(n, 1)],
                                               in1=lower[:, :], op0=ALU.is_equal, op1=ALU.mult, accum_out=count[:, u % H:u % H + 1]).then_inc(counted, 1)

            def choose(n, h, done):
                nc.vector.tensor_scalar(away[:, :], srcf[:, ds(n, H)], spare[:, 0:1], None, ALU.subtract).then_inc(step, 1)
                dve.wait_ge(step, 2 * done + 1)
                dve.wait_ge(counted, H * done + H + 2)
                nc.vector.scalar_tensor_tensor(out=away[:, :], in0=count[:, :], scalar=0.0, in1=away[:, :], op0=ALU.is_equal, op1=ALU.mult).then_inc(step, 1)
                dve.wait_ge(step, 2 * done + 2)
                dve.wait_ge(retired, H * done + H)
                nc.vector.tensor_scalar(idx[:, h * H:(h + 1) * H], away[:, :], spare[:, 0:1], None, ALU.add).then_inc(chosen, 1)

            dve.wait_ge(loaded[0], 32)
            for u in range(H):
                count_before(u, u)
            choose(0, 0, 0)
            nc.vector.reg_load(window, g.window[0:1, 0:8])
            for u in range(HOT):
                build(0, u, nc.vector.snap(window[u], min_val=0, max_val=NT - 2), u)
            for u in range(MIX):
                share(0, u, u)

            def round(i, last=False):
                for u in range(U):
                    h, final = u // H, last and u >= H
                    if u % H == 0:
                        windows(i, h, 8 - HOT if final else 8)
                    w = None if last and u + HOT >= U else nc.vector.snap(window[u % 8], min_val=0, max_val=NT - 2)
                    if u % H == 0:
                        if not final:
                            dve.wait_ge(loaded[1 - h], 32 * (i + h + 1))
                    if not (last and u + HOT >= U):
                        build(i, (u + HOT) % U, w, U * i + u + HOT)
                    if not final:
                        count_before((u + H) % U, U * i + u + H)
                    if not (last and u + MIX >= U):
                        share(i, (u + MIX) % U, U * i + u + MIX)
                    n = U * i + u
                    dve.wait_ge(summed, n + 5)
                    dve.wait_ge(retired, n + 1)
                    nc.vector.tensor_copy(rows[:, u, :], g.ps[4 + u % 4][:, 0:D]).then_inc(ready, 1)
                    if u % H == H - 1 and not final:
                        choose(U * i + (h + 1) * H, 1 - h, 2 * i + h + 1)
            with nc.vector.Fori(0, ET // U - 1) as i:
                round(i)
            round(ET // U - 1, last=True)


def sum_tables(nc, g, tables):
    with ExitStack() as stack:
        sem = lambda n: nc.alloc_semaphore(g.tag + "t_" + n)
        part = [stack.enter_context(nc.sbuf_tensor(g.tag + f"t_part{k}", [P, NT, D], F32)) for k in range(2)]
        loaded = [sem(f"loaded{k}") for k in range(TABLES)]
        added = sem("added")
        block = stack.enter_context(nc.Block(g.tag + "sum_tables"))
        dst = [g.acc, part[0], part[1], part[0]]

        @block.sync
        def _(sp):
            for k in range(TABLES):
                if k == 3:
                    sp.wait_ge(added, 1)
                sp.dma_start(dst[k][:, :, :], tables[k][0:ROWS, :].rearrange("(t p) d -> p t d", p=P)).then_inc(loaded[k], 16)

        @block.vector
        def _(dve):
            dve.wait_ge(loaded[0], 16)
            for k in range(1, TABLES):
                dve.wait_ge(loaded[k], 16)
                if k > 1:
                    dve.wait_ge(added, k - 1)
                nc.vector.tensor_tensor(g.acc[:, :, :], g.acc[:, :, :], dst[k][:, :, :], ALU.add).then_inc(added, 1)
            dve.wait_ge(added, TABLES - 1)


def layer2_gnn(nc, g, a, table):
    layer_norm(nc, g, None)
    scatter_edges(nc, g, a, g.tables)
    sum_tables(nc, g, g.tables)
    with ExitStack() as stack:
        sb = lambda n, s: stack.enter_context(nc.sbuf_tensor(g.tag + n, s, F32))
        wl, wr, bias = sb("wl", [P, 2, D]), sb("wr", [P, 2, D]), sb("bias", [1, 3, D])
        load_weights(nc, g, "l2g", [(wl[:, :, :], rows_in(a.l2g_w_l)), (wr[:, :, :], rows_in(a.l2g_w_r)),
                                    (bias[:, 0, :], a.l2g_b_l), (bias[:, 1, :], a.l2g_b_r)])
        with ExitStack() as s2:
            step = nc.alloc_semaphore(g.tag + "bias_step")
            block = s2.enter_context(nc.Block(g.tag + "bias"))

            @block.vector
            def _(dve):
                nc.vector.tensor_tensor(bias[:, 2, :], bias[:, 0, :], bias[:, 1, :], ALU.add).then_inc(step, 1)
                dve.wait_ge(step, 1)
        project(nc, g, "l2g", [wl, wr], bias[0:1, 2, :], D,
                [("pool", lambda out, t: nc.gpsimd.tensor_copy(out, g.acc[:, ds(t, 1), :])),
                 ("dve", lambda out, t: nc.vector.tensor_copy(out, g.xn[:, ds(t, 1), :]))],
                lambda dve, bank, t, s: nc.vector.tensor_tensor(g.x[:, ds(t, 1), :], g.x[:, ds(t, 1), :], bank, ALU.add))


C3 = 128


def node_steps(nc, g, name, steps, table=None, rows=None):
    with ExitStack() as stack:
        step, stored = nc.alloc_semaphore(g.tag + name + "_step"), nc.alloc_semaphore(g.tag + name + "_stored")
        block = stack.enter_context(nc.Block(g.tag + name))

        @block.vector
        def _(dve):
            for n, s in enumerate(steps):
                s().then_inc(step, 1)
                dve.wait_ge(step, n + 1)

        @block.sync
        def _(sp):
            if table is not None:
                sp.wait_ge(step, len(steps))
                sp.dma_start(table.rearrange("(t p) d -> p t d", p=P), rows).then_inc(stored, 16)
                sp.wait_ge(stored, 16)


def layer3_gnn(nc, g, a, table):
    layer_norm(nc, g, None)
    htable = nc.dram_tensor("gcn_rows", (ROWS, C3), F32).ap()
    htable2 = nc.dram_tensor("gcn_rows2", (ROWS, C3), F32).ap()
    with ExitStack() as stack:
        sb = lambda n, s: stack.enter_context(nc.sbuf_tensor(g.tag + n, s, F32))
        w1, w2, b1, b2 = sb("w1", [P, 2, C3]), sb("w2", [P, 1, D]), sb("b1", [P, C3]), sb("b2", [1, D])
        dinv, hs = sb("dinv", [P, NT]), sb("hs", [P, NT, C3])
        load_weights(nc, g, "l3g", [(w1[:, :, :], rows_in(a.l3g_w1)), (w2[:, 0, :], a.l3g_w2), (b1[:, :], across(a.l3g_b1)), (b2[:, :], a.l3g_b2)])
        with ExitStack() as s2:
            step = nc.alloc_semaphore(g.tag + "dinv_step")
            block = s2.enter_context(nc.Block(g.tag + "dinv"))

            @block.scalar
            def _(act):
                nc.scalar.activation(dinv[:, :], g.deg[:, :], ACT.Sqrt, bias=g.ones[:, 0:1]).then_inc(step, 1)

            @block.vector
            def _(dve):
                dve.wait_ge(step, 1)
                nc.vector.reciprocal(dinv[:, :], dinv[:, :]).then_inc(step, 1)
                dve.wait_ge(step, 2)
        wide = [P, NT, C3]
        acc = g.acc[:, :, :].rearrange("p t d -> p (t d)")[:, 0:NT * C3].rearrange("p (t d) -> p t d", d=C3)
        dw = dinv[:, :].unsqueeze(2).to_broadcast(wide)
        tt = lambda out, x, y, op: (lambda: nc.vector.tensor_tensor(out, x, y, op))
        project(nc, g, "gcn1", [w1], None, C3,
                [("pool", lambda out, t: nc.gpsimd.tensor_copy(out, g.xn[:, ds(t, 1), :]))],
                lambda dve, bank, t, s: nc.vector.tensor_scalar(hs[:, ds(t, 1), :], bank, dinv[:, ds(t, 1)], None, ALU.mult))
        node_steps(nc, g, "gcn_rows", [], htable, hs[:, :, :])
        sum_edges(nc, g, htable, C3, name="gcn_sum1")
        node_steps(nc, g, "gcn_mid", [
            tt(acc, acc, hs[:, :, :], ALU.add), tt(acc, acc, dw, ALU.mult),
            tt(acc, acc, b1[:, :].unsqueeze(1).to_broadcast(wide), ALU.add),
            lambda: nc.vector.tensor_scalar(acc, acc, 0.0, None, ALU.max),
            tt(hs[:, :, :], acc, dw, ALU.mult)], htable2, hs[:, :, :])
        sum_edges(nc, g, htable2, C3, name="gcn_sum2")
        node_steps(nc, g, "gcn_end", [tt(acc, acc, hs[:, :, :], ALU.add), tt(hs[:, :, :], acc, dw, ALU.mult)])
        project(nc, g, "gcn2", [w2], b2[0:1, :], D,
                [("pool", lambda out, t: nc.gpsimd.tensor_copy(out, hs[:, ds(t, 1), :]))],
                lambda dve, bank, t, s: nc.vector.tensor_tensor(g.x[:, ds(t, 1), :], g.x[:, ds(t, 1), :], bank, ALU.add), chunks=1)


def store_out(nc, g, src, out):
    with ExitStack() as stack:
        stored = nc.alloc_semaphore("out_stored")
        block = stack.enter_context(nc.Block("store_out"))

        @block.sync
        def _(sp):
            sp.dma_start(out[0:FULL * P, :].rearrange("(t p) d -> p t d", p=P), src[:, 0:FULL, :]).then_inc(stored, 16)
            sp.dma_start(out[FULL * P:NODES, :], src[0:REST, FULL, :]).then_inc(stored, 16)
            sp.wait_ge(stored, 32)


def build(nc, a, out, stages):
    g = Core()
    g.tag = ""
    with ExitStack() as stack:
        tensors(nc, g, stack)
        table = nc.dram_tensor("xn_rows", (ROWS, D), F32).ap()
        load_graph(nc, g, a)
        for s in stages:
            g.tag = s.__name__ + "_"
            held = nc.snapshot_sems()
            s(nc, g, a, table)
            nc.clear_and_free_semaphores(nc.allocated_since(held))
            nc.all_engine_barrier()
        store_out(nc, g, g.x, out)


def _layout(inputs):
    import numpy as _np
    n = lambda v: _np.ascontiguousarray(_np.asarray(v))
    v = {k: _np.asarray(x) for k, x in inputs.items()}
    pad = _np.full(ET * P - EDGES, 3199, _np.int32)
    row = lambda u: _np.concatenate([u, pad])
    cols = lambda u: n(row(u).reshape(ET, P).T)
    flat = lambda u: n(u.reshape(-1))
    one = lambda u: n(u.reshape(1, -1))
    laid = {"x": n(v["x"]), "src_cols": cols(v["src"]), "dst_cols": cols(v["dst"]),
            "l0g_w_self_t": n(v["L0_gnn_W_self"].T), "l0g_w_neigh_t": n(v["L0_gnn_W_neigh"].T), "l0g_b_self": one(v["L0_gnn_b_self"]),
            "l0f_wr": flat(v["L0_ffn_wr"]), "l0f_br": n(v["L0_ffn_br"]), "l0f_w1": n(v["L0_ffn_w1"]), "l0f_w2": n(v["L0_ffn_w2"]),
            "l0f_b1_cols": n(v["L0_ffn_b1"].reshape(-1, P).T), "l0f_b2": one(v["L0_ffn_b2"]),
            "l1g_w_t": n(v["L1_gnn_W"].T), "l1g_w": n(v["L1_gnn_W"]), "l1g_a_src_cols": n(v["L1_gnn_a_src"].reshape(2, P).T),
            "l1g_a_dst_cols": n(v["L1_gnn_a_dst"].reshape(2, P).T), "l1g_edge_w_t": n(v["L1_gnn_edge_W"].T),
            "l1g_edge_b": one(v["L1_gnn_edge_b"]), "l1g_bias": n(v["L1_gnn_bias"]),
            "edge_attr_t": n(_np.concatenate([_np.concatenate([v["edge_attr_3"], _np.zeros((ET * P - EDGES, 3), _np.float32)]).T,
                                              _np.ones((1, ET * P), _np.float32)])),
            "l1f_gate_w": n(v["L1_ffn_gate_w"]), "l1f_gate_b": one(v["L1_ffn_gate_b"]), "l1f_w1": n(v["L1_ffn_w1"]), "l1f_w2": n(v["L1_ffn_w2"]),
            "l1f_b1_cols": n(v["L1_ffn_b1"].reshape(-1, P).T), "l1f_b2": n(v["L1_ffn_b2"]),
            "l2f_gamma": n(v["L2_ffn_gamma"]), "l2f_beta": n(v["L2_ffn_beta"]), "l2f_wr": n(v["L2_ffn_Wr"]), "l2f_br": one(v["L2_ffn_br"]),
            "l2f_w1": n(v["L2_ffn_W1"]), "l2f_b1": flat(v["L2_ffn_b1"]), "l2f_w2": n(v["L2_ffn_W2"]), "l2f_b2": flat(v["L2_ffn_b2"]),
            "l3f_w1": n(v["L3_ffn_W1"]), "l3f_b1_cols": n(v["L3_ffn_b1"].reshape(-1, P).T), "l3f_wg": n(v["L3_ffn_Wg"]),
            "l3f_bg": one(v["L3_ffn_bg"]), "l3f_wd": n(v["L3_ffn_Wd"]), "l3f_bd": flat(v["L3_ffn_bd"]),
            "l2g_w_l": n(v["L2_gnn_weight_l"]), "l2g_w_r": n(v["L2_gnn_weight_r"]), "l2g_b_l": one(v["L2_gnn_bias_l"]), "l2g_b_r": one(v["L2_gnn_bias_r"]),
            "edge_weight_cols": n(_np.concatenate([v["edge_weight"], _np.zeros(ET * P - EDGES, _np.float32)]).reshape(ET, P).T),
            "src_row": n(row(v["src"])),
            "l3g_w1": n(v["L3_gnn_W1"]), "l3g_w2": n(v["L3_gnn_W2"]), "l3g_b1": n(v["L3_gnn_b1"]), "l3g_b2": one(v["L3_gnn_b2"]),
            "dst_row": n(_np.concatenate([_np.full(1, -1, _np.int32), row(v["dst"]), _np.full(1, -1, _np.int32)]))}
    return laid


def kernel(**inputs):
    import numpy as _np
    import concourse.bacc as _bacc
    from concourse import mybir as _mybir
    from concourse.bass_utils import run_bass_kernel_spmd as _run

    nc = _bacc.Bacc("TRN2", target_bir_lowering=False, num_devices=1)
    laid = _layout(inputs)
    a = Core()
    arrays = {}
    for name, v in laid.items():
        arrays[f"in_{name}"] = v
        a.__dict__[name] = nc.dram_tensor(f"in_{name}", v.shape, _mybir.dt.from_np(v.dtype), kind="ExternalInput").ap()
    out = nc.dram_tensor("out_0", (NODES, D), F32, kind="ExternalOutput").ap()
    build(nc, a, out, STAGES)
    r = _run(nc, [arrays], core_ids=[0])
    return r.results[0]["out_0"]
STAGES = [layer0_gnn, layer0_ffn, layer1_gnn, layer1_ffn, layer2_gnn, layer2_ffn, layer3_gnn, layer3_ffn]
```

```python
import concourse.bass as bass
from concourse import mybir
from concourse.bass import ds
from contextlib import ExitStack

F32, I32, U32 = mybir.dt.float32, mybir.dt.int32, mybir.dt.uint32
ALU, ACT, AX = mybir.AluOpType, mybir.ActivationFunctionType, mybir.AxisListType
P = 128
NODES, D = 3125, 256
EDGES = 53125
NT = 26
ROWS = NT * P
FULL = NODES // P
REST = NODES - FULL * P
ET = 416
U = 16
H = U // 2
Q = 4
PARTS = U // Q
EPS = 1e-5


class Core:
    pass


def tensors(nc, g, stack):
    def sb(name, shape, dt=F32):
        return stack.enter_context(nc.sbuf_tensor(g.tag + name, shape, dt))
    g.x = sb("x_nodes", [P, NT, D])
    g.xn = sb("xn_nodes", [P, NT, D])
    g.acc = sb("edge_sums", [P, NT, D])
    g.acct = sb("edge_sums_turned", [P, 2, ROWS])
    g.deg = sb("in_degree", [P, NT])
    g.srcc = sb("src_cols", [P, ET + H], I32)
    g.dstc = sb("dst_cols", [P, ET], I32)
    g.local = sb("dst_local", [P, ET + 8])
    g.window = sb("dst_window", [1, ET], I32)
    g.ident = sb("identity", [P, P])
    g.iota = sb("iota_row", [P, 2 * P])
    g.ones = sb("ones", [P, P])
    g.node_id = sb("node_id", [P, NT])
    g.eps = sb("eps", [P, 1])
    g.stats = sb("ln_stats", [P, NT, 6])
    g.mv = sb("ln_mean_var", [P, NT, 2])
    g.rstd = sb("ln_rstd", [P, NT])
    g.ps = [stack.enter_context(nc.psum_tensor(f"bank{b}", [P, 512], F32)) for b in range(8)]


def load_graph(nc, g, a):
    with ExitStack() as stack:
        sem = lambda n: nc.alloc_semaphore(g.tag + n)
        x_cleared, x_loaded, idx_loaded = sem("x_cleared"), sem("x_loaded"), sem("idx_loaded")
        consts, ident0, win = sem("consts"), sem("ident_cleared"), sem("win_ready")
        win_sum, step = sem("win_sum"), sem("window_step")
        wi = stack.enter_context(nc.sbuf_tensor(g.tag + "window_tile", [1, ET], I32))
        df = stack.enter_context(nc.sbuf_tensor(g.tag + "dst_f", [P, ET], F32))
        block = stack.enter_context(nc.Block(g.tag + "load_graph"))

        @block.sync
        def _(sp):
            sp.dma_start(g.dstc[:, :], a.dst_cols).then_inc(idx_loaded, 16)
            sp.dma_start(g.srcc[:, 0:ET], a.src_cols).then_inc(idx_loaded, 16)
            sp.wait_ge(x_cleared, 1)
            sp.dma_start(g.x[:, 0:FULL, :], a.x[0:FULL * P, :].rearrange("(t p) d -> p t d", p=P)).then_inc(x_loaded, 16)
            sp.dma_start(g.x[0:REST, FULL, :], a.x[FULL * P:NODES, :]).then_inc(x_loaded, 16)
            sp.wait_ge(x_loaded, 32)

        @block.gpsimd
        def _(pool):
            nc.gpsimd.memset(g.ident[:, :], 0.0).then_inc(ident0, 1)
            nc.gpsimd.iota(g.iota[:, :], [[1, 2 * P]], base=0, channel_multiplier=0,
                           allow_small_or_imprecise_dtypes=True).then_inc(consts, 1)
            nc.gpsimd.iota(g.node_id[:, :], [[P, NT]], base=0, channel_multiplier=1,
                           allow_small_or_imprecise_dtypes=True).then_inc(consts, 1)
            pool.wait_ge(ident0, 1)
            nc.gpsimd.affine_select(out=g.ident[:, :], in_=g.ident[:, :], compare_op=ALU.not_equal, fill=1.0,
                                    base=0, pattern=[[-1, P]], channel_multiplier=1).then_inc(consts, 1)

        @block.vector
        def _(dve):
            nc.vector.memset(g.x[:, FULL:NT, :], 0.0).then_inc(x_cleared, 1)
            nc.vector.memset(g.ones[:, :], 1.0).then_inc(consts, 1)
            nc.vector.memset(g.eps[:, :], EPS).then_inc(consts, 1)
            nc.vector.memset(g.local[:, ET:ET + 8], 0.0).then_inc(consts, 1)
            nc.vector.memset(g.srcc[:, ET:ET + H], 0).then_inc(consts, 1)
            dve.wait_ge(idx_loaded, 32)
            nc.vector.tensor_scalar(wi[:, :], g.dstc[0:1, :], 7, None, ALU.logical_shift_right).then_inc(step, 1)
            nc.vector.tensor_copy(df[:, :], g.dstc[:, :]).then_inc(win, 1)
            dve.wait_ge(step, 1)
            nc.vector.tensor_copy(g.window[:, :], wi[:, :]).then_inc(step, 1)
            dve.wait_ge(win_sum, 1)
            nc.vector.tensor_tensor(g.local[:, 0:ET], df[:, :], g.ps[0][:, 0:ET], ALU.subtract).then_inc(step, 1)
            dve.wait_ge(step, 3)

        @block.tensor
        def _(pe):
            pe.wait_ge(win, 1)
            pe.wait_ge(consts, 7)
            nc.tensor.matmul(g.ps[0][:, 0:ET], g.ones[0:1, :], df[0:1, :], start=True, stop=True).then_inc(win_sum, 1)


def layer_norm(nc, g, table, meanwhile=None):
    with ExitStack() as stack:
        sem = lambda n: nc.alloc_semaphore(g.tag + n)
        stat, aggr, root, inv, normed, stored = (sem("ln_" + n) for n in ("stat", "aggr", "root", "inv", "normed", "stored"))
        block = stack.enter_context(nc.Block(g.tag + "layer_norm"))

        @block.vector
        def _(dve):
            for t in range(NT):
                nc.vector.bn_stats(g.stats[:, t, :], g.x[:, t, :]).then_inc(stat, 1)
            dve.wait_ge(stat, NT)
            for t in range(NT):
                nc.vector.bn_aggr(g.mv[:, t, :], g.stats[:, t, :]).then_inc(aggr, 1)
            dve.wait_ge(root, 1)
            nc.vector.reciprocal(g.rstd[:, :], g.rstd[:, :]).then_inc(inv, 1)
            dve.wait_ge(inv, 1)
            for t in range(NT):
                nc.vector.tensor_scalar(g.xn[:, t, :], g.x[:, t, :], g.mv[:, t, 0:1], g.rstd[:, t:t + 1],
                                        ALU.subtract, ALU.mult).then_inc(normed, 1)

        @block.scalar
        def _(act):
            act.wait_ge(aggr, NT)
            nc.scalar.activation(g.rstd[:, :], g.mv[:, :, 1], ACT.Sqrt, bias=g.eps[:, 0:1]).then_inc(root, 1)

        @block.sync
        def _(sp):
            if meanwhile is not None:
                meanwhile(sp)
            sp.wait_ge(normed, NT)
            if table is None:
                return
            sp.dma_start(table.rearrange("(t p) d -> p t d", p=P), g.xn[:, :, :]).then_inc(stored, 16)
            sp.wait_ge(stored, 16)


def copy_indices(nc, g, act, i, idx, copied, used):
    for h in range(2):
        act.wait_ge(used, U * i + (h + 1) * H)
        nc.scalar.activation(idx[:, h * H:(h + 1) * H], g.srcc[:, ds(U * i + h * H, H)], ACT.Copy).then_inc(copied, 1)


def copy_next_indices(nc, g, act, i, h, idx, copied, used):
    act.wait_ge(used, U * i + (h + 2) * H)
    nc.scalar.activation(idx[:, (1 - h) * H:(2 - h) * H], g.srcc[:, ds(U * i + (h + 1) * H, H)], ACT.Copy).then_inc(copied, 1)


def gather_sources(nc, g, pool, table, rows, idx, copied, used, claimed, gathered):
    with nc.gpsimd.Fori(0, ET // U) as i:
        for u in range(U):
            if u % H == 0:
                pool.wait_ge(copied, 2 * i + u // H + 1)
            pool.wait_ge(used, U * i + u + 1)
            pool.sem_inc(claimed, 1)
            nc.gpsimd.indirect_dma_start(rows[:, u, :], None, table,
                                         bass.IndirectOffsetOnAxis(ap=idx[:, u:u + 1].bitcast(U32), axis=0)).then_inc(gathered[u], 16)


def turn_sums(nc, g, name, chunks, den_t=None, den=None):
    with ExitStack() as stack:
        turned, back = nc.alloc_semaphore(g.tag + name + "_turned"), [nc.alloc_semaphore(g.tag + name + f"_back{k}") for k in range(2)]
        block = stack.enter_context(nc.Block(g.tag + name + "_turn_sums"))
        W, acc = chunks * P, g.acc[:, :, :].rearrange("p t d -> p (t d)")

        @block.tensor
        def _(pe):
            for t in range(NT):
                if t >= 4:
                    pe.wait_ge(back[t % 2], (t - 4) // 2 + 1)
                for c in range(chunks):
                    last = nc.tensor.transpose(g.ps[t % 4][:, c * P:(c + 1) * P], g.acct[:, c, t * P:(t + 1) * P], g.ident[:, :])
                if den is not None:
                    last = nc.tensor.transpose(g.ps[t % 4][:, W:W + HEADS], den_t[:, t * P:(t + 1) * P], g.ident[0:HEADS, 0:HEADS])
                last.then_inc(turned, 1)

        @block.vector
        def _(dve):
            for t in range(0, NT, 2):
                dve.wait_ge(turned, t + 1)
                last = nc.vector.tensor_copy(acc[:, t * W:(t + 1) * W], g.ps[t % 4][:, 0:W])
                if den is not None:
                    last = nc.vector.tensor_copy(den[:, t, :], g.ps[t % 4][:, W:W + HEADS])
                last.then_inc(back[0], 1)
            dve.wait_ge(back[0], NT // 2)

        @block.scalar
        def _(act):
            for t in range(1, NT, 2):
                act.wait_ge(turned, t + 1)
                last = nc.scalar.activation(acc[:, t * W:(t + 1) * W], g.ps[t % 4][:, 0:W], ACT.Copy)
                if den is not None:
                    last = nc.scalar.activation(den[:, t, :], g.ps[t % 4][:, W:W + HEADS], ACT.Copy)
                last.then_inc(back[1], 1)
            act.wait_ge(back[1], NT // 2)


def sum_edges(nc, g, table, width, count_degree=False, name="sum", meanwhile=None):
    chunks = width // P
    with ExitStack() as stack:
        sem = lambda n: nc.alloc_semaphore(g.tag + name + n)
        sb = lambda n, s, d=F32: stack.enter_context(nc.sbuf_tensor(g.tag + name + n, s, d))
        gathered = [sem(f"gathered{u}") for u in range(U)]
        copied, hot, summed, added, cleared, claimed = sem("idx_copied"), sem("hot_ready"), sem("tile_summed"), sem("tile_added"), sem("acc_cleared"), sem("slot_claimed")
        idx, rows, onehot = sb("gather_idx", [P, U], I32), sb("gathered_rows", [P, U, width]), sb("onehot", [P, 4, P])
        deg_row = sb("deg_row", [1, ROWS]) if count_degree else None
        with ExitStack() as s2:
            block = s2.enter_context(nc.Block(g.tag + name + "sum_edges"))

            @block.gpsimd
            def _(pool):
                gather_sources(nc, g, pool, table, rows, idx, copied, summed, claimed, gathered)

            @block.scalar
            def _(act):
                with nc.scalar.Fori(0, ET // U) as i:
                    copy_indices(nc, g, act, i, idx, copied, summed)

            @block.sync
            def _(sp):
                if meanwhile is not None:
                    meanwhile(sp)

            @block.tensor
            def _(pe):
                pe.sem_inc(summed, U)
                with nc.tensor.Fori(0, ET // U) as i:
                    for u in range(U):
                        pe.wait_ge(hot, U * i + u + 1)
                        pe.wait_ge(added, U * i + u + 1)
                        pe.wait_ge(gathered[u], 16 * (i + 1))
                        if count_degree:
                            nc.tensor.matmul(g.ps[4 + u % 4][0:1, 0:P], g.ones[:, 0:1], onehot[:, u % 4, :], start=True, stop=True)
                        for c in range(chunks):
                            last = nc.tensor.matmul(g.ps[u % 4][:, c * P:(c + 1) * P], rows[:, u, c * P:(c + 1) * P],
                                                    onehot[:, u % 4, :], start=True, stop=True)
                        last.then_inc(summed, 1)

            @block.vector
            def _(dve):
                base = [nc.vector.alloc_register(g.tag + name + f"base{u}") for u in range(8)]
                nc.vector.memset(g.acct[:, 0:chunks, :], 0.0).then_inc(cleared, 1)
                if count_degree:
                    nc.vector.memset(deg_row[:, :], 0.0).then_inc(cleared, 1)
                dve.wait_ge(cleared, 1 + count_degree)

                def build(n, slot):
                    nc.vector.tensor_scalar(onehot[:, slot, :], g.iota[:, 0:P], g.local[:, ds(n, 1)], None, ALU.is_equal).then_inc(hot, 1)
                build(0, 0)
                build(1, 1)
                nc.vector.sem_inc(added, 4)
                with nc.vector.Fori(0, ET // U) as i:
                    for u in range(U):
                        if u % 8 == 0:
                            nc.vector.reg_load(base, g.dstc[0:1, ds(U * i + u, 8)])
                        build(U * i + u + 2, (u + 2) % 4)
                        b = nc.vector.snap(base[u % 8], min_val=0, max_val=ROWS - P)
                        dve.wait_ge(summed, U * i + u + 1 + U)
                        dve.wait_ge(added, U * i + u + 4)
                        if count_degree:
                            nc.vector.tensor_tensor(deg_row[:, ds(b, P)], deg_row[:, ds(b, P)], g.ps[4 + u % 4][0:1, 0:P], ALU.add)
                        nc.vector.tensor_tensor(g.acct[:, 0:chunks, ds(b, P)], g.acct[:, 0:chunks, ds(b, P)],
                                                g.ps[u % 4][:, 0:width].rearrange("p (c n) -> p c n", c=chunks), ALU.add).then_inc(added, 1)
        if count_degree:
            with ExitStack() as s2:
                turned, placed = sem("deg_turned"), sem("deg_placed")
                block = s2.enter_context(nc.Block(g.tag + name + "turn_degree"))

                @block.tensor
                def _(pe):
                    for t in range(NT):
                        last = nc.tensor.matmul(g.ps[0][:, t:t + 1], deg_row[0:1, t * P:(t + 1) * P], g.ones[0:1, 0:1], start=True, stop=True)
                    last.then_inc(turned, 1)

                @block.vector
                def _(dve):
                    dve.wait_ge(turned, 1)
                    nc.vector.tensor_copy(g.deg[:, :], g.ps[0][:, 0:NT]).then_inc(placed, 1)
                    dve.wait_ge(placed, 1)
    turn_sums(nc, g, name, chunks)


def project(nc, g, name, weights, bias, width, stage, finish, chunks=2, meanwhile=None):
    K = len(weights)
    with ExitStack() as stack:
        sem = lambda n: nc.alloc_semaphore(g.tag + name + n)
        staged = [sem(f"_staged{k}") for k in range(K)]
        turned, lhs_ready, product, used = sem("_turned"), sem("_lhs_ready"), sem("_product"), sem("_used")
        rows = stack.enter_context(nc.sbuf_tensor(g.tag + name + "_rows", [P, 2, K, chunks * P], F32))
        lhs = stack.enter_context(nc.sbuf_tensor(g.tag + name + "_lhs", [P, 2, K * chunks * P], F32))
        block = stack.enter_context(nc.Block(g.tag + name))

        def staging(eng, who, t, s):
            for k in range(K):
                if stage[k][0] == who:
                    eng.wait_ge(turned, t + 1)
                    stage[k][1](rows[:, s, k, :], t).then_inc(staged[k], 1)

        @block.sync
        def _(sp):
            if meanwhile is not None:
                meanwhile(sp)

        @block.gpsimd
        def _(pool):
            if any(who == "pool" for who, f in stage):
                with nc.gpsimd.Fori(0, NT // 2) as i:
                    for s in range(2):
                        staging(pool, "pool", 2 * i + s, s)

        @block.tensor
        def _(pe):
            pe.sem_inc(turned, 2)
            pe.sem_inc(product, 2)
            def turn(i):
                for s in range(2):
                    t = 2 * i + s
                    pe.wait_ge(lhs_ready, t + 1)
                    for k in range(K):
                        pe.wait_ge(staged[k], t + 1)
                        for c in range(chunks):
                            last = nc.tensor.transpose(g.ps[s][:, (chunks * k + c) * P:(chunks * k + c + 1) * P],
                                                       rows[:, s, k, c * P:(c + 1) * P], g.ident[:, :])
                    last.then_inc(turned, 1)

            def multiply(i):
                for s in range(2):
                    t = 2 * i + s
                    pe.wait_ge(lhs_ready, t + 3)
                    pe.wait_ge(used, t + 1)
                    if bias is not None:
                        nc.tensor.matmul(g.ps[2 + s][:, 0:width], g.ones[0:1, :], bias, start=True, stop=False)
                    for k in range(K):
                        for c in range(chunks):
                            last = nc.tensor.matmul(g.ps[2 + s][:, 0:width], lhs[:, s, (chunks * k + c) * P:(chunks * k + c + 1) * P],
                                                    weights[k][:, c, 0:width], start=(bias is None and k == 0 and c == 0),
                                                    stop=(k == K - 1 and c == chunks - 1))
                    last.then_inc(product, 1)

            turn(0)
            with nc.tensor.Fori(0, NT // 2 - 1) as i:
                turn(i + 1)
                multiply(i)
            multiply(NT // 2 - 1)

        @block.scalar
        def _(act):
            act.sem_inc(lhs_ready, 2)
            with nc.scalar.Fori(0, NT // 2) as i:
                for s in range(2):
                    t = 2 * i + s
                    staging(act, "act", t, s)
                    act.wait_ge(turned, t + 3)
                    act.wait_ge(product, t + 1)
                    nc.scalar.activation(lhs[:, s, :], g.ps[s][:, 0:K * chunks * P], ACT.Copy).then_inc(lhs_ready, 1)

        @block.vector
        def _(dve):
            dve.sem_inc(used, 2)
            def stage_pair(i):
                for s in range(2):
                    staging(dve, "dve", 2 * i + s, s)

            def finish_pair(i):
                for s in range(2):
                    t = 2 * i + s
                    dve.wait_ge(product, t + 3)
                    finish(dve, g.ps[2 + s][:, 0:width], t, s).then_inc(used, 1)

            stage_pair(0)
            with nc.vector.Fori(0, NT // 2 - 1) as i:
                stage_pair(i + 1)
                finish_pair(i)
            finish_pair(NT // 2 - 1)


def load_weights(nc, g, name, pairs):
    with ExitStack() as stack:
        loaded = nc.alloc_semaphore(g.tag + name + "_loaded")
        block = stack.enter_context(nc.Block(g.tag + name + "_load"))

        @block.sync
        def _(sp):
            for dst, src in pairs:
                sp.dma_start(dst, src).then_inc(loaded, 16)
            sp.wait_ge(loaded, 16 * len(pairs))


def loads(nc, g, name, pairs):
    loaded = nc.alloc_semaphore(g.tag + name + "_loaded")

    def run(sp):
        for dst, src in pairs:
            sp.dma_start(dst, src).then_inc(loaded, 16)
        sp.wait_ge(loaded, 16 * len(pairs))
    return run


def rows_in(w, c=P):
    return w.rearrange("(c p) n -> p c n", p=c)


def across(v):
    return v.rearrange("(o n) -> o n", o=1).to_broadcast([P, v.shape[0]])


def layer0_gnn(nc, g, a, table):
    with ExitStack() as stack:
        sb = lambda n, s: stack.enter_context(nc.sbuf_tensor(g.tag + n, s, F32))
        w_self, w_neigh, b_self, inv = sb("w_self", [P, 2, D]), sb("w_neigh", [P, 2, D]), sb("b_self", [1, D]), sb("inv_deg", [P, NT])
        layer_norm(nc, g, table, loads(nc, g, "l0g", [(w_self[:, :, :], rows_in(a.l0g_w_self_t)), (w_neigh[:, :, :], rows_in(a.l0g_w_neigh_t)),
                                                      (b_self[:, :], a.l0g_b_self)]))
        layer0_sums(nc, g, table)
        layer0_products(nc, g, w_self, w_neigh, b_self, inv)


def layer0_sums(nc, g, table):
    g.tables = source_tables(nc)
    with ExitStack() as stack:
        zeros = stack.enter_context(nc.sbuf_tensor(g.tag + "zeros", [P, 4 * D], F32))
        zero, zeroed = nc.alloc_semaphore(g.tag + "zero"), nc.alloc_semaphore(g.tag + "zeroed")

        def meanwhile(sp):
            sp.wait_ge(zero, 1)
            clear_tables(nc, g, sp, zeros, g.tables, zeroed)
        with ExitStack() as s2:
            block = s2.enter_context(nc.Block(g.tag + "zeros"))

            @block.vector
            def _(dve):
                nc.vector.memset(zeros[:, :], 0.0).then_inc(zero, 1)
        sum_edges(nc, g, table, D, count_degree=True, meanwhile=meanwhile)


def layer0_products(nc, g, w_self, w_neigh, b_self, inv):
    with ExitStack() as s2:
        step = nc.alloc_semaphore(g.tag + "inv_step")
        block = s2.enter_context(nc.Block(g.tag + "inv_degree"))

        @block.vector
        def _(dve):
            nc.vector.tensor_scalar(inv[:, :], g.deg[:, :], 1.0, None, ALU.max).then_inc(step, 1)
            dve.wait_ge(step, 1)
            nc.vector.reciprocal(inv[:, :], inv[:, :]).then_inc(step, 1)
            dve.wait_ge(step, 2)

    project(nc, g, "l0g", [w_self, w_neigh], b_self[0:1, :], D,
            [("pool", lambda out, t: nc.gpsimd.tensor_copy(out, g.xn[:, ds(t, 1), :])),
             ("dve", lambda out, t: nc.vector.tensor_scalar(out, g.acc[:, ds(t, 1), :], inv[:, ds(t, 1)], None, ALU.mult))],
            lambda dve, bank, t, s: nc.vector.tensor_tensor(g.x[:, ds(t, 1), :], g.x[:, ds(t, 1), :], bank, ALU.add))


def turn_nodes(nc, g, xnt):
    with ExitStack() as stack:
        turned, placed = nc.alloc_semaphore(g.tag + "turn_turned"), [nc.alloc_semaphore(g.tag + f"turn_placed{k}") for k in range(2)]
        block = stack.enter_context(nc.Block(g.tag + "turn_nodes"))
        placing = lambda t: (xnt[:, :, t * P:(t + 1) * P], g.ps[t % 4][:, 0:D].rearrange("p (c n) -> p c n", c=2))

        @block.tensor
        def _(pe):
            for t in range(NT):
                if t >= 4:
                    pe.wait_ge(placed[t % 2], (t - 4) // 2 + 1)
                nc.tensor.transpose(g.ps[t % 4][:, 0:P], g.xn[:, t, 0:P], g.ident[:, :])
                nc.tensor.transpose(g.ps[t % 4][:, P:D], g.xn[:, t, P:D], g.ident[:, :]).then_inc(turned, 1)

        @block.vector
        def _(dve):
            for t in range(0, NT, 2):
                dve.wait_ge(turned, t + 1)
                nc.vector.tensor_copy(*placing(t)).then_inc(placed[0], 1)

        @block.scalar
        def _(act):
            for t in range(1, NT, 2):
                act.wait_ge(turned, t + 1)
                nc.scalar.activation(*placing(t), ACT.Copy).then_inc(placed[1], 1)


KEEP = max(1, int(0.5 * NODES)) - 1
H0 = 1024
NEG = -3.0e38


def layer0_ffn(nc, g, a, table):
    scratch = nc.dram_tensor("score_scratch", (ROWS,), F32).ap()
    with ExitStack() as stack:
        sb = lambda n, s: stack.enter_context(nc.sbuf_tensor(g.tag + n, s, F32))
        wr, br = sb("wr_rows", [P, D]), sb("br", [P, 1])
        w1, b1, w2, b2 = sb("l0_w1", [P, 2, H0]), sb("l0_b1", [P, H0 // P]), sb("l0_w2", [P, H0 // P, D]), sb("l0_b2", [1, D])
        scores, gate, srow, xnt = sb("scores", [P, NT]), sb("gate", [P, NT]), sb("score_row", [P, ROWS]), g.acct
        layer_norm(nc, g, None, loads(nc, g, "l0f", [(wr[:, :], across(a.l0f_wr)), (br[:, :], across(a.l0f_br)), (w1[:, :, :], rows_in(a.l0f_w1)),
                                 (b1[:, :], a.l0f_b1_cols), (w2[:, :, :], rows_in(a.l0f_w2)), (b2[:, :], a.l0f_b2)]))
        turn_nodes(nc, g, xnt)
        G = 2 * P
        NF = H0 // P
        with ExitStack() as s2:
            sem = lambda n: nc.alloc_semaphore(g.tag + "mod_" + n)
            ranked, selected, hidden, active, summed, used, passed = (sem(n) for n in
                ("ranked", "selected", "hidden", "active", "summed", "used", "passed"))
            above, ahead, same = (s2.enter_context(nc.sbuf_tensor(g.tag + n, [P, NT], F32)) for n in ("above", "ahead", "same"))
            junk = s2.enter_context(nc.sbuf_tensor(g.tag + "rank_junk", [P, 3, ROWS], F32))
            before = s2.enter_context(nc.sbuf_tensor(g.tag + "before", [P, P], F32))
            dot, scored, turned_scores, copied, stored, across_in = (sem(n) for n in ("dot", "scored", "turned_scores", "scores_copied", "scores_stored", "scores_across"))
            prod, score_rows = (s2.enter_context(nc.sbuf_tensor(g.tag + n, s, F32)) for n, s in (("router_prod", [P, 4, D]), ("score_rows", [NT, P])))
            ht = s2.enter_context(nc.sbuf_tensor(g.tag + "hidden_t", [P, NF, G], F32))
            block = s2.enter_context(nc.Block(g.tag + "mod_ffn"))

            @block.gpsimd
            def _(pool):
                nc.gpsimd.affine_select(out=before[:, :], in_=g.ones[:, :], compare_op=ALU.is_gt, fill=0.0, base=0,
                                        pattern=[[-1, P]], channel_multiplier=1).then_inc(passed, 1)
                with nc.gpsimd.Fori(0, NT) as t:
                    nc.gpsimd.tensor_tensor(g.x[:, ds(t, 1), :], g.x[:, ds(t, 1), :], g.xn[:, ds(t, 1), :], ALU.add).then_inc(passed, 1)

            @block.sync
            def _(sp):
                sp.wait_ge(copied, 1)
                sp.dma_start(scratch.rearrange("(t p) -> t p", p=P), score_rows[:, :]).then_inc(stored, 16)
                sp.wait_ge(stored, 16)
                sp.dma_start(srow[:, :], across(scratch)).then_inc(across_in, 16)

            @block.tensor
            def _(pe):
                pe.wait_ge(scored, 1)
                nc.tensor.transpose(g.ps[6][0:NT, 0:P], scores[:, 0:NT], g.ident[:, :]).then_inc(turned_scores, 1)
                pe.sem_inc(hidden, 4)
                with nc.tensor.Fori(0, ROWS // G) as i:
                    for f in range(NF):
                        pe.wait_ge(active, NF * i + f + 1)
                        for c in range(2):
                            last = nc.tensor.matmul(g.ps[f % 4][:, 0:G], w1[:, c, f * P:(f + 1) * P],
                                                    xnt[:, c, ds(i * G, G)], start=(c == 0), stop=(c == 1))
                        last.then_inc(hidden, 1)
                    for s in range(2):
                        pe.wait_ge(used, 2 * i + s + 1)
                        nc.tensor.matmul(g.ps[4 + s][:, 0:D], g.ones[0:1, :], b2[0:1, :], start=True, stop=False)
                        for f in range(NF):
                            if s == 0:
                                pe.wait_ge(active, NF * i + f + 5)
                            last = nc.tensor.matmul(g.ps[4 + s][:, 0:D], ht[:, f, s * P:(s + 1) * P], w2[:, f, :],
                                                    start=False, stop=(f == NF - 1))
                        last.then_inc(summed, 1)

            @block.scalar
            def _(act):
                act.sem_inc(active, 4)
                act.sem_inc(summed, 2)
                act.sem_inc(used, 2)
                with nc.scalar.Fori(0, ROWS // G) as i:
                    for f in range(NF):
                        act.wait_ge(hidden, NF * i + f + 5)
                        if f == 0:
                            act.wait_ge(summed, 2 * i + 2)
                        nc.scalar.activation(ht[:, f, :], g.ps[f % 4][:, 0:G], ACT.Gelu_apprx_tanh,
                                             bias=b1[:, f:f + 1]).then_inc(active, 1)
                    for s in range(2):
                        act.wait_ge(summed, 2 * i + s + 3)
                        nc.scalar.activation(g.acc[:, ds(2 * i + s, 1), :], g.ps[4 + s][:, 0:D], ACT.Copy).then_inc(used, 1)

            @block.vector
            def _(dve):
                for t in range(NT):
                    if t >= 4:
                        dve.wait_ge(dot, t - 3)
                    nc.vector.scalar_tensor_tensor(out=prod[:, t % 4, :], in0=g.xn[:, t, :], scalar=1.0, in1=wr[:, :],
                                                   op0=ALU.mult, op1=ALU.mult, accum_out=scores[:, t:t + 1]).then_inc(dot, 1)
                dve.wait_ge(dot, NT)
                nc.vector.tensor_scalar(scores[:, :], scores[:, :], br[:, 0:1], None, ALU.add).then_inc(scored, 1)
                dve.wait_ge(turned_scores, 1)
                nc.vector.tensor_copy(score_rows[:, :], g.ps[6][0:NT, 0:P]).then_inc(copied, 1)
                dve.wait_ge(across_in, 16)
                dve.wait_ge(passed, 1)
                n = 0
                for t in range(FULL + 1):
                    for k, (lo, hi, op, to) in enumerate(((0, t * P, ALU.is_ge, ahead), (t * P, NODES, ALU.is_gt, above))):
                        if n >= 3:
                            dve.wait_ge(ranked, n - 2)
                        if hi > lo:
                            nc.vector.tensor_scalar(junk[:, k, lo:hi], srow[:, lo:hi], scores[:, t:t + 1], 0.0, op, ALU.add,
                                                    accum_out=to[:, t:t + 1]).then_inc(ranked, 1)
                        else:
                            nc.vector.memset(to[:, t:t + 1], 0.0).then_inc(ranked, 1)
                        n += 1
                    w = min(P, NODES - t * P)
                    if n >= 3:
                        dve.wait_ge(ranked, n - 2)
                    nc.vector.scalar_tensor_tensor(out=junk[:, 2, 0:w], in0=srow[:, t * P:t * P + w], scalar=scores[:, t:t + 1],
                                                   in1=before[:, 0:w], op0=ALU.is_equal, op1=ALU.mult,
                                                   accum_out=same[:, t:t + 1]).then_inc(ranked, 1)
                    n += 1
                for to in (above, ahead, same):
                    nc.vector.memset(to[:, FULL + 1:NT], 0.0).then_inc(ranked, 1)
                    n += 1
                dve.wait_ge(ranked, n)
                nc.vector.tensor_tensor(above[:, :], above[:, :], ahead[:, :], ALU.add).then_inc(selected, 1)
                dve.wait_ge(selected, 1)
                nc.vector.tensor_tensor(above[:, :], above[:, :], same[:, :], ALU.add).then_inc(selected, 1)
                dve.wait_ge(selected, 2)
                nc.vector.scalar_tensor_tensor(out=gate[:, :], in0=above[:, :], scalar=float(KEEP), in1=scores[:, :],
                                               op0=ALU.is_lt, op1=ALU.mult).then_inc(selected, 1)
                dve.wait_ge(selected, 3)
                dve.wait_ge(passed, NT + 1)
                dve.wait_ge(used, NT + 2)
                with nc.vector.Fori(0, NT) as t:
                    nc.vector.scalar_tensor_tensor(out=g.x[:, ds(t, 1), :], in0=g.acc[:, ds(t, 1), :], scalar=gate[:, ds(t, 1)],
                                                   in1=g.x[:, ds(t, 1), :], op0=ALU.mult, op1=ALU.add)


HEADS, HD = 8, 32
BF16 = mybir.dt.bfloat16
ENC = 3 * 3 * 3 + 3
SLOPE = 0.2
CH = 16
CT = ET // CH
CE = CT * P
AW = HEADS + D + HEADS


def layer1_gnn(nc, g, a, table):
    htable = nc.dram_tensor("gat_rows", (ROWS, D), F32).ap()
    stable = nc.dram_tensor("gat_source_scores", (ROWS, HEADS), F32).ap()
    with ExitStack() as stack:
        sb = lambda n, s, d=F32: stack.enter_context(nc.sbuf_tensor(g.tag + n, s, d))
        alpha = sb("alpha", [P, ET, HEADS])
        den = sb("denominator", [P, NT, HEADS])
        gat_features(nc, g, a, htable, stable, alpha)
        edge_softmax(nc, g, a, alpha)
        weighted_sum(nc, g, htable, alpha, den)
        with ExitStack() as s2:
            bias = s2.enter_context(nc.sbuf_tensor(g.tag + "bias", [P, D], F32))
            load_weights(nc, g, "gat_bias", [(bias[:, :], across(a.l1g_bias))])
            step = nc.alloc_semaphore(g.tag + "out_step")
            block = s2.enter_context(nc.Block(g.tag + "gat_out"))
            heads = lambda v: v.rearrange("p t (h d) -> p (t h) d", d=HD)

            @block.vector
            def _(dve):
                nc.vector.tensor_scalar(den[:, :, :], den[:, :, :], 1e-10, None, ALU.max).then_inc(step, 1)
                dve.wait_ge(step, 1)
                nc.vector.reciprocal(den[:, :, :], den[:, :, :]).then_inc(step, 1)
                dve.wait_ge(step, 2)
                nc.vector.tensor_tensor(heads(g.acc[:, :, :]), heads(g.acc[:, :, :]),
                                        den[:, :, :].rearrange("p t h -> p (t h)").unsqueeze(2).to_broadcast([P, NT * HEADS, HD]),
                                        ALU.mult).then_inc(step, 1)
                dve.wait_ge(step, 3)
                nc.vector.tensor_tensor(g.x[:, :, :], g.x[:, :, :], g.acc[:, :, :], ALU.add).then_inc(step, 1)
                dve.wait_ge(step, 4)
                nc.vector.tensor_tensor(g.x[:, :, :], g.x[:, :, :], bias[:, :].unsqueeze(1).to_broadcast([P, NT, D]),
                                        ALU.add).then_inc(step, 1)
                dve.wait_ge(step, 5)


def gat_features(nc, g, a, htable, stable, alpha):
    with ExitStack() as stack:
        sb = lambda n, s, d=F32: stack.enter_context(nc.sbuf_tensor(g.tag + n, s, d))
        wt, w, acol, blockd = sb("w_t", [P, 2, AW]), sb("w", [P, 2, D]), sb("a_cols", [P, 4]), sb("a_blocks", [P, 2, 2 * HEADS])
        hs = sb("h_nodes", [P, NT, AW])
        edge_w, w_rows = sb("edge_w", [4, D]), sb("edge_w_rows", [ENC, D], BF16)
        layer_norm(nc, g, None, loads(nc, g, "gat", [(wt[:, :, HEADS:HEADS + D], rows_in(a.l1g_w_t)), (w[:, :, :], rows_in(a.l1g_w)),
                                    (acol[:, 0:2], a.l1g_a_src_cols), (acol[:, 2:4], a.l1g_a_dst_cols),
                                    (edge_w[0:3, :], a.l1g_edge_w_t), (edge_w[3:4, :], a.l1g_edge_b)]))
        with ExitStack() as s2:
            sem = lambda n: nc.alloc_semaphore(g.tag + n)
            spread, masked, folded, placed = sem("a_spread"), sem("a_masked"), sem("a_folded"), sem("a_placed")
            block = s2.enter_context(nc.Block(g.tag + "fold_scores"))

            @block.vector
            def _(dve):
                for c in range(2):
                    for k in range(2):
                        nc.vector.tensor_scalar(blockd[:, c, k * HEADS:(k + 1) * HEADS], g.ones[:, 0:HEADS],
                                                acol[:, 2 * k + c:2 * k + c + 1], None, ALU.mult).then_inc(spread, 1)
                dve.wait_ge(folded, 1)
                for c in range(2):
                    nc.vector.tensor_copy(wt[:, c, 0:HEADS], g.ps[c][:, 0:HEADS]).then_inc(placed, 1)
                    nc.vector.tensor_copy(wt[:, c, HEADS + D:AW], g.ps[c][:, HEADS:2 * HEADS]).then_inc(placed, 1)
                dve.wait_ge(placed, 4)

            @block.gpsimd
            def _(pool):
                pool.wait_ge(spread, 4)
                for c in range(2):
                    v = blockd[:, c, :].rearrange("p (k h) -> p k h", k=2)
                    nc.gpsimd.affine_select(out=v, in_=v, compare_op=ALU.is_ge, fill=0.0, base=c * P,
                                            pattern=[[0, 2], [-HD, HEADS]], channel_multiplier=1).then_inc(masked, 1)
                pool.wait_ge(masked, 2)
                for c in range(2):
                    v = blockd[:, c, :].rearrange("p (k h) -> p k h", k=2)
                    nc.gpsimd.affine_select(out=v, in_=v, compare_op=ALU.is_ge, fill=0.0, base=HD - 1 - c * P,
                                            pattern=[[0, 2], [HD, HEADS]], channel_multiplier=-1).then_inc(masked, 1)

            @block.tensor
            def _(pe):
                pe.wait_ge(masked, 4)
                for m in range(2):
                    for c in range(2):
                        last = nc.tensor.matmul(g.ps[m][:, 0:2 * HEADS], w[:, c, m * P:(m + 1) * P], blockd[:, c, :],
                                                start=(c == 0), stop=(c == 1))
                last.then_inc(folded, 1)

        project(nc, g, "gat_h", [wt], None, AW,
                [("pool", lambda out, t: nc.gpsimd.tensor_copy(out, g.xn[:, ds(t, 1), :]))],
                lambda dve, bank, t, s: nc.vector.tensor_copy(hs[:, ds(t, 1), :], bank))
        with ExitStack() as s2:
            stored = nc.alloc_semaphore(g.tag + "h_stored")
            block = s2.enter_context(nc.Block(g.tag + "store_h"))

            @block.sync
            def _(sp):
                sp.dma_start(htable.rearrange("(t p) d -> p t d", p=P), hs[:, :, HEADS:HEADS + D]).then_inc(stored, 16)
                sp.dma_start(stable.rearrange("(t p) d -> p t d", p=P), hs[:, :, 0:HEADS]).then_inc(stored, 16)
                sp.wait_ge(stored, 32)
        attr_parts = split_encoding(nc, g, a, edge_w, w_rows)
        edge_scores(nc, g, hs, a, attr_parts, w_rows, stable, alpha)


def split_encoding(nc, g, a, edge_w, w_rows):
    parts = nc.dram_tensor("attr_parts", (3, 3 * ET * P), BF16).ap()
    w_parts = nc.dram_tensor("edge_w_parts", (3, 4, D), BF16).ap()
    with ExitStack() as stack:
        sb = lambda n, s, d=F32: stack.enter_context(nc.sbuf_tensor(g.tag + "x_" + n, s, d))
        step, loaded, stored, placed = (nc.alloc_semaphore(g.tag + "x_" + n) for n in ("step", "loaded", "stored", "placed"))
        n = 3 * ET
        attr, rest, split = sb("attr", [P, n]), sb("rest", [P, n]), sb("split", [P, 3, n], BF16)
        w_rest, w_split = sb("w_rest", [4, D]), sb("w_split", [4, 3, D], BF16)
        block = stack.enter_context(nc.Block(g.tag + "split_encoding"))

        @block.sync
        def _(sp):
            sp.dma_start(attr[:, :], a.edge_attr_flat).then_inc(loaded, 16)
            sp.wait_ge(step, 10)
            sp.dma_start(w_parts.rearrange("j k d -> k j d"), w_split[:, :, :]).then_inc(stored, 16)
            sp.dma_start(parts.rearrange("i (p n) -> p i n", p=P), split[:, :, :]).then_inc(stored, 16)
            sp.wait_ge(stored, 32)
            for j in range(3):
                for i in range(3):
                    sp.dma_start(w_rows[9 * j + 3 * i:9 * j + 3 * i + 3, :], w_parts[j, 0:3, :]).then_inc(placed, 16)
            sp.dma_start(w_rows[27:ENC, :], w_parts[:, 3, :]).then_inc(placed, 16)
            sp.wait_ge(placed, 160)

        @block.vector
        def _(dve):
            count = [0]

            def done(ins):
                count[0] += 1
                ins.then_inc(step, 1)
                dve.wait_ge(step, count[0])

            def three(v, rest, out):
                done(nc.vector.tensor_copy(out(0), v))
                done(nc.vector.tensor_tensor(rest, v, out(0), ALU.subtract))
                done(nc.vector.tensor_copy(out(1), rest))
                done(nc.vector.tensor_tensor(rest, rest, out(1), ALU.subtract))
                done(nc.vector.tensor_copy(out(2), rest))
            three(edge_w[:, :], w_rest[:, :], lambda k: w_split[:, k, :])
            dve.wait_ge(loaded, 16)
            three(attr[:, :], rest[:, :], lambda k: split[:, k, :])
    return parts


def edge_scores(nc, g, hs, a, attr_parts, w_rows, stable, alpha):
    with ExitStack() as stack:
        sem = lambda n: nc.alloc_semaphore(g.tag + "s_" + n)
        gathered = [sem(f"gathered{u}") for u in range(U)]
        attrs = [sem(f"attrs{q}") for q in range(PARTS)]
        copied, claimed, hot, looked, encoded, relued, based, mixed, reduced = (sem(n) for n in (
            "idx_copied", "claimed", "hot", "looked_up", "encoded", "relued", "based", "mixed", "reduced"))
        sb = lambda n, s, d=F32: stack.enter_context(nc.sbuf_tensor(g.tag + "s_" + n, s, d))
        idx, rows = sb("idx", [P, U], I32), sb("rows", [P, U, HEADS])
        dst, onehot_t = sb("dst_across", [P, PARTS, Q * P], I32), sb("onehot_t", [P, 4, 2, P])
        enc, mix, edge_attr = sb("enc", [P, 4, D]), sb("mix", [P, 4, D]), sb("edge_attr", [ENC, PARTS, Q * P], BF16)
        ones_set = sem("ones_set")
        base_score = sb("base_score", [P, ET, HEADS])
        block = stack.enter_context(nc.Block(g.tag + "edge_scores"))
        hflat = hs[:, :, :].rearrange("p t d -> p (t d)")

        @block.gpsimd
        def _(pool):
            gather_sources(nc, g, pool, stable, rows, idx, copied, based, claimed, gathered)

        @block.sync
        def _(sp):
            sp.wait_ge(ones_set, 1)
            by_part = attr_parts.rearrange("i (k n) -> (i k) n", k=3)
            with nc.sync.Fori(0, ET // U) as i:
                for q in range(PARTS):
                    sp.wait_ge(mixed, U * i + (q + 1) * Q)
                    at = PARTS * i + q
                    sp.dma_start(dst[:, q, :], a.dst_row[ds(at * (Q * P) + 1, Q * P)]
                                 .rearrange("(o n) -> o n", o=1).to_broadcast([P, Q * P])).then_inc(attrs[q], 16)
                    for j in range(3):
                        sp.dma_start(edge_attr[9 * j:9 * j + 9, q, :], by_part[:, ds(at * (Q * P), Q * P)]).then_inc(attrs[q], 16)

        @block.tensor
        def _(pe):
            window = [nc.tensor.alloc_register(g.tag + f"pe_window{u}") for u in range(8)]
            pe.sem_inc(looked, 4)
            pe.sem_inc(encoded, 2)
            with nc.tensor.Fori(0, ET // U) as i:
                for u in range(U):
                    n = U * i + u
                    if u % 8 == 0:
                        nc.tensor.reg_load(window, g.window[0:1, ds(U * i + u, 8)])
                    if u % Q == 0:
                        pe.wait_ge(attrs[u // Q], 64 * (i + 1))
                    pe.wait_ge(relued, n + 1)
                    nc.tensor.matmul(g.ps[u % 4][:, 0:D], edge_attr[:, u // Q, u % Q * P:(u % Q + 1) * P], w_rows[:, :],
                                     start=True, stop=True).then_inc(encoded, 1)
                    w = nc.tensor.snap(window[u % 8], min_val=0, max_val=NT - 2)
                    pe.wait_ge(hot, n + 1)
                    pe.wait_ge(based, n + U - 3)
                    for k in range(2):
                        last = nc.tensor.matmul(g.ps[4 + u % 4][:, 0:D + HEADS], onehot_t[:, u % 4, k, :],
                                                hflat[:, ds(w * AW + (k * AW + HEADS), D + HEADS)], start=(k == 0), stop=(k == 1))
                    last.then_inc(looked, 1)

        @block.scalar
        def _(act):
            act.sem_inc(relued, 4)
            nc.scalar.activation(idx[:, 0:H], g.srcc[:, 0:H], ACT.Copy).then_inc(copied, 1)
            with nc.scalar.Fori(0, ET // U) as i:
                for u in range(U):
                    if u % H == 0:
                        copy_next_indices(nc, g, act, i, u // H, idx, copied, based)
                    n = U * i + u
                    act.wait_ge(encoded, n + 3)
                    act.wait_ge(mixed, n + U - 3)
                    nc.scalar.activation(enc[:, u % 4, :], g.ps[u % 4][:, 0:D], ACT.Relu).then_inc(relued, 1)

        @block.vector
        def _(dve):
            window = [nc.vector.alloc_register(g.tag + f"dve_window{u}") for u in range(8)]
            nc.vector.memset(edge_attr[:, :, :], 1.0).then_inc(ones_set, 1)
            dve.sem_inc(based, U)
            dve.sem_inc(mixed, U)

            def use(i, n, u):
                dve.wait_ge(looked, n + 5)
                dve.wait_ge(relued, n + 5)
                nc.vector.tensor_tensor(mix[:, u % 4, :], g.ps[4 + u % 4][:, 0:D], enc[:, u % 4, :], ALU.mult).then_inc(mixed, 1)
                dve.wait_ge(gathered[u], 16 * (i + 1))
                nc.vector.tensor_tensor(base_score[:, ds(n, 1), :], g.ps[4 + u % 4][:, D:D + HEADS].unsqueeze(1),
                                        rows[:, u, 0:HEADS].unsqueeze(1), ALU.add).then_inc(based, 1)

            def reduce(n, u):
                dve.wait_ge(mixed, n + U + 1)
                nc.vector.tensor_reduce(alpha[:, ds(n, 1), :], mix[:, u % 4, :].rearrange("p (o h d) -> p o h d", o=1, d=HD),
                                        AX.X, ALU.add).then_inc(reduced, 1)

            def build(i, n, u, w):
                if u % Q == 0:
                    dve.wait_ge(attrs[u // Q], 64 * (i + 1))
                nc.vector.tensor_tensor(onehot_t[:, u % 4, :, :], dst[:, u // Q, u % Q * P:(u % Q + 1) * P].unsqueeze(1).to_broadcast([P, 2, P]),
                                        g.node_id[:, ds(w, 2)].unsqueeze(2).to_broadcast([P, 2, P]), ALU.is_equal).then_inc(hot, 1)

            LAG = 2
            nc.vector.reg_load(window, g.window[0:1, 0:8])
            for u in range(LAG):
                build(0, u, u, nc.vector.snap(window[u], min_val=0, max_val=NT - 2))

            def round(i, first=False, last=False):
                for u in range(U):
                    if u % 8 == 0:
                        k = 8 - LAG if last and u else 8
                        nc.vector.reg_load(window[0:k], g.window[0:1, ds(U * i + u + LAG, k)])
                    m = u + LAG
                    if not (last and m >= U):
                        w = nc.vector.snap(window[u % 8], min_val=0, max_val=NT - 2)
                        build(i + m // U, U * i + m, m % U, w)
                    use(i, U * i + u, u)
                    if not (first and u == 0):
                        reduce(U * i + u - 1, (u - 1) % U)
            round(0, first=True)
            with nc.vector.Fori(1, ET // U - 1) as i:
                round(i)
            round(ET // U - 1, last=True)
            reduce(ET - 1, U - 1)
            dve.wait_ge(reduced, ET)
            dve.wait_ge(based, ET + U)
            nc.vector.tensor_tensor(alpha[:, :, :], alpha[:, :, :], base_score[:, :, :], ALU.add).then_inc(reduced, 1)
            dve.wait_ge(reduced, ET + 1)


def edge_softmax(nc, g, a, alpha):
    BIG = 1e30
    by_chunk = alpha[:, :, :].rearrange("p (c i) h -> p i c h", c=CH)
    by_chunk4 = alpha[:, :, :].rearrange("p (c i) h -> p c i h", c=CH)
    with ExitStack() as stack:
        sem = lambda n: nc.alloc_semaphore(g.tag + "m_" + n)
        sb = lambda n, s, d=F32: stack.enter_context(nc.sbuf_tensor(g.tag + n, s, d))
        dst_loaded, turned, placed, step, diff, ends, wide, expd, back, home = (sem(n) for n in (
            "dst", "turned", "placed", "step", "diff", "ends", "wide", "exp", "back", "home"))
        ordered = sb("ordered", [P, CT, CH * HEADS])
        dst = sb("dst_chunks", [P, CE + 2], I32)
        score, fwd, bwd = sb("score_t", [P, CE]), sb("fwd", [P, CE]), sb("bwd", [P, CE])
        fresh, fresh_b = g.acct[:, 0, :], g.acct[:, 1, :]
        edge, row = sb("chunk_edge", [P, 4]), sb("chunk_edge_row", [1, 4 * P])
        dist, same, before = sb("dist", [P, P], I32), sb("same_head", [P, P], I32), sb("chunk_mask", [P, 2, P])
        cand, cand2, carry, same_f, dist_f = sb("cand", [P, 2, P]), sb("cand2", [P, 2, P]), sb("carry", [P, 2]), sb("same_f", [P, P]), sb("dist_f", [P, P])
        block = stack.enter_context(nc.Block(g.tag + "edge_softmax"))
        groups = [(q, min(4, CT - q)) for q in range(0, CT, 4)]

        @block.sync
        def _(sp):
            for c in range(CH):
                sp.dma_start(dst[c * HEADS:(c + 1) * HEADS, :],
                             a.dst_row[c * CE:c * CE + CE + 2].rearrange("(o n) -> o n", o=1).to_broadcast([HEADS, CE + 2])).then_inc(dst_loaded, 16)

        @block.gpsimd
        def _(pool):
            nc.gpsimd.iota(dist[:, :], [[-1, P]], base=0, channel_multiplier=1).then_inc(diff, 1)

        @block.tensor
        def _(pe):
            pe.wait_ge(ends, 1)
            for k, (q, m) in enumerate(groups):
                if k >= 4:
                    pe.wait_ge(placed, k - 3)
                for i in range(m):
                    last = nc.tensor.transpose(g.ps[k % 4][:, i * P:(i + 1) * P], ordered[:, q + i, :], g.ident[:, :])
                last.then_inc(turned, 1)
            pe.wait_ge(ends, 2)
            for r in range(4):
                last = nc.tensor.transpose(g.ps[4][0:1, r * P:(r + 1) * P], edge[:, r:r + 1], g.ident[:, :])
            last.then_inc(wide, 1)
            pe.wait_ge(ends, 3)
            nc.tensor.matmul(g.ps[5][:, :], g.ones[0:1, :], row[0:1, :], start=True, stop=True).then_inc(wide, 1)
            for k, (q, m) in enumerate(groups):
                pe.wait_ge(expd, k + 1)
                if k >= 4:
                    pe.wait_ge(home, k - 3)
                for i in range(m):
                    last = nc.tensor.transpose(g.ps[k % 4][:, i * P:(i + 1) * P], score[:, (q + i) * P:(q + i + 1) * P], g.ident[:, :])
                last.then_inc(back, 1)

        @block.scalar
        def _(act):
            for k, (q, m) in enumerate(groups):
                act.wait_ge(turned, k + 1)
                nc.scalar.activation(score[:, q * P:(q + m) * P], g.ps[k % 4][:, 0:m * P], ACT.Copy).then_inc(placed, 1)
            for k, (q, m) in enumerate(groups):
                if k == 0:
                    act.wait_ge(step, 18)
                nc.scalar.activation(score[:, q * P:(q + m) * P], score[:, q * P:(q + m) * P], ACT.Exp).then_inc(expd, 1)

        @block.vector
        def _(dve):
            count = [0]

            def done(ins):
                count[0] += 1
                ins.then_inc(step, 1)
                dve.wait_ge(step, count[0])

            prev, cur, nxt = dst[:, 0:CE], dst[:, 1:CE + 1], dst[:, 2:CE + 2]
            flat = fwd[:, :].rearrange("p (t h) -> p t h", h=HEADS)
            done(nc.vector.tensor_scalar(flat, alpha[:, :, :], SLOPE, None, ALU.mult))
            nc.vector.tensor_tensor(ordered[:, :, :].rearrange("p i (c h) -> p c i h", c=CH), by_chunk4,
                                    fwd[:, :].rearrange("p (c i h) -> p c i h", c=CH, h=HEADS), ALU.max).then_inc(ends, 1)
            dve.wait_ge(diff, 1)
            done(nc.vector.tensor_scalar(same[:, :], dist[:, :], 7, None, ALU.bitwise_and))
            done(nc.vector.tensor_scalar(same_f[:, :], same[:, :], 0.0, None, ALU.is_equal))
            done(nc.vector.tensor_copy(dist_f[:, :], dist[:, :]))
            done(nc.vector.scalar_tensor_tensor(out=before[:, 0, :], in0=dist_f[:, :], scalar=0.0, in1=same_f[:, :], op0=ALU.is_gt, op1=ALU.mult))
            done(nc.vector.scalar_tensor_tensor(out=before[:, 1, :], in0=dist_f[:, :], scalar=0.0, in1=same_f[:, :], op0=ALU.is_lt, op1=ALU.mult))
            dve.wait_ge(dst_loaded, 16 * CH)
            done(nc.vector.tensor_tensor(fresh[:, :], cur, prev, ALU.not_equal))
            done(nc.vector.tensor_scalar(fresh[:, :], fresh[:, :], -BIG, None, ALU.mult))
            done(nc.vector.tensor_tensor(fresh_b[:, :], cur, nxt, ALU.not_equal))
            done(nc.vector.tensor_scalar(fresh_b[:, :], fresh_b[:, :], -BIG, None, ALU.mult))
            dve.wait_ge(placed, len(groups))

            def runs(first, last):
                nc.vector.tensor_tensor_scan(fwd[:, :], fresh[:, :], score[:, :], first, ALU.add, ALU.max)
                done(nc.vector.tensor_tensor_scan(bwd[:, ::-1], fresh_b[:, ::-1], score[:, ::-1], last, ALU.add, ALU.max))
            runs(-BIG, -BIG)
            nc.vector.tensor_copy(edge[:, 0:1], fwd[:, CE - 1:CE])
            nc.vector.tensor_copy(edge[:, 1:2], bwd[:, 0:1])
            nc.vector.tensor_copy(edge[:, 2:3], cur[:, CE - 1:CE])
            nc.vector.tensor_copy(edge[:, 3:4], cur[:, 0:1]).then_inc(ends, 1)
            dve.wait_ge(wide, 1)
            nc.vector.tensor_copy(row[:, :], g.ps[4][0:1, :]).then_inc(ends, 1)
            dve.wait_ge(wide, 2)
            at = lambda r: g.ps[5][:, r * P:(r + 1) * P]
            nc.vector.scalar_tensor_tensor(out=cand[:, 0, :], in0=at(2), scalar=edge[:, 3:4], in1=before[:, 0, :], op0=ALU.is_equal, op1=ALU.mult)
            done(nc.vector.scalar_tensor_tensor(out=cand[:, 1, :], in0=at(3), scalar=edge[:, 2:3], in1=before[:, 1, :], op0=ALU.is_equal, op1=ALU.mult))
            done(nc.vector.tensor_tensor(cand2[:, :, :], cand[:, :, :], g.ps[5][:, 0:2 * P].rearrange("p (k n) -> p k n", k=2), ALU.mult))
            done(nc.vector.tensor_scalar(cand[:, :, :], cand[:, :, :], 1.0, BIG, ALU.subtract, ALU.mult))
            done(nc.vector.tensor_tensor(cand[:, :, :], cand[:, :, :], cand2[:, :, :], ALU.add))
            done(nc.vector.tensor_reduce(carry[:, :], cand[:, :, :], AX.X, ALU.max))
            nc.vector.tensor_tensor_scan(fwd[:, :], fresh[:, :], score[:, :], carry[:, 0:1], ALU.add, ALU.max)
            nc.vector.tensor_tensor_scan(bwd[:, ::-1], fresh_b[:, ::-1], score[:, ::-1], carry[:, 1:2], ALU.add, ALU.max).then_inc(step, 1)
            count[0] += 1
            dve.wait_ge(step, count[0])
            nc.vector.tensor_tensor(fwd[:, :], fwd[:, :], bwd[:, :], ALU.max).then_inc(diff, 1)
            dve.wait_ge(diff, 2)
            nc.vector.tensor_tensor(score[:, :], score[:, :], fwd[:, :], ALU.subtract).then_inc(step, 1)
            assert count[0] == 17
            for k, (q, m) in enumerate(groups):
                dve.wait_ge(back, k + 1)
                nc.vector.tensor_copy(by_chunk[:, q:q + m], g.ps[k % 4][:, 0:m * P].rearrange("p (i c h) -> p i c h", i=m, c=CH)).then_inc(home, 1)
            dve.wait_ge(home, len(groups))


def weighted_sum(nc, g, htable, weight, den):
    with ExitStack() as stack:
        sem = lambda n: nc.alloc_semaphore(g.tag + "w_" + n)
        gathered = [sem(f"gathered{u}") for u in range(U)]
        copied, claimed, weighed, weights, summed, added, cleared = (sem(n) for n in (
            "idx_copied", "claimed", "weighed", "weights", "summed", "added", "cleared"))
        negated, far, hot = sem("negated"), sem("far"), sem("hot")
        sb = lambda n, s, d=F32: stack.enter_context(nc.sbuf_tensor(g.tag + "w_" + n, s, d))
        idx, rows = sb("idx", [P, U], I32), sb("rows", [P, U, D])
        onehot, part, dist = sb("onehot", [P, 4, P]), sb("part", [P, 4, D + HEADS]), sb("dist", [P, 2, P])
        minus_local = sb("minus_local", [P, ET])
        den_t = sb("den_turned", [HEADS, ROWS])
        with ExitStack() as s2:
            block = s2.enter_context(nc.Block(g.tag + "weighted_sum"))

            @block.gpsimd
            def _(pool):
                gather_sources(nc, g, pool, htable, rows, idx, copied, weighed, claimed, gathered)

            @block.tensor
            def _(pe):
                pe.sem_inc(summed, 4)
                with nc.tensor.Fori(0, ET // U) as i:
                    for u in range(U):
                        n = U * i + u
                        pe.wait_ge(hot, n + 3)
                        pe.wait_ge(weighed, n + U + 1)
                        pe.wait_ge(added, n + 1)
                        nc.tensor.matmul(g.ps[4 + u % 4][0:HEADS, 0:P], part[:, u % 4, D:D + HEADS], onehot[:, u % 4, :], start=True, stop=True)
                        for c in range(2):
                            last = nc.tensor.matmul(g.ps[u % 4][:, c * P:(c + 1) * P], part[:, u % 4, c * P:(c + 1) * P],
                                                    onehot[:, u % 4, :], start=True, stop=True)
                        last.then_inc(summed, 1)

            @block.scalar
            def _(act):
                nc.scalar.activation(idx[:, 0:H], g.srcc[:, 0:H], ACT.Copy).then_inc(copied, 1)
                act.sem_inc(hot, 2)
                act.wait_ge(negated, 1)
                with nc.scalar.Fori(0, ET // U) as i:
                    for u in range(U):
                        n = U * i + u
                        if u % H == 0:
                            copy_next_indices(nc, g, act, i, u // H, idx, copied, weighed)
                        act.wait_ge(hot, n + 1)
                        nc.scalar.activation(dist[:, u % 2, :], g.iota[:, 0:P], ACT.Abs, bias=minus_local[:, ds(n, 1)]).then_inc(far, 1)
                        act.wait_ge(summed, n + 1)
                        nc.scalar.activation(part[:, u % 4, D:D + HEADS].unsqueeze(1), weight[:, ds(U * i + u, 1), :], ACT.Copy).then_inc(weights, 1)
                        act.wait_ge(far, n + 1)
                        nc.scalar.activation(onehot[:, u % 4, :], dist[:, u % 2, :], ACT.Relu, bias=g.ones[:, 0:1], scale=-1.0).then_inc(hot, 1)

            @block.vector
            def _(dve):
                base = [nc.vector.alloc_register(g.tag + f"base{u}") for u in range(8)]
                nc.vector.memset(g.acct[:, :, :], 0.0).then_inc(cleared, 1)
                nc.vector.memset(den_t[:, :], 0.0).then_inc(cleared, 1)
                nc.vector.tensor_scalar(minus_local[:, :], g.local[:, 0:ET], -1.0, None, ALU.mult).then_inc(negated, 1)
                dve.wait_ge(cleared, 2)
                dve.sem_inc(weighed, U)
                dve.sem_inc(added, 4)

                def weigh(i, n, u):
                    if not (isinstance(n, int) and n < 4):
                        dve.wait_ge(summed, n + 1)
                    dve.wait_ge(gathered[u], 16 * (i + 1))
                    nc.vector.tensor_tensor(part[:, u % 4, 0:D].rearrange("p (h d) -> p h d", d=HD),
                                            rows[:, u, :].rearrange("p (h d) -> p h d", d=HD),
                                            weight[:, ds(n, 1), :].rearrange("p o h -> p (o h)").unsqueeze(2).to_broadcast([P, HEADS, HD]),
                                            ALU.mult).then_inc(weighed, 1)

                def collect(n, u, b):
                    dve.wait_ge(summed, n + 5)
                    dve.wait_ge(added, n + 4)
                    nc.vector.tensor_tensor(den_t[:, ds(b, P)], den_t[:, ds(b, P)], g.ps[4 + u % 4][0:HEADS, 0:P], ALU.add)
                    nc.vector.tensor_tensor(g.acct[:, :, ds(b, P)], g.acct[:, :, ds(b, P)],
                                            g.ps[u % 4][:, 0:D].rearrange("p (c n) -> p c n", c=2), ALU.add).then_inc(added, 1)

                LAG = 2
                for u in range(LAG):
                    weigh(0, u, u)

                def round(i, last=False):
                    for u in range(U):
                        if u % 8 == 0:
                            nc.vector.reg_load(base, g.dstc[0:1, ds(U * i + u, 8)])
                        m = u + LAG
                        if not (last and m >= U):
                            weigh(i + m // U, U * i + m, m % U)
                        collect(U * i + u, u, nc.vector.snap(base[u % 8], min_val=0, max_val=ROWS - P))
                with nc.vector.Fori(0, ET // U - 1) as i:
                    round(i)
                round(ET // U - 1, last=True)
        turn_sums(nc, g, "w", 2, den_t, den)


E = 8


class Route:
    pass


def route(nc, g, name, logits, picks, capacity, slots, r, clear, meanwhile=None):
    with ExitStack() as stack:
        sem = lambda n: nc.alloc_semaphore(g.tag + name + n)
        sb = lambda n, s, d=F32: stack.enter_context(nc.sbuf_tensor(g.tag + name + n, s, d))
        step, masks, counted, shifted, expd, zeroed, zero = (sem(n) for n in (
            "_step", "_masks", "_counted", "_shifted", "_exp", "_zeroed", "_zero"))
        wide = [P, NT, E]
        rev, valid, number, upto = sb("_rev", [P, E]), sb("_valid", [P, NT]), sb("_number", [P, NT]), sb("_upto", [P, P])
        best, first = [sb(f"_best{k}", [P, NT]) for k in range(2)], sb("_first", [P, NT])
        pick = [sb(f"_pick{k}", wide) for k in range(picks)]
        tmp, rest, every, cum, totals, incl = sb("_tmp", wide), sb("_rest", wide), sb("_every", wide), sb("_cum", wide), sb("_totals", wide), sb("_incl", wide)
        zeros, ni, nf, ends = sb("_zeros", [P, NT]), sb("_ni", [P, E], I32), sb("_nf", [P, E]), sb("_ends", [P, E])
        start, rowf, flag, place, tile_no, owner = sb("_start", [P, E]), sb("_rowf", [P, NT]), sb("_flag", [P, NT]), sb("_place", [P, NT]), sb("_tile_no", [1, 64]), sb("_owner", [1, 64])
        expt, z = sb("_expt", wide), sb("_z", [P, NT])
        block = stack.enter_context(nc.Block(g.tag + name))
        per_node = lambda v: v[:, :].unsqueeze(2).to_broadcast(wide)
        per_expert = lambda v: v[:, :].unsqueeze(1).to_broadcast(wide)

        @block.sync
        def _(sp):
            dram, zero_rows, n = clear
            sp.wait_ge(zero, 1)
            for k in range(n):
                sp.dma_start(dram[k], zero_rows).then_inc(zeroed, 16)
            if meanwhile is not None:
                meanwhile(sp)
            sp.wait_ge(zeroed, 16 * n)

        @block.gpsimd
        def _(pool):
            nc.gpsimd.memset(clear[1], 0.0).then_inc(zero, 1)
            nc.gpsimd.iota(rev[:, :], [[-1, E]], base=E, channel_multiplier=0, allow_small_or_imprecise_dtypes=True).then_inc(masks, 1)
            nc.gpsimd.iota(number[:, :], [[P, NT]], base=0, channel_multiplier=1, allow_small_or_imprecise_dtypes=True).then_inc(masks, 1)
            nc.gpsimd.iota(tile_no[:, :], [[1, 64]], base=0, channel_multiplier=0, allow_small_or_imprecise_dtypes=True).then_inc(masks, 1)
            nc.gpsimd.affine_select(out=upto[:, :], in_=g.ones[:, :], compare_op=ALU.is_ge, fill=0.0, base=0,
                                    pattern=[[1, P]], channel_multiplier=-1).then_inc(masks, 1)
            nc.gpsimd.affine_select(out=valid[:, :], in_=g.ones[:, 0:NT], compare_op=ALU.is_ge, fill=0.0, base=NODES - 1,
                                    pattern=[[-P, NT]], channel_multiplier=-1).then_inc(masks, 1)

        @block.tensor
        def _(pe):
            pe.wait_ge(counted, 1)
            nc.tensor.matmul(g.ps[0][:, 0:NT * E], upto[:, :], every[:, :, :].rearrange("p t e -> p (t e)"), start=True, stop=True)
            nc.tensor.matmul(g.ps[1][:, 0:NT * E], g.ones[:, :], every[:, :, :].rearrange("p t e -> p (t e)"), start=True, stop=True).then_inc(counted, 1)

        @block.scalar
        def _(act):
            act.wait_ge(shifted, 1)
            if picks == 1:
                nc.scalar.activation(expt[:, :, :], tmp[:, :, :], ACT.Exp).then_inc(expd, 1)
            else:
                nc.scalar.activation(z[:, :], z[:, :], ACT.Exp).then_inc(expd, 1)

        @block.vector
        def _(dve):
            count = [0]

            def done(ins):
                count[0] += 1
                ins.then_inc(step, 1)
                dve.wait_ge(step, count[0])

            dve.wait_ge(masks, 5)
            done(nc.vector.memset(zeros[:, :], 0.0))
            left = logits
            for k in range(picks):
                done(nc.vector.tensor_reduce(best[k][:, :], left[:, :, :], AX.X, ALU.max))
                done(nc.vector.tensor_tensor(tmp[:, :, :], left[:, :, :], per_node(best[k]), ALU.is_equal))
                done(nc.vector.tensor_tensor(tmp[:, :, :], tmp[:, :, :], per_expert(rev), ALU.mult))
                done(nc.vector.tensor_reduce(first[:, :], tmp[:, :, :], AX.X, ALU.max))
                done(nc.vector.tensor_tensor(pick[k][:, :, :], per_expert(rev), per_node(first), ALU.is_equal))
                if k + 1 < picks:
                    done(nc.vector.scalar_tensor_tensor(out=rest[:, :, :], in0=pick[k][:, :, :], scalar=-1e30, in1=left[:, :, :],
                                                        op0=ALU.mult, op1=ALU.add))
                    left = rest
                done(nc.vector.tensor_tensor(pick[k][:, :, :], pick[k][:, :, :], per_node(valid), ALU.mult))
            if picks == 2:
                done(nc.vector.tensor_tensor(every[:, :, :], pick[0][:, :, :], pick[1][:, :, :], ALU.add))
                nc.vector.tensor_tensor(z[:, :], best[1][:, :], best[0][:, :], ALU.subtract).then_inc(shifted, 1)
            else:
                done(nc.vector.tensor_copy(every[:, :, :], pick[0][:, :, :]))
                nc.vector.tensor_tensor(tmp[:, :, :], logits[:, :, :], per_node(best[0]), ALU.subtract).then_inc(shifted, 1)
            dve.sem_inc(counted, 1)
            dve.wait_ge(expd, 1)
            if picks == 1:
                done(nc.vector.tensor_reduce(z[:, :], expt[:, :, :], AX.X, ALU.add))
                done(nc.vector.reciprocal(r.weight[:, 0, :], z[:, :]))
            else:
                done(nc.vector.tensor_scalar(flag[:, :], z[:, :], 1.0, None, ALU.add))
                done(nc.vector.reciprocal(r.weight[:, 0, :], flag[:, :]))
                done(nc.vector.tensor_tensor(r.weight[:, 1, :], r.weight[:, 0, :], z[:, :], ALU.mult))
            dve.wait_ge(counted, 2)
            done(nc.vector.tensor_copy(totals[:, :, :], g.ps[1][:, 0:NT * E].rearrange("p (t e) -> p t e", e=E)))
            for e in range(E):
                last = nc.vector.tensor_tensor_scan(incl[:, :, e], totals[:, :, e], zeros[:, :], 0.0, ALU.add, ALU.add)
            done(last)
            done(nc.vector.tensor_tensor(cum[:, :, :], incl[:, :, :], totals[:, :, :], ALU.subtract))
            done(nc.vector.tensor_tensor(cum[:, :, :], cum[:, :, :], g.ps[0][:, 0:NT * E].rearrange("p (t e) -> p t e", e=E), ALU.add))
            if capacity:
                done(nc.vector.tensor_scalar(start[:, :], rev[:, :], -float(slots), float(E * slots), ALU.mult, ALU.add))
            else:
                done(nc.vector.tensor_scalar(ni[:, :], incl[:, NT - 1, :], float(P - 1), None, ALU.add))
                done(nc.vector.tensor_scalar(ni[:, :], ni[:, :], 7, None, ALU.logical_shift_right))
                done(nc.vector.tensor_copy(nf[:, :], ni[:, :]))
                done(nc.vector.tensor_tensor_scan(ends[:, :], nf[:, :], zeros[:, 0:E], 0.0, ALU.add, ALU.add))
                done(nc.vector.tensor_tensor(start[:, :], ends[:, :], nf[:, :], ALU.subtract))
                done(nc.vector.tensor_scalar(start[:, :], start[:, :], float(P), None, ALU.mult))
                done(nc.vector.memset(owner[:, :], 0.0))
                for e in range(E - 1):
                    done(nc.vector.scalar_tensor_tensor(out=owner[:, :], in0=tile_no[:, :], scalar=ends[0:1, e:e + 1], in1=owner[:, :],
                                                        op0=ALU.is_ge, op1=ALU.add))
                done(nc.vector.tensor_copy(r.expert[:, :], owner[:, 0:r.expert.shape[1]]))
            for k in range(picks):
                done(nc.vector.tensor_tensor(tmp[:, :, :], pick[k][:, :, :], cum[:, :, :], ALU.mult))
                done(nc.vector.tensor_reduce(rowf[:, :], tmp[:, :, :], AX.X, ALU.add))
                done(nc.vector.tensor_tensor(tmp[:, :, :], pick[k][:, :, :], per_expert(start), ALU.mult))
                done(nc.vector.tensor_reduce(place[:, :], tmp[:, :, :], AX.X, ALU.add))
                if capacity:
                    done(nc.vector.tensor_scalar(flag[:, :], rowf[:, :], float(capacity), None, ALU.is_le))
                    done(nc.vector.tensor_tensor(r.weight[:, k, :], r.weight[:, k, :], flag[:, :], ALU.mult))
                    done(nc.vector.tensor_tensor(flag[:, :], flag[:, :], valid[:, :], ALU.mult))
                else:
                    done(nc.vector.tensor_copy(flag[:, :], valid[:, :]))
                done(nc.vector.tensor_scalar(z[:, :], rowf[:, :], float(capacity or ROWS * 2), -1.0, ALU.min, ALU.add))
                done(nc.vector.tensor_tensor(z[:, :], z[:, :], place[:, :], ALU.add))
                done(nc.vector.tensor_scalar(r.read[:, k, :], z[:, :], 0.0, None, ALU.max))
                done(nc.vector.tensor_scalar(rowf[:, :], rowf[:, :], -1.0, None, ALU.add))
                done(nc.vector.tensor_tensor(rowf[:, :], rowf[:, :], place[:, :], ALU.add))
                done(nc.vector.tensor_tensor(rowf[:, :], rowf[:, :], flag[:, :], ALU.mult))
                done(nc.vector.tensor_scalar(flag[:, :], flag[:, :], -1.0, 1.0, ALU.mult, ALU.add))
                done(nc.vector.tensor_scalar(place[:, :], number[:, :], float(r.spare + k * ROWS), None, ALU.add))
                done(nc.vector.tensor_tensor(place[:, :], place[:, :], flag[:, :], ALU.mult))
                done(nc.vector.tensor_tensor(r.write[:, k, :], rowf[:, :], place[:, :], ALU.add))


def new_route(nc, g, stack, name, picks, rows):
    r = Route()
    sb = lambda n, s, d=F32: stack.enter_context(nc.sbuf_tensor(g.tag + name + n, s, d))
    r.weight, r.read, r.write = sb("_weight", [P, picks, NT]), sb("_read", [P, picks, NT], I32), sb("_write", [P, picks, NT], I32)
    r.expert, r.spare, r.rows = sb("_expert", [1, rows // P], I32), rows, rows
    r.sorted = nc.dram_tensor(g.tag + name + "_sorted", (rows + picks * ROWS, D), F32).ap()
    r.result = nc.dram_tensor(g.tag + name + "_result", (rows, D), F32).ap()
    return r


def clear_rows(r, zeros):
    n = zeros.shape[1] // D
    v = r.sorted[0:r.rows, :].rearrange("(k p j) d -> k p (j d)", p=P, j=n)
    return v, zeros, r.rows // (P * n)


def send(nc, pool, r, picks, src, sent):
    for k in range(picks):
        for t in range(NT):
            nc.gpsimd.indirect_dma_start(
                r.sorted, bass.IndirectOffsetOnAxis(ap=r.write[:, k, t:t + 1].bitcast(U32), axis=0),
                src[:, t, :], None).then_inc(sent, 16)


def send_rows(nc, g, name, r, picks, src):
    with ExitStack() as stack:
        sent = nc.alloc_semaphore(g.tag + name + "_sent")
        block = stack.enter_context(nc.Block(g.tag + name + "_send"))

        @block.gpsimd
        def _(pool):
            send(nc, pool, r, picks, src, sent)
            pool.wait_ge(sent, 16 * NT * picks)


def collect_rows(nc, g, name, r, picks, out, guard=False):
    S, G = 8, 4
    with ExitStack() as stack:
        sem = lambda n: nc.alloc_semaphore(g.tag + name + n)
        back = [sem(f"_back{s}") for s in range(S)]
        used = sem("_used")
        rows = stack.enter_context(nc.sbuf_tensor(g.tag + name + "_back_rows", [P, S, D], F32))
        block = stack.enter_context(nc.Block(g.tag + name + "_collect"))
        order = [(t, k) for t in range(NT) for k in range(picks)]

        @block.gpsimd
        def _(pool):
            for n, (t, k) in enumerate(order):
                if n >= S:
                    pool.wait_ge(used, n - S + 1)
                nc.gpsimd.indirect_dma_start(
                    rows[:, n % S, :], None, r.result,
                    bass.IndirectOffsetOnAxis(ap=r.read[:, k, t:t + 1].bitcast(U32), axis=0)).then_inc(back[n % S], 16)

        if guard:
            step = sem("_guard_step")
            mask = stack.enter_context(nc.sbuf_tensor(g.tag + name + "_mask", [P, G * D], mybir.dt.uint8))
            caps = stack.enter_context(nc.sbuf_tensor(g.tag + name + "_caps", [P, 3], F32))
            BIGGEST = 3.4028234663852886e38

        @block.vector
        def _(dve):
            count = [0]

            def done(ins):
                count[0] += 1
                ins.then_inc(step, 1)
                dve.wait_ge(step, count[0])

            def guard_tiles(lo, hi):
                y, m = g.acc[:, lo:hi, :].rearrange("p t d -> p (t d)"), mask[:, 0:(hi - lo) * D]
                cap = lambda k: caps[:, k:k + 1].to_broadcast([P, (hi - lo) * D])
                for k, (op, v) in enumerate(((ALU.is_gt, BIGGEST), (ALU.is_lt, -BIGGEST))):
                    done(nc.vector.tensor_scalar(m, y, v, None, op))
                    done(nc.vector.copy_predicated(y, m, cap(k)))
                done(nc.vector.tensor_tensor(m, y, y, ALU.not_equal))
                done(nc.vector.copy_predicated(y, m, cap(2)))
                done(nc.vector.tensor_tensor(g.x[:, lo:hi, :], g.x[:, lo:hi, :], g.acc[:, lo:hi, :], ALU.add))

            if guard:
                for k, v in enumerate((1e4, -1e4, 0.0)):
                    done(nc.vector.memset(caps[:, k:k + 1], v))
            for n, (t, k) in enumerate(order):
                dve.wait_ge(back[n % S], 16 * (n // S + 1))
                if k:
                    dve.wait_ge(used, n)
                if out is None:
                    nc.vector.tensor_scalar(g.acc[:, t, :], rows[:, n % S, :], r.weight[:, k, t:t + 1], None, ALU.mult).then_inc(used, 1)
                else:
                    nc.vector.scalar_tensor_tensor(out=out[:, t, :], in0=rows[:, n % S, :], scalar=r.weight[:, k, t:t + 1],
                                                   in1=out[:, t, :], op0=ALU.mult, op1=ALU.add).then_inc(used, 1)
                if guard and ((n + 1) % G == 0 or n + 1 == NT):
                    dve.wait_ge(used, n + 1)
                    guard_tiles(n // G * G, n + 1)
            dve.wait_ge(used, len(order))


def gate_logits(nc, g, name, src, wg, bg, logits, meanwhile=None):
    project(nc, g, name, [wg], bg, E,
            [("pool", lambda out, t: nc.gpsimd.tensor_copy(out, src[:, ds(t, 1), :]))],
            lambda dve, bank, t, s: nc.vector.tensor_copy(logits[:, ds(t, 1), :], bank), meanwhile=meanwhile)


CAP, SLOTS, H1 = -(-5 * NODES // (4 * E)), 512, 1024


def layer1_ffn(nc, g, a, table):
    with ExitStack() as stack:
        sb = lambda n, s, d=F32: stack.enter_context(nc.sbuf_tensor(g.tag + n, s, d))
        wg, bg, logits = sb("gate_w", [P, 2, E]), sb("gate_b", [1, E]), sb("logits", [P, NT, E])
        r = new_route(nc, g, stack, "sw", 1, E * SLOTS)
        layer_norm(nc, g, None, loads(nc, g, "sw", [(wg[:, :, :], rows_in(a.l1f_gate_w)), (bg[:, :], a.l1f_gate_b)]))
        gate_logits(nc, g, "sw_gate", g.xn, wg, bg[0:1, :], logits)
        with ExitStack() as s2:
            zeros = s2.enter_context(nc.sbuf_tensor(g.tag + "zero_rows", [P, 8 * D], F32))
            route(nc, g, "sw_route", logits, 1, CAP, SLOTS, r, clear_rows(r, zeros[:, :]))
        NF, NR = H1 // P, SLOTS // P
        with ExitStack() as s2:
            sem = lambda n: nc.alloc_semaphore(g.tag + "e_" + n)
            sb2 = lambda n, s: s2.enter_context(nc.sbuf_tensor(g.tag + "e_" + n, s, F32))
            loaded = [sem(f"loaded{s}") for s in range(2)]
            stored = [sem(f"stored{s}") for s in range(2)]
            turned, xt_ready, hidden, active, product, copied, freed = (
                sem(n) for n in ("turned", "xt_ready", "hidden", "active", "product", "copied", "freed"))
            sent = sem("sent")
            w1, w2, b1, b2 = sb2("w1", [P, 2, 2, H1]), sb2("w2", [P, 2, NF, D]), sb2("b1", [P, 2, NF]), sb2("b2", [1, 2, D])
            rows, xt, ht, y = sb2("rows", [P, 2, NR, D]), sb2("xt", [P, 2, SLOTS]), sb2("ht", [P, NF, SLOTS]), sb2("y", [P, 2, NR, D])
            block = s2.enter_context(nc.Block(g.tag + "experts"))

            @block.sync
            def _(sp):
                def load_expert(i, s):
                    e = 2 * i + s
                    for dst, src in ((w1[:, s, :, :], a.l1f_w1[ds(e, 1), :, :].rearrange("e (c p) h -> p (e c) h", p=P)),
                                     (b1[:, s, :], a.l1f_b1_cols[:, ds(e * NF, NF)]),
                                     (w2[:, s, :, :], a.l1f_w2[ds(e, 1), :, :].rearrange("e (c p) h -> p (e c) h", p=P)),
                                     (b2[:, s, :], a.l1f_b2[ds(e, 1), :])):
                        sp.dma_start(dst, src).then_inc(loaded[s], 16)

                def load_rows(i, s):
                    sp.dma_start(rows[:, s, :, :], r.sorted[ds((2 * i + s) * SLOTS, SLOTS), :].rearrange("(r p) d -> p r d", p=P)).then_inc(loaded[s], 16)

                for s in range(2):
                    load_expert(0, s)
                sp.wait_ge(sent, 16 * NT)
                for s in range(2):
                    load_rows(0, s)
                with nc.sync.Fori(1, E // 2) as i:
                    for s in range(2):
                        sp.wait_ge(product, NR * (2 * i + s) + NR)
                        load_expert(i, s)
                        load_rows(i, s)

            @block.tensor
            def _(pe):
                pe.sem_inc(product, 2 * NR)
                pe.sem_inc(hidden, 4)

                def turn_rows(i, s):
                    pe.wait_ge(loaded[s], 80 * (i + 1))
                    for c in range(2):
                        pe.wait_ge(xt_ready, 2 * (2 * i + s) + c + 1)
                        for n in range(NR):
                            last = nc.tensor.transpose(g.ps[c][:, n * P:(n + 1) * P], rows[:, s, n, c * P:(c + 1) * P], g.ident[:, :])
                        last.then_inc(turned, 1)

                def first_layer(i, s):
                    e = 2 * i + s
                    pe.wait_ge(xt_ready, 2 * e + 4)
                    for f in range(NF):
                        pe.wait_ge(active, NF * e + f + 1)
                        for c in range(2):
                            last = nc.tensor.matmul(g.ps[2 + f % 4][:, :], w1[:, s, c, f * P:(f + 1) * P], xt[:, c, :],
                                                    start=(c == 0), stop=(c == 1))
                        last.then_inc(hidden, 1)

                def second_layer(i, s):
                    e = 2 * i + s
                    for n in range(NR):
                        pe.wait_ge(copied, NR * e + n + 1)
                        nc.tensor.matmul(g.ps[6 + n % 2][:, 0:D], g.ones[0:1, :], b2[0:1, s, :], start=True, stop=False)
                        for f in range(NF):
                            if n == 0:
                                pe.wait_ge(active, NF * e + f + 5)
                            last = nc.tensor.matmul(g.ps[6 + n % 2][:, 0:D], ht[:, f, n * P:(n + 1) * P], w2[:, s, f, :],
                                                    start=False, stop=(f == NF - 1))
                        last.then_inc(product, 1)

                turn_rows(0, 0)
                with nc.tensor.Fori(0, E // 2 - 1) as i:
                    for s in range(2):
                        first_layer(i, s)
                        turn_rows(i + s, 1 - s)
                        second_layer(i, s)
                i = E // 2 - 1
                first_layer(i, 0)
                turn_rows(i, 1)
                second_layer(i, 0)
                first_layer(i, 1)
                second_layer(i, 1)

            @block.scalar
            def _(act):
                act.sem_inc(xt_ready, 2)
                act.sem_inc(active, 4)
                with nc.scalar.Fori(0, E // 2) as i:
                    for s in range(2):
                        e = 2 * i + s
                        act.wait_ge(hidden, NF * e + 4)
                        for c in range(2):
                            act.wait_ge(turned, 2 * e + c + 1)
                            nc.scalar.activation(xt[:, c, :], g.ps[c][:, :], ACT.Copy).then_inc(xt_ready, 1)
                        act.wait_ge(product, NR * (e + 2))
                        for f in range(NF):
                            act.wait_ge(hidden, NF * e + f + 5)
                            nc.scalar.activation(ht[:, f, :], g.ps[2 + f % 4][:, :], ACT.Relu, bias=b1[:, s, f:f + 1]).then_inc(active, 1)

            @block.vector
            def _(dve):
                dve.sem_inc(copied, 2)
                dve.sem_inc(freed, 2)
                with nc.vector.Fori(0, E // 2) as i:
                    for s in range(2):
                        dve.wait_ge(freed, 2 * i + s + 1)
                        for n in range(NR):
                            dve.wait_ge(product, NR * (2 * i + s) + n + 2 * NR + 1)
                            nc.vector.tensor_copy(y[:, s, n, :], g.ps[6 + n % 2][:, 0:D]).then_inc(copied, 1)

            @block.gpsimd
            def _(pool):
                send(nc, pool, r, 1, g.xn, sent)
                with nc.gpsimd.Fori(0, E // 2) as i:
                    for s in range(2):
                        e = 2 * i + s
                        pool.wait_ge(copied, NR * (e + 1) + 2)
                        pool.dma_start(r.result[ds(e * SLOTS, SLOTS), :].rearrange("(r p) d -> p r d", p=P), y[:, s, :, :]).then_inc(stored[s], 16)
                        pool.wait_ge(stored[s], 16 * (i + 1))
                        pool.sem_inc(freed, 1)

        collect_rows(nc, g, "sw", r, 1, None, guard=True)


H2 = 512
T2 = (2 * NODES + E * (P - 1)) // P
T2 += T2 % 2


def norm_again(nc, g, gamma, beta, out):
    with ExitStack() as stack:
        sem = lambda n: nc.alloc_semaphore(g.tag + "again_" + n)
        stat, aggr, root, inv, normed, scaled = (sem(n) for n in ("stat", "aggr", "root", "inv", "normed", "scaled"))
        block = stack.enter_context(nc.Block(g.tag + "norm_again"))

        @block.vector
        def _(dve):
            for t in range(NT):
                nc.vector.bn_stats(g.stats[:, t, :], g.xn[:, t, :]).then_inc(stat, 1)
            dve.wait_ge(stat, NT)
            for t in range(NT):
                nc.vector.bn_aggr(g.mv[:, t, :], g.stats[:, t, :]).then_inc(aggr, 1)
            dve.wait_ge(root, 1)
            nc.vector.reciprocal(g.rstd[:, :], g.rstd[:, :]).then_inc(inv, 1)
            dve.wait_ge(inv, 1)
            for t in range(NT):
                nc.vector.tensor_scalar(out[:, t, :], g.xn[:, t, :], g.mv[:, t, 0:1], g.rstd[:, t:t + 1],
                                        ALU.subtract, ALU.mult).then_inc(normed, 1)
            dve.wait_ge(normed, NT)
            wide = [P, NT, D]
            nc.vector.tensor_tensor(out[:, :, :], out[:, :, :], gamma[:, :].unsqueeze(1).to_broadcast(wide), ALU.mult).then_inc(scaled, 1)
            dve.wait_ge(scaled, 1)
            nc.vector.tensor_tensor(out[:, :, :], out[:, :, :], beta[:, :].unsqueeze(1).to_broadcast(wide), ALU.add).then_inc(scaled, 1)
            dve.wait_ge(scaled, 2)

        @block.scalar
        def _(act):
            act.wait_ge(aggr, NT)
            nc.scalar.activation(g.rstd[:, :], g.mv[:, :, 1], ACT.Sqrt, bias=g.eps[:, 0:1]).then_inc(root, 1)


def store_tiles(nc, pool, pairs, result, y, copied, stored, freed):
    def pair(i, first=False):
        for s in range(2):
            pool.wait_ge(copied, 2 * i + s + 3)
            pool.dma_start(result[ds((2 * i + s) * P, P), :], y[:, s, :]).then_inc(stored[s], 16)
            if not (first and s == 0):
                pool.wait_ge(stored[1 - s], 16 * (i + s))
                pool.sem_inc(freed, 1)
    pair(0, first=True)
    with nc.gpsimd.Fori(1, pairs) as i:
        pair(i)
    pool.wait_ge(stored[1], 16 * pairs)


def layer2_ffn(nc, g, a, table):
    with ExitStack() as stack:
        sb = lambda n, s, d=F32: stack.enter_context(nc.sbuf_tensor(g.tag + n, s, d))
        r = new_route(nc, g, stack, "mo", 2, T2 * P)
        NC = H2 // P
        w1, w2 = sb("w1", [P, 2, E * H2]), sb("w2", [P, NC, E * D])
        flat = g.xn[:, :, :].rearrange("p t d -> p (t d)")
        b1, b2 = flat[:, 0:E * H2], flat[:, E * H2:E * (H2 + D)]
        by_expert = lambda w, c: w[:, c * P:(c + 1) * P, :].rearrange("e p h -> p e h")
        weights = ([(w1[:, c, :].rearrange("p (e h) -> p e h", e=E), by_expert(a.l2f_w1, c)) for c in range(2)]
                   + [(w2[:, c, :].rearrange("p (e h) -> p e h", e=E), by_expert(a.l2f_w2, c)) for c in range(NC)])
        with ExitStack() as s2:
            sb2 = lambda n, s: s2.enter_context(nc.sbuf_tensor(g.tag + n, s, F32))
            gamma, beta, wr, br, logits = sb2("gamma", [P, D]), sb2("beta", [P, D]), sb2("wr", [P, 2, E]), sb2("br", [1, E]), sb2("logits", [P, NT, E])
            layer_norm(nc, g, None, loads(nc, g, "mo", [(gamma[:, :], across(a.l2f_gamma)), (beta[:, :], across(a.l2f_beta)),
                                       (wr[:, :, :], rows_in(a.l2f_wr)), (br[:, :], a.l2f_br)]))
            norm_again(nc, g, gamma, beta, g.acc)
            gate_logits(nc, g, "mo_gate", g.acc, wr, br[0:1, :], logits, loads(nc, g, "mo_experts", weights))
            route(nc, g, "mo_route", logits, 2, None, None, r, clear_rows(r, g.acct[:, 0, 0:4 * D]),
                  loads(nc, g, "mo_biases", [(b1, across(a.l2f_b1)), (b2, across(a.l2f_b2))]))
        send_rows(nc, g, "mo", r, 2, g.acc)
        with ExitStack() as s2:
            sem = lambda n: nc.alloc_semaphore(g.tag + "e_" + n)
            loaded = [sem(f"loaded{s}") for s in range(2)]
            stored = [sem(f"stored{s}") for s in range(2)]
            turned, xt_ready, hidden, biased, active, turned_h, ht_ready, product, copied, freed = (sem(n) for n in (
                "turned", "xt_ready", "hidden", "biased", "active", "turned_h", "ht_ready", "product", "copied", "freed"))
            two = lambda k, lo, n: g.acct[:, k, lo:lo + 2 * n].rearrange("p (s n) -> p s n", s=2)
            rows, xt, h, ht, y = two(0, 0, D), two(0, 2 * D, D), two(0, 4 * D, H2), two(1, 0, H2), two(1, 2 * H2, D)
            block = s2.enter_context(nc.Block(g.tag + "experts"))

            @block.sync
            def _(sp):
                with nc.sync.Fori(0, T2 // 2) as i:
                    for s in range(2):
                        sp.wait_ge(turned, 2 * i + s + 1)
                        sp.dma_start(rows[:, s, :], r.sorted[ds((2 * i + s) * P, P), :]).then_inc(loaded[s], 16)

            PAIRS = T2 // 2

            @block.tensor
            def _(pe):
                own = [nc.tensor.alloc_register(g.tag + f"owner{s}") for s in range(2)]
                own2 = [nc.tensor.alloc_register(g.tag + f"owner_out{s}") for s in range(2)]
                pe.sem_inc(turned, 2)
                pe.sem_inc(hidden, 2)
                pe.sem_inc(turned_h, 2)
                pe.sem_inc(product, 2)

                def turn_rows(i):
                    for s in range(2):
                        pe.wait_ge(loaded[s], 16 * (i + 1))
                        pe.wait_ge(xt_ready, 2 * i + s + 1)
                        nc.tensor.transpose(g.ps[s][:, 0:P], rows[:, s, 0:P], g.ident[:, :])
                        nc.tensor.transpose(g.ps[s][:, P:D], rows[:, s, P:D], g.ident[:, :]).then_inc(turned, 1)

                def first_layer(i):
                    nc.tensor.reg_load(own, r.expert[0:1, ds(2 * i, 2)])
                    for s in range(2):
                        t = 2 * i + s
                        e = nc.tensor.snap(own[s], min_val=0, max_val=E - 1)
                        pe.wait_ge(xt_ready, t + 3)
                        pe.wait_ge(biased, t + 1)
                        for c in range(2):
                            last = nc.tensor.matmul(g.ps[2 + s][:, :], xt[:, s, c * P:(c + 1) * P], w1[:, c, ds(e * H2, H2)],
                                                    start=(c == 0), stop=(c == 1))
                        last.then_inc(hidden, 1)

                def turn_hidden(i):
                    for s in range(2):
                        t = 2 * i + s
                        pe.wait_ge(active, t + 1)
                        pe.wait_ge(ht_ready, t + 1)
                        for c in range(NC):
                            last = nc.tensor.transpose(g.ps[4 + s][:, c * P:(c + 1) * P], h[:, s, c * P:(c + 1) * P], g.ident[:, :])
                        last.then_inc(turned_h, 1)

                def second_layer(i):
                    nc.tensor.reg_load(own2, r.expert[0:1, ds(2 * i, 2)])
                    for s in range(2):
                        t = 2 * i + s
                        e = nc.tensor.snap(own2[s], min_val=0, max_val=E - 1)
                        pe.wait_ge(ht_ready, t + 3)
                        pe.wait_ge(copied, t + 1)
                        for c in range(NC):
                            last = nc.tensor.matmul(g.ps[6 + s][:, 0:D], ht[:, s, c * P:(c + 1) * P], w2[:, c, ds(e * D, D)],
                                                    start=(c == 0), stop=(c == NC - 1))
                        last.then_inc(product, 1)

                turn_rows(0)
                first_layer(0)
                with nc.tensor.Fori(0, PAIRS - 1) as i:
                    turn_rows(i + 1)
                    turn_hidden(i)
                    first_layer(i + 1)
                    second_layer(i)
                turn_hidden(PAIRS - 1)
                second_layer(PAIRS - 1)

            @block.scalar
            def _(act):
                act.sem_inc(xt_ready, 2)
                with nc.scalar.Fori(0, PAIRS) as i:
                    for s in range(2):
                        t = 2 * i + s
                        act.wait_ge(turned, t + 3)
                        act.wait_ge(hidden, t + 1)
                        nc.scalar.activation(xt[:, s, :], g.ps[s][:, 0:D], ACT.Copy).then_inc(xt_ready, 1)
                    for s in range(2):
                        t = 2 * i + s
                        act.wait_ge(biased, t + 3)
                        nc.scalar.activation(h[:, s, :], h[:, s, :], ACT.Gelu).then_inc(active, 1)

            @block.vector
            def _(dve):
                own = [nc.vector.alloc_register(g.tag + f"dve_owner{s}") for s in range(2)]
                own2 = [nc.vector.alloc_register(g.tag + f"dve_owner_out{s}") for s in range(2)]
                dve.sem_inc(biased, 2)
                dve.sem_inc(ht_ready, 2)
                dve.sem_inc(copied, 2)
                dve.sem_inc(freed, 2)

                def add_bias(i):
                    nc.vector.reg_load(own, r.expert[0:1, ds(2 * i, 2)])
                    for s in range(2):
                        t = 2 * i + s
                        e = nc.vector.snap(own[s], min_val=0, max_val=E - 1)
                        dve.wait_ge(hidden, t + 3)
                        dve.wait_ge(turned_h, t + 1)
                        nc.vector.tensor_tensor(h[:, s, :], g.ps[2 + s][:, :], b1[:, ds(e * H2, H2)], ALU.add).then_inc(biased, 1)

                def copy_hidden(i):
                    for s in range(2):
                        t = 2 * i + s
                        dve.wait_ge(turned_h, t + 3)
                        dve.wait_ge(product, t + 1)
                        nc.vector.tensor_copy(ht[:, s, :], g.ps[4 + s][:, :]).then_inc(ht_ready, 1)

                def finish(i):
                    nc.vector.reg_load(own2, r.expert[0:1, ds(2 * i, 2)])
                    for s in range(2):
                        t = 2 * i + s
                        e = nc.vector.snap(own2[s], min_val=0, max_val=E - 1)
                        dve.wait_ge(product, t + 3)
                        dve.wait_ge(freed, t + 1)
                        nc.vector.tensor_tensor(y[:, s, :], g.ps[6 + s][:, 0:D], b2[:, ds(e * D, D)], ALU.add).then_inc(copied, 1)

                add_bias(0)
                copy_hidden(0)
                with nc.vector.Fori(1, PAIRS) as i:
                    add_bias(i)
                    finish(i - 1)
                    copy_hidden(i)
                finish(PAIRS - 1)

            @block.gpsimd
            def _(pool):
                store_tiles(nc, pool, T2 // 2, r.result, y, copied, stored, freed)

        collect_rows(nc, g, "mo", r, 2, g.x)


H3 = 1024
T3 = (NODES + E * (P - 1)) // P
T3 += T3 % 2


def layer3_ffn(nc, g, a, table):
    NF = H3 // P
    with ExitStack() as stack:
        sb = lambda n, s, d=F32: stack.enter_context(nc.sbuf_tensor(g.tag + n, s, d))
        r = new_route(nc, g, stack, "top", 1, T3 * P)
        w1, b1, wd, bd = sb("w1", [P, 2, H3]), sb("b1", [P, NF]), sb("wd", [P, NF, E * D]), g.acc[:, :, :].rearrange("p t d -> p (t d)")[:, 0:E * D]
        with ExitStack() as s1:
            sb1 = lambda n, s: s1.enter_context(nc.sbuf_tensor(g.tag + n, s, F32))
            wg, bg, logits = sb1("wg", [P, NF, E]), sb1("bg", [1, E]), sb1("logits", [P, NT, E])
            layer_norm(nc, g, None, loads(nc, g, "top", [(w1[:, :, :], rows_in(a.l3f_w1)), (b1[:, :], a.l3f_b1_cols),
                                        (wg[:, :, :], rows_in(a.l3f_wg)), (bg[:, :], a.l3f_bg)]))
            with ExitStack() as s2:
                sem = lambda n: nc.alloc_semaphore(g.tag + "g_" + n)
                xnt = g.acct
                ht = s2.enter_context(nc.sbuf_tensor(g.tag + "g_ht", [P, NF, 2 * P], F32))
                turn_nodes(nc, g, xnt)
                hidden, active, product, used = sem("hidden"), sem("active"), sem("product"), sem("used")
                block = s2.enter_context(nc.Block(g.tag + "gate"))
                G = 2 * P
                experts_in = loads(nc, g, "top_experts", [
                    (wd[:, f, :].rearrange("p (e h) -> p e h", e=E), a.l3f_wd[:, f * P:(f + 1) * P, :].rearrange("e p h -> p e h")) for f in range(NF)]
                    + [(bd, across(a.l3f_bd))])

                @block.sync
                def _(sp):
                    experts_in(sp)

                @block.tensor
                def _(pe):
                    pe.sem_inc(hidden, 4)
                    pe.sem_inc(product, 2)
                    with nc.tensor.Fori(0, ROWS // G) as i:
                        for f in range(NF):
                            pe.wait_ge(active, NF * i + f + 1)
                            for c in range(2):
                                last = nc.tensor.matmul(g.ps[f % 4][:, 0:G], w1[:, c, f * P:(f + 1) * P], xnt[:, c, ds(i * G, G)],
                                                        start=(c == 0), stop=(c == 1))
                            last.then_inc(hidden, 1)
                        for s in range(2):
                            pe.wait_ge(used, 2 * i + s + 1)
                            nc.tensor.matmul(g.ps[4 + s][:, 0:E], g.ones[0:1, :], bg[0:1, :], start=True, stop=False)
                            for f in range(NF):
                                if s == 0:
                                    pe.wait_ge(active, NF * i + f + 5)
                                last = nc.tensor.matmul(g.ps[4 + s][:, 0:E], ht[:, f, s * P:(s + 1) * P], wg[:, f, :],
                                                        start=False, stop=(f == NF - 1))
                            last.then_inc(product, 1)

                @block.scalar
                def _(act):
                    act.sem_inc(active, 4)
                    with nc.scalar.Fori(0, ROWS // G) as i:
                        act.wait_ge(product, 2 * i + 2)
                        for f in range(NF):
                            act.wait_ge(hidden, NF * i + f + 5)
                            nc.scalar.activation(ht[:, f, :], g.ps[f % 4][:, 0:G], ACT.Gelu, bias=b1[:, f:f + 1]).then_inc(active, 1)

                @block.vector
                def _(dve):
                    dve.sem_inc(used, 2)
                    with nc.vector.Fori(0, ROWS // G) as i:
                        for s in range(2):
                            dve.wait_ge(product, 2 * i + s + 3)
                            nc.vector.tensor_copy(logits[:, ds(2 * i + s, 1), :], g.ps[4 + s][:, 0:E]).then_inc(used, 1)

            route(nc, g, "top_route", logits, 1, None, None, r, clear_rows(r, g.acct[:, 0, 0:4 * D]))
        send_rows(nc, g, "top", r, 1, g.xn)
        with ExitStack() as s2:
            sem = lambda n: nc.alloc_semaphore(g.tag + "e_" + n)
            sb2 = lambda n, s: s2.enter_context(nc.sbuf_tensor(g.tag + "e_" + n, s, F32))
            stored = [sem(f"stored{s}") for s in range(2)]
            loaded, turned, xt_ready, hidden, active, product, copied, freed = (sem(n) for n in (
                "loaded", "turned", "xt_ready", "hidden", "active", "product", "copied", "freed"))
            rows, xt, ht, y = sb2("rows", [P, 2, D]), sb2("xt", [P, 2, 2 * P]), sb2("ht", [P, NF, 2 * P]), sb2("y", [P, 2, D])
            block = s2.enter_context(nc.Block(g.tag + "experts"))

            @block.sync
            def _(sp):
                with nc.sync.Fori(0, T3 // 2) as i:
                    sp.wait_ge(turned, i + 1)
                    sp.dma_start(rows[:, :, :], r.sorted[ds(2 * i * P, 2 * P), :].rearrange("(r p) d -> p r d", p=P)).then_inc(loaded, 16)

            @block.tensor
            def _(pe):
                own = [nc.tensor.alloc_register(g.tag + f"owner{s}") for s in range(2)]
                pe.sem_inc(turned, 1)
                pe.sem_inc(hidden, 3)
                pe.sem_inc(product, 2)

                def turn_rows(i):
                    pe.wait_ge(loaded, 16 * (i + 1))
                    pe.wait_ge(xt_ready, i + 1)
                    for c in range(2):
                        for s in range(2):
                            last = nc.tensor.transpose(g.ps[0][:, (2 * c + s) * P:(2 * c + s + 1) * P], rows[:, s, c * P:(c + 1) * P], g.ident[:, :])
                    last.then_inc(turned, 1)

                def first_layer(i):
                    pe.wait_ge(xt_ready, i + 2)
                    for f in range(NF):
                        pe.wait_ge(active, NF * i + f + 1)
                        for c in range(2):
                            last = nc.tensor.matmul(g.ps[1 + f % 4][:, 0:2 * P], w1[:, c, f * P:(f + 1) * P], xt[:, c, :],
                                                    start=(c == 0), stop=(c == 1))
                        last.then_inc(hidden, 1)

                def second_layer(i):
                    nc.tensor.reg_load(own, r.expert[0:1, ds(2 * i, 2)])
                    for s in range(2):
                        t = 2 * i + s
                        e = nc.tensor.snap(own[s], min_val=0, max_val=E - 1)
                        pe.wait_ge(copied, t + 1)
                        for f in range(NF):
                            if s == 0:
                                pe.wait_ge(active, NF * i + f + 5)
                            last = nc.tensor.matmul(g.ps[5 + s][:, 0:D], ht[:, f, s * P:(s + 1) * P], wd[:, f, ds(e * D, D)],
                                                    start=(f == 0), stop=(f == NF - 1))
                        last.then_inc(product, 1)

                turn_rows(0)
                with nc.tensor.Fori(0, T3 // 2 - 1) as i:
                    first_layer(i)
                    turn_rows(i + 1)
                    second_layer(i)
                first_layer(T3 // 2 - 1)
                second_layer(T3 // 2 - 1)

            @block.scalar
            def _(act):
                act.sem_inc(xt_ready, 1)
                act.sem_inc(active, 4)

                def copy_rows(i):
                    act.wait_ge(turned, i + 2)
                    act.wait_ge(hidden, NF * i + 3)
                    nc.scalar.activation(xt[:, :, :], g.ps[0][:, :].rearrange("p (c n) -> p c n", c=2), ACT.Copy).then_inc(xt_ready, 1)

                def activate(i):
                    act.wait_ge(product, 2 * i + 2)
                    for f in range(NF):
                        act.wait_ge(hidden, NF * i + f + 4)
                        nc.scalar.activation(ht[:, f, :], g.ps[1 + f % 4][:, 0:2 * P], ACT.Gelu, bias=b1[:, f:f + 1]).then_inc(active, 1)

                copy_rows(0)
                with nc.scalar.Fori(0, T3 // 2 - 1) as i:
                    activate(i)
                    copy_rows(i + 1)
                activate(T3 // 2 - 1)

            @block.vector
            def _(dve):
                own = [nc.vector.alloc_register(g.tag + f"dve_owner{s}") for s in range(2)]
                dve.sem_inc(copied, 2)
                dve.sem_inc(freed, 2)
                with nc.vector.Fori(0, T3 // 2) as i:
                    nc.vector.reg_load(own, r.expert[0:1, ds(2 * i, 2)])
                    for s in range(2):
                        t = 2 * i + s
                        e = nc.vector.snap(own[s], min_val=0, max_val=E - 1)
                        dve.wait_ge(product, t + 3)
                        dve.wait_ge(freed, t + 1)
                        nc.vector.tensor_tensor(y[:, s, :], g.ps[5 + s][:, 0:D], bd[:, ds(e * D, D)], ALU.add).then_inc(copied, 1)

            @block.gpsimd
            def _(pool):
                store_tiles(nc, pool, T3 // 2, r.result, y, copied, stored, freed)

        collect_rows(nc, g, "top", r, 1, g.x)


TABLES = 4


def source_tables(nc):
    return [nc.dram_tensor(f"source_sums{k}", (ROWS + P, D), F32).ap() for k in range(TABLES)]


def clear_tables(nc, g, sp, zeros, tables, zeroed):
    n = 0
    for k in range(TABLES):
        for r0 in range(0, ROWS + P, 4 * P):
            m = min(4, (ROWS + P - r0) // P)
            sp.dma_start(tables[k][r0:r0 + m * P, :].rearrange("(p j) d -> p (j d)", p=P), zeros[:, 0:m * D]).then_inc(zeroed, 16)
            n += 16
    sp.wait_ge(zeroed, n)


def split_nodes(nc, g, parts):
    with ExitStack() as stack:
        sem = lambda n: nc.alloc_semaphore(g.tag + "p_" + n)
        cut, rest, one, two = sem("cut"), sem("rest"), g.xn[:, :, :].rearrange("p t d -> p (t d)"), g.acc[:, :, :].rearrange("p t d -> p (t d)")
        block = stack.enter_context(nc.Block(g.tag + "split_nodes"))
        N, n = 4, NT * D // 4

        @block.scalar
        def _(act):
            for k in range(3):
                for c in range(N):
                    if k:
                        act.wait_ge(rest, N * (k - 1) + c + 1)
                    nc.scalar.activation(parts[:, k, c * n:(c + 1) * n], (two if k else one)[:, c * n:(c + 1) * n], ACT.Copy).then_inc(cut, 1)
            act.wait_ge(cut, 3 * N)

        @block.vector
        def _(dve):
            for k in range(2):
                for c in range(N):
                    dve.wait_ge(cut, N * k + c + 1)
                    if k:
                        dve.wait_ge(rest, c + 1)
                    nc.vector.tensor_tensor(two[:, c * n:(c + 1) * n], (two if k else one)[:, c * n:(c + 1) * n],
                                            parts[:, k, c * n:(c + 1) * n], ALU.subtract).then_inc(rest, 1)


def scatter_edges(nc, g, a, tables):
    with ExitStack() as stack:
        sem = lambda n: nc.alloc_semaphore(g.tag + "s_" + n)
        sb = lambda n, s, d=F32: stack.enter_context(nc.sbuf_tensor(g.tag + "s_" + n, s, d))
        weights, srcf = sb("weights", [P, ET + 8]), sb("srcf", [P, ET + 8])
        loaded = [sem(f"loaded{q}") for q in range(PARTS)]
        scattered = [sem(f"scattered{k}") for k in range(TABLES)]
        prep, weights_in, hot, looked, placed, mixed, summed, ready, claimed, counted, step, chosen, retired = (sem(n) for n in (
            "prep", "weights_in", "hot", "looked", "placed", "mixed", "summed", "ready", "claimed", "counted", "step", "chosen", "retired"))
        src, dst = sb("src_across", [P, PARTS, Q * P], I32), sb("dst_across", [P, PARTS, Q * P], I32)
        idx, count, spare, away, lower, junk = sb("idx", [P, U], I32), sb("count", [P, Q]), sb("spare", [P, 1]), sb("away", [P, Q]), sb("lower", [P, P]), sb("junk", [P, Q, P])
        onehot_t, mix, parts = sb("onehot_t", [P, 4, 2, P], BF16), sb("mix", [P, 4, P]), sb("xn_parts", [P, 3, NT * D], BF16)
        found, rows = sb("found", [P, 4, D]), sb("rows", [P, U, D])
        split_nodes(nc, g, parts)
        block = stack.enter_context(nc.Block(g.tag + "scatter_edges"))

        @block.sync
        def _(sp):
            sp.dma_start(weights[:, 0:ET], a.edge_weight_cols).then_inc(weights_in, 16)
            with nc.sync.Fori(0, ET // U) as i:
                for q in range(PARTS):
                    sp.wait_ge(mixed, U * i + (q + 1) * Q)
                    for t, v, first in ((src, a.src_row, 0), (dst, a.dst_row, 1)):
                        sp.dma_start(t[:, q, :], v[ds((PARTS * i + q) * Q * P + first, Q * P)]
                                     .rearrange("(o n) -> o n", o=1).to_broadcast([P, Q * P])).then_inc(loaded[q], 16)

        @block.gpsimd
        def _(pool):
            nc.gpsimd.affine_select(out=lower[:, :], in_=g.ones[:, :], compare_op=ALU.is_gt, fill=0.0, base=0,
                                    pattern=[[-1, P]], channel_multiplier=1).then_inc(prep, 1)
            nc.gpsimd.iota(spare[:, :], [[0, 1]], base=ROWS, channel_multiplier=1, allow_small_or_imprecise_dtypes=True).then_inc(prep, 1)

            def round(i):
                first = isinstance(i, int)
                for u in range(U):
                    k = u % TABLES
                    if u % Q == 0:
                        pool.wait_ge(chosen, PARTS * i + u // Q + 1)
                    pool.wait_ge(ready, U * i + u + 5)
                    pool.sem_inc(claimed, 1)
                    nc.gpsimd.indirect_dma_start(
                        tables[k], bass.IndirectOffsetOnAxis(ap=idx[:, u:u + 1].bitcast(U32), axis=0),
                        rows[:, u, :], None, bounds_check=ROWS + P - 1, compute_op=ALU.add).then_inc(scattered[k], 16)
                    n = (k + 1) % TABLES
                    if first and u < TABLES - 1:
                        continue
                    pool.wait_ge(scattered[n], 16 * (U // TABLES * i + u // TABLES + (1 if k == TABLES - 1 else 0)))
                    pool.sem_inc(retired, 1)
            round(0)
            with nc.gpsimd.Fori(1, ET // U) as i:
                round(i)
            for k in range(TABLES):
                pool.wait_ge(scattered[k], 16 * ET // TABLES)

        @block.tensor
        def _(pe):
            window = [nc.tensor.alloc_register(g.tag + f"sw{u}") for u in range(8)]
            pe.sem_inc(summed, 4)
            pe.sem_inc(looked, 4)
            with nc.tensor.Fori(0, ET // U) as i:
                for v in range(0, U, 4):
                    if v % 8 == 0:
                        nc.tensor.reg_load(window, g.window[0:1, ds(U * i + v, 8)])
                    four = range(v, v + 4)
                    for u in four:
                        w = nc.tensor.snap(window[u % 8], min_val=0, max_val=NT - 2)
                        pe.wait_ge(hot, U * i + u + 1)
                        for k in range(2):
                            for j in range(3):
                                last = nc.tensor.matmul(g.ps[u % 4][:, 0:D], onehot_t[:, u % 4, k, :], parts[:, j, ds(w * D + k * D, D)],
                                                        start=(k == 0 and j == 0), stop=(k == 1 and j == 2))
                        last.then_inc(looked, 1)
                    pe.wait_ge(ready, U * i + v + 4)
                    for u in four:
                        if u % 2 == 0:
                            pe.wait_ge(mixed, U * i + u + U + 2)
                        pe.wait_ge(placed, U * i + u + 1)
                        nc.tensor.matmul(g.ps[4 + u % 4][:, 0:D], mix[:, u % 4, :], found[:, u % 4, :], start=True, stop=True).then_inc(summed, 1)

        @block.scalar
        def _(act):
            act.sem_inc(ready, 4)
            act.sem_inc(retired, U)
            with nc.scalar.Fori(0, ET // U) as i:
                for v in range(0, U, 4):
                    four = range(v, v + 4)
                    for u in four:
                        act.wait_ge(looked, U * i + u + 5)
                        nc.scalar.activation(found[:, u % 4, :], g.ps[u % 4][:, 0:D], ACT.Copy).then_inc(placed, 1)
                    act.wait_ge(retired, U * i + v + 4)
                    for u in four:
                        act.wait_ge(summed, U * i + u + 5)
                        nc.scalar.activation(rows[:, u, :], g.ps[4 + u % 4][:, 0:D], ACT.Copy).then_inc(ready, 1)

        @block.vector
        def _(dve):
            window = [nc.vector.alloc_register(g.tag + f"dve_window{u}") for u in range(8)]
            dve.sem_inc(mixed, U)
            nc.vector.tensor_copy(srcf[:, 0:ET], g.srcc[:, 0:ET]).then_inc(prep, 1)
            dve.wait_ge(prep, 3)
            dve.wait_ge(weights_in, 16)
            HOT, MIX = 4, 2

            def windows(i, h, count=8):
                nc.vector.reg_load(window[0:count], g.window[0:1, ds(U * i + h * H + HOT, count)])

            def build(i, u, w, n):
                nc.vector.tensor_tensor(onehot_t[:, u % 4, :, :], dst[:, u // Q, u % Q * P:(u % Q + 1) * P].unsqueeze(1).to_broadcast([P, 2, P]),
                                        g.node_id[:, ds(w, 2)].unsqueeze(2).to_broadcast([P, 2, P]), ALU.is_equal).then_inc(hot, 1)

            def share(i, u, n):
                nc.vector.tensor_scalar(mix[:, u % 4, :], src[:, u // Q, u % Q * P:(u % Q + 1) * P], srcf[:, ds(n, 1)],
                                        weights[:, ds(n, 1)], ALU.is_equal, ALU.mult).then_inc(mixed, 1)

            def count_before(u, n):
                nc.vector.scalar_tensor_tensor(out=junk[:, u % Q, :], in0=src[:, u // Q, u % Q * P:(u % Q + 1) * P], scalar=srcf[:, ds(n, 1)],
                                               in1=lower[:, :], op0=ALU.is_equal, op1=ALU.mult, accum_out=count[:, u % Q:u % Q + 1]).then_inc(counted, 1)

            def choose(n, q, done):
                if not (isinstance(done, int) and done == 0):
                    dve.wait_ge(chosen, done)
                nc.vector.tensor_scalar(away[:, :], srcf[:, ds(n, Q)], spare[:, 0:1], None, ALU.subtract).then_inc(step, 1)
                dve.wait_ge(step, 2 * done + 1)
                dve.wait_ge(counted, Q * done + Q)
                nc.vector.scalar_tensor_tensor(out=away[:, :], in0=count[:, :], scalar=0.0, in1=away[:, :], op0=ALU.is_equal, op1=ALU.mult).then_inc(step, 1)
                dve.wait_ge(step, 2 * done + 2)
                dve.wait_ge(retired, Q * done + Q)
                nc.vector.tensor_scalar(idx[:, q * Q:(q + 1) * Q], away[:, :], spare[:, 0:1], None, ALU.add).then_inc(chosen, 1)

            dve.wait_ge(loaded[0], 32)
            for u in range(Q):
                count_before(u, u)
            choose(0, 0, 0)
            nc.vector.reg_load(window, g.window[0:1, 0:8])
            for u in range(HOT):
                build(0, u, nc.vector.snap(window[u], min_val=0, max_val=NT - 2), u)
            for u in range(MIX):
                share(0, u, u)

            def round(i, last=False):
                for u in range(U):
                    final = last and u >= U - Q
                    if u % 8 == 0:
                        windows(i, u // 8, 8 - HOT if last and u else 8)
                    w = None if last and u + HOT >= U else nc.vector.snap(window[u % 8], min_val=0, max_val=NT - 2)
                    if u % Q == 0 and not final:
                        q = u // Q + 1
                        dve.wait_ge(loaded[q % PARTS], 32 * (i + q // PARTS + 1))
                    dve.wait_ge(looked, U * i + u + 5)
                    if not (last and u + HOT >= U):
                        build(i, (u + HOT) % U, w, U * i + u + HOT)
                    if not final:
                        count_before((u + Q) % U, U * i + u + Q)
                    dve.wait_ge(summed, U * i + u + 3)
                    if not (last and u + MIX >= U):
                        share(i, (u + MIX) % U, U * i + u + MIX)
                    if u % Q == Q - 1 and not final:
                        choose(U * i + u + 1, (u // Q + 1) % PARTS, PARTS * i + u // Q + 1)
            with nc.vector.Fori(0, ET // U - 1) as i:
                round(i)
            round(ET // U - 1, last=True)


def sum_tables(nc, g, tables):
    with ExitStack() as stack:
        sem = lambda n: nc.alloc_semaphore(g.tag + "t_" + n)
        part = [stack.enter_context(nc.sbuf_tensor(g.tag + f"t_part{k}", [P, NT, D], F32)) for k in range(2)]
        loaded = [sem(f"loaded{k}") for k in range(TABLES)]
        added = sem("added")
        block = stack.enter_context(nc.Block(g.tag + "sum_tables"))
        dst = [g.acc] + [part[k % 2] for k in range(TABLES - 1)]

        @block.sync
        def _(sp):
            for k in range(TABLES):
                if k >= 3:
                    sp.wait_ge(added, k - 2)
                sp.dma_start(dst[k][:, :, :], tables[k][0:ROWS, :].rearrange("(t p) d -> p t d", p=P)).then_inc(loaded[k], 16)

        @block.vector
        def _(dve):
            dve.wait_ge(loaded[0], 16)
            for k in range(1, TABLES):
                dve.wait_ge(loaded[k], 16)
                if k > 1:
                    dve.wait_ge(added, k - 1)
                nc.vector.tensor_tensor(g.acc[:, :, :], g.acc[:, :, :], dst[k][:, :, :], ALU.add).then_inc(added, 1)
            dve.wait_ge(added, TABLES - 1)


def layer2_gnn(nc, g, a, table):
    with ExitStack() as stack:
        sb = lambda n, s: stack.enter_context(nc.sbuf_tensor(g.tag + n, s, F32))
        wl, wr, bias = sb("wl", [P, 2, D]), sb("wr", [P, 2, D]), sb("bias", [1, 3, D])
        layer_norm(nc, g, None, loads(nc, g, "l2g", [(wl[:, :, :], rows_in(a.l2g_w_l)), (wr[:, :, :], rows_in(a.l2g_w_r)),
                                    (bias[:, 0, :], a.l2g_b_l), (bias[:, 1, :], a.l2g_b_r)]))
        scatter_edges(nc, g, a, g.tables)
        sum_tables(nc, g, g.tables)
        with ExitStack() as s2:
            step = nc.alloc_semaphore(g.tag + "bias_step")
            block = s2.enter_context(nc.Block(g.tag + "bias"))

            @block.vector
            def _(dve):
                nc.vector.tensor_tensor(bias[:, 2, :], bias[:, 0, :], bias[:, 1, :], ALU.add).then_inc(step, 1)
                dve.wait_ge(step, 1)
        project(nc, g, "l2g", [wl, wr], bias[0:1, 2, :], D,
                [("pool", lambda out, t: nc.gpsimd.tensor_copy(out, g.acc[:, ds(t, 1), :])),
                 ("dve", lambda out, t: nc.vector.tensor_copy(out, g.xn[:, ds(t, 1), :]))],
                lambda dve, bank, t, s: nc.vector.tensor_tensor(g.x[:, ds(t, 1), :], g.x[:, ds(t, 1), :], bank, ALU.add))


C3 = 128


def node_steps(nc, g, name, steps, table=None, rows=None):
    with ExitStack() as stack:
        step, stored = nc.alloc_semaphore(g.tag + name + "_step"), nc.alloc_semaphore(g.tag + name + "_stored")
        block = stack.enter_context(nc.Block(g.tag + name))

        @block.vector
        def _(dve):
            for n, s in enumerate(steps):
                s().then_inc(step, 1)
                dve.wait_ge(step, n + 1)

        @block.sync
        def _(sp):
            if table is not None:
                sp.wait_ge(step, len(steps))
                sp.dma_start(table.rearrange("(t p) d -> p t d", p=P), rows).then_inc(stored, 16)
                sp.wait_ge(stored, 16)


def layer3_gnn(nc, g, a, table):
    htable = nc.dram_tensor("gcn_rows", (ROWS, C3), F32).ap()
    htable2 = nc.dram_tensor("gcn_rows2", (ROWS, C3), F32).ap()
    with ExitStack() as stack:
        sb = lambda n, s: stack.enter_context(nc.sbuf_tensor(g.tag + n, s, F32))
        w1, w2, b1, b2 = sb("w1", [P, 2, C3]), sb("w2", [P, 1, D]), sb("b1", [P, C3]), sb("b2", [1, D])
        dinv, hs = sb("dinv", [P, NT]), sb("hs", [P, NT, C3])
        layer_norm(nc, g, None, loads(nc, g, "l3g", [(w1[:, :, :], rows_in(a.l3g_w1)), (w2[:, 0, :], a.l3g_w2), (b1[:, :], across(a.l3g_b1)), (b2[:, :], a.l3g_b2)]))
        with ExitStack() as s2:
            step = nc.alloc_semaphore(g.tag + "dinv_step")
            block = s2.enter_context(nc.Block(g.tag + "dinv"))

            @block.scalar
            def _(act):
                nc.scalar.activation(dinv[:, :], g.deg[:, :], ACT.Sqrt, bias=g.ones[:, 0:1]).then_inc(step, 1)

            @block.vector
            def _(dve):
                dve.wait_ge(step, 1)
                nc.vector.reciprocal(dinv[:, :], dinv[:, :]).then_inc(step, 1)
                dve.wait_ge(step, 2)
        wide = [P, NT, C3]
        acc = g.acc[:, :, :].rearrange("p t d -> p (t d)")[:, 0:NT * C3].rearrange("p (t d) -> p t d", d=C3)
        dw = dinv[:, :].unsqueeze(2).to_broadcast(wide)
        tt = lambda out, x, y, op: (lambda: nc.vector.tensor_tensor(out, x, y, op))
        project(nc, g, "gcn1", [w1], None, C3,
                [("pool", lambda out, t: nc.gpsimd.tensor_copy(out, g.xn[:, ds(t, 1), :]))],
                lambda dve, bank, t, s: nc.vector.tensor_scalar(hs[:, ds(t, 1), :], bank, dinv[:, ds(t, 1)], None, ALU.mult))
        node_steps(nc, g, "gcn_rows", [], htable, hs[:, :, :])
        sum_edges(nc, g, htable, C3, name="gcn_sum1")
        node_steps(nc, g, "gcn_mid", [
            tt(acc, acc, hs[:, :, :], ALU.add), tt(acc, acc, dw, ALU.mult),
            tt(acc, acc, b1[:, :].unsqueeze(1).to_broadcast(wide), ALU.add),
            lambda: nc.vector.tensor_scalar(acc, acc, 0.0, None, ALU.max),
            tt(hs[:, :, :], acc, dw, ALU.mult)], htable2, hs[:, :, :])
        sum_edges(nc, g, htable2, C3, name="gcn_sum2")
        node_steps(nc, g, "gcn_end", [tt(acc, acc, hs[:, :, :], ALU.add), tt(hs[:, :, :], acc, dw, ALU.mult)])
        project(nc, g, "gcn2", [w2], b2[0:1, :], D,
                [("pool", lambda out, t: nc.gpsimd.tensor_copy(out, hs[:, ds(t, 1), :]))],
                lambda dve, bank, t, s: nc.vector.tensor_tensor(g.x[:, ds(t, 1), :], g.x[:, ds(t, 1), :], bank, ALU.add), chunks=1)


def store_out(nc, g, src, out):
    with ExitStack() as stack:
        stored = nc.alloc_semaphore("out_stored")
        block = stack.enter_context(nc.Block("store_out"))

        @block.sync
        def _(sp):
            sp.dma_start(out[0:FULL * P, :].rearrange("(t p) d -> p t d", p=P), src[:, 0:FULL, :]).then_inc(stored, 16)
            sp.dma_start(out[FULL * P:NODES, :], src[0:REST, FULL, :]).then_inc(stored, 16)
            sp.wait_ge(stored, 32)


def build(nc, a, out, stages):
    g = Core()
    g.tag = ""
    with ExitStack() as stack:
        tensors(nc, g, stack)
        table = nc.dram_tensor("xn_rows", (ROWS, D), F32).ap()
        load_graph(nc, g, a)
        for s in stages:
            g.tag = s.__name__ + "_"
            held = nc.snapshot_sems()
            s(nc, g, a, table)
            nc.clear_and_free_semaphores(nc.allocated_since(held))
            nc.all_engine_barrier()
        store_out(nc, g, g.x, out)


def _layout(inputs):
    import numpy as _np
    n = lambda v: _np.ascontiguousarray(_np.asarray(v))
    v = {k: _np.asarray(x) for k, x in inputs.items()}
    pad = _np.full(ET * P - EDGES, 3199, _np.int32)
    row = lambda u: _np.concatenate([u, pad])
    cols = lambda u: n(row(u).reshape(ET, P).T)
    flat = lambda u: n(u.reshape(-1))
    one = lambda u: n(u.reshape(1, -1))
    laid = {"x": n(v["x"]), "src_cols": cols(v["src"]), "dst_cols": cols(v["dst"]),
            "l0g_w_self_t": n(v["L0_gnn_W_self"].T), "l0g_w_neigh_t": n(v["L0_gnn_W_neigh"].T), "l0g_b_self": one(v["L0_gnn_b_self"]),
            "l0f_wr": flat(v["L0_ffn_wr"]), "l0f_br": n(v["L0_ffn_br"]), "l0f_w1": n(v["L0_ffn_w1"]), "l0f_w2": n(v["L0_ffn_w2"]),
            "l0f_b1_cols": n(v["L0_ffn_b1"].reshape(-1, P).T), "l0f_b2": one(v["L0_ffn_b2"]),
            "l1g_w_t": n(v["L1_gnn_W"].T), "l1g_w": n(v["L1_gnn_W"]), "l1g_a_src_cols": n(v["L1_gnn_a_src"].reshape(2, P).T),
            "l1g_a_dst_cols": n(v["L1_gnn_a_dst"].reshape(2, P).T), "l1g_edge_w_t": n(v["L1_gnn_edge_W"].T),
            "l1g_edge_b": one(v["L1_gnn_edge_b"]), "l1g_bias": n(v["L1_gnn_bias"]),
            "edge_attr_flat": n(_np.concatenate([v["edge_attr_3"], _np.zeros((ET * P - EDGES, 3), _np.float32)]).T).reshape(P, -1),
            "l1f_gate_w": n(v["L1_ffn_gate_w"]), "l1f_gate_b": one(v["L1_ffn_gate_b"]), "l1f_w1": n(v["L1_ffn_w1"]), "l1f_w2": n(v["L1_ffn_w2"]),
            "l1f_b1_cols": n(v["L1_ffn_b1"].reshape(-1, P).T), "l1f_b2": n(v["L1_ffn_b2"]),
            "l2f_gamma": n(v["L2_ffn_gamma"]), "l2f_beta": n(v["L2_ffn_beta"]), "l2f_wr": n(v["L2_ffn_Wr"]), "l2f_br": one(v["L2_ffn_br"]),
            "l2f_w1": n(v["L2_ffn_W1"]), "l2f_b1": flat(v["L2_ffn_b1"]), "l2f_w2": n(v["L2_ffn_W2"]), "l2f_b2": flat(v["L2_ffn_b2"]),
            "l3f_w1": n(v["L3_ffn_W1"]), "l3f_b1_cols": n(v["L3_ffn_b1"].reshape(-1, P).T), "l3f_wg": n(v["L3_ffn_Wg"]),
            "l3f_bg": one(v["L3_ffn_bg"]), "l3f_wd": n(v["L3_ffn_Wd"]), "l3f_bd": flat(v["L3_ffn_bd"]),
            "l2g_w_l": n(v["L2_gnn_weight_l"]), "l2g_w_r": n(v["L2_gnn_weight_r"]), "l2g_b_l": one(v["L2_gnn_bias_l"]), "l2g_b_r": one(v["L2_gnn_bias_r"]),
            "edge_weight_cols": n(_np.concatenate([v["edge_weight"], _np.zeros(ET * P - EDGES, _np.float32)]).reshape(ET, P).T),
            "src_row": n(row(v["src"])),
            "l3g_w1": n(v["L3_gnn_W1"]), "l3g_w2": n(v["L3_gnn_W2"]), "l3g_b1": n(v["L3_gnn_b1"]), "l3g_b2": one(v["L3_gnn_b2"]),
            "dst_row": n(_np.concatenate([_np.full(1, -1, _np.int32), row(v["dst"]), _np.full(1, -1, _np.int32)]))}
    return laid


def kernel(**inputs):
    import numpy as _np
    import concourse.bacc as _bacc
    from concourse import mybir as _mybir
    from concourse.bass_utils import run_bass_kernel_spmd as _run

    nc = _bacc.Bacc("TRN2", target_bir_lowering=False, num_devices=1)
    laid = _layout(inputs)
    a = Core()
    arrays = {}
    for name, v in laid.items():
        arrays[f"in_{name}"] = v
        a.__dict__[name] = nc.dram_tensor(f"in_{name}", v.shape, _mybir.dt.from_np(v.dtype), kind="ExternalInput").ap()
    out = nc.dram_tensor("out_0", (NODES, D), F32, kind="ExternalOutput").ap()
    build(nc, a, out, STAGES)
    r = _run(nc, [arrays], core_ids=[0])
    return r.results[0]["out_0"]
STAGES = [layer0_gnn, layer0_ffn, layer1_gnn, layer1_ffn, layer2_gnn, layer2_ffn, layer3_gnn, layer3_ffn]
```
